# Optimizing a Trainium2 kernel written in Bass

```python
import numpy as np
import jax
import jax.numpy as jnp

def _softmax(x, axis=-1):
    return jax.nn.softmax(x, axis=axis)

def _gelu(x):
    return jax.nn.gelu(x, approximate=True)

def _silu(x):
    return jax.nn.silu(x)

def _sigmoid(x):
    return jax.nn.sigmoid(x)

def _layernorm(x, axis=-1, eps=1e-05):
    m = jnp.mean(x, axis=axis, keepdims=True)
    v = jnp.var(x, axis=axis, keepdims=True)
    return (x - m) / jnp.sqrt(v + eps)

def _scatter_add(tgt, idx, src, axis=0):
    return tgt.at[idx].add(src)

def _segment_sum(src, seg, n):
    return jax.ops.segment_sum(src, seg, n)
kernel_name = 'mk_decoder_preln_d4_seqx_r8_cf24da'

def setup_inputs(seed: int=0):
    np.random.seed(seed)
    _w = jnp.asarray

    def _rec_inputs():
        import jax
        import jax.numpy as jnp
        _rk = jax.random.key(seed)
        x = 4.136e-05 + 0.9999 * jax.random.normal(jax.random.fold_in(_rk, 1), (32, 56, 128), jnp.float32)
        _lenS = 56 - jax.random.randint(jax.random.fold_in(_rk, 7), (32,), 0, max(1, 56 // 4) + 1, jnp.int32)
        _lenS2 = 1500 - jax.random.randint(jax.random.fold_in(_rk, 8), (32,), 0, max(1, 1500 // 4) + 1, jnp.int32)
        _ctx_1024P = jax.random.normal(jax.random.fold_in(_rk, 11), (32, 16, 128), jnp.float32)
        _ctx_1024c = jax.random.dirichlet(jax.random.fold_in(_rk, 511), 0.3 * jnp.ones((16,), jnp.float32), (32, 1500))
        _ctx_1024t = jnp.einsum('bsk,bkd->bsd', _ctx_1024c, _ctx_1024P)
        _ctx_1024t = _ctx_1024t * jax.lax.rsqrt(jnp.mean(jnp.square(_ctx_1024t)) + 1e-12) * 0.953939
        ctx_1024 = -7.10856e-05 + 0.999911 * (_ctx_1024t + 0.3 * jax.random.normal(jax.random.fold_in(_rk, 611), (32, 1500, 128), jnp.float32))
        return (x, ctx_1024)
    x, ctx_1024 = _rec_inputs()

    def _L0_attn_setup():
        import jax, jax.numpy as jnp
        import numpy as np
        B, T, D = (4, 256, 128)
        H, Dh = (16, 64)
        key = jax.random.key(seed)
        ks = jax.random.split(key, 5)
        std_qkv = float(np.sqrt(2.0 / (Dh * D)))
        std_o = float(np.sqrt(2.0 / (D * Dh)))
        return {'x': jax.random.normal(ks[0], (B, T, D), dtype=jnp.float32), 'W_Q': jax.random.normal(ks[1], (H, Dh, D), dtype=jnp.float32) * std_qkv, 'b_Q': jnp.zeros((H, Dh), dtype=jnp.float32), 'W_K': jax.random.normal(ks[2], (H, Dh, D), dtype=jnp.float32) * std_qkv, 'b_K': jnp.zeros((H, Dh), dtype=jnp.float32), 'W_V': jax.random.normal(ks[3], (H, Dh, D), dtype=jnp.float32) * std_qkv, 'b_V': jnp.zeros((H, Dh), dtype=jnp.float32), 'W_O': jax.random.normal(ks[4], (H, D, Dh), dtype=jnp.float32) * std_o, 'b_O': jnp.zeros((D,), dtype=jnp.float32)}
    _L0_attn_all = _L0_attn_setup()
    _L0_attn_in = {k: v for k, v in _L0_attn_all.items() if k in ('W_Q', 'b_Q', 'W_K', 'b_K', 'W_V', 'b_V', 'W_O', 'b_O')}
    del _L0_attn_all

    def _L0_xattn_setup():
        import jax, jax.numpy as jnp
        import numpy as np
        key = jax.random.key(seed)
        k1, k2 = jax.random.split(key)
        B, N, M, D = (32, 256, 32, 128)
        h_enc = jax.random.normal(k1, (B, N, D), dtype=jnp.float32)
        h_dec = jax.random.normal(k2, (B, M, D), dtype=jnp.float32)
        return {'h_enc': h_enc, 'h_dec': h_dec}
    _L0_xattn_all = _L0_xattn_setup()
    _L0_xattn_in = {k: v for k, v in _L0_xattn_all.items() if k in ()}
    del _L0_xattn_all

    def _L0_ffn_setup():
        import jax, jax.numpy as jnp
        import numpy as np
        B, S, DIM = (4, 512, 128)
        BASE_COUPLING = 0.1
        NUM_CYCLES = 3

        def _gelu(x):
            return jax.nn.gelu(x, approximate=False)

        def _coupling_net(h, w1, b1, w2, b2, w3, b3, w4, b4):
            h = _gelu(h @ w1 + b1)
            h = _gelu(h @ w2 + b2)
            h = _gelu(h @ w3 + b3)
            return jax.nn.sigmoid(h @ w4 + b4)

        def _global_net(h, w1, b1, w2, b2, w3, b3):
            h = _gelu(h @ w1 + b1)
            h = _gelu(h @ w2 + b2)
            return jax.nn.sigmoid(h @ w3 + b3)

        def _twist(x):
            o_r, o_i, p_r, p_i = jnp.split(x, 4, axis=-1)
            return jnp.concatenate([p_r, -p_i, -o_r, o_i], axis=-1)
        key = jax.random.key(seed)
        ks = jax.random.split(key, 9)
        d = DIM

        def w(k, fan_in, fan_out):
            return jax.random.normal(k, (fan_in, fan_out), dtype=jnp.float32) / np.sqrt(fan_in).astype(np.float32)
        inp = {'x': jax.random.normal(ks[0], (B, S, d), dtype=jnp.float32)}
        cn_dims = [(d, d), (d, d // 2), (d // 2, d // 4), (d // 4, 1)]
        for i, (a, b) in enumerate(cn_dims):
            inp[f'cn_w{i + 1}'] = w(ks[1 + i], a, b)
            inp[f'cn_b{i + 1}'] = jnp.zeros((b,), dtype=jnp.float32)
        gc_dims = [(d, d // 2), (d // 2, d // 4), (d // 4, 1)]
        for i, (a, b) in enumerate(gc_dims):
            inp[f'gc_w{i + 1}'] = w(ks[5 + i], a, b)
            inp[f'gc_b{i + 1}'] = jnp.zeros((b,), dtype=jnp.float32)
        inp['adaptive_range'] = jnp.full((1,), 0.2, dtype=jnp.float32)
        return inp
    _L0_ffn_all = _L0_ffn_setup()
    _L0_ffn_in = {k: v for k, v in _L0_ffn_all.items() if k in ('cn_w1', 'cn_b1', 'cn_w2', 'cn_b2', 'cn_w3', 'cn_b3', 'cn_w4', 'cn_b4', 'gc_w1', 'gc_b1', 'gc_w2', 'gc_b2', 'gc_w3', 'gc_b3', 'adaptive_range')}
    del _L0_ffn_all

    def _L1_attn_setup():
        import jax, jax.numpy as jnp
        import numpy as np
        D = 128
        KERNEL = 4

        def _causal_depthwise_conv(x, w, b):
            B, L, d = x.shape
            xp = jnp.pad(x, ((0, 0), (KERNEL - 1, 0), (0, 0)))
            out = b[None, None, :]
            for k in range(KERNEL):
                out = out + xp[:, k:k + L, :] * w[:, 0, k][None, None, :]
            return out

        def _parallel_scan(a_t, b_t):
            a = a_t.astype(jnp.float32)
            b = b_t.astype(jnp.float32)
            log_A = jnp.clip(jnp.cumsum(jnp.log(jnp.clip(a, 1e-07)), axis=1), -80.0, None)
            A = jnp.exp(log_A)
            h = A * jnp.cumsum(b * jnp.exp(-log_A), axis=1)
            return h.astype(a_t.dtype)

        def _rmsnorm(x, w, eps=1e-06):
            ms = jnp.mean(jnp.square(x.astype(jnp.float32)), axis=-1, keepdims=True)
            return (x * jax.lax.rsqrt(ms + eps)).astype(x.dtype) * w
        key = jax.random.key(seed)
        ks = jax.random.split(key, 8)
        B, L, d = (4, 1024, D)
        x = jax.random.normal(ks[0], (B, L, d), dtype=jnp.float32)
        conv_weight = jax.random.normal(ks[1], (d, 1, KERNEL), dtype=jnp.float32) * 0.02
        conv_bias = jnp.zeros((d,), dtype=jnp.float32)
        lim = 1.0 / np.sqrt(d)
        Wr_w = jax.random.uniform(ks[2], (d, d), jnp.float32, -lim, lim)
        Wr_b = jax.random.uniform(ks[3], (d,), jnp.float32, -lim, lim)
        Wi_w = jax.random.uniform(ks[4], (d, d), jnp.float32, -lim, lim)
        Wi_b = jax.random.uniform(ks[5], (d,), jnp.float32, -lim, lim)
        log_a = jnp.full((d,), 7.5, dtype=jnp.float32)
        out_w = jax.random.uniform(ks[6], (d, d), jnp.float32, -lim, lim)
        norm_w = jnp.ones((d,), dtype=jnp.float32)
        return {'x': x, 'conv_weight': conv_weight, 'conv_bias': conv_bias, 'Wr_w': Wr_w, 'Wr_b': Wr_b, 'Wi_w': Wi_w, 'Wi_b': Wi_b, 'log_a': log_a, 'out_w': out_w, 'norm_w': norm_w}
    _L1_attn_all = _L1_attn_setup()
    _L1_attn_in = {k: v for k, v in _L1_attn_all.items() if k in ('conv_weight', 'conv_bias', 'Wr_w', 'Wr_b', 'Wi_w', 'Wi_b', 'log_a', 'out_w', 'norm_w')}
    del _L1_attn_all

    def _L1_xattn_setup():
        import jax, jax.numpy as jnp
        import numpy as np
        EMBED_DIM = 128
        HEADS = 16
        HEAD_DIM = EMBED_DIM // HEADS
        key = jax.random.key(seed)
        ks = jax.random.split(key, 12)
        B, Sq, Sk, E = (4, 256, 256, EMBED_DIM)
        s = 1.0 / np.sqrt(E)
        return {'query': jax.random.normal(ks[0], (B, Sq, E), jnp.float32), 'key': jax.random.normal(ks[1], (B, Sk, E), jnp.float32), 'value': jax.random.normal(ks[2], (B, Sk, E), jnp.float32), 'Wq': jax.random.normal(ks[3], (E, E), jnp.float32) * s, 'bq': jnp.zeros((E,), jnp.float32), 'Wk': jax.random.normal(ks[4], (E, E), jnp.float32) * s, 'bk': jnp.zeros((E,), jnp.float32), 'Wv': jax.random.normal(ks[5], (E, E), jnp.float32) * s, 'bv': jnp.zeros((E,), jnp.float32), 'Wo': jax.random.normal(ks[6], (E, E), jnp.float32) * s, 'bo': jnp.zeros((E,), jnp.float32)}
    _L1_xattn_all = _L1_xattn_setup()
    _L1_xattn_in = {k: v for k, v in _L1_xattn_all.items() if k in ('Wq', 'bq', 'Wk', 'bk', 'Wv', 'bv', 'Wo', 'bo')}
    del _L1_xattn_all

    def _L1_ffn_setup():
        import jax, jax.numpy as jnp
        import numpy as np
        B, S, H = (2, 256, 128)
        I = 64
        E_R, E_Z = (32, 8)
        E_T = E_R + E_Z
        K = 6
        SCALE = 2.5
        W_INIT = 0.02
        key = jax.random.key(seed)
        k0, k1, k2, k3 = jax.random.split(key, 4)
        return {'hidden_states': jax.random.normal(k0, (B, S, H), jnp.float32), 'classifier_weight': jax.random.normal(k1, (E_T, H), jnp.float32) * W_INIT, 'e_score_correction_bias': jnp.zeros((E_T,), jnp.float32), 'gate_up_proj': jax.random.normal(k2, (E_T, 2 * I, H), jnp.float32) * W_INIT, 'down_proj': jax.random.normal(k3, (E_R, H, I), jnp.float32) * W_INIT}
    _L1_ffn_all = _L1_ffn_setup()
    _L1_ffn_in = {k: v for k, v in _L1_ffn_all.items() if k in ('classifier_weight', 'e_score_correction_bias', 'gate_up_proj', 'down_proj')}
    del _L1_ffn_all

    def _L2_attn_setup():
        import jax, jax.numpy as jnp
        import numpy as np
        B, T, D = (4, 128, 128)
        H, DK, DV = (16, 32, 32)
        GAMMA = 0.99

        def _xavier(key, shape, gain=0.1):
            fan_in, fan_out = shape
            lim = gain * jnp.sqrt(6.0 / (fan_in + fan_out))
            return jax.random.uniform(key, shape, jnp.float32, -lim, lim)

        def _hla_forward(x, Wq, Wk, Wv, Wo):
            Bs, Ts, _ = x.shape
            q = (x @ Wq).reshape(Bs, Ts, H, DK).transpose(1, 0, 2, 3)
            k = (x @ Wk).reshape(Bs, Ts, H, DK).transpose(1, 0, 2, 3)
            v = (x @ Wv).reshape(Bs, Ts, H, DV).transpose(1, 0, 2, 3)
            S_K0 = jnp.zeros((Bs, H, DK, DK), x.dtype)
            C_QV0 = jnp.zeros((Bs, H, DK, DV), x.dtype)
            G0 = jnp.zeros((Bs, H, DK, DV), x.dtype)

            def step(carry, qkv):
                S_K, C_QV, G = carry
                q_t, k_t, v_t = qkv
                C_prev = GAMMA * C_QV
                k_C = jnp.einsum('bhk,bhkv->bhv', k_t, C_prev)
                G = GAMMA * G + k_t[..., :, None] * k_C[..., None, :]
                S_K = GAMMA * S_K + k_t[..., :, None] * k_t[..., None, :]
                C_QV = C_prev + q_t[..., :, None] * v_t[..., None, :]
                S_C = jnp.einsum('bhij,bhjv->bhiv', S_K, C_QV)
                o_t = jnp.einsum('bhk,bhkv->bhv', q_t, S_C - G)
                return ((S_K, C_QV, G), o_t)
            _, outs = jax.lax.scan(step, (S_K0, C_QV0, G0), (q, k, v))
            out = outs.transpose(1, 0, 2, 3).reshape(Bs, Ts, H * DV)
            return out @ Wo
        key = jax.random.key(seed)
        kx, kq, kk, kv, ko = jax.random.split(key, 5)
        return {'x': jax.random.normal(kx, (B, T, D), jnp.float32), 'Wq': _xavier(kq, (D, H * DK)), 'Wk': _xavier(kk, (D, H * DK)), 'Wv': _xavier(kv, (D, H * DV)), 'Wo': _xavier(ko, (H * DV, D))}
    _L2_attn_all = _L2_attn_setup()
    _L2_attn_in = {k: v for k, v in _L2_attn_all.items() if k in ('Wq', 'Wk', 'Wv', 'Wo')}
    del _L2_attn_all

    def _L2_xattn_setup():
        import jax, jax.numpy as jnp
        import numpy as np
        B, S, D, H = (1, 512, 128, 16)
        DH = D // H
        SCALE = D ** 0.5
        key = jax.random.key(seed)
        ks = jax.random.split(key, 11)
        s = lambda i, shape, sc=1.0: jax.random.normal(ks[i], shape, dtype=jnp.float32) * sc
        w_init = 1.0 / np.sqrt(D)
        return {'q': s(0, (B, S, D)), 'k': s(1, (B, S, D)), 'v': s(2, (B, S, D)), 'Wq': s(3, (H, D, DH), w_init), 'bq': jnp.zeros((H, DH), jnp.float32), 'Wk': s(4, (H, D, DH), w_init), 'bk': jnp.zeros((H, DH), jnp.float32), 'Wv': s(5, (H, D, DH), w_init), 'bv': jnp.zeros((H, DH), jnp.float32), 'Wo': s(6, (D, D), w_init), 'bo': jnp.zeros((D,), jnp.float32)}
    _L2_xattn_all = _L2_xattn_setup()
    _L2_xattn_in = {k: v for k, v in _L2_xattn_all.items() if k in ('Wq', 'bq', 'Wk', 'bk', 'Wv', 'bv', 'Wo', 'bo')}
    del _L2_xattn_all

    def _L2_ffn_setup():
        import jax, jax.numpy as jnp
        import numpy as np
        B, T, D = (2, 256, 128)
        E, DFF, TOPK = (8, 512, 2)
        TEMPERATURE = 1.0
        key = jax.random.key(seed)
        k_x, k_w1, k_w2, k_r = jax.random.split(key, 4)
        x = jax.random.normal(k_x, (B, T, D), dtype=jnp.float32)
        W1 = jax.random.normal(k_w1, (E, DFF, D), dtype=jnp.float32) * 0.02
        W2 = jax.random.normal(k_w2, (E, D, DFF), dtype=jnp.float32) * 0.02
        Wr = jax.random.normal(k_r, (E, D), dtype=jnp.float32) * 0.02
        return {'x': x, 'W1': W1, 'W2': W2, 'Wr': Wr}
    _L2_ffn_all = _L2_ffn_setup()
    _L2_ffn_in = {k: v for k, v in _L2_ffn_all.items() if k in ('W1', 'W2', 'Wr')}
    del _L2_ffn_all

    def _L3_attn_setup():
        import jax, jax.numpy as jnp
        import numpy as np
        D = 128
        H = 16
        KVH = 4
        HD = D // H
        LAT = 32
        WIN = 32
        B, S = (1, 256)
        BASE_G, BASE_L = (1000000.0, 10000.0)
        EPS = 1e-06

        def rmsnorm(x, w):
            return x * jax.lax.rsqrt(jnp.mean(x * x, axis=-1, keepdims=True) + EPS) * w

        def qk_norm(x):
            return x * jax.lax.rsqrt(jnp.mean(x * x, axis=-1, keepdims=True) + EPS)

        def rope(x, base):
            s, hd = (x.shape[-2], x.shape[-1])
            inv_freq = 1.0 / base ** (jnp.arange(0, hd, 2, dtype=jnp.float32) / hd)
            freqs = jnp.arange(s, dtype=jnp.float32)[:, None] * inv_freq[None, :]
            cos, sin = (jnp.cos(freqs), jnp.sin(freqs))
            xe, xo = (x[..., ::2], x[..., 1::2])
            out = jnp.stack([xe * cos - xo * sin, xe * sin + xo * cos], axis=-1)
            return out.reshape(x.shape)

        def split_heads(x, n_heads):
            b, s, _ = x.shape
            return x.reshape(b, s, n_heads, HD).transpose(0, 2, 1, 3)

        def repeat_kv(x):
            return jnp.repeat(x, H // KVH, axis=1)

        def sdpa(q, k, v, mask):
            scores = jnp.einsum('bhqd,bhkd->bhqk', q, k) / np.sqrt(HD).astype(np.float32)
            scores = jnp.where(mask, scores, jnp.float32(-1e+30))
            probs = jax.nn.softmax(scores, axis=-1)
            return jnp.einsum('bhqk,bhkd->bhqd', probs, v)

        def merge_heads(x):
            b, h, s, hd = x.shape
            return x.transpose(0, 2, 1, 3).reshape(b, s, h * hd)

        def global_latent_attn(x, wq, w_kv_down, w_k_up, w_v_up, wo):
            q = split_heads(x @ wq, H)
            latent = x @ w_kv_down
            k = split_heads(latent @ w_k_up, KVH)
            v = split_heads(latent @ w_v_up, KVH)
            q, k = (rope(q, BASE_G), rope(k, BASE_G))
            q, k = (qk_norm(q), qk_norm(k))
            k, v = (repeat_kv(k), repeat_kv(v))
            i = jnp.arange(x.shape[1])
            causal = i[:, None] >= i[None, :]
            return merge_heads(sdpa(q, k, v, causal)) @ wo

        def local_gqa_attn(x, wq, wk, wv, wo):
            q = split_heads(x @ wq, H)
            k = split_heads(x @ wk, KVH)
            v = split_heads(x @ wv, KVH)
            q, k = (rope(q, BASE_L), rope(k, BASE_L))
            q, k = (qk_norm(q), qk_norm(k))
            k, v = (repeat_kv(k), repeat_kv(v))
            i = jnp.arange(x.shape[1])
            diff = i[:, None] - i[None, :]
            mask = (diff >= 0) & (diff < WIN)
            return merge_heads(sdpa(q, k, v, mask)) @ wo
        key = jax.random.key(seed)
        ks = jax.random.split(key, 12)
        std = 0.02
        return {'hidden': jax.random.normal(ks[0], (B, S, D), dtype=jnp.float32), 'norm1_w': jnp.ones((D,), jnp.float32), 'norm2_w': jnp.ones((D,), jnp.float32), 'g_wq': jax.random.normal(ks[1], (D, H * HD), jnp.float32) * std, 'g_kv_down': jax.random.normal(ks[2], (D, LAT), jnp.float32) * std, 'g_k_up': jax.random.normal(ks[3], (LAT, KVH * HD), jnp.float32) * std, 'g_v_up': jax.random.normal(ks[4], (LAT, KVH * HD), jnp.float32) * std, 'g_wo': jax.random.normal(ks[5], (D, D), jnp.float32) * std, 'l_wq': jax.random.normal(ks[6], (D, H * HD), jnp.float32) * std, 'l_wk': jax.random.normal(ks[7], (D, KVH * HD), jnp.float32) * std, 'l_wv': jax.random.normal(ks[8], (D, KVH * HD), jnp.float32) * std, 'l_wo': jax.random.normal(ks[9], (D, D), jnp.float32) * std}
    _L3_attn_all = _L3_attn_setup()
    _L3_attn_in = {k: v for k, v in _L3_attn_all.items() if k in ('norm1_w', 'norm2_w', 'g_wq', 'g_kv_down', 'g_k_up', 'g_v_up', 'g_wo', 'l_wq', 'l_wk', 'l_wv', 'l_wo')}
    del _L3_attn_all

    def _L3_xattn_setup():
        import jax, jax.numpy as jnp
        import numpy as np
        import math
        N_HEADS = 16
        D_MODEL = 128
        D_K = D_MODEL // N_HEADS
        key = jax.random.key(seed)
        ks = jax.random.split(key, 11)
        B, S = (4, 256)
        scale = 1.0 / math.sqrt(D_MODEL)
        return {'q': jax.random.normal(ks[0], (B, S, D_MODEL), jnp.float32), 'k': jax.random.normal(ks[1], (B, S, D_MODEL), jnp.float32), 'v': jax.random.normal(ks[2], (B, S, D_MODEL), jnp.float32), 'Wq': jax.random.normal(ks[3], (D_MODEL, D_MODEL), jnp.float32) * scale, 'bq': jax.random.normal(ks[4], (D_MODEL,), jnp.float32) * 0.01, 'Wk': jax.random.normal(ks[5], (D_MODEL, D_MODEL), jnp.float32) * scale, 'bk': jax.random.normal(ks[6], (D_MODEL,), jnp.float32) * 0.01, 'Wv': jax.random.normal(ks[7], (D_MODEL, D_MODEL), jnp.float32) * scale, 'bv': jax.random.normal(ks[8], (D_MODEL,), jnp.float32) * 0.01, 'Wo': jax.random.normal(ks[9], (D_MODEL, D_MODEL), jnp.float32) * scale, 'bo': jax.random.normal(ks[10], (D_MODEL,), jnp.float32) * 0.01}
    _L3_xattn_all = _L3_xattn_setup()
    _L3_xattn_in = {k: v for k, v in _L3_xattn_all.items() if k in ('Wq', 'bq', 'Wk', 'bk', 'Wv', 'bv', 'Wo', 'bo')}
    del _L3_xattn_all

    def _L3_ffn_setup():
        import jax, jax.numpy as jnp
        import numpy as np
        E, G, TOPK = (32, 16, 2)
        HID, INTER, A_INTER = (128, 256, 128)
        CAP_FACTOR = 1.25
        SCALE = 0.05

        def _stats(x):
            mean = x.mean(-1, keepdims=True)
            std = jnp.std(x, axis=-1, keepdims=True, ddof=1)
            mn = x.min(-1, keepdims=True)
            mx = x.max(-1, keepdims=True)
            l2 = jnp.linalg.norm(x, axis=-1, keepdims=True)
            sp = (jnp.abs(x) < 1e-06).astype(x.dtype).mean(-1, keepdims=True)
            return jnp.concatenate([mean, std, mn, mx, l2, sp], -1)
        key = jax.random.key(seed)
        ks = jax.random.split(key, 8)
        B, N = (4, 128)
        s = lambda k, shape, sc: jax.random.normal(k, shape, jnp.float32) * sc
        return {'x': jax.random.normal(ks[0], (B, N, HID), jnp.float32), 'r1_w': s(ks[1], (HID // 2, HID + 6), 0.02), 'r1_b': jnp.zeros((HID // 2,), jnp.float32), 'r2_w': s(ks[2], (E, HID // 2), 0.02), 'w_up': s(ks[3], (E, 2 * INTER, HID), 0.02), 'w_down': s(ks[4], (E, HID, INTER), 0.02), 'a_up': s(ks[5], (G, 2 * A_INTER, HID), 0.02), 'a_down': s(ks[6], (G, HID, A_INTER), 0.02)}
    _L3_ffn_all = _L3_ffn_setup()
    _L3_ffn_in = {k: v for k, v in _L3_ffn_all.items() if k in ('r1_w', 'r1_b', 'r2_w', 'w_up', 'w_down', 'a_up', 'a_down')}
    del _L3_ffn_all
    return {'x': x, 'ctx_1024': ctx_1024, 'L0_attn_W_Q': _L0_attn_in['W_Q'], 'L0_attn_b_Q': _L0_attn_in['b_Q'], 'L0_attn_W_K': _L0_attn_in['W_K'], 'L0_attn_b_K': _L0_attn_in['b_K'], 'L0_attn_W_V': _L0_attn_in['W_V'], 'L0_attn_b_V': _L0_attn_in['b_V'], 'L0_attn_W_O': _L0_attn_in['W_O'], 'L0_attn_b_O': _L0_attn_in['b_O'], 'L0_ffn_cn_w1': _L0_ffn_in['cn_w1'], 'L0_ffn_cn_b1': _L0_ffn_in['cn_b1'], 'L0_ffn_cn_w2': _L0_ffn_in['cn_w2'], 'L0_ffn_cn_b2': _L0_ffn_in['cn_b2'], 'L0_ffn_cn_w3': _L0_ffn_in['cn_w3'], 'L0_ffn_cn_b3': _L0_ffn_in['cn_b3'], 'L0_ffn_cn_w4': _L0_ffn_in['cn_w4'], 'L0_ffn_cn_b4': _L0_ffn_in['cn_b4'], 'L0_ffn_gc_w1': _L0_ffn_in['gc_w1'], 'L0_ffn_gc_b1': _L0_ffn_in['gc_b1'], 'L0_ffn_gc_w2': _L0_ffn_in['gc_w2'], 'L0_ffn_gc_b2': _L0_ffn_in['gc_b2'], 'L0_ffn_gc_w3': _L0_ffn_in['gc_w3'], 'L0_ffn_gc_b3': _L0_ffn_in['gc_b3'], 'L0_ffn_adaptive_range': _L0_ffn_in['adaptive_range'], 'L1_attn_conv_weight': _L1_attn_in['conv_weight'], 'L1_attn_conv_bias': _L1_attn_in['conv_bias'], 'L1_attn_Wr_w': _L1_attn_in['Wr_w'], 'L1_attn_Wr_b': _L1_attn_in['Wr_b'], 'L1_attn_Wi_w': _L1_attn_in['Wi_w'], 'L1_attn_Wi_b': _L1_attn_in['Wi_b'], 'L1_attn_log_a': _L1_attn_in['log_a'], 'L1_attn_out_w': _L1_attn_in['out_w'], 'L1_attn_norm_w': _L1_attn_in['norm_w'], 'L1_xattn_Wq': _L1_xattn_in['Wq'], 'L1_xattn_bq': _L1_xattn_in['bq'], 'L1_xattn_Wk': _L1_xattn_in['Wk'], 'L1_xattn_bk': _L1_xattn_in['bk'], 'L1_xattn_Wv': _L1_xattn_in['Wv'], 'L1_xattn_bv': _L1_xattn_in['bv'], 'L1_xattn_Wo': _L1_xattn_in['Wo'], 'L1_xattn_bo': _L1_xattn_in['bo'], 'L1_ffn_classifier_weight': _L1_ffn_in['classifier_weight'], 'L1_ffn_e_score_correction_bias': _L1_ffn_in['e_score_correction_bias'], 'L1_ffn_gate_up_proj': _L1_ffn_in['gate_up_proj'], 'L1_ffn_down_proj': _L1_ffn_in['down_proj'], 'L2_attn_Wq': _L2_attn_in['Wq'], 'L2_attn_Wk': _L2_attn_in['Wk'], 'L2_attn_Wv': _L2_attn_in['Wv'], 'L2_attn_Wo': _L2_attn_in['Wo'], 'L2_xattn_Wq': _L2_xattn_in['Wq'], 'L2_xattn_bq': _L2_xattn_in['bq'], 'L2_xattn_Wk': _L2_xattn_in['Wk'], 'L2_xattn_bk': _L2_xattn_in['bk'], 'L2_xattn_Wv': _L2_xattn_in['Wv'], 'L2_xattn_bv': _L2_xattn_in['bv'], 'L2_xattn_Wo': _L2_xattn_in['Wo'], 'L2_xattn_bo': _L2_xattn_in['bo'], 'L2_ffn_W1': _L2_ffn_in['W1'], 'L2_ffn_W2': _L2_ffn_in['W2'], 'L2_ffn_Wr': _L2_ffn_in['Wr'], 'L3_attn_norm1_w': _L3_attn_in['norm1_w'], 'L3_attn_norm2_w': _L3_attn_in['norm2_w'], 'L3_attn_g_wq': _L3_attn_in['g_wq'], 'L3_attn_g_kv_down': _L3_attn_in['g_kv_down'], 'L3_attn_g_k_up': _L3_attn_in['g_k_up'], 'L3_attn_g_v_up': _L3_attn_in['g_v_up'], 'L3_attn_g_wo': _L3_attn_in['g_wo'], 'L3_attn_l_wq': _L3_attn_in['l_wq'], 'L3_attn_l_wk': _L3_attn_in['l_wk'], 'L3_attn_l_wv': _L3_attn_in['l_wv'], 'L3_attn_l_wo': _L3_attn_in['l_wo'], 'L3_xattn_Wq': _L3_xattn_in['Wq'], 'L3_xattn_bq': _L3_xattn_in['bq'], 'L3_xattn_Wk': _L3_xattn_in['Wk'], 'L3_xattn_bk': _L3_xattn_in['bk'], 'L3_xattn_Wv': _L3_xattn_in['Wv'], 'L3_xattn_bv': _L3_xattn_in['bv'], 'L3_xattn_Wo': _L3_xattn_in['Wo'], 'L3_xattn_bo': _L3_xattn_in['bo'], 'L3_ffn_r1_w': _L3_ffn_in['r1_w'], 'L3_ffn_r1_b': _L3_ffn_in['r1_b'], 'L3_ffn_r2_w': _L3_ffn_in['r2_w'], 'L3_ffn_w_up': _L3_ffn_in['w_up'], 'L3_ffn_w_down': _L3_ffn_in['w_down'], 'L3_ffn_a_up': _L3_ffn_in['a_up'], 'L3_ffn_a_down': _L3_ffn_in['a_down']}

def reference(x, ctx_1024, L0_attn_W_Q, L0_attn_b_Q, L0_attn_W_K, L0_attn_b_K, L0_attn_W_V, L0_attn_b_V, L0_attn_W_O, L0_attn_b_O, L0_ffn_cn_w1, L0_ffn_cn_b1, L0_ffn_cn_w2, L0_ffn_cn_b2, L0_ffn_cn_w3, L0_ffn_cn_b3, L0_ffn_cn_w4, L0_ffn_cn_b4, L0_ffn_gc_w1, L0_ffn_gc_b1, L0_ffn_gc_w2, L0_ffn_gc_b2, L0_ffn_gc_w3, L0_ffn_gc_b3, L0_ffn_adaptive_range, L1_attn_conv_weight, L1_attn_conv_bias, L1_attn_Wr_w, L1_attn_Wr_b, L1_attn_Wi_w, L1_attn_Wi_b, L1_attn_log_a, L1_attn_out_w, L1_attn_norm_w, L1_xattn_Wq, L1_xattn_bq, L1_xattn_Wk, L1_xattn_bk, L1_xattn_Wv, L1_xattn_bv, L1_xattn_Wo, L1_xattn_bo, L1_ffn_classifier_weight, L1_ffn_e_score_correction_bias, L1_ffn_gate_up_proj, L1_ffn_down_proj, L2_attn_Wq, L2_attn_Wk, L2_attn_Wv, L2_attn_Wo, L2_xattn_Wq, L2_xattn_bq, L2_xattn_Wk, L2_xattn_bk, L2_xattn_Wv, L2_xattn_bv, L2_xattn_Wo, L2_xattn_bo, L2_ffn_W1, L2_ffn_W2, L2_ffn_Wr, L3_attn_norm1_w, L3_attn_norm2_w, L3_attn_g_wq, L3_attn_g_kv_down, L3_attn_g_k_up, L3_attn_g_v_up, L3_attn_g_wo, L3_attn_l_wq, L3_attn_l_wk, L3_attn_l_wv, L3_attn_l_wo, L3_xattn_Wq, L3_xattn_bq, L3_xattn_Wk, L3_xattn_bk, L3_xattn_Wv, L3_xattn_bv, L3_xattn_Wo, L3_xattn_bo, L3_ffn_r1_w, L3_ffn_r1_b, L3_ffn_r2_w, L3_ffn_w_up, L3_ffn_w_down, L3_ffn_a_up, L3_ffn_a_down):
    import jax
    import jax.numpy as jnp

    def _L0_attn_ref(x, W_Q, b_Q, W_K, b_K, W_V, b_V, W_O, b_O):
        import jax, jax.numpy as jnp
        import numpy as np
        B, T, D = (4, 256, 128)
        H, Dh = (16, 64)
        Q = jnp.einsum('btd,hkd->bthk', x, W_Q) + b_Q
        K = jnp.einsum('btd,hkd->bthk', x, W_K) + b_K
        V = jnp.einsum('btd,hkd->bthk', x, W_V) + b_V
        d_head = W_Q.shape[1]
        scores = jnp.einsum('bqhk,bshk->bhqs', Q, K) / jnp.sqrt(jnp.asarray(d_head, x.dtype))
        attn = jax.nn.softmax(scores, axis=-1)
        out_h = jnp.einsum('bhqs,bshk->bqhk', attn, V)
        return jnp.einsum('bqhk,hdk->bqd', out_h, W_O) + b_O

    def _L0_xattn_ref(h_enc, h_dec):
        import jax, jax.numpy as jnp
        import numpy as np
        e = jnp.einsum('bnd,bmd->bnm', h_enc, h_dec)
        a = jax.nn.softmax(e, axis=1)
        c = jnp.einsum('bnm,bnd->bmd', a, h_enc)
        return c

    def _L0_ffn_ref(x, cn_w1, cn_b1, cn_w2, cn_b2, cn_w3, cn_b3, cn_w4, cn_b4, gc_w1, gc_b1, gc_w2, gc_b2, gc_w3, gc_b3, adaptive_range):
        import jax, jax.numpy as jnp
        import numpy as np
        B, S, DIM = (4, 512, 128)
        BASE_COUPLING = 0.1
        NUM_CYCLES = 3

        def _gelu(x):
            return jax.nn.gelu(x, approximate=False)

        def _coupling_net(h, w1, b1, w2, b2, w3, b3, w4, b4):
            h = _gelu(h @ w1 + b1)
            h = _gelu(h @ w2 + b2)
            h = _gelu(h @ w3 + b3)
            return jax.nn.sigmoid(h @ w4 + b4)

        def _global_net(h, w1, b1, w2, b2, w3, b3):
            h = _gelu(h @ w1 + b1)
            h = _gelu(h @ w2 + b2)
            return jax.nn.sigmoid(h @ w3 + b3)

        def _twist(x):
            o_r, o_i, p_r, p_i = jnp.split(x, 4, axis=-1)
            return jnp.concatenate([p_r, -p_i, -o_r, o_i], axis=-1)
        global_context = x.mean(axis=1, keepdims=True)
        gf = _global_net(global_context, gc_w1, gc_b1, gc_w2, gc_b2, gc_w3, gc_b3)
        out = x
        for _ in range(NUM_CYCLES):
            tf = _coupling_net(out, cn_w1, cn_b1, cn_w2, cn_b2, cn_w3, cn_b3, cn_w4, cn_b4)
            combined = 0.7 * gf + 0.3 * tf
            coupling = BASE_COUPLING + adaptive_range * (combined - 0.5) * 2.0
            out = out + coupling * _twist(out)
        return out

    def _L1_attn_ref(x, conv_weight, conv_bias, Wr_w, Wr_b, Wi_w, Wi_b, log_a, out_w, norm_w):
        import jax, jax.numpy as jnp
        import numpy as np
        D = 128
        KERNEL = 4

        def _causal_depthwise_conv(x, w, b):
            B, L, d = x.shape
            xp = jnp.pad(x, ((0, 0), (KERNEL - 1, 0), (0, 0)))
            out = b[None, None, :]
            for k in range(KERNEL):
                out = out + xp[:, k:k + L, :] * w[:, 0, k][None, None, :]
            return out

        def _parallel_scan(a_t, b_t):
            a = a_t.astype(jnp.float32)
            b = b_t.astype(jnp.float32)
            log_A = jnp.clip(jnp.cumsum(jnp.log(jnp.clip(a, 1e-07)), axis=1), -80.0, None)
            A = jnp.exp(log_A)
            h = A * jnp.cumsum(b * jnp.exp(-log_A), axis=1)
            return h.astype(a_t.dtype)

        def _rmsnorm(x, w, eps=1e-06):
            ms = jnp.mean(jnp.square(x.astype(jnp.float32)), axis=-1, keepdims=True)
            return (x * jax.lax.rsqrt(ms + eps)).astype(x.dtype) * w
        x_conv = _causal_depthwise_conv(x, conv_weight, conv_bias)
        r_t = jax.nn.sigmoid(x_conv @ Wr_w.T + Wr_b)
        i_t = jax.nn.sigmoid(x_conv @ Wi_w.T + Wi_b)
        a_base = jax.nn.sigmoid(log_a.astype(jnp.float32)).astype(x.dtype)
        a_t = jnp.power(a_base[None, None, :], 8.0 * r_t)
        b_t = jnp.sqrt(jnp.clip(1.0 - a_t * a_t, 1e-06, None)) * (i_t * x_conv)
        h = _parallel_scan(a_t, b_t)
        return _rmsnorm(h @ out_w.T, norm_w)

    def _L1_xattn_ref(query, key, value, Wq, bq, Wk, bk, Wv, bv, Wo, bo):
        import jax, jax.numpy as jnp
        import numpy as np
        EMBED_DIM = 128
        HEADS = 16
        HEAD_DIM = EMBED_DIM // HEADS
        B, Sq, E = query.shape
        Sk = key.shape[1]
        H, D = (HEADS, HEAD_DIM)
        Q = (query @ Wq + bq).reshape(B, Sq, H, D).transpose(0, 2, 1, 3)
        K = (key @ Wk + bk).reshape(B, Sk, H, D).transpose(0, 2, 1, 3)
        V = (value @ Wv + bv).reshape(B, Sk, H, D).transpose(0, 2, 1, 3)
        scores = jnp.einsum('bhqd,bhkd->bhqk', Q, K) / jnp.sqrt(jnp.float32(D))
        attn = jax.nn.softmax(scores, axis=-1)
        out = jnp.einsum('bhqk,bhkd->bhqd', attn, V)
        out = out.transpose(0, 2, 1, 3).reshape(B, Sq, E)
        return out @ Wo + bo

    def _L1_ffn_ref(hidden_states, classifier_weight, e_score_correction_bias, gate_up_proj, down_proj):
        import jax, jax.numpy as jnp
        import numpy as np
        B, S, H = (2, 256, 128)
        I = 64
        E_R, E_Z = (32, 8)
        E_T = E_R + E_Z
        K = 6
        SCALE = 2.5
        W_INIT = 0.02
        orig_shape = hidden_states.shape
        x = hidden_states.reshape(-1, H).astype(jnp.float32)
        T = x.shape[0]
        logits = x @ classifier_weight.T
        scores = jax.nn.softmax(logits, axis=-1)
        _, topk_idx = jax.lax.top_k(scores + e_score_correction_bias[None, :], K)
        topk_w = jnp.take_along_axis(scores, topk_idx, axis=1) * SCALE
        w_full = jnp.zeros((T, E_T), jnp.float32).at[jnp.arange(T)[:, None], topk_idx].add(topk_w)
        zero_w = w_full[:, E_R:].sum(axis=-1, keepdims=True)
        out0 = x * zero_w
        routed_w = w_full[:, :E_R].T

        def body(out, xs):
            Wgu, Wd, we = xs
            gate, up = jnp.split(x @ Wgu.T, 2, axis=-1)
            y = jax.nn.silu(gate) * up @ Wd.T
            return (out + we[:, None] * y, None)
        out, _ = jax.lax.scan(body, out0, (gate_up_proj[:E_R], down_proj, routed_w))
        return out.reshape(orig_shape).astype(hidden_states.dtype)

    def _L2_attn_ref(x, Wq, Wk, Wv, Wo):
        import jax, jax.numpy as jnp
        import numpy as np
        B, T, D = (4, 128, 128)
        H, DK, DV = (16, 32, 32)
        GAMMA = 0.99

        def _xavier(key, shape, gain=0.1):
            fan_in, fan_out = shape
            lim = gain * jnp.sqrt(6.0 / (fan_in + fan_out))
            return jax.random.uniform(key, shape, jnp.float32, -lim, lim)

        def _hla_forward(x, Wq, Wk, Wv, Wo):
            Bs, Ts, _ = x.shape
            q = (x @ Wq).reshape(Bs, Ts, H, DK).transpose(1, 0, 2, 3)
            k = (x @ Wk).reshape(Bs, Ts, H, DK).transpose(1, 0, 2, 3)
            v = (x @ Wv).reshape(Bs, Ts, H, DV).transpose(1, 0, 2, 3)
            S_K0 = jnp.zeros((Bs, H, DK, DK), x.dtype)
            C_QV0 = jnp.zeros((Bs, H, DK, DV), x.dtype)
            G0 = jnp.zeros((Bs, H, DK, DV), x.dtype)

            def step(carry, qkv):
                S_K, C_QV, G = carry
                q_t, k_t, v_t = qkv
                C_prev = GAMMA * C_QV
                k_C = jnp.einsum('bhk,bhkv->bhv', k_t, C_prev)
                G = GAMMA * G + k_t[..., :, None] * k_C[..., None, :]
                S_K = GAMMA * S_K + k_t[..., :, None] * k_t[..., None, :]
                C_QV = C_prev + q_t[..., :, None] * v_t[..., None, :]
                S_C = jnp.einsum('bhij,bhjv->bhiv', S_K, C_QV)
                o_t = jnp.einsum('bhk,bhkv->bhv', q_t, S_C - G)
                return ((S_K, C_QV, G), o_t)
            _, outs = jax.lax.scan(step, (S_K0, C_QV0, G0), (q, k, v))
            out = outs.transpose(1, 0, 2, 3).reshape(Bs, Ts, H * DV)
            return out @ Wo
        return _hla_forward(x, Wq, Wk, Wv, Wo)

    def _L2_xattn_ref(q, k, v, Wq, bq, Wk, bk, Wv, bv, Wo, bo):
        import jax, jax.numpy as jnp
        import numpy as np
        B, S, D, H = (1, 512, 128, 16)
        DH = D // H
        SCALE = D ** 0.5
        Q = jnp.einsum('bsd,hde->bhse', q, Wq) + bq[None, :, None, :]
        K = jnp.einsum('bsd,hde->bhse', k, Wk) + bk[None, :, None, :]
        V = jnp.einsum('bsd,hde->bhse', v, Wv) + bv[None, :, None, :]
        scores = jnp.einsum('bhse,bhte->bhst', Q, K) / SCALE
        attn = jax.nn.softmax(scores, axis=-1)
        out = jnp.einsum('bhst,bhte->bhse', attn, V)
        concat = out.transpose(0, 2, 1, 3).reshape(q.shape[0], q.shape[1], H * DH)
        return concat @ Wo + bo

    def _L2_ffn_ref(x, W1, W2, Wr):
        import jax, jax.numpy as jnp
        import numpy as np
        B, T, D = (2, 256, 128)
        E, DFF, TOPK = (8, 512, 2)
        TEMPERATURE = 1.0
        logits = jnp.einsum('btd,ed->bte', x, Wr)
        probs = jax.nn.softmax(logits / TEMPERATURE, axis=-1)
        topk_vals, topk_idx = jax.lax.top_k(probs, TOPK)
        router_weights = topk_vals / topk_vals.sum(-1, keepdims=True)
        one_hot = jax.nn.one_hot(topk_idx, E, dtype=x.dtype)
        gate = jnp.einsum('btk,btke->bte', router_weights, one_hot)
        h = jax.nn.silu(jnp.einsum('btd,efd->btef', x, W1))
        y = jnp.einsum('btef,edf->bted', h, W2)
        out = jnp.einsum('bte,bted->btd', gate, y)
        return out

    def _L3_attn_ref(hidden, norm1_w, norm2_w, g_wq, g_kv_down, g_k_up, g_v_up, g_wo, l_wq, l_wk, l_wv, l_wo):
        import jax, jax.numpy as jnp
        import numpy as np
        D = 128
        H = 16
        KVH = 4
        HD = D // H
        LAT = 32
        WIN = 32
        B, S = (1, 256)
        BASE_G, BASE_L = (1000000.0, 10000.0)
        EPS = 1e-06

        def rmsnorm(x, w):
            return x * jax.lax.rsqrt(jnp.mean(x * x, axis=-1, keepdims=True) + EPS) * w

        def qk_norm(x):
            return x * jax.lax.rsqrt(jnp.mean(x * x, axis=-1, keepdims=True) + EPS)

        def rope(x, base):
            s, hd = (x.shape[-2], x.shape[-1])
            inv_freq = 1.0 / base ** (jnp.arange(0, hd, 2, dtype=jnp.float32) / hd)
            freqs = jnp.arange(s, dtype=jnp.float32)[:, None] * inv_freq[None, :]
            cos, sin = (jnp.cos(freqs), jnp.sin(freqs))
            xe, xo = (x[..., ::2], x[..., 1::2])
            out = jnp.stack([xe * cos - xo * sin, xe * sin + xo * cos], axis=-1)
            return out.reshape(x.shape)

        def split_heads(x, n_heads):
            b, s, _ = x.shape
            return x.reshape(b, s, n_heads, HD).transpose(0, 2, 1, 3)

        def repeat_kv(x):
            return jnp.repeat(x, H // KVH, axis=1)

        def sdpa(q, k, v, mask):
            scores = jnp.einsum('bhqd,bhkd->bhqk', q, k) / np.sqrt(HD).astype(np.float32)
            scores = jnp.where(mask, scores, jnp.float32(-1e+30))
            probs = jax.nn.softmax(scores, axis=-1)
            return jnp.einsum('bhqk,bhkd->bhqd', probs, v)

        def merge_heads(x):
            b, h, s, hd = x.shape
            return x.transpose(0, 2, 1, 3).reshape(b, s, h * hd)

        def global_latent_attn(x, wq, w_kv_down, w_k_up, w_v_up, wo):
            q = split_heads(x @ wq, H)
            latent = x @ w_kv_down
            k = split_heads(latent @ w_k_up, KVH)
            v = split_heads(latent @ w_v_up, KVH)
            q, k = (rope(q, BASE_G), rope(k, BASE_G))
            q, k = (qk_norm(q), qk_norm(k))
            k, v = (repeat_kv(k), repeat_kv(v))
            i = jnp.arange(x.shape[1])
            causal = i[:, None] >= i[None, :]
            return merge_heads(sdpa(q, k, v, causal)) @ wo

        def local_gqa_attn(x, wq, wk, wv, wo):
            q = split_heads(x @ wq, H)
            k = split_heads(x @ wk, KVH)
            v = split_heads(x @ wv, KVH)
            q, k = (rope(q, BASE_L), rope(k, BASE_L))
            q, k = (qk_norm(q), qk_norm(k))
            k, v = (repeat_kv(k), repeat_kv(v))
            i = jnp.arange(x.shape[1])
            diff = i[:, None] - i[None, :]
            mask = (diff >= 0) & (diff < WIN)
            return merge_heads(sdpa(q, k, v, mask)) @ wo
        x = hidden
        x = x + global_latent_attn(rmsnorm(x, norm1_w), g_wq, g_kv_down, g_k_up, g_v_up, g_wo)
        x = x + local_gqa_attn(rmsnorm(x, norm2_w), l_wq, l_wk, l_wv, l_wo)
        return x

    def _L3_xattn_ref(q, k, v, Wq, bq, Wk, bk, Wv, bv, Wo, bo):
        import jax, jax.numpy as jnp
        import numpy as np
        import math
        N_HEADS = 16
        D_MODEL = 128
        D_K = D_MODEL // N_HEADS
        B, S, _ = q.shape

        def proj(x, W, b):
            y = x @ W.T + b
            return y.reshape(B, -1, N_HEADS, D_K).transpose(0, 2, 1, 3)
        qh = proj(q, Wq, bq)
        kh = proj(k, Wk, bk)
        vh = proj(v, Wv, bv)
        scores = jnp.einsum('bhqd,bhkd->bhqk', qh, kh) / math.sqrt(D_K)
        attn = jax.nn.softmax(scores, axis=-1)
        out = jnp.einsum('bhqk,bhkd->bhqd', attn, vh)
        concat = out.transpose(0, 2, 1, 3).reshape(B, -1, D_MODEL)
        return concat @ Wo.T + bo

    def _L3_ffn_ref(x, r1_w, r1_b, r2_w, w_up, w_down, a_up, a_down):
        import jax, jax.numpy as jnp
        import numpy as np
        E, G, TOPK = (32, 16, 2)
        HID, INTER, A_INTER = (128, 256, 128)
        CAP_FACTOR = 1.25
        SCALE = 0.05

        def _stats(x):
            mean = x.mean(-1, keepdims=True)
            std = jnp.std(x, axis=-1, keepdims=True, ddof=1)
            mn = x.min(-1, keepdims=True)
            mx = x.max(-1, keepdims=True)
            l2 = jnp.linalg.norm(x, axis=-1, keepdims=True)
            sp = (jnp.abs(x) < 1e-06).astype(x.dtype).mean(-1, keepdims=True)
            return jnp.concatenate([mean, std, mn, mx, l2, sp], -1)
        B, N, C = x.shape
        xf = x.reshape(-1, C)
        T = xf.shape[0]
        cap = int(CAP_FACTOR * T / E)
        ri = jnp.concatenate([xf, _stats(xf)], -1)
        h = jax.nn.gelu(ri @ r1_w.T + r1_b, approximate=False)
        probs = jax.nn.softmax(h @ r2_w.T, -1)
        topp, topi = jax.lax.top_k(probs, TOPK)
        wnorm = topp / topp.sum(-1, keepdims=True)
        eids = jnp.arange(E)
        hit = topi[..., None] == eids
        routed = hit.any(1)
        Wc = jnp.where(hit, wnorm[..., None], 0.0).sum(1)
        score = jnp.where(routed, probs, -jnp.inf)
        idx = jnp.argsort(-score, axis=0)[:cap].T
        valid = jnp.take_along_axis(routed.T, idx, 1)
        w = jnp.take_along_axis(Wc.T, idx, 1) * valid
        xe = xf[idx]
        up = jnp.einsum('eci,eji->ecj', xe, w_up)
        gate, upv = jnp.split(up, 2, axis=-1)
        hact = jax.nn.silu(gate) * upv
        ye = jnp.einsum('ecj,eoj->eco', hact, w_down)
        out = jnp.zeros((T, C), xf.dtype).at[idx.reshape(-1)].add((w[..., None] * ye).reshape(-1, C))
        Wmask = jnp.zeros((T, E), xf.dtype).at[idx, eids[:, None]].add(w)
        gw = SCALE * Wmask.reshape(T, G, E // G).sum(-1)
        aup = jnp.einsum('tc,gjc->tgj', xf, a_up)
        ag, av = jnp.split(aup, 2, axis=-1)
        ah = jax.nn.silu(ag) * av
        ay = jnp.einsum('tgj,goj->tgo', ah, a_down)
        out = out + jnp.einsum('tg,tgo->to', gw, ay)
        return out.reshape(B, N, C)
    x = x + _L0_attn_ref(_layernorm(x, axis=-1), L0_attn_W_Q, L0_attn_b_Q, L0_attn_W_K, L0_attn_b_K, L0_attn_W_V, L0_attn_b_V, L0_attn_W_O, L0_attn_b_O)
    x = x + _L0_xattn_ref(ctx_1024, _layernorm(x, axis=-1))
    x = x + _L0_ffn_ref(_layernorm(x, axis=-1), L0_ffn_cn_w1, L0_ffn_cn_b1, L0_ffn_cn_w2, L0_ffn_cn_b2, L0_ffn_cn_w3, L0_ffn_cn_b3, L0_ffn_cn_w4, L0_ffn_cn_b4, L0_ffn_gc_w1, L0_ffn_gc_b1, L0_ffn_gc_w2, L0_ffn_gc_b2, L0_ffn_gc_w3, L0_ffn_gc_b3, L0_ffn_adaptive_range)
    x = x + _L1_attn_ref(_layernorm(x, axis=-1), L1_attn_conv_weight, L1_attn_conv_bias, L1_attn_Wr_w, L1_attn_Wr_b, L1_attn_Wi_w, L1_attn_Wi_b, L1_attn_log_a, L1_attn_out_w, L1_attn_norm_w)
    x = x + _L1_xattn_ref(_layernorm(x, axis=-1), ctx_1024, ctx_1024, L1_xattn_Wq, L1_xattn_bq, L1_xattn_Wk, L1_xattn_bk, L1_xattn_Wv, L1_xattn_bv, L1_xattn_Wo, L1_xattn_bo)
    x = x + _L1_ffn_ref(_layernorm(x, axis=-1), L1_ffn_classifier_weight, L1_ffn_e_score_correction_bias, L1_ffn_gate_up_proj, L1_ffn_down_proj)
    x = x + _L2_attn_ref(_layernorm(x, axis=-1), L2_attn_Wq, L2_attn_Wk, L2_attn_Wv, L2_attn_Wo)
    x = x + _L2_xattn_ref(_layernorm(x, axis=-1), ctx_1024, ctx_1024, L2_xattn_Wq, L2_xattn_bq, L2_xattn_Wk, L2_xattn_bk, L2_xattn_Wv, L2_xattn_bv, L2_xattn_Wo, L2_xattn_bo)
    x = x + _L2_ffn_ref(_layernorm(x, axis=-1), L2_ffn_W1, L2_ffn_W2, L2_ffn_Wr)
    x = x + _L3_attn_ref(_layernorm(x, axis=-1), L3_attn_norm1_w, L3_attn_norm2_w, L3_attn_g_wq, L3_attn_g_kv_down, L3_attn_g_k_up, L3_attn_g_v_up, L3_attn_g_wo, L3_attn_l_wq, L3_attn_l_wk, L3_attn_l_wv, L3_attn_l_wo)
    x = x + _L3_xattn_ref(_layernorm(x, axis=-1), ctx_1024, ctx_1024, L3_xattn_Wq, L3_xattn_bq, L3_xattn_Wk, L3_xattn_bk, L3_xattn_Wv, L3_xattn_bv, L3_xattn_Wo, L3_xattn_bo)
    x = x + _L3_ffn_ref(_layernorm(x, axis=-1), L3_ffn_r1_w, L3_ffn_r1_b, L3_ffn_r2_w, L3_ffn_w_up, L3_ffn_w_down, L3_ffn_a_up, L3_ffn_a_down)
    return x

_drawn_inputs = setup_inputs


def setup_inputs(seed=0):
    import zlib

    import numpy as np

    out = dict(_drawn_inputs(seed))
    spreads = {'L0_attn_b_Q': (0.0, 0.8),
     'L0_attn_b_K': (0.0, 2.0),
     'L0_attn_b_V': (0.0, 0.1),
     'L0_attn_b_O': (0.0, 0.1),
     'L0_ffn_cn_b1': (0.0, 2.0),
     'L0_ffn_cn_b2': (0.0, 2.0),
     'L0_ffn_cn_b3': (0.0, 2.0),
     'L0_ffn_gc_b1': (0.0, 0.8),
     'L0_ffn_gc_b2': (0.0, 2.0),
     'L1_attn_conv_bias': (0.0, 0.1),
     'L1_attn_log_a': (7.5, 0.2),
     'L1_attn_norm_w': (1.0, 0.2),
     'L1_xattn_bq': (0.0, 0.8),
     'L1_xattn_bk': (0.0, 2.0),
     'L1_xattn_bv': (0.0, 0.1),
     'L1_xattn_bo': (0.0, 0.1),
     'L1_ffn_e_score_correction_bias': (0.0, 0.386),
     'L2_xattn_bq': (0.0, 2.0),
     'L2_xattn_bk': (0.0, 2.0),
     'L2_xattn_bv': (0.0, 0.8),
     'L2_xattn_bo': (0.0, 0.8),
     'L3_attn_norm1_w': (1.0, 0.6),
     'L3_attn_norm2_w': (1.0, 0.6),
     'L3_ffn_r1_b': (0.0, 2.0)}
    factors = {'L0_attn_W_Q': 8.0,
     'L0_attn_W_K': 8.0,
     'L0_attn_W_V': 2.92,
     'L0_ffn_cn_w1': 8.0,
     'L0_ffn_cn_w2': 8.0,
     'L0_ffn_cn_w3': 8.0,
     'L0_ffn_cn_w4': 6.398,
     'L0_ffn_gc_w1': 7.838,
     'L0_ffn_gc_w2': 7.1,
     'L0_ffn_gc_w3': 7.52,
     'L1_attn_Wr_w': 8.0,
     'L1_attn_Wr_b': 8.0,
     'L1_attn_Wi_w': 4.602,
     'L1_attn_Wi_b': 4.539,
     'L1_ffn_classifier_weight': 5.327,
     'L1_ffn_gate_up_proj': 8.0,
     'L1_ffn_down_proj': 8.0,
     'L2_attn_Wq': 8.0,
     'L2_attn_Wk': 8.0,
     'L2_attn_Wv': 8.0,
     'L2_attn_Wo': 8.0,
     'L2_xattn_Wq': 19.303,
     'L2_xattn_Wk': 18.01,
     'L2_ffn_W1': 20.455,
     'L2_ffn_W2': 18.069,
     'L2_ffn_Wr': 26.008,
     'L3_attn_g_wq': 31.912,
     'L3_attn_g_kv_down': 8.0,
     'L3_attn_g_k_up': 33.84,
     'L3_attn_g_v_up': 8.0,
     'L3_attn_g_wo': 8.0,
     'L3_attn_l_wq': 60.608,
     'L3_attn_l_wk': 64.0,
     'L3_attn_l_wv': 7.807,
     'L3_attn_l_wo': 7.713,
     'L3_xattn_bq': 64.0,
     'L3_xattn_bk': 64.0,
     'L3_xattn_bv': 64.0,
     'L3_xattn_bo': 64.0,
     'L3_ffn_r1_w': 24.71,
     'L3_ffn_r2_w': 8.0,
     'L3_ffn_w_up': 8.0,
     'L3_ffn_w_down': 21.36,
     'L3_ffn_a_up': 64.0,
     'L3_ffn_a_down': 64.0,
     'L2_xattn_Wv': 4.048,
     'L2_xattn_Wo': 3.927,
     'L3_xattn_Wq': 8.0,
     'L3_xattn_Wk': 8.0,
     'L3_xattn_Wv': 8.0,
     'L3_xattn_Wo': 8.0}
    for name, (base, spread) in spreads.items():
        noise = np.random.default_rng([zlib.crc32(name.encode()), seed]).standard_normal(out[name].shape)
        drawn = base * np.exp(spread * noise) if base else spread * noise
        out[name] = jnp.asarray(drawn.astype(out[name].dtype))
    for name, factor in factors.items():
        out[name] = (out[name] * factor).astype(out[name].dtype)
    return out
```

```python
from contextlib import ExitStack

import numpy as np
import concourse.bass as bass
from concourse import mybir

ALU = mybir.AluOpType
ACT = mybir.ActivationFunctionType
F32 = mybir.dt.float32
AX_X = mybir.AxisListType.X

P = 128
B = 32
S = 56
SP = 64
NP_ = B // 2
NK = 1500
KC = 125
NC_ = NK // KC
KB = 500
NB_ = NK // KB
CH = 4
CB = B // CH
CT = CB * S
CW = CB * SP
HX = 16
DX = P // HX
LN_EPS = 1e-5
RMS_EPS = 1e-6


class Step:

    def __init__(self, engine, semaphore, done=0):
        self.engine, self.semaphore, self.done, self.n = engine, semaphore, done, 0

    def __call__(self, instruction):
        self.n += 1
        instruction.then_inc(self.semaphore, 1)
        self.engine.wait_ge(self.semaphore, self.done + self.n)


class Chip:

    def __init__(self, nc, ctx, dram):
        self.nc, self.ctx, self.dram = nc, ctx, dram
        self.x = self.sbuf("x", [P, B, SP])
        self.xn_lead = self.sbuf("xn_lead", [P, SP + B * SP])
        self.xn = self.xn_lead[:, SP:].rearrange("p (b s) -> p b s", s=SP)
        self.ps = ctx.enter_context(nc.psum_tensor("ps", [P, 8, 512], F32))
        self.ones = self.sbuf("ones", [P, P])
        self.mean = self.sbuf("mean", [P, P])
        self.ident = self.sbuf("ident", [P, P])
        self.credit = self.sbuf("credit", [P, 4])
        self.eps = self.sbuf("eps", [P, 2])
        self.norm_calls = self.centre_calls = 0
        self.stage_sems = []
        self.norm_sems = {k: ctx.enter_context(nc.semaphore("norm_" + k)) for k in ("mean", "centred", "squared", "power", "log", "inverse", "out")}

    def sbuf(self, name, shape, dtype=F32):
        return self.ctx.enter_context(self.nc.sbuf_tensor(name, shape, dtype))

    def sem(self, name):
        semaphore = self.nc.alloc_semaphore(name=name)
        self.stage_sems.append(semaphore)
        return semaphore

    def end_stage(self):
        nc = self.nc
        with nc.Block(no_gpsimd_drain=True) as block:
            @block.gpsimd
            def _(pool):
                for semaphore in self.stage_sems:
                    pool.sem_clear(semaphore)
        for semaphore in self.stage_sems:
            nc.release_semaphore(semaphore)
        self.stage_sems = []


def spread(ap, axis, n):
    a = ap.unsqueeze(axis)
    shape = list(a.shape)
    shape[axis] = n
    return a.to_broadcast(shape)


def load_stage(chip, out):
    nc = chip.nc
    x_landed = chip.sem("x_landed")
    cleared = chip.sem("cleared")
    ident_cleared = chip.sem("ident_cleared")
    with nc.Block() as block:
        @block.sync
        def _(sp):
            sp.wait_ge(cleared, 1)
            for g in range(4):
                sp.dma_start(chip.x[32 * g:32 * g + 32, :, 0:S], chip.dram["x"][32 * g:32 * g + 32]).then_inc(x_landed, 16)
            sp.wait_ge(x_landed, 64)

        @block.vector
        def _(dve):
            nc.vector.memset(chip.x[:], 0.0).then_inc(cleared, 1)
            nc.vector.memset(chip.xn_lead[:], 0.0)
            nc.vector.memset(chip.ones[:], 1.0)
            nc.vector.memset(chip.mean[:], 1.0 / P)
            nc.vector.memset(chip.eps[:, 0:1], LN_EPS)
            nc.vector.memset(chip.eps[:, 1:2], RMS_EPS)

        @block.gpsimd
        def _(pool):
            nc.gpsimd.memset(chip.ident[:], 0.0).then_inc(ident_cleared, 1)
            pool.wait_ge(ident_cleared, 1)
            nc.gpsimd.affine_select(out=chip.ident[:], in_=chip.ident[:], compare_op=ALU.not_equal, fill=1.0,
                                    base=0, pattern=[[-1, P]], channel_multiplier=1).then_inc(ident_cleared, 1)


def store_stage(chip, src, out):
    nc = chip.nc
    stored = chip.sem("stored")
    with nc.Block() as block:
        @block.sync
        def _(sp):
            for g in range(4):
                sp.dma_start(out[32 * g:32 * g + 32], src[32 * g:32 * g + 32, :, 0:S]).then_inc(stored, 16)
            sp.wait_ge(stored, 64)


def normalise(chip, src, dst, centre, weight=None):
    nc, ps = chip.nc, chip.ps
    s = chip.norm_sems
    done = CH * chip.norm_calls
    done_centred = CH * chip.centre_calls
    tag = str(chip.norm_calls)
    which = 0 if centre else 1
    chip.norm_calls += 1
    chip.centre_calls += centre
    with ExitStack() as own, nc.Block(no_gpsimd_drain=True) as block:
        sq = own.enter_context(nc.sbuf_tensor("norm_sq" + tag, [P, CH, CW], F32))
        root = own.enter_context(nc.sbuf_tensor("norm_root" + tag, [P, CH, CW], F32))
        flat = src.rearrange("p (c b) s -> p c (b s)", c=CH)
        goal = dst.rearrange("p (c b) s -> p c (b s)", c=CH)
        centred = goal if centre else flat

        @block.tensor
        def _(pe):
            for c in range(CH):
                if centre:
                    nc.tensor.matmul(ps[:, c, :], chip.mean[:], flat[:, c, :], start=True, stop=True).then_inc(s["mean"], 1)
            for c in range(CH):
                pe.wait_ge(s["squared"], done + c + 1)
                nc.tensor.matmul(ps[:, 4 + c, :], chip.mean[:], sq[:, c, :], start=True, stop=True).then_inc(s["power"], 1)

        @block.scalar
        def _(act):
            for c in range(CH):
                if centre:
                    act.wait_ge(s["centred"], done_centred + c + 1)
                nc.scalar.activation(sq[:, c, :], centred[:, c, :], ACT.Square).then_inc(s["squared"], 1)
            for c in range(CH):
                act.wait_ge(s["power"], done + c + 1)
                nc.scalar.activation(root[:, c, :], ps[:, 4 + c, :], ACT.Ln, bias=chip.eps[:, which:which + 1]).then_inc(s["log"], 1)
            for c in range(CH):
                act.wait_ge(s["log"], done + c + 1)
                nc.scalar.activation(root[:, c, :], root[:, c, :], ACT.Exp, scale=-0.5).then_inc(s["inverse"], 1)

        @block.vector
        def _(dve):
            for c in range(CH):
                if centre:
                    dve.wait_ge(s["mean"], done_centred + c + 1)
                    nc.vector.tensor_tensor(goal[:, c, :], flat[:, c, :], ps[:, c, :], ALU.subtract).then_inc(s["centred"], 1)
            for c in range(CH):
                if centre:
                    dve.wait_ge(s["centred"], done_centred + c + 1)
                dve.wait_ge(s["inverse"], done + c + 1)
                if weight is None:
                    nc.vector.tensor_tensor(goal[:, c, :], centred[:, c, :], root[:, c, :], ALU.mult).then_inc(s["out"], 1)
                else:
                    nc.vector.scalar_tensor_tensor(goal[:, c, :], centred[:, c, :], weight, root[:, c, :], ALU.mult, ALU.mult).then_inc(s["out"], 1)


def self_attention_0(chip):
    nc, ps, xn, x = chip.nc, chip.ps, chip.xn, chip.x
    DH = 64
    HJ = HX // 2
    landed = chip.sem("a0_weights_landed")
    pads_clear = chip.sem("a0_pads_clear")
    tokens_ready = chip.sem("a0_tokens_ready")
    q_done, k_done, v_done = (chip.sem("a0_%s_done" % k) for k in "qkv")
    q_kept, k_kept, v_kept = (chip.sem("a0_%s_kept" % k) for k in "qkv")
    scores_done, shifted, exp_done = (chip.sem("a0_" + k) for k in ("scores_done", "shifted", "exp_done"))
    probs_ready, turned, probs_kept = (chip.sem("a0_" + k) for k in ("probs_ready", "turned", "probs_kept"))
    mixed, mixed_kept, projected, added = (chip.sem("a0_" + k) for k in ("mixed", "mixed_kept", "projected", "added"))
    dve_chain = chip.sem("a0_dve_chain")
    with ExitStack() as own:
        def sbuf(name, shape):
            return own.enter_context(nc.sbuf_tensor("a0_" + name, shape, F32))
        wq, wk, wv = (sbuf(n, [P, HX * DH]) for n in ("wq", "wk", "wv"))
        wo = sbuf("wo", [P, HJ, P])
        bq, bk, bv = (sbuf(n, [P, HJ]) for n in ("bq", "bk", "bv"))
        bo = sbuf("bo", [P, 1])
        tokens = sbuf("tokens", [P, P])
        q = sbuf("q", [P, HJ, P])
        k = sbuf("k", [P, HJ, 2, 2, SP])
        v = sbuf("v", [P, 2, HJ, 2, DH])
        probs = sbuf("probs", [P, HX, SP])
        probs_t = sbuf("probs_t", [P, HJ, P])
        mix = sbuf("mix", [P, HJ, 2, SP])
        top, total, inverse = (sbuf(n, [P, HX]) for n in ("top", "total", "inverse"))
        scores = ps[:, 6:8, :].rearrange("p k (h s) -> p (k h) s", s=SP)[:, :, 0:S]
        block = own.enter_context(nc.Block(no_gpsimd_drain=True))

        @block.sync
        def _(sp):
            for dst, name in ((wq, "L0_attn_W_Q"), (wk, "L0_attn_W_K"), (wv, "L0_attn_W_V"), (wo, "L0_attn_W_O"),
                              (bq, "L0_attn_b_Q"), (bk, "L0_attn_b_K"), (bv, "L0_attn_b_V"), (bo, "L0_attn_b_O")):
                sp.dma_start(dst[:], chip.dram[name]).then_inc(landed, 16)

        @block.tensor
        def _(pe):
            pe.wait_ge(landed, 8 * 16)
            with pe.Fori(0, NP_) as i:
                pe.wait_ge(tokens_ready, i + 1)
                for w, bank, done in ((wq, 0, q_done), (wk, 2, k_done)):
                    for j in range(HJ):
                        mm = nc.tensor.matmul(ps[:, bank + j // 4, P * (j % 4):P * (j % 4) + P], w[:, P * j:P * j + P],
                                              tokens[:], start=True, stop=True)
                    mm.then_inc(done, 1)
                pe.wait_ge(added, i + 1)
                for b in range(2):
                    for odd in range(2):
                        mm = nc.tensor.matmul(ps[64 * odd:64 * odd + 64, 4 + b, :], tokens[:, SP * b:SP * b + SP],
                                              wv[:, 512 * odd:512 * odd + 512], start=True, stop=True)
                mm.then_inc(v_done, 1)
                pe.wait_ge(q_kept, i + 1)
                pe.wait_ge(k_kept, 2 * i + 2)
                for j in range(HJ):
                    for b in range(2):
                        mm = nc.tensor.matmul(ps[64 * b:64 * b + 64, 6 + j // 4, P * (j % 4):P * (j % 4) + P],
                                              q[:, j, SP * b:SP * b + SP], k[:, j, b].rearrange("p h s -> p (h s)"),
                                              start=True, stop=True)
                mm.then_inc(scores_done, 1)
                pe.wait_ge(probs_ready, i + 1)
                for j in range(HJ):
                    mm = nc.tensor.transpose(ps[:, j // 4, P * (j % 4):P * (j % 4) + P],
                                             probs[:, 2 * j:2 * j + 2, :].rearrange("p h s -> p (h s)"), chip.ident[:])
                mm.then_inc(turned, 1)
                pe.wait_ge(probs_kept, i + 1)
                pe.wait_ge(v_kept, i + 1)
                for j in range(HJ):
                    for b in range(2):
                        mm = nc.tensor.matmul(ps[:, 2 + j // 4, P * (j % 4) + SP * b:P * (j % 4) + SP * b + S],
                                              v[:, b, j].rearrange("p h d -> p (h d)"), probs_t[:, j, SP * b:SP * b + S],
                                              start=True, stop=True)
                mm.then_inc(mixed, 1)
                pe.wait_ge(mixed_kept, i + 1)
                for j in range(HJ):
                    mm = nc.tensor.matmul(ps[:, 4, 0:P], wo[:, j, :], mix[:, j].rearrange("p b s -> p (b s)"),
                                          start=(j == 0), stop=(j == HJ - 1))
                mm.then_inc(projected, 1)

        @block.scalar
        def _(act):
            act.wait_ge(pads_clear, 1)
            with act.Fori(0, NP_) as i:
                act.wait_ge(v_done, i + 1)
                nc.scalar.copy(tokens[:], xn.rearrange("p b s -> p (b s)")[:, bass.ds(i * P, P)]).then_inc(tokens_ready, 1)
                act.wait_ge(v_done, i + 2)
                nc.scalar.copy(v[0:64, :, :, 0, :], ps[0:64, 4:6, :].rearrange("p b (j d) -> p b j d", d=DH))
                nc.scalar.copy(v[64:P, :, :, 1, :], ps[64:P, 4:6, :].rearrange("p b (j d) -> p b j d", d=DH)).then_inc(v_kept, 1)
                act.wait_ge(shifted, i + 1)
                nc.scalar.activation(probs[:, :, 0:S], probs[:, :, 0:S], ACT.Exp, scale=DH ** -0.5).then_inc(exp_done, 1)
                act.wait_ge(turned, i + 1)
                nc.scalar.copy(probs_t[:], ps[:, 0:2, :].rearrange("p k (j c) -> p (k j) c", c=P)).then_inc(probs_kept, 1)

        @block.vector
        def _(dve):
            nc.vector.memset(probs[:], 0.0).then_inc(v_done, 1)
            nc.vector.memset(k[:], 0.0).then_inc(added, 1)
            nc.vector.memset(mix[:], 0.0)
            nc.vector.memset(v[:], 0.0).then_inc(pads_clear, 1)
            dve.wait_ge(landed, 8 * 16)
            with dve.Fori(0, NP_) as i:
                dve.wait_ge(q_done, i + 1)
                nc.vector.tensor_tensor(q[:], ps[:, 0:2, :].rearrange("p k (j c) -> p (k j) c", c=P),
                                        spread(bq[:], 2, P), ALU.add).then_inc(q_kept, 1)
                dve.wait_ge(k_done, i + 1)
                for odd in range(2):
                    r = slice(64 * odd, 64 * odd + 64)
                    nc.vector.tensor_tensor(k[r, :, :, odd, :], ps[r, 2:4, :].rearrange("p k (j b s) -> p (k j) b s", j=4, b=2),
                                            spread(spread(bk[r], 2, 2), 3, SP), ALU.add).then_inc(k_kept, 1)
                dve.wait_ge(scores_done, i + 1)
                step = Step(dve, dve_chain, 3 * i)
                step(nc.vector.tensor_reduce(top[:], scores, AX_X, ALU.max))
                nc.vector.tensor_tensor(probs[:, :, 0:S], scores, spread(top[:], 2, S), ALU.subtract).then_inc(shifted, 1)
                dve.wait_ge(exp_done, i + 1)
                step(nc.vector.tensor_reduce(total[:], probs[:, :, 0:S], AX_X, ALU.add))
                step(nc.vector.reciprocal(inverse[:], total[:]))
                nc.vector.tensor_tensor(probs[:, :, 0:S], probs[:, :, 0:S], spread(inverse[:], 2, S),
                                        ALU.mult).then_inc(probs_ready, 1)
                dve.wait_ge(mixed, i + 1)
                nc.vector.tensor_tensor(
                    mix[:, :, :, 0:S], ps[:, 2:4, :].rearrange("p k (j b s) -> p (k j) b s", j=4, b=2)[:, :, :, 0:S],
                    spread(spread(bv[:], 2, 2), 3, S), ALU.add).then_inc(mixed_kept, 1)
                dve.wait_ge(projected, i + 1)
                pair = x[:, bass.ds(2 * i, 2), 0:S]
                nc.vector.scalar_tensor_tensor(pair, ps[:, 4, 0:P].rearrange("p (b s) -> p b s", s=SP)[:, :, 0:S],
                                               bo[:, 0:1], pair, ALU.add, ALU.add).then_inc(added, 1)


def context_mixing(chip):
    nc, ps, xn, x = chip.nc, chip.ps, chip.xn, chip.x
    landed = [chip.sem("cm_context_landed%d" % u) for u in range(2)]
    tokens_ready, top_ready, exp_done, probs_ready, turned, probs_kept = (
        chip.sem("cm_" + k) for k in ("tokens_ready", "top_ready", "exp_done", "probs_ready", "turned", "probs_kept"))
    scores_done, mixed, added = ([chip.sem("cm_%s%d" % (k, u)) for u in range(2)] for k in ("scores_done", "mixed", "added"))
    dve_chain = chip.sem("cm_dve_chain")
    with ExitStack() as own:
        def sbuf(name, shape):
            return own.enter_context(nc.sbuf_tensor("cm_" + name, shape, F32))
        ctx_t = [sbuf("ctx_t%d" % u, [P, 2, NK]) for u in range(2)]
        ctx_n = [sbuf("ctx_n%d" % u, [KC, 2, NC_, P]) for u in range(2)]
        tokens = [sbuf("tokens%d" % u, [P, P]) for u in range(2)]
        probs = [sbuf("probs%d" % u, [P, NB_, KB]) for u in range(2)]
        probs_t = [sbuf("probs_t%d" % u, [KC, NC_, P]) for u in range(2)]
        top = [sbuf("top%d" % u, [P, 1]) for u in range(2)]
        low = [sbuf("low%d" % u, [P, 1]) for u in range(2)]
        total = [sbuf("total%d" % u, [P, 1]) for u in range(2)]
        inverse = [sbuf("inverse%d" % u, [P, 1]) for u in range(2)]
        block = own.enter_context(nc.Block(no_gpsimd_drain=True))

        @block.sync
        def _(sp):
            with sp.Fori(0, NP_ // 2) as i:
                for u in range(2):
                    sp.wait_ge(mixed[u], i + 1)
                    for b in range(2):
                        seq = bass.ds(4 * i + 2 * u + b, 1)
                        sp.dma_start(ctx_t[u][:, b], chip.dram["ctx_t"][seq].rearrange("a p n -> (a p) n")).then_inc(landed[u], 16)
                        sp.dma_start(ctx_n[u][:, b], chip.dram["ctx_n"][seq].rearrange("a p c d -> (a p) c d")).then_inc(landed[u], 16)

        @block.tensor
        def _(pe):
            with pe.Fori(0, NP_ // 2) as i:
                for u in range(2):
                    pe.wait_ge(landed[u], 64 * i + 64)
                    pe.wait_ge(added[u], i + 1)
                    pe.wait_ge(tokens_ready, 2 * i + u + 1)
                    for n in range(NB_):
                        for b in range(2):
                            mm = nc.tensor.matmul(ps[SP * b:SP * b + SP, 3 * u + n, 0:KB], tokens[u][:, SP * b:SP * b + SP],
                                                  ctx_t[u][:, b, KB * n:KB * n + KB], start=True, stop=True)
                    mm.then_inc(scores_done[u], 1)
                for u in range(2):
                    pe.wait_ge(probs_ready, 2 * i + u + 1)
                    rows = probs[u].rearrange("p n k -> p (n k)")
                    for c in range(NC_):
                        mm = nc.tensor.transpose(ps[0:KC, 3 * u + c // 4, P * (c % 4):P * (c % 4) + P],
                                                 rows[:, KC * c:KC * c + KC], chip.ident[:])
                    mm.then_inc(turned, 1)
                    pe.wait_ge(probs_kept, 2 * i + u + 1)
                    for b in range(2):
                        for c in range(NC_):
                            mm = nc.tensor.matmul(ps[:, 6 + u, SP * b:SP * b + SP], ctx_n[u][:, b, c, :],
                                                  probs_t[u][:, c, SP * b:SP * b + SP], start=(c == 0), stop=(c == NC_ - 1))
                    mm.then_inc(mixed[u], 1)

        @block.scalar
        def _(act):
            with act.Fori(0, NP_ // 2) as i:
                for u in range(2):
                    act.wait_ge(scores_done[u], i + 1)
                    nc.scalar.copy(tokens[u][:], xn[:, bass.ds(4 * i + 2 * u, 2), :].rearrange("p b s -> p (b s)")).then_inc(tokens_ready, 1)
                for u in range(2):
                    act.wait_ge(top_ready, 2 * i + u + 1)
                    nc.scalar.activation(probs[u][:], ps[:, 3 * u:3 * u + 3, 0:KB], ACT.Exp, bias=low[u][:, 0:1],
                                         accum_out=total[u][:, 0:1]).then_inc(exp_done, 1)
                for u in range(2):
                    act.wait_ge(turned, 2 * i + u + 1)
                    nc.scalar.copy(probs_t[u][:], ps[0:KC, 3 * u:3 * u + 3, :].rearrange("p k (c s) -> p (k c) s", s=P)).then_inc(probs_kept, 1)

        @block.vector
        def _(dve):
            for u in range(2):
                nc.vector.memset(top[u][:], 0.0).then_inc(mixed[u], 1)
                nc.vector.memset(low[u][:], 0.0).then_inc(added[u], 1)
                nc.vector.memset(total[u][:], 0.0).then_inc(scores_done[u], 1)
            with dve.Fori(0, NP_ // 2) as i:
                for u in range(2):
                    dve.wait_ge(scores_done[u], i + 2)
                    Step(dve, dve_chain, 4 * i + u)(
                        nc.vector.tensor_reduce(top[u][:], ps[:, 3 * u:3 * u + 3, 0:KB], mybir.AxisListType.XY, ALU.max))
                    nc.vector.tensor_scalar(low[u][:], top[u][:], -1.0, None, ALU.mult).then_inc(top_ready, 1)
                for u in range(2):
                    dve.wait_ge(exp_done, 2 * i + u + 1)
                    step = Step(dve, dve_chain, 4 * i + 2 + u)
                    step(nc.vector.reciprocal(inverse[u][:], total[u][:]))
                    nc.vector.tensor_scalar(probs[u][:], probs[u][:], inverse[u][:, 0:1], None, ALU.mult).then_inc(probs_ready, 1)
                for u in range(2):
                    dve.wait_ge(mixed[u], i + 2)
                    pair = x[:, bass.ds(4 * i + 2 * u, 2), 0:S]
                    nc.vector.tensor_tensor(pair, pair, ps[:, 6 + u, 0:P].rearrange("p (b s) -> p b s", s=SP)[:, :, 0:S], ALU.add).then_inc(added[u], 1)


def coupled_twist(chip):
    nc, ps, xn, x = chip.nc, chip.ps, chip.xn, chip.x
    CYCLES = 3
    cleared, landed, ready = chip.sem("ct_cleared"), chip.sem("ct_landed"), chip.sem("ct_constants_ready")
    sums_ready = chip.sem("ct_sums_ready")
    global_done, global_kept = chip.sem("ct_global_done"), chip.sem("ct_global_kept")
    layer_done, layer_kept, twisted, coupled = (chip.sem("ct_" + k) for k in ("layer_done", "layer_kept", "twisted", "coupled"))
    stepped, dve_chain, added = chip.sem("ct_stepped"), chip.sem("ct_dve_chain"), chip.sem("ct_added")
    D2, D4 = P // 2, P // 4
    with ExitStack() as own:
        def sbuf(name, shape):
            return own.enter_context(nc.sbuf_tensor("ct_" + name, shape, F32))
        weights, biases = sbuf("weights", [P, 5, P]), sbuf("biases", [P, 5])
        cw2, cw3, gw1, gw2, cw1 = (weights[:, n] for n in range(5))
        cb2, cb3, gb1, gb2, cb1 = (biases[:, n:n + 1] for n in range(5))
        cw4, gw3 = sbuf("cw4", [P, 1]), sbuf("gw3", [P, 1])
        cb4, gb3 = sbuf("cb4", [P, 1]), sbuf("gb3", [P, 1])
        reach = sbuf("reach", [P, 1])
        twist = sbuf("twist", [P, P])
        cw4_all, gw3_all = sbuf("cw4_all", [P, P]), sbuf("gw3_all", [P, P])
        sums, g1, g2, gf, base = sbuf("sums", [P, B]), sbuf("g1", [P, B]), sbuf("g2", [P, B]), sbuf("gf", [P, B]), sbuf("base", [P, B])
        gain_g, gain_t, low = sbuf("gain_g", [P, 1]), sbuf("gain_t", [P, 1]), sbuf("low", [P, 1])
        hidden = [sbuf("hidden%d" % c, [P, CT]) for c in range(CH)]
        coupling = [sbuf("coupling%d" % c, [P, CT]) for c in range(CH)]
        y = [xn[:, CB * c:CB * c + CB, 0:S] for c in range(CH)]
        x_of = [x[:, CB * c:CB * c + CB, 0:S] for c in range(CH)]
        wide = [ps[:, 4 + c, 0:CT].rearrange("p (b s) -> p b s", s=S) for c in range(CH)]
        loads = [(cw1, "cn_w1"), (cw2[:, 0:D2], "cn_w2"), (cw3[0:D2, 0:D4], "cn_w3"), (cw4[0:D4], "cn_w4"),
                 (cb1, "cn_b1"), (cb2[0:D2], "cn_b2"), (cb3[0:D4], "cn_b3"), (gw1[:, 0:D2], "gc_w1"),
                 (gw2[0:D2, 0:D4], "gc_w2"), (gw3[0:D4], "gc_w3"), (gb1[0:D2], "gc_b1"), (gb2[0:D4], "gc_b2")]
        to_all = [(cb4, "cn_b4"), (gb3, "gc_b3"), (reach, "adaptive_range")]
        n_loads = len(loads) + len(to_all) + 1
        block = own.enter_context(nc.Block(no_gpsimd_drain=True))

        @block.sync
        def _(sp):
            sp.wait_ge(cleared, 4)
            for dst, name in loads:
                sp.dma_start(dst, chip.dram["L0_ffn_" + name]).then_inc(landed, 16)
            for dst, name in to_all:
                sp.dma_start(dst[:], chip.dram["L0_ffn_" + name].to_broadcast([P, 1])).then_inc(landed, 16)
            sp.dma_start(twist[:], chip.dram["twist"]).then_inc(landed, 16)

        @block.tensor
        def _(pe):
            pe.wait_ge(landed, 16 * n_loads)
            pe.wait_ge(ready, 2)
            pe.wait_ge(sums_ready, 1)
            nc.tensor.matmul(ps[:, 4, 0:B], gw1, sums[:], start=True, stop=True).then_inc(global_done, 1)
            pe.wait_ge(global_kept, 1)
            nc.tensor.matmul(ps[:, 5, 0:B], gw2, g1[:], start=True, stop=True).then_inc(global_done, 1)
            pe.wait_ge(global_kept, 2)
            nc.tensor.matmul(ps[:, 6, 0:B], gw3_all[:], g2[:], start=True, stop=True).then_inc(global_done, 1)
            pe.wait_ge(global_kept, 3)
            with pe.Fori(0, CYCLES) as i:
                for c in range(CH):
                    pe.wait_ge(stepped, CH * i + c + 1)
                    nc.tensor.matmul(ps[:, c, 0:CT], cw1, y[c], start=True, stop=True).then_inc(layer_done, 1)
                    nc.tensor.matmul(ps[:, 4 + c, 0:CT], twist[:], y[c], start=True, stop=True).then_inc(twisted, 1)
                for c in range(CH):
                    pe.wait_ge(layer_kept, 16 * i + c + 1)
                    nc.tensor.matmul(ps[:, c, 0:CT], cw2, hidden[c][:], start=True, stop=True).then_inc(layer_done, 1)
                for c in range(CH):
                    pe.wait_ge(layer_kept, 16 * i + 4 + c + 1)
                    nc.tensor.matmul(ps[:, c, 0:CT], cw3, hidden[c][:], start=True, stop=True).then_inc(layer_done, 1)
                for c in range(CH):
                    pe.wait_ge(layer_kept, 16 * i + 8 + c + 1)
                    nc.tensor.matmul(ps[:, c, 0:CT], cw4_all[:], hidden[c][:], start=True, stop=True).then_inc(layer_done, 1)

        @block.scalar
        def _(act):
            act.wait_ge(landed, 16 * n_loads)
            act.wait_ge(global_done, 1)
            nc.scalar.activation(g1[:], ps[:, 4, 0:B], ACT.Gelu, bias=gb1, scale=1.0 / S).then_inc(global_kept, 1)
            act.wait_ge(global_done, 2)
            nc.scalar.activation(g2[:], ps[:, 5, 0:B], ACT.Gelu, bias=gb2).then_inc(global_kept, 1)
            act.wait_ge(global_done, 3)
            nc.scalar.activation(gf[:], ps[:, 6, 0:B], ACT.Sigmoid, bias=gb3[:, 0:1]).then_inc(global_kept, 1)
            with act.Fori(0, CYCLES) as i:
                for n, bias in enumerate((cb1, cb2, cb3)):
                    for c in range(CH):
                        act.wait_ge(layer_done, 16 * i + 4 * n + c + 1)
                        nc.scalar.activation(hidden[c][:], ps[:, c, 0:CT], ACT.Gelu, bias=bias).then_inc(layer_kept, 1)
                for c in range(CH):
                    act.wait_ge(layer_done, 16 * i + 12 + c + 1)
                    nc.scalar.activation(coupling[c][:], ps[:, c, 0:CT], ACT.Sigmoid, bias=cb4[:, 0:1]).then_inc(layer_kept, 1)

        @block.vector
        def _(dve):
            for buffer in (weights, biases, cw4, gw3):
                nc.vector.memset(buffer[:], 0.0).then_inc(cleared, 1)
            nc.vector.tensor_reduce(sums[:], xn[:, :, 0:S], AX_X, ALU.add).then_inc(sums_ready, 1)
            dve.wait_ge(landed, 16 * n_loads)
            step = Step(dve, dve_chain)
            nc.vector.tensor_copy(cw4_all[:], cw4[:, 0:1].to_broadcast([P, P])).then_inc(ready, 1)
            nc.vector.tensor_copy(gw3_all[:], gw3[:, 0:1].to_broadcast([P, P])).then_inc(ready, 1)
            step(nc.vector.tensor_scalar(gain_g[:], reach[:], 1.4, None, ALU.mult))
            step(nc.vector.tensor_scalar(gain_t[:], reach[:], 0.6, None, ALU.mult))
            step(nc.vector.tensor_scalar(low[:], reach[:], -1.0, 0.1, ALU.mult, ALU.add))
            dve.wait_ge(global_kept, 3)
            step(nc.vector.tensor_scalar(base[:], gf[:], gain_g[:, 0:1], low[:, 0:1], ALU.mult, ALU.add))
            for c in range(CH):
                nc.vector.tensor_tensor(x_of[c], x_of[c], y[c], ALU.add).then_inc(stepped, 1)
            with dve.Fori(0, CYCLES) as i:
                for c in range(CH):
                    dve.wait_ge(layer_kept, 16 * i + 12 + c + 1)
                    dve.wait_ge(twisted, CH * i + c + 1)
                    cc = coupling[c].rearrange("p (b s) -> p b s", s=S)
                    step = Step(dve, coupled, 8 * i + 2 * c)
                    step(nc.vector.scalar_tensor_tensor(cc, cc, gain_t[:, 0:1], spread(base[:, CB * c:CB * c + CB], 2, S), ALU.mult, ALU.add))
                    step(nc.vector.tensor_tensor(cc, cc, wide[c], ALU.mult))
                    nc.vector.tensor_tensor(x_of[c], x_of[c], cc, ALU.add).then_inc(added, 1)
                    dve.wait_ge(added, CH * i + c + 1)
                    nc.vector.tensor_tensor(y[c], y[c], cc, ALU.add).then_inc(stepped, 1)


def gated_recurrence(chip):
    nc, ps, xn, x = chip.nc, chip.ps, chip.xn, chip.x
    W = B * SP
    TAPS = 4
    landed, conv_ready, gates_done, gates_kept = (chip.sem("gr_" + k) for k in ("landed", "conv_ready", "gates_done", "gates_kept"))
    dve_chain, act_chain = chip.sem("gr_dve_chain"), chip.sem("gr_act_chain")
    rate_ready, decay_ready, sums_ready = chip.sem("gr_rate_ready"), chip.sem("gr_decay_ready"), chip.sem("gr_sums_ready")
    root_needed, root_ready = chip.sem("gr_root_needed"), chip.sem("gr_root_ready")
    h_ready, out_done, squared, power_done, root_kept, added = (
        chip.sem("gr_" + k) for k in ("h_ready", "out_done", "squared", "power_done", "root_kept", "added"))
    with ExitStack() as own:
        def sbuf(name, shape):
            return own.enter_context(nc.sbuf_tensor("gr_" + name, shape, F32))
        wr, wi, wo = sbuf("wr", [P, P]), sbuf("wi", [P, P]), sbuf("wo", [P, P])
        taps, bc, br, bi, log_a, norm_w = sbuf("taps", [P, TAPS]), *(sbuf(n, [P, 1]) for n in ("bc", "br", "bi", "log_a", "norm_w"))
        rate = sbuf("rate", [P, 1])
        conv, r_gate, i_gate, alive, work = (sbuf(n, [P, W]) for n in ("conv", "r_gate", "i_gate", "alive", "work"))
        out_sb = sbuf("out", [P, CH, CW])
        flat = chip.xn_lead[:]
        loads = [(wr, "Wr_w"), (wi, "Wi_w"), (wo, "out_w"), (taps, "conv_weight"), (bc, "conv_bias"), (br, "Wr_b"), (bi, "Wi_b"),
                 (log_a, "log_a"), (norm_w, "norm_w")]
        block = own.enter_context(nc.Block(no_gpsimd_drain=True))

        @block.sync
        def _(sp):
            for dst, name in loads:
                sp.dma_start(dst[:], chip.dram["L1_attn_" + name]).then_inc(landed, 16)

        @block.tensor
        def _(pe):
            pe.wait_ge(conv_ready, 1)
            for c in range(CH):
                cols = conv[:, CW * c:CW * c + CW]
                nc.tensor.matmul(ps[:, c, :], wr[:], cols, start=True, stop=True).then_inc(gates_done, 1)
            for c in range(CH):
                cols = conv[:, CW * c:CW * c + CW]
                nc.tensor.matmul(ps[:, 4 + c, :], wi[:], cols, start=True, stop=True).then_inc(gates_done, 1)
            pe.wait_ge(h_ready, 1)
            for c in range(CH):
                nc.tensor.matmul(ps[:, c, :], wo[:], conv[:, CW * c:CW * c + CW], start=True, stop=True).then_inc(out_done, 1)
            for c in range(CH):
                pe.wait_ge(squared, c + 1)
                nc.tensor.matmul(ps[:, 4 + c, :], chip.mean[:], work[:, CW * c:CW * c + CW], start=True, stop=True).then_inc(power_done, 1)

        @block.scalar
        def _(act):
            act.wait_ge(landed, 16 * len(loads))
            for c in range(CH):
                act.wait_ge(gates_done, c + 1)
                nc.scalar.activation(r_gate[:, CW * c:CW * c + CW], ps[:, c, :], ACT.Sigmoid, bias=br[:, 0:1]).then_inc(gates_kept, 1)
            for c in range(CH):
                act.wait_ge(gates_done, 4 + c + 1)
                nc.scalar.activation(i_gate[:, CW * c:CW * c + CW], ps[:, 4 + c, :], ACT.Sigmoid, bias=bi[:, 0:1]).then_inc(gates_kept, 1)
            step = Step(act, act_chain)
            step(nc.scalar.activation(rate[:], log_a[:], ACT.Exp, scale=-1.0))
            nc.scalar.activation(rate[:], rate[:], ACT.Ln, bias=1.0).then_inc(rate_ready, 1)
            act.wait_ge(decay_ready, 1)
            nc.scalar.activation(r_gate[:], work[:], ACT.Exp).then_inc(rate_ready, 1)
            act.wait_ge(root_needed, 1)
            nc.scalar.activation(r_gate[:], r_gate[:], ACT.Sqrt).then_inc(root_ready, 1)
            act.wait_ge(sums_ready, 1)
            step(nc.scalar.activation(i_gate[:], work[:], ACT.Exp, scale=-1.0))
            nc.scalar.activation(work[:], work[:], ACT.Exp).then_inc(root_ready, 1)
            for c in range(CH):
                act.wait_ge(out_done, c + 1)
                nc.scalar.copy(out_sb[:, c, :], ps[:, c, :]).then_inc(act_chain, 1)
                act.wait_ge(act_chain, 3 + c)
                nc.scalar.activation(work[:, CW * c:CW * c + CW], out_sb[:, c, :], ACT.Square).then_inc(squared, 1)
            for c in range(CH):
                act.wait_ge(power_done, c + 1)
                nc.scalar.activation(r_gate[:, CW * c:CW * c + CW], ps[:, 4 + c, :], ACT.Sqrt, bias=chip.eps[:, 1:2]).then_inc(root_kept, 1)

        @block.vector
        def _(dve):
            step = Step(dve, dve_chain)
            nc.vector.memset(alive[:], 1.0)
            step(nc.vector.memset(work[:], 1.0))
            step(nc.vector.memset(alive.rearrange("p (b s) -> p b s", s=SP)[:, :, 0:1], 0.0))
            dve.wait_ge(landed, 16 * len(loads))
            step(nc.vector.tensor_scalar(conv[:], flat[:, SP:SP + W], taps[:, 3:4], bc[:, 0:1], ALU.mult, ALU.add))
            for t in range(TAPS - 1):
                shift = TAPS - 1 - t
                last = nc.vector.scalar_tensor_tensor(conv[:], flat[:, SP - shift:SP - shift + W], taps[:, t:t + 1], conv[:], ALU.mult, ALU.add)
                if t < TAPS - 2:
                    step(last)
            last.then_inc(conv_ready, 1)
            dve.wait_ge(rate_ready, 1)
            step(nc.vector.tensor_scalar(rate[:], rate[:], -8.0, None, ALU.mult))
            dve.wait_ge(gates_kept, 4)
            nc.vector.tensor_scalar(work[:], r_gate[:], rate[:, 0:1], None, ALU.mult).then_inc(decay_ready, 1)
            dve.wait_ge(decay_ready, 1)
            dve.wait_ge(rate_ready, 2)
            step(nc.vector.tensor_scalar(work[:], work[:], float(np.log(np.float32(1e-7))), None, ALU.max))
            step(nc.vector.tensor_tensor(r_gate[:], r_gate[:], r_gate[:], ALU.mult))
            step(nc.vector.tensor_scalar(r_gate[:], r_gate[:], -1.0, 1.0, ALU.mult, ALU.add))
            nc.vector.tensor_scalar(r_gate[:], r_gate[:], 1e-6, None, ALU.max).then_inc(root_needed, 1)
            step(nc.vector.tensor_tensor_scan(out_sb.rearrange("p c w -> p (c w)"), alive[:], work[:], 0.0, ALU.mult, ALU.add))
            dve.wait_ge(gates_kept, 8)
            step(nc.vector.tensor_tensor(conv[:], conv[:], i_gate[:], ALU.mult))
            nc.vector.tensor_scalar(work[:], out_sb.rearrange("p c w -> p (c w)"), -80.0, None, ALU.max).then_inc(sums_ready, 1)
            dve.wait_ge(root_ready, 1)
            step(nc.vector.tensor_tensor(conv[:], conv[:], r_gate[:], ALU.mult))
            dve.wait_ge(root_ready, 2)
            step(nc.vector.tensor_tensor(conv[:], conv[:], i_gate[:], ALU.mult))
            step(nc.vector.tensor_tensor_scan(out_sb.rearrange("p c w -> p (c w)"), alive[:], conv[:], 0.0, ALU.mult, ALU.add))
            nc.vector.tensor_tensor(conv[:], out_sb.rearrange("p c w -> p (c w)"), work[:], ALU.mult).then_inc(h_ready, 1)
            dve.wait_ge(h_ready, 1)
            for c in range(CH):
                cols = slice(CW * c, CW * c + CW)
                dve.wait_ge(root_kept, c + 1)
                step(nc.vector.reciprocal(r_gate[:, cols], r_gate[:, cols]))
                step(nc.vector.scalar_tensor_tensor(r_gate[:, cols], r_gate[:, cols], norm_w[:, 0:1], out_sb[:, c, :], ALU.mult, ALU.mult))
                goal = x[:, CB * c:CB * c + CB, 0:S]
                nc.vector.tensor_tensor(goal, goal, r_gate[:, cols].rearrange("p (b s) -> p b s", s=SP)[:, :, 0:S], ALU.add).then_inc(added, 1)


XR = HX * S
XT = XR // P
HEAD_OF = [min(P * t // S, HX - 4) for t in range(XT)]
WIN = 4 * DX


def cross_attention(chip, layer, scale):
    nc, ps, xn, x = chip.nc, chip.ps, chip.xn, chip.x
    tag = "x%d_" % layer
    G = 3
    CG = NC_ // G
    landed, weights_landed, cleared = (chip.sem(tag + k) for k in ("landed", "weights_landed", "cleared"))
    q_done, k_done, v_done, q_ready, k_kept, v_kept = (chip.sem(tag + k) for k in ("q_done", "k_done", "v_done", "q_ready", "k_kept", "v_kept"))
    scores_done, low_ready, exp_done, turned = (chip.sem(tag + k) for k in ("scores_done", "low_ready", "exp_done", "turned"))
    kept_by_act, kept_by_dve, mixed, heads_ready, folded, fold_kept = (
        chip.sem(tag + k) for k in ("kept_by_act", "kept_by_dve", "mixed", "heads_ready", "folded", "fold_kept"))
    projected, added, dve_chain = (chip.sem(tag + k) for k in ("projected", "added", "dve_chain"))
    PROJ, TURN, MIX = 6, 6, 7
    with ExitStack() as own:
        def sbuf(name, shape):
            return own.enter_context(nc.sbuf_tensor(tag + name, shape, F32))
        wq, wk, wv, wo = (sbuf(n, [P, P]) for n in ("wq", "wk", "wv", "wo"))
        bq, bk, bv, bo = (sbuf(n, [P, 1]) for n in ("bq", "bk", "bv", "bo"))
        own_head, window, fold = sbuf("own_head", [P, HX]), sbuf("window", [P, XT, WIN]), sbuf("fold", [P, XT, S])
        ctx_t = sbuf("ctx_t", [P, NK])
        keys, values = sbuf("keys", [P, NB_, KB]), sbuf("values", [KC, NC_, P])
        q, q_diag = sbuf("q", [P, S]), sbuf("q_diag", [P, HX, S])
        probs = [sbuf("probs%d" % u, [P, NB_, KB]) for u in range(2)]
        probs_t = [sbuf("probs_t%d" % g, [KC, CG, P]) for g in range(G)]
        top, low, total, inverse = (sbuf(n, [P, XT]) for n in ("top", "low", "total", "inverse"))
        heads = sbuf("heads", [P, XT, P])
        mix = sbuf("mix", [P, B + 1, S])
        q_rows = q_diag.rearrange("p h s -> p (h s)")
        block = own.enter_context(nc.Block(no_gpsimd_drain=True))

        @block.sync
        def _(sp):
            for dst, name in ((wq, "Wq"), (wk, "Wk"), (wv, "Wv"), (wo, "Wo"), (bq, "bq"), (bk, "bk"), (bv, "bv"), (bo, "bo")):
                sp.dma_start(dst[:], chip.dram["L%d_xattn_%s" % (layer, name)]).then_inc(weights_landed, 16)
            for dst, name in ((own_head, "own_head"), (window, "window"), (fold, "fold")):
                sp.dma_start(dst[:], chip.dram[name]).then_inc(weights_landed, 16)
            with sp.Fori(0, B) as i:
                sp.wait_ge(v_done, i + 1)
                sp.dma_start(ctx_t[:], chip.dram["ctx_t"][bass.ds(i, 1)].rearrange("a p n -> (a p) n")).then_inc(landed, 16)

        @block.tensor
        def _(pe):
            def scores(i, t, n):
                mm = nc.tensor.matmul(ps[:, 3 * (t % 2) + n, 0:KB], q_rows[:, P * t:P * t + P], keys[:, n, :], start=True, stop=True)
                if n == NB_ - 1:
                    mm.then_inc(scores_done, 1)

            def turn(i, t, g):
                rows = probs[t % 2].rearrange("p n k -> p (n k)")
                for c in range(CG):
                    k0 = KC * (CG * g + c)
                    mm = nc.tensor.transpose(ps[0:KC, TURN, P * c:P * c + P], rows[:, k0:k0 + KC], chip.ident[:])
                mm.then_inc(turned, 1)

            def mix_values(i, t, g):
                h0 = DX * HEAD_OF[t]
                for c in range(CG):
                    mm = nc.tensor.matmul(ps[:, MIX, WIN * t:WIN * t + WIN], probs_t[g][:, c, :], values[:, CG * g + c, h0:h0 + WIN],
                                          start=(g == 0 and c == 0), stop=(g == G - 1 and c == CG - 1))
                if g == G - 1 and t == XT - 1:
                    mm.then_inc(mixed, 1)

            def fold_heads():
                for t in range(XT):
                    mm = nc.tensor.matmul(ps[:, TURN, 0:S], heads[:, t, :], fold[:, t, :], start=(t == 0), stop=(t == XT - 1))
                mm.then_inc(folded, 1)

            pe.wait_ge(weights_landed, 11 * 16)
            with pe.Fori(0, B) as i:
                nc.tensor.matmul(ps[:, PROJ, 0:S], wq[:], xn[:, bass.ds(i, 1), 0:S].rearrange("p b s -> p (b s)"),
                                 start=True, stop=True).then_inc(q_done, 1)
                pe.wait_ge(landed, 16 * i + 16)
                for n in range(NB_):
                    mm = nc.tensor.matmul(ps[:, n, 0:KB], wk[:], ctx_t[:, KB * n:KB * n + KB], start=True, stop=True)
                mm.then_inc(k_done, 1)
                for c in range(NC_):
                    mm = nc.tensor.matmul(ps[0:KC, 3 + c // 4, P * (c % 4):P * (c % 4) + P], ctx_t[:, KC * c:KC * c + KC], wv[:],
                                          start=True, stop=True)
                mm.then_inc(v_done, 1)
                pe.wait_ge(k_kept, i + 1)
                pe.wait_ge(q_ready, i + 1)
                for n in range(NB_):
                    scores(i, 0, n)
                pe.wait_ge(heads_ready, i + 1)
                fold_heads()
                pe.wait_ge(v_kept, i + 1)
                for n in range(NB_):
                    scores(i, 1, n)
                pe.wait_ge(fold_kept, i + 1)
                for t in range(XT):
                    more = t + 2 < XT
                    pe.wait_ge(exp_done, XT * i + t + 1)
                    turn(i, t, 0)
                    if more:
                        scores(i, t + 2, 0)
                    pe.wait_ge(kept_by_act, 2 * XT * i + 2 * t + 1)
                    turn(i, t, 1)
                    mix_values(i, t, 0)
                    if more:
                        scores(i, t + 2, 1)
                    pe.wait_ge(kept_by_dve, XT * i + t + 1)
                    turn(i, t, 2)
                    mix_values(i, t, 1)
                    if more:
                        scores(i, t + 2, 2)
                    pe.wait_ge(kept_by_act, 2 * XT * i + 2 * t + 2)
                    mix_values(i, t, 2)
            pe.wait_ge(heads_ready, B + 1)
            fold_heads()
            pe.wait_ge(fold_kept, B + 1)
            for c in range(CH):
                nc.tensor.matmul(ps[:, c, 0:CT], wo[:], mix[:, 1 + CB * c:1 + CB * c + CB, :].rearrange("p b s -> p (b s)"),
                                 start=True, stop=True).then_inc(projected, 1)

        @block.scalar
        def _(act):
            def exponentials(i, t):
                act.wait_ge(low_ready, XT * i + t + 1)
                nc.scalar.activation(probs[t % 2][:], ps[:, 3 * (t % 2):3 * (t % 2) + 3, 0:KB], ACT.Exp, bias=low[:, t:t + 1],
                                     scale=scale, accum_out=total[:, t:t + 1]).then_inc(exp_done, 1)

            def keep(i, t, g):
                act.wait_ge(turned, G * XT * i + G * t + g + 1)
                nc.scalar.copy(probs_t[g][:], ps[0:KC, TURN, :].rearrange("p (c r) -> p c r", r=P)).then_inc(kept_by_act, 1)

            act.wait_ge(weights_landed, 11 * 16)
            with act.Fori(0, B) as i:
                act.wait_ge(k_done, i + 1)
                nc.scalar.activation(keys[:], ps[:, 0:NB_, 0:KB], ACT.Identity, bias=bk[:, 0:1]).then_inc(k_kept, 1)
                exponentials(i, 0)
                for t in range(XT):
                    keep(i, t, 0)
                    if t + 1 < XT:
                        exponentials(i, t + 1)
                    keep(i, t, 2)

        @block.vector
        def _(dve):
            def row_tops(i, t):
                dve.wait_ge(scores_done, XT * i + t + 1)
                nc.vector.tensor_reduce(top[:, t:t + 1], ps[:, 3 * (t % 2):3 * (t % 2) + 3, 0:KB], mybir.AxisListType.XY,
                                        ALU.max).then_inc(dve_chain, 1)
                dve.wait_ge(dve_chain, LINKS * i + 1 + t + 1)
                nc.vector.tensor_scalar(low[:, t:t + 1], top[:, t:t + 1], -scale, None, ALU.mult).then_inc(low_ready, 1)

            LINKS = 2 + XT
            nc.vector.memset(heads[:], 0.0).then_inc(heads_ready, 1)
            nc.vector.memset(chip.credit[:, 0:1], 0.0).then_inc(v_done, 1)
            dve.wait_ge(weights_landed, 11 * 16)
            with dve.Fori(0, B) as i:
                dve.wait_ge(q_done, i + 1)
                nc.vector.tensor_scalar(q[:], ps[:, PROJ, 0:S], bq[:, 0:1], None, ALU.add).then_inc(dve_chain, 1)
                dve.wait_ge(dve_chain, LINKS * i + 1)
                nc.vector.tensor_tensor(q_diag[:], spread(q[:], 1, HX), spread(own_head[:], 2, S), ALU.mult).then_inc(q_ready, 1)
                dve.wait_ge(v_done, i + 2)
                nc.vector.tensor_copy(values[:], ps[0:KC, 3:6, :].rearrange("p k (c d) -> p (k c) d", d=P)).then_inc(v_kept, 1)
                row_tops(i, 0)
                dve.wait_ge(folded, i + 1)
                nc.vector.tensor_scalar(mix[:, bass.ds(i, 1), :].rearrange("p b s -> p (b s)"), ps[:, TURN, 0:S], bv[:, 0:1], None,
                                        ALU.add).then_inc(fold_kept, 1)
                row_tops(i, 1)
                for t in range(XT):
                    dve.wait_ge(turned, G * XT * i + G * t + 1 + 1)
                    nc.vector.tensor_copy(probs_t[1][:], ps[0:KC, TURN, :].rearrange("p (c r) -> p c r", r=P)).then_inc(kept_by_dve, 1)
                    if t + 2 < XT:
                        row_tops(i, t + 2)
                dve.wait_ge(exp_done, XT * i + XT)
                nc.vector.reciprocal(inverse[:], total[:]).then_inc(dve_chain, 1)
                dve.wait_ge(dve_chain, LINKS * i + 2 + XT)
                dve.wait_ge(mixed, i + 1)
                for t in range(XT):
                    h0 = DX * HEAD_OF[t]
                    last = nc.vector.scalar_tensor_tensor(heads[:, t, h0:h0 + WIN], ps[:, MIX, WIN * t:WIN * t + WIN],
                                                          inverse[:, t:t + 1], window[:, t, :], ALU.mult, ALU.mult)
                last.then_inc(heads_ready, 1)
            dve.wait_ge(folded, B + 1)
            nc.vector.tensor_scalar(mix[:, B, :], ps[:, TURN, 0:S], bv[:, 0:1], None, ALU.add).then_inc(fold_kept, 1)
            for c in range(CH):
                goal = x[:, CB * c:CB * c + CB, 0:S]
                dve.wait_ge(projected, c + 1)
                nc.vector.scalar_tensor_tensor(goal, ps[:, c, 0:CT].rearrange("p (b s) -> p b s", s=S), bo[:, 0:1], goal,
                                               ALU.add, ALU.add).then_inc(added, 1)


MARK = -2.0 ** 100


def spacer(n):
    return -2.0 ** (90 + n)


class Router:

    def __init__(self, chip, own, tag, experts, k, bias=None, scale=None):
        nc = chip.nc
        self.chip, self.tag, self.e, self.k, self.scale = chip, tag, experts, k, scale
        e = experts

        def sbuf(name, shape):
            return own.enter_context(nc.sbuf_tensor(tag + name, shape, F32))
        self.bias = bias
        self.top1, self.total = sbuf("top1", [P, NP_]), sbuf("total", [P, NP_])
        self.scores, self.weights = sbuf("scores", [P, NP_, e]), sbuf("weights", [P, NP_, e])
        self.found = sbuf("found", [P, NP_, e + 8 - k])
        self.marked = sbuf("marked", [P, NP_, e + 8 - k])
        self.top8 = sbuf("top8", [P, NP_, 8])
        self.logits_done, self.shifted, self.exp_done, self.chain, self.ready = (
            chip.sem(tag + n) for n in ("logits_done", "shifted", "exp_done", "route_chain", "weights_ready"))
        self.logits = chip.ps[:, 0:2, :].rearrange("p k (t e) -> p (k t) e", e=64)[:, :, 0:e]

    def make_logits(self, pe, source, weight):
        nc = self.chip.nc
        for t in range(NP_):
            mm = nc.tensor.matmul(self.chip.ps[:, t // 8, 64 * (t % 8):64 * (t % 8) + self.e], source[:, P * t:P * t + P], weight,
                                  start=True, stop=True)
        mm.then_inc(self.logits_done, 1)

    def exponentials(self, act):
        act.wait_ge(self.shifted, 1)
        self.chip.nc.scalar.activation(self.scores[:], self.scores[:], ACT.Exp).then_inc(self.exp_done, 1)

    def choose(self, dve):
        nc, e, k = self.chip.nc, self.e, self.k
        step = Step(dve, self.chain)
        for n in range(8 - k):
            nc.vector.memset(self.found[:, :, e + n:e + n + 1], spacer(n))
        dve.wait_ge(self.logits_done, 1)
        step(nc.vector.tensor_reduce(self.top1[:], self.logits, AX_X, ALU.max))
        nc.vector.tensor_tensor(self.scores[:], self.logits, spread(self.top1[:], 2, e), ALU.subtract).then_inc(self.shifted, 1)
        dve.wait_ge(self.exp_done, 1)
        step(nc.vector.tensor_reduce(self.total[:], self.scores[:], AX_X, ALU.add))
        step(nc.vector.reciprocal(self.total[:], self.total[:]))
        step(nc.vector.tensor_tensor(self.scores[:], self.scores[:], spread(self.total[:], 2, e), ALU.mult))
        if self.bias is None:
            step(nc.vector.tensor_copy(self.found[:, :, 0:e], self.scores[:]))
        else:
            step(nc.vector.tensor_tensor(self.found[:, :, 0:e], self.scores[:], spread(self.bias, 1, NP_), ALU.add))
        for t in range(NP_):
            last = nc.vector.max(self.top8[:, t, :], self.found[:, t, 0:e])
        step(last)
        for n in range(8 - k):
            last = nc.vector.memset(self.top8[:, :, k + n:k + n + 1], spacer(n))
        step(last)
        for t in range(NP_):
            last = nc.vector.match_replace(self.marked[:, t, :], self.top8[:, t, :], self.found[:, t, :], MARK)
        step(last)
        if self.scale is not None:
            step(nc.vector.tensor_scalar(self.weights[:], self.marked[:, :, 0:e], MARK, self.scale, ALU.is_equal, ALU.mult))
            nc.vector.tensor_tensor(self.weights[:], self.weights[:], self.scores[:], ALU.mult).then_inc(self.ready, 1)
        else:
            step(nc.vector.tensor_scalar(self.marked[:, :, 0:e], self.marked[:, :, 0:e], MARK, None, ALU.is_equal))
            step(nc.vector.tensor_tensor(self.weights[:], self.marked[:, :, 0:e], self.scores[:], ALU.mult))
            step(nc.vector.tensor_reduce(self.total[:], self.weights[:], AX_X, ALU.add))
            step(nc.vector.reciprocal(self.total[:], self.total[:]))
            nc.vector.tensor_tensor(self.weights[:], self.weights[:], spread(self.total[:], 2, e), ALU.mult).then_inc(self.ready, 1)
        return step


def experts(chip, tag, name, groups, subs, rows, gated, weight_rows):
    nc, ps, xn, x = chip.nc, chip.ps, chip.xn, chip.x
    landed = [chip.sem(tag + "landed%d" % u) for u in range(2)]
    used = [chip.sem(tag + "used%d" % u) for u in range(2)]
    zero_ready, up_done, gate_kept, hidden_ready, weighted, summed, added = (
        chip.sem(tag + k) for k in ("zero_ready", "up_done", "gate_kept", "hidden_ready", "weighted", "summed", "added"))
    M = 3 if gated else 2
    steps = [(u, s, c) for u in range(2) for s in range(subs) for c in range(CH)]
    N = len(steps)
    with ExitStack() as own:
        def sbuf(name, shape):
            return own.enter_context(nc.sbuf_tensor(tag + name, shape, F32))
        w = [sbuf("w%d" % u, [P, subs, M, P]) for u in range(2)]
        share = [sbuf("share%d" % u, [P, B * S]) for u in range(2)]
        silu = [sbuf("silu%d" % k, [P, CT]) for k in range(2)]
        hidden = [sbuf("hidden%d" % k, [P, CT]) for k in range(2)]
        zero = sbuf("zero", [P, P])
        tokens = [xn[:, CB * c:CB * c + CB, 0:S] for c in range(CH)]
        block = own.enter_context(nc.Block(no_gpsimd_drain=True))

        @block.sync
        def _(sp):
            with sp.Fori(0, groups // 2) as i:
                for u in range(2):
                    sp.wait_ge(used[u], i + 1)
                    sp.dma_start(w[u][:], chip.dram[name][bass.ds(2 * i + u, 1)].rearrange("g p s m d -> (g p) s m d")).then_inc(landed[u], 16)
                    for r in range(rows):
                        n = P // rows
                        sp.dma_start(share[u][n * r:n * r + n, :], weight_rows[bass.ds(rows * (2 * i + u) + r, 1), :].to_broadcast([n, B * S])).then_inc(landed[u], 16)

        @block.tensor
        def _(pe):
            def up(i, n):
                u, s, c = steps[n]
                if s == 0 and c == 0:
                    pe.wait_ge(landed[u], 16 * (rows + 1) * i + 16 * (rows + 1))
                for m in range(M - 1):
                    mm = nc.tensor.matmul(ps[:, 4 + 2 * (n % 2) + m, 0:CT], w[u][:, s, m, :], tokens[c], start=True, stop=True)
                mm.then_inc(up_done, 1)

            def down(i, n):
                u, s, c = steps[n]
                pe.wait_ge(hidden_ready, N * i + n + 1)
                mm = nc.tensor.matmul(ps[:, c, 0:CT], w[u][:, s, M - 1, :], hidden[n % 2][:], start=False, stop=False, skip_group_check=True)
                if s == subs - 1 and c == CH - 1:
                    mm.then_inc(used[u], 1)

            pe.wait_ge(zero_ready, 1)
            for c in range(CH):
                nc.tensor.matmul(ps[:, c, 0:CT], zero[:], tokens[c], start=True, stop=False, skip_group_check=True)
            with pe.Fori(0, groups // 2) as i:
                for n in range(N):
                    up(i, n)
                    if n:
                        down(i, n - 1)
                down(i, N - 1)
            for c in range(CH):
                nc.tensor.matmul(ps[:, c, 0:CT], zero[:], tokens[c], start=False, stop=True, skip_group_check=True).then_inc(summed, 1)

        @block.scalar
        def _(act):
            with act.Fori(0, groups // 2) as i:
                for n in range(N):
                    act.wait_ge(up_done, N * i + n + 1)
                    nc.scalar.activation(silu[n % 2][:], ps[:, 4 + 2 * (n % 2), 0:CT], ACT.Silu).then_inc(gate_kept, 1)

        @block.vector
        def _(dve):
            nc.vector.memset(zero[:], 0.0).then_inc(zero_ready, 1)
            for u in range(2):
                nc.vector.memset(chip.credit[:, u:u + 1], 0.0).then_inc(used[u], 1)
            with dve.Fori(0, groups // 2) as i:
                for n in range(N):
                    u, s, c = steps[n]
                    if s == 0 and c == 0:
                        dve.wait_ge(landed[u], 16 * (rows + 1) * i + 16 * (rows + 1))
                    if gated:
                        dve.wait_ge(up_done, N * i + n + 1)
                        nc.vector.tensor_tensor(hidden[n % 2][:], ps[:, 5 + 2 * (n % 2), 0:CT], share[u][:, CT * c:CT * c + CT], ALU.mult).then_inc(weighted, 1)
                        dve.wait_ge(weighted, N * i + n + 1)
                        dve.wait_ge(gate_kept, N * i + n + 1)
                        nc.vector.tensor_tensor(hidden[n % 2][:], hidden[n % 2][:], silu[n % 2][:], ALU.mult).then_inc(hidden_ready, 1)
                    else:
                        dve.wait_ge(gate_kept, N * i + n + 1)
                        nc.vector.tensor_tensor(hidden[n % 2][:], silu[n % 2][:], share[u][:, CT * c:CT * c + CT], ALU.mult).then_inc(hidden_ready, 1)
            for c in range(CH):
                goal = x[:, CB * c:CB * c + CB, 0:S]
                dve.wait_ge(summed, c + 1)
                nc.vector.tensor_tensor(goal, goal, ps[:, c, 0:CT].rearrange("p (b s) -> p b s", s=S), ALU.add).then_inc(added, 1)


def mixture_1(chip):
    nc, ps, xn, x = chip.nc, chip.ps, chip.xn, chip.x
    E_R, E_Z, K = 32, 8, 6
    E = E_R + E_Z
    scratch = nc.dram_tensor("m1_weight_rows", (E, B * S), F32, kind="Internal").ap()
    landed, turned, rows_kept, stored, passed, added, mask_ready, product_ready = (
        chip.sem("m1_" + k) for k in ("landed", "turned", "rows_kept", "stored", "passed", "added", "mask_ready", "product_ready"))
    with ExitStack() as own:
        def sbuf(name, shape):
            return own.enter_context(nc.sbuf_tensor("m1_" + name, shape, F32))
        classifier, bias = sbuf("classifier", [P, E]), sbuf("bias", [P, E])
        rows, passing, product = sbuf("rows", [E, NP_ * P]), sbuf("passing", [E, P]), sbuf("product", [P, CT])
        router = Router(chip, own, "m1_", E, K, bias[:], 2.5)
        flat = xn.rearrange("p b s -> p (b s)")
        block = own.enter_context(nc.Block())

        @block.sync
        def _(sp):
            sp.dma_start(classifier[:], chip.dram["L1_ffn_classifier_weight"]).then_inc(landed, 16)
            sp.dma_start(bias[:], chip.dram["L1_ffn_e_score_correction_bias"].to_broadcast([P, E])).then_inc(landed, 16)
            sp.wait_ge(rows_kept, 1)
            sp.dma_start(scratch.rearrange("e (b s) -> e b s", s=S), rows.rearrange("e (b s) -> e b s", s=SP)[:, :, 0:S]).then_inc(stored, 16)
            sp.wait_ge(stored, 16)

        @block.tensor
        def _(pe):
            pe.wait_ge(landed, 32)
            router.make_logits(pe, flat, classifier[:])
            pe.wait_ge(router.ready, 1)
            for t in range(NP_):
                mm = nc.tensor.transpose(ps[0:E, 4 + t // 4, P * (t % 4):P * (t % 4) + P], router.weights[:, t, :], chip.ident[:])
            mm.then_inc(turned, 1)
            pe.wait_ge(rows_kept, 1)
            pe.wait_ge(mask_ready, 2)
            for c in range(CH):
                nc.tensor.matmul(ps[:, c, 0:CT], passing[:], rows[:, CW * c:CW * c + CW].rearrange("e (b s) -> e b s", s=SP)[:, :, 0:S],
                                 start=True, stop=True).then_inc(passed, 1)

        @block.scalar
        def _(act):
            router.exponentials(act)
            act.wait_ge(turned, 1)
            nc.scalar.copy(rows[:], ps[0:E, 4:8, :].rearrange("e k n -> e (k n)")).then_inc(rows_kept, 1)

        @block.vector
        def _(dve):
            nc.vector.memset(passing[:], 0.0).then_inc(mask_ready, 1)
            dve.wait_ge(mask_ready, 1)
            nc.vector.memset(passing[E_R:E, :], 1.0).then_inc(mask_ready, 1)
            dve.wait_ge(landed, 32)
            router.choose(dve)
            for c in range(CH):
                goal, tokens = (v[:, CB * c:CB * c + CB, 0:S] for v in (x, xn))
                dve.wait_ge(passed, c + 1)
                if c:
                    dve.wait_ge(added, c)
                nc.vector.tensor_tensor(product.rearrange("p (b s) -> p b s", s=S), tokens,
                                        ps[:, c, 0:CT].rearrange("p (b s) -> p b s", s=S), ALU.mult).then_inc(product_ready, 1)
                dve.wait_ge(product_ready, c + 1)
                nc.vector.tensor_tensor(goal, goal, product.rearrange("p (b s) -> p b s", s=S), ALU.add).then_inc(added, 1)
    experts(chip, "e1_", "L1_ffn_experts", E_R // 2, 1, 2, True, scratch)


def mixture_2(chip):
    nc, ps, xn = chip.nc, chip.ps, chip.xn
    E, K, DFF = 8, 2, 512
    scratch = nc.dram_tensor("m2_weight_rows", (E, B * S), F32, kind="Internal").ap()
    landed, turned, rows_kept, stored = (chip.sem("m2_" + k) for k in ("landed", "turned", "rows_kept", "stored"))
    with ExitStack() as own:
        def sbuf(name, shape):
            return own.enter_context(nc.sbuf_tensor("m2_" + name, shape, F32))
        classifier = sbuf("classifier", [P, E])
        rows = sbuf("rows", [E, NP_ * P])
        router = Router(chip, own, "m2_", E, K)
        block = own.enter_context(nc.Block())

        @block.sync
        def _(sp):
            sp.dma_start(classifier[:], chip.dram["L2_ffn_Wr"]).then_inc(landed, 16)
            sp.wait_ge(rows_kept, 1)
            sp.dma_start(scratch.rearrange("e (b s) -> e b s", s=S), rows.rearrange("e (b s) -> e b s", s=SP)[:, :, 0:S]).then_inc(stored, 16)
            sp.wait_ge(stored, 16)

        @block.tensor
        def _(pe):
            pe.wait_ge(landed, 16)
            router.make_logits(pe, xn.rearrange("p b s -> p (b s)"), classifier[:])
            pe.wait_ge(router.ready, 1)
            for t in range(NP_):
                mm = nc.tensor.transpose(ps[0:E, 4 + t // 4, P * (t % 4):P * (t % 4) + P], router.weights[:, t, :], chip.ident[:])
            mm.then_inc(turned, 1)

        @block.scalar
        def _(act):
            router.exponentials(act)
            act.wait_ge(turned, 1)
            nc.scalar.copy(rows[:], ps[0:E, 4:8, :].rearrange("e k n -> e (k n)")).then_inc(rows_kept, 1)

        @block.vector
        def _(dve):
            router.choose(dve)
    experts(chip, "e2_", "L2_ffn_experts", E, DFF // P, 1, False, scratch)


def mixture_3(chip):
    nc, ps, xn = chip.nc, chip.ps, chip.xn
    E, A, K, INTER, HR, NS = 32, 16, 2, 256, P // 2, 6
    CAP = int(1.25 * B * S / E)
    ROUNDS = -(-CAP // 8)
    LAST = CAP - 8 * (ROUNDS - 1)
    T = B * S
    scratch = nc.dram_tensor("m3_weight_scratch", (E, T), F32, kind="Internal").ap()
    scratch_a = nc.dram_tensor("m3_adapter_scratch", (A, T), F32, kind="Internal").ap()
    sems = ("cleared landed tokens_turned tokens_kept stats_ready stats_turned stats_kept hidden_done hidden_kept squared rooted"
            " weights_turned weights_kept scores_ready scores_turned scores_kept chain rows_ready paired paired_kept stored")
    s = {k: chip.sem("m3_" + k) for k in sems.split()}
    with ExitStack() as own:
        def sbuf(name, shape):
            return own.enter_context(nc.sbuf_tensor("m3_" + name, shape, F32))
        r1, r1s, r2, rb = sbuf("r1", [P, P]), sbuf("r1s", [NS, P]), sbuf("r2", [P, E]), sbuf("rb", [P, 1])
        pairs = sbuf("pairs", [E, A])
        by_token, square = sbuf("by_token", [P, NP_, P]), sbuf("square", [P, NP_, P])
        stats = sbuf("stats", [P, NP_, NS])
        stats_t = sbuf("stats_t", [NS, NP_ * P])
        hidden = sbuf("hidden", [P, NP_ * P])
        routed = sbuf("routed", [P, NP_, E])
        weight_rows = sbuf("weight_rows", [E, NP_ * P])
        score_rows, top8 = sbuf("score_rows", [E, T + 8 - LAST]), sbuf("row_top8", [E, 8])
        final, adapters = sbuf("final", [E, T]), sbuf("adapters", [A, CH, CT])
        router = Router(chip, own, "m3_", E, K)
        flat = xn.rearrange("p b s -> p (b s)")
        block = own.enter_context(nc.Block())

        def real(rows):
            return rows.rearrange("e (b s) -> e b s", s=SP)[:, :, 0:S]

        @block.sync
        def _(sp):
            sp.wait_ge(s["cleared"], 4)
            for dst, name in ((r1[:, 0:HR], "r1"), (r1s[:, 0:HR], "r1_stats"), (r2[0:HR, :], "r2"), (rb[0:HR], "r1_b"), (pairs[:], "pairs")):
                sp.dma_start(dst, chip.dram["L3_ffn_" + name]).then_inc(s["landed"], 16)
            sp.wait_ge(s["rows_ready"], 1)
            sp.dma_start(scratch, final[:]).then_inc(s["stored"], 16)
            sp.wait_ge(s["paired_kept"], 4)
            sp.dma_start(scratch_a, adapters.rearrange("a c n -> a (c n)")).then_inc(s["stored"], 16)
            sp.wait_ge(s["stored"], 32)

        @block.tensor
        def _(pe):
            for t in range(NP_):
                mm = nc.tensor.transpose(ps[:, t // 4, P * (t % 4):P * (t % 4) + P], flat[:, P * t:P * t + P], chip.ident[:])
            mm.then_inc(s["tokens_turned"], 1)
            pe.wait_ge(s["stats_ready"], 1)
            for t in range(NP_):
                mm = nc.tensor.transpose(ps[0:NS, 4 + t // 4, P * (t % 4):P * (t % 4) + P], stats[:, t, :], chip.ident[:])
            mm.then_inc(s["stats_turned"], 1)
            pe.wait_ge(s["stats_kept"], 1)
            pe.wait_ge(s["landed"], 5 * 16)
            for c in range(CH):
                nc.tensor.matmul(ps[:, c, :], r1[:], flat[:, CW * c:CW * c + CW], start=True, stop=False)
                nc.tensor.matmul(ps[:, c, :], r1s[:], stats_t[:, CW * c:CW * c + CW], start=False, stop=True).then_inc(s["hidden_done"], 1)
            pe.wait_ge(s["hidden_kept"], CH)
            router.make_logits(pe, hidden, r2[:])
            pe.wait_ge(router.ready, 1)
            for t in range(NP_):
                mm = nc.tensor.transpose(ps[0:E, 4 + t // 4, P * (t % 4):P * (t % 4) + P], router.weights[:, t, :], chip.ident[:])
            mm.then_inc(s["weights_turned"], 1)
            pe.wait_ge(s["scores_ready"], 1)
            for t in range(NP_):
                mm = nc.tensor.transpose(ps[0:E, t // 4, P * (t % 4):P * (t % 4) + P], routed[:, t, :], chip.ident[:])
            mm.then_inc(s["scores_turned"], 1)
            pe.wait_ge(s["rows_ready"], 1)
            for c in range(CH):
                nc.tensor.matmul(ps[0:A, 4 + c, 0:CT], pairs[:], final[:, CT * c:CT * c + CT], start=True, stop=True).then_inc(s["paired"], 1)

        @block.scalar
        def _(act):
            act.wait_ge(s["tokens_turned"], 1)
            nc.scalar.copy(by_token[:], ps[:, 0:4, :].rearrange("p k (t d) -> p (k t) d", d=P)).then_inc(s["tokens_kept"], 1)
            act.wait_ge(s["squared"], 1)
            nc.scalar.activation(stats[:, :, 1], stats[:, :, 1], ACT.Sqrt, scale=1.0 / (P - 1)).then_inc(s["rooted"], 1)
            nc.scalar.activation(stats[:, :, 4], stats[:, :, 4], ACT.Sqrt).then_inc(s["rooted"], 1)
            act.wait_ge(s["stats_turned"], 1)
            nc.scalar.copy(stats_t[:], ps[0:NS, 4:8, :].rearrange("e k n -> e (k n)")).then_inc(s["stats_kept"], 1)
            act.wait_ge(s["landed"], 5 * 16)
            for c in range(CH):
                act.wait_ge(s["hidden_done"], c + 1)
                nc.scalar.activation(hidden[:, CW * c:CW * c + CW], ps[:, c, :], ACT.Gelu, bias=rb[:, 0:1]).then_inc(s["hidden_kept"], 1)
            router.exponentials(act)
            act.wait_ge(s["weights_turned"], 1)
            nc.scalar.copy(weight_rows[:], ps[0:E, 4:8, :].rearrange("e k n -> e (k n)")).then_inc(s["weights_kept"], 1)
            for c in range(CH):
                act.wait_ge(s["paired"], c + 1)
                nc.scalar.copy(adapters[:, c, :], ps[0:A, 4 + c, 0:CT]).then_inc(s["paired_kept"], 1)

        @block.vector
        def _(dve):
            step = Step(dve, s["chain"])
            for buffer in (r1, r1s, r2, rb):
                nc.vector.memset(buffer[:], 0.0).then_inc(s["cleared"], 1)
            dve.wait_ge(s["tokens_kept"], 1)
            nc.vector.tensor_reduce(stats[:, :, 2], by_token[:], AX_X, ALU.min)
            nc.vector.tensor_reduce(stats[:, :, 3], by_token[:], AX_X, ALU.max)
            step(nc.vector.tensor_reduce(stats[:, :, 0], by_token[:], AX_X, ALU.add))
            step(nc.vector.tensor_scalar(stats[:, :, 0], stats[:, :, 0], 1.0 / P, None, ALU.mult))
            step(nc.vector.tensor_tensor(square[:], by_token[:], by_token[:], ALU.mult))
            step(nc.vector.tensor_reduce(stats[:, :, 4], square[:], AX_X, ALU.add))
            step(nc.vector.scalar_tensor_tensor(square[:], by_token[:], -1.0, by_token[:], ALU.mult, ALU.max))
            step(nc.vector.tensor_scalar(square[:], square[:], 1e-6, None, ALU.is_lt))
            step(nc.vector.tensor_reduce(stats[:, :, 5], square[:], AX_X, ALU.add))
            step(nc.vector.tensor_scalar(stats[:, :, 5], stats[:, :, 5], 1.0 / P, None, ALU.mult))
            step(nc.vector.tensor_tensor(by_token[:], by_token[:], spread(stats[:, :, 0], 2, P), ALU.subtract))
            step(nc.vector.tensor_tensor(by_token[:], by_token[:], by_token[:], ALU.mult))
            nc.vector.tensor_reduce(stats[:, :, 1], by_token[:], AX_X, ALU.add).then_inc(s["squared"], 1)
            dve.wait_ge(s["rooted"], 2)
            nc.vector.memset(chip.credit[:, 2:3], 0.0).then_inc(s["stats_ready"], 1)
            router.choose(dve)
            step(nc.vector.tensor_scalar(routed[:], router.marked[:, :, 0:E], -1.0, None, ALU.add))
            step(nc.vector.tensor_tensor(router.scores[:], router.scores[:], router.marked[:, :, 0:E], ALU.mult))
            nc.vector.tensor_tensor(routed[:], routed[:], router.scores[:], ALU.add).then_inc(s["scores_ready"], 1)
            for n in range(8 - LAST):
                nc.vector.memset(score_rows[:, T + n:T + n + 1], spacer(n))
            dve.wait_ge(s["scores_turned"], 1)
            for c in range(CH):
                last = nc.vector.tensor_copy(score_rows[:, CT * c:CT * c + CT].rearrange("e (b s) -> e b s", s=S),
                                             ps[0:E, c, :].rearrange("e (b s) -> e b s", s=SP)[:, :, 0:S])
            step(last)
            for n in range(ROUNDS):
                step(nc.vector.max(top8[:], score_rows[:, 0:T]))
                if n == ROUNDS - 1:
                    for k in range(LAST, 8):
                        last = nc.vector.memset(top8[:, k:k + 1], spacer(k - LAST))
                    step(last)
                step(nc.vector.match_replace(score_rows[:], top8[:], score_rows[:], MARK))
            step(nc.vector.tensor_scalar(final[:], score_rows[:, 0:T], MARK, None, ALU.is_equal))
            dve.wait_ge(s["weights_kept"], 1)
            nc.vector.tensor_tensor(final.rearrange("e (b s) -> e b s", s=S), final.rearrange("e (b s) -> e b s", s=S),
                                    real(weight_rows), ALU.mult).then_inc(s["rows_ready"], 1)
    experts(chip, "e3_", "L3_ffn_experts", E, INTER // P, 1, True, scratch)
    experts(chip, "e4_", "L3_ffn_adapters", A, 1, 1, True, scratch_a)


def linear_attention_2(chip):
    nc, ps, xn, x = chip.nc, chip.ps, chip.xn, chip.x
    DH, HG, HJ = 32, 4, HX // 4
    HP = HX // 2
    sems = ("weights_landed cleared tokens_ready q_done k_done v_done q_kept k_kept v_kept products_done masked"
            " mixing_done mixing_kept mixed mixed_kept projected added")
    s = {k: chip.sem("la_" + k) for k in sems.split()}
    with ExitStack() as own:
        def sbuf(name, shape):
            return own.enter_context(nc.sbuf_tensor("la_" + name, shape, F32))
        wq, wk, wv = (sbuf(n, [P, HX * DH]) for n in ("wq", "wk", "wv"))
        wo = sbuf("wo", [P, 2, HP, P])
        quarter, left, right, decay = sbuf("quarter", [P, HG]), sbuf("left", [P, SP]), sbuf("right", [P, SP]), sbuf("decay", [P, SP])
        tokens = sbuf("tokens", [P, P])
        q_diag = sbuf("q_diag", [P, HJ, HG, P])
        k_twice = sbuf("k_twice", [P, HJ, 2, 2, SP])
        v_diag = sbuf("v_diag", [P, HX, 2, DH])
        lhs, rhs = sbuf("lhs", [P, 2, HX, SP]), sbuf("rhs", [P, 2, HX, SP])
        mixing = sbuf("mixing", [P, HX, SP])
        mixed = sbuf("mixed", [P, HP, NP_, SP])
        block = own.enter_context(nc.Block(no_gpsimd_drain=True))

        @block.sync
        def _(sp):
            for dst, name in ((wq, "Wq"), (wk, "Wk"), (wv, "Wv"), (wo, "Wo")):
                sp.dma_start(dst[:], chip.dram["L2_attn_" + name]).then_inc(s["weights_landed"], 16)
            for dst, name in ((quarter, "quarter"), (left, "la_left"), (right, "la_right"), (decay, "la_decay")):
                sp.dma_start(dst[:], chip.dram[name]).then_inc(s["weights_landed"], 16)

        @block.tensor
        def _(pe):
            pe.wait_ge(s["weights_landed"], 8 * 16)
            with pe.Fori(0, NP_) as i:
                pe.wait_ge(s["tokens_ready"], i + 1)
                pe.wait_ge(s["mixing_kept"], i + 1)
                for w, bank, done in ((wq, 0, "q_done"), (wk, 1, "k_done")):
                    for j in range(HJ):
                        mm = nc.tensor.matmul(ps[:, bank, P * j:P * j + P], w[:, P * j:P * j + P], tokens[:], start=True, stop=True)
                    mm.then_inc(s[done], 1)
                for b in range(2):
                    mm = nc.tensor.matmul(ps[SP * b:SP * b + SP, 2, :], tokens[:, SP * b:SP * b + SP], wv[:], start=True, stop=True)
                mm.then_inc(s["v_done"], 1)
                pe.wait_ge(s["q_kept"], i + 1)
                pe.wait_ge(s["k_kept"], i + 1)
                for b in range(2):
                    for j in range(HJ):
                        mm = nc.tensor.matmul(ps[:, 3 + 2 * b + j // 2, 256 * (j % 2):256 * (j % 2) + 256],
                                              k_twice[:, j, b].rearrange("p r s -> p (r s)"),
                                              q_diag[:, j, :, SP * b:SP * b + SP], start=True, stop=True)
                mm.then_inc(s["products_done"], 1)
                pe.wait_ge(s["masked"], i + 1)
                for h in range(HX):
                    for b in range(2):
                        mm = nc.tensor.matmul(ps[SP * b:SP * b + SP, h // 8, SP * (h % 8):SP * (h % 8) + SP], lhs[:, b, h, :],
                                              rhs[:, b, h, :], start=True, stop=True)
                mm.then_inc(s["mixing_done"], 1)
                pe.wait_ge(s["mixing_kept"], i + 2)
                pe.wait_ge(s["v_kept"], i + 1)
                pe.wait_ge(s["mixed_kept"], i + 1)
                for h in range(HX):
                    r = 64 * (h % 2)
                    mm = nc.tensor.matmul(ps[r:r + 64, 7, SP * (h // 2):SP * (h // 2) + SP], v_diag[:, h].rearrange("p b d -> p (b d)"),
                                          mixing[:, h, :], start=True, stop=True)
                mm.then_inc(s["mixed"], 1)
            pe.wait_ge(s["mixed_kept"], NP_ + 1)
            for n in range(4):
                b, half = n % 2, n // 2
                for j in range(HP):
                    mm = nc.tensor.matmul(ps[:, n, 0:CT], wo[:, b, j, :], mixed[:, j, 8 * half:8 * half + 8, 0:S],
                                          start=(j == 0), stop=(j == HP - 1))
                mm.then_inc(s["projected"], 1)

        @block.scalar
        def _(act):
            act.wait_ge(s["weights_landed"], 8 * 16)
            act.wait_ge(s["cleared"], 1)
            with act.Fori(0, NP_) as i:
                act.wait_ge(s["v_done"], i + 1)
                nc.scalar.copy(tokens[:], xn.rearrange("p b s -> p (b s)")[:, bass.ds(i * P, P)]).then_inc(s["tokens_ready"], 1)
                act.wait_ge(s["q_done"], i + 1)
                for g in range(HG):
                    last = nc.scalar.mul(q_diag[:, :, g, :], ps[:, 0, :].rearrange("p (j c) -> p j c", c=P), quarter[:, g:g + 1])
                last.then_inc(s["q_kept"], 1)
                act.wait_ge(s["v_done"], i + 2)
                for b in range(2):
                    r = slice(64 * b, 64 * b + 64)
                    last = nc.scalar.copy(v_diag[r, :, b, :], ps[r, 2, :].rearrange("p (h d) -> p h d", d=DH))
                last.then_inc(s["v_kept"], 1)
                act.wait_ge(s["mixed"], i + 1)
                nc.scalar.copy(mixed[:, :, bass.ds(i, 1), :].rearrange("p j n s -> p j (n s)"),
                               ps[:, 7, :].rearrange("p (j s) -> p j s", s=SP)).then_inc(s["mixed_kept"], 1)

        @block.vector
        def _(dve):
            nc.vector.memset(v_diag[:], 0.0).then_inc(s["cleared"], 1)
            for n, name in enumerate(("v_done", "mixing_kept", "mixed_kept")):
                nc.vector.memset(chip.credit[:, n:n + 1], 0.0).then_inc(s[name], 1)
            dve.wait_ge(s["weights_landed"], 8 * 16)
            with dve.Fori(0, NP_) as i:
                dve.wait_ge(s["k_done"], i + 1)
                for r in range(2):
                    last = nc.vector.tensor_copy(k_twice[:, :, :, r, :], ps[:, 1, :].rearrange("p (j b s) -> p j b s", j=HJ, b=2))
                last.then_inc(s["k_kept"], 1)
                dve.wait_ge(s["products_done"], i + 1)
                products = ps[:, 3:7, :].rearrange("p k (h s) -> p (k h) s", s=SP)
                nc.vector.tensor_tensor(lhs.rearrange("p b h s -> p (b h) s"), products, spread(left[:], 1, 2 * HX), ALU.mult)
                nc.vector.tensor_tensor(rhs.rearrange("p b h s -> p (b h) s"), products, spread(right[:], 1, 2 * HX), ALU.mult).then_inc(s["masked"], 1)
                dve.wait_ge(s["mixing_done"], i + 1)
                nc.vector.tensor_tensor(mixing[:], ps[:, 0:2, :].rearrange("p k (h s) -> p (k h) s", s=SP), spread(decay[:], 1, HX),
                                        ALU.mult).then_inc(s["mixing_kept"], 1)
            for n in range(4):
                b, half = n % 2, n // 2
                goal = x.rearrange("p (n b) s -> p n b s", b=2)[:, 8 * half:8 * half + 8, b, 0:S]
                dve.wait_ge(s["projected"], n + 1)
                nc.vector.tensor_tensor(goal, goal, ps[:, n, 0:CT].rearrange("p (n s) -> p n s", s=S), ALU.add).then_inc(s["added"], 1)


def rotary_attention(chip, tag, src, res, latent):
    nc, ps = chip.nc, chip.ps
    KV, REP = 4, HX // 4
    LAT = 32
    U = 2 * CH
    SCALE = DX ** -0.5
    sems = ("cleared landed spread latent_done latent_kept made kept rotated turned_cos roped squared power log root normed"
            " pair_ready diag_ready scores_done shifted exp_done turned turned_kept v_done v_kept mixed scaled flipped flipped_kept"
            " projected added chain")
    s = {k: chip.sem(tag + k) for k in sems.split()}
    with ExitStack() as own:
        def sbuf(name, shape):
            return own.enter_context(nc.sbuf_tensor(tag + name, shape, F32))
        wq, wo, rot, mean8 = (sbuf(n, [P, P]) for n in ("wq", "wo", "rot", "mean8"))
        wdown = sbuf("wdown", [P, P])
        wkv = sbuf("wkv", [P, 2, KV * DX])
        wk, wv = sbuf("wk", [P, P]), sbuf("wv", [P, 2, P])
        cos, sin, mask, own_head = sbuf("cos", [P, S]), sbuf("sin", [P, S]), sbuf("mask", [P, S]), sbuf("own_head", [P, HX])
        low = sbuf("low", [P, B, SP])
        qn, kn = sbuf("qn", [P, B, SP]), sbuf("kn", [P, B, SP])
        raw = [sbuf("raw%d" % n, [P, CT]) for n in range(4)]
        work = [sbuf("work%d" % n, [P, CT]) for n in range(4)]
        source = low if latent else src
        q_pair, v_pair = sbuf("q_pair", [P, P]), sbuf("v_pair", [P, P])
        k_diag = sbuf("k_diag", [P, 2, HX, S])
        probs, probs_t = sbuf("probs", [P, HX, SP]), sbuf("probs_t", [P, HX // 2, P])
        top, total, inverse = (sbuf(n, [P, HX]) for n in ("top", "total", "inverse"))
        values = sbuf("values", [P, 2, P])
        mix = sbuf("mix", [P, P])
        mix_t = sbuf("mix_t", [P, B, SP])
        first = chip.sem(tag + "weights_ready")
        loads = [(wq[:], "wq"), (wo[:], "wo")]
        if latent:
            loads += [(wdown[:, 0:LAT], "kv_down"), (wkv[0:LAT, 0], "k_up"), (wkv[0:LAT, 1], "v_up")]
        else:
            loads += [(wkv[:, 0], "wk"), (wkv[:, 1], "wv")]
        consts = ((rot, "rotate"), (mean8, "mean8"), (cos, tag + "cos"), (sin, tag + "sin"), (mask, tag + "mask"), (own_head, "own_head"))
        n_loads = len(loads) + len(consts)

        def unit(n):
            c = n % CH
            return c, n < CH

        with nc.Block(no_gpsimd_drain=True) as block:
            @block.sync
            def _(sp):
                sp.wait_ge(s["cleared"], 2)
                for dst, name in loads:
                    sp.dma_start(dst, chip.dram["L3_attn_" + tag + name]).then_inc(s["landed"], 16)
                for dst, name in consts:
                    sp.dma_start(dst[:], chip.dram[name]).then_inc(s["landed"], 16)

            @block.tensor
            def _(pe):
                pe.wait_ge(s["landed"], 16 * n_loads)
                if latent:
                    for c in range(CH):
                        nc.tensor.matmul(ps[:, 4 + c, 0:CT], wdown[:], src[:, CB * c:CB * c + CB, 0:S], start=True, stop=True).then_inc(s["latent_done"], 1)
                    pe.wait_ge(s["latent_kept"], CH)
                pe.wait_ge(first, 1)

                def make(n):
                    c, queries = unit(n)
                    t = (src if queries else source)[:, CB * c:CB * c + CB, 0:S]
                    if n >= 4:
                        pe.wait_ge(s["log"], n - 3)
                    nc.tensor.matmul(ps[:, n % 4, 0:CT], (wq if queries else wk)[:], t, start=True, stop=True).then_inc(s["made"], 1)

                def rotate(n):
                    pe.wait_ge(s["kept"], n + 1)
                    nc.tensor.matmul(ps[:, 4 + n % 4, 0:CT], rot[:], raw[n % 4][:], start=True, stop=True).then_inc(s["rotated"], 1)

                def power(n):
                    pe.wait_ge(s["squared"], n + 1)
                    nc.tensor.matmul(ps[:, n % 4, 0:CT], mean8[:], work[n % 4][:], start=True, stop=True).then_inc(s["power"], 1)

                for half in range(2):
                    for n in range(4 * half, 4 * half + 4):
                        make(n)
                    for n in range(4 * half, 4 * half + 4):
                        rotate(n)
                    for n in range(4 * half, 4 * half + 4):
                        power(n)

            @block.scalar
            def _(act):
                if latent:
                    for c in range(CH):
                        act.wait_ge(s["latent_done"], c + 1)
                        nc.scalar.copy(low[:, CB * c:CB * c + CB, 0:S], ps[:, 4 + c, 0:CT].rearrange("p (b s) -> p b s", s=S)).then_inc(s["latent_kept"], 1)
                for half in range(2):
                    units = range(4 * half, 4 * half + 4)
                    for n in units:
                        act.wait_ge(s["made"], n + 1)
                        if n >= 4:
                            act.wait_ge(s["normed"], n - 3)
                        nc.scalar.copy(raw[n % 4][:], ps[:, n % 4, 0:CT]).then_inc(s["kept"], 1)
                    for n in units:
                        act.wait_ge(s["roped"], n + 1)
                        nc.scalar.activation(work[n % 4][:], raw[n % 4][:], ACT.Square).then_inc(s["squared"], 1)
                    for n in units:
                        act.wait_ge(s["power"], n + 1)
                        nc.scalar.activation(work[n % 4][:], ps[:, n % 4, 0:CT], ACT.Ln, bias=chip.eps[:, 1:2]).then_inc(s["log"], 1)
                        act.wait_ge(s["log"], n + 1)
                        nc.scalar.activation(work[n % 4][:], work[n % 4][:], ACT.Exp, scale=-0.5).then_inc(s["root"], 1)

            @block.vector
            def _(dve):
                step = Step(dve, s["chain"])
                nc.vector.memset(low[:], 0.0)
                nc.vector.memset(qn[:], 0.0)
                nc.vector.memset(kn[:], 0.0)
                nc.vector.memset(probs[:], 0.0)
                nc.vector.memset(wdown[:], 0.0).then_inc(s["cleared"], 1)
                nc.vector.memset(wkv[:], 0.0).then_inc(s["cleared"], 1)
                step(nc.vector.memset(wv[:], 0.0))
                dve.wait_ge(s["landed"], 16 * n_loads)
                for kv in range(KV):
                    nc.vector.tensor_copy(wk[:, REP * DX * kv:REP * DX * (kv + 1)].rearrange("p (r d) -> p r d", d=DX),
                                          spread(wkv[:, 0, DX * kv:DX * kv + DX], 1, REP))
                    for odd in range(2):
                        v4 = wv[:, odd, REP * DX * kv:REP * DX * (kv + 1)].rearrange("p (r d) -> p r d", d=DX)
                        last = nc.vector.tensor_copy(v4[:, odd::2, :], spread(wkv[:, 1, DX * kv:DX * kv + DX], 1, REP // 2))
                last.then_inc(first, 1)
                for half in range(2):
                    units = range(4 * half, 4 * half + 4)
                    for n in units:
                        r3, w3 = (v[n % 4].rearrange("p (b s) -> p b s", s=S) for v in (raw, work))
                        dve.wait_ge(s["rotated"], n + 1)
                        step(nc.vector.tensor_tensor(w3, ps[:, 4 + n % 4, 0:CT].rearrange("p (b s) -> p b s", s=S), spread(sin[:], 1, CB), ALU.mult))
                        step(nc.vector.tensor_tensor(r3, r3, spread(cos[:], 1, CB), ALU.mult))
                        nc.vector.tensor_tensor(r3, r3, w3, ALU.add).then_inc(s["roped"], 1)
                    for n in units:
                        c, queries = unit(n)
                        r3, w3 = (v[n % 4].rearrange("p (b s) -> p b s", s=S) for v in (raw, work))
                        dve.wait_ge(s["root"], n + 1)
                        nc.vector.tensor_tensor((qn if queries else kn)[:, CB * c:CB * c + CB, 0:S], r3, w3, ALU.mult).then_inc(s["normed"], 1)

        with nc.Block(no_gpsimd_drain=True) as block:
            @block.tensor
            def _(pe):
                with pe.Fori(0, NP_) as i:
                    pe.wait_ge(s["flipped_kept"], i + 1)
                    pe.wait_ge(s["pair_ready"], 2 * i + 2)
                    for b in range(2):
                        for odd in range(2):
                            mm = nc.tensor.matmul(ps[64 * odd:64 * odd + 64, 4, P * b:P * b + P], v_pair[:, SP * b:SP * b + SP], wv[:, odd, :],
                                                  start=True, stop=True)
                    mm.then_inc(s["v_done"], 1)
                    pe.wait_ge(s["diag_ready"], i + 1)
                    for half in range(2):
                        for b in range(2):
                            mm = nc.tensor.matmul(ps[SP * b:SP * b + SP, half, :].rearrange("p (h s) -> p h s", s=SP)[:, :, 0:S],
                                                  q_pair[:, SP * b:SP * b + SP], k_diag[:, b, 8 * half:8 * half + 8, :], start=True, stop=True)
                    mm.then_inc(s["scores_done"], 1)
                    pe.wait_ge(s["exp_done"], i + 1)
                    for j in range(HX // 2):
                        mm = nc.tensor.transpose(ps[:, 2 + j // 4, P * (j % 4):P * (j % 4) + P],
                                                 probs[:, 2 * j:2 * j + 2, :].rearrange("p h s -> p (h s)"), chip.ident[:])
                    mm.then_inc(s["turned"], 1)
                    pe.wait_ge(s["turned_kept"], i + 1)
                    pe.wait_ge(s["v_kept"], i + 1)
                    for j in range(HX // 2):
                        for b in range(2):
                            mm = nc.tensor.matmul(ps[SP * b:SP * b + SP, 5, 16 * j:16 * j + 16], probs_t[:, j, SP * b:SP * b + SP],
                                                  values[:, b, 16 * j:16 * j + 16], start=True, stop=True)
                    mm.then_inc(s["mixed"], 1)
                    pe.wait_ge(s["scaled"], i + 1)
                    nc.tensor.transpose(ps[:, 4, 0:P], mix[:], chip.ident[:]).then_inc(s["flipped"], 1)
                pe.wait_ge(s["flipped_kept"], NP_ + 1)
                for c in range(CH):
                    nc.tensor.matmul(ps[:, c, 0:CT], wo[:], mix_t[:, CB * c:CB * c + CB, 0:S], start=True, stop=True).then_inc(s["projected"], 1)

            @block.scalar
            def _(act):
                with act.Fori(0, NP_) as i:
                    act.wait_ge(s["scores_done"], i + 1)
                    for dst, v in ((q_pair, qn), (v_pair, source)):
                        nc.scalar.copy(dst[:], v.rearrange("p b s -> p (b s)")[:, bass.ds(i * P, P)]).then_inc(s["pair_ready"], 1)
                    act.wait_ge(s["v_done"], i + 1)
                    nc.scalar.copy(values[:], ps[:, 4, 0:2 * P].rearrange("p (b d) -> p b d", d=P)).then_inc(s["v_kept"], 1)
                    act.wait_ge(s["shifted"], i + 1)
                    nc.scalar.activation(probs[:, :, 0:S], probs[:, :, 0:S], ACT.Exp).then_inc(s["exp_done"], 1)
                    act.wait_ge(s["turned"], i + 1)
                    nc.scalar.copy(probs_t[:], ps[:, 2:4, :].rearrange("p k (j c) -> p (k j) c", c=P)).then_inc(s["turned_kept"], 1)
                    act.wait_ge(s["flipped"], i + 1)
                    nc.scalar.copy(mix_t.rearrange("p b s -> p (b s)")[:, bass.ds(i * P, P)], ps[:, 4, 0:P]).then_inc(s["flipped_kept"], 1)

            @block.vector
            def _(dve):
                for n, name in enumerate(("scores_done", "flipped_kept")):
                    nc.vector.memset(chip.credit[:, n:n + 1], 0.0).then_inc(s[name], 1)
                done = s["chain"]
                base = 1 + 2 * U
                with dve.Fori(0, NP_) as i:
                    dve.wait_ge(s["scores_done"], i + 1)
                    for b in range(2):
                        last = nc.vector.tensor_tensor(k_diag[:, b], spread(kn[:, bass.ds(2 * i + b, 1), 0:S].rearrange("p b s -> p (b s)"), 1, HX),
                                                       spread(own_head[:], 2, S), ALU.mult)
                    last.then_inc(s["diag_ready"], 1)
                    dve.wait_ge(s["scores_done"], i + 2)
                    scores = ps[:, 0:2, :].rearrange("p k (h s) -> p (k h) s", s=SP)[:, :, 0:S]
                    step = Step(dve, done, 4 * i + base)
                    step(nc.vector.scalar_tensor_tensor(probs[:, :, 0:S], scores, SCALE, spread(mask[:], 1, HX), ALU.mult, ALU.add))
                    step(nc.vector.tensor_reduce(top[:], probs[:, :, 0:S], AX_X, ALU.max))
                    nc.vector.tensor_tensor(probs[:, :, 0:S], probs[:, :, 0:S], spread(top[:], 2, S), ALU.subtract).then_inc(s["shifted"], 1)
                    dve.wait_ge(s["exp_done"], i + 1)
                    step(nc.vector.tensor_reduce(total[:], probs[:, :, 0:S], AX_X, ALU.add))
                    step(nc.vector.reciprocal(inverse[:], total[:]))
                    dve.wait_ge(s["mixed"], i + 1)
                    nc.vector.tensor_tensor(mix.rearrange("p (h d) -> p h d", d=DX), ps[:, 5, 0:P].rearrange("p (h d) -> p h d", d=DX),
                                            spread(inverse[:], 2, DX), ALU.mult).then_inc(s["scaled"], 1)
                for c in range(CH):
                    goal = res[:, CB * c:CB * c + CB, 0:S]
                    dve.wait_ge(s["projected"], c + 1)
                    nc.vector.tensor_tensor(goal, goal, ps[:, c, 0:CT].rearrange("p (b s) -> p b s", s=S), ALU.add).then_inc(s["added"], 1)


def rotary_attention_3(chip):
    nc, x, xn = chip.nc, chip.x, chip.xn
    landed, added = chip.sem("ra_norms_landed"), chip.sem("ra_added")
    with ExitStack() as own:
        norms = own.enter_context(nc.sbuf_tensor("ra_norms", [P, 2], F32))
        normed = own.enter_context(nc.sbuf_tensor("ra_normed", [P, B, SP], F32))
        with nc.Block(no_gpsimd_drain=True) as block:
            @block.sync
            def _(sp):
                sp.dma_start(norms[:], chip.dram["L3_attn_norms"]).then_inc(landed, 16)
                sp.wait_ge(landed, 16)
        normalise(chip, xn, normed, False, norms[:, 0:1])
        rotary_attention(chip, "g_", normed, xn, True)
        normalise(chip, xn, normed, False, norms[:, 1:2])
        rotary_attention(chip, "l_", normed, xn, False)
        with nc.Block(no_gpsimd_drain=True) as block:
            @block.vector
            def _(dve):
                nc.vector.tensor_tensor(x[:, :, 0:S], x[:, :, 0:S], xn[:, :, 0:S], ALU.add).then_inc(added, 1)


STAGES = [self_attention_0, context_mixing, coupled_twist, gated_recurrence, lambda chip: cross_attention(chip, 1, DX ** -0.5),
          mixture_1, linear_attention_2, lambda chip: cross_attention(chip, 2, P ** -0.5), mixture_2,
          rotary_attention_3, lambda chip: cross_attention(chip, 3, DX ** -0.5), mixture_3]


def more_layouts(a, d):
    ctx = a["ctx_1024"]
    d["ctx_t"] = ctx.transpose(0, 2, 1)
    d["ctx_n"] = ctx.reshape(B, NC_, KC, P).transpose(0, 2, 1, 3)
    for k in ("w1", "w2", "w3", "w4"):
        d["L0_ffn_cn_" + k] = a["L0_ffn_cn_" + k]
    for k in ("w1", "w2", "w3"):
        d["L0_ffn_gc_" + k] = a["L0_ffn_gc_" + k]
    for k in ("cn_b1", "cn_b2", "cn_b3", "cn_b4", "gc_b1", "gc_b2", "gc_b3", "adaptive_range"):
        d["L0_ffn_" + k] = a["L0_ffn_" + k].reshape(-1, 1)
    twist = np.zeros((P, P), np.float32)
    for m in range(P):
        twist[(m + 64) % P, m] = (1.0, -1.0, -1.0, 1.0)[m // 32]
    d["twist"] = twist
    for k in ("Wr_w", "Wi_w", "out_w"):
        d["L1_attn_" + k] = a["L1_attn_" + k].T
    d["L1_attn_conv_weight"] = a["L1_attn_conv_weight"][:, 0, :]
    for k in ("conv_bias", "Wr_b", "Wi_b", "log_a", "norm_w"):
        d["L1_attn_" + k] = a["L1_attn_" + k].reshape(-1, 1)
    for n in (1, 2, 3):
        for k in ("Wq", "Wk", "Wv", "Wo"):
            w = a["L%d_xattn_%s" % (n, k)]
            d["L%d_xattn_%s" % (n, k)] = w if n == 1 or (n == 2 and k == "Wo") else w.transpose(1, 0, 2).reshape(P, P) if n == 2 else w.T
        for k in ("bq", "bk", "bv", "bo"):
            d["L%d_xattn_%s" % (n, k)] = a["L%d_xattn_%s" % (n, k)].reshape(-1, 1)
    head_of_feature = np.arange(P) // DX
    d["own_head"] = (head_of_feature[:, None] == np.arange(HX)).astype(np.float32)
    row = np.arange(XT * P).reshape(XT, P)
    window, fold = np.zeros((P, XT, WIN), np.float32), np.zeros((P, XT, S), np.float32)
    for t in range(XT):
        for r in range(P):
            head, query = divmod(int(row[t, r]), S)
            k0 = DX * (head - HEAD_OF[t])
            window[r, t, k0:k0 + DX] = 1.0
            fold[r, t, query] = 1.0
    d["window"], d["fold"] = window, fold


    def blocks(*parts):
        return np.stack(parts, axis=3)

    w = a["L1_ffn_gate_up_proj"][:32].reshape(16, 2, 2, 64, P)
    gate, up = (w[:, :, k].reshape(16, 1, P, P).transpose(0, 3, 1, 2) for k in range(2))
    down = a["L1_ffn_down_proj"].reshape(16, 2, P, 64).transpose(0, 1, 3, 2).reshape(16, P, 1, P)
    d["L1_ffn_experts"] = blocks(gate, up, down)
    d["L1_ffn_classifier_weight"] = a["L1_ffn_classifier_weight"].T
    d["L1_ffn_e_score_correction_bias"] = a["L1_ffn_e_score_correction_bias"].reshape(1, -1)
    d["L2_ffn_Wr"] = a["L2_ffn_Wr"].T
    d["L2_ffn_experts"] = blocks(a["L2_ffn_W1"].reshape(8, 4, P, P).transpose(0, 3, 1, 2),
                                 a["L2_ffn_W2"].reshape(8, P, 4, P).transpose(0, 3, 2, 1))
    for n, groups, subs in (("", 32, 2), ("a", 16, 1)):
        w = a["L3_ffn_a_up" if n else "L3_ffn_w_up"].reshape(groups, 2, subs, P, P)
        gate, up = (w[:, k].transpose(0, 3, 1, 2) for k in range(2))
        down = a["L3_ffn_a_down" if n else "L3_ffn_w_down"].reshape(groups, P, subs, P).transpose(0, 3, 2, 1)
        d["L3_ffn_adapters" if n else "L3_ffn_experts"] = blocks(gate, up, down)
    d["L3_ffn_r1"] = a["L3_ffn_r1_w"][:, :P].T
    d["L3_ffn_r1_stats"] = a["L3_ffn_r1_w"][:, P:].T
    d["L3_ffn_r2"] = a["L3_ffn_r2_w"].T
    d["L3_ffn_r1_b"] = a["L3_ffn_r1_b"].reshape(-1, 1)
    d["L3_ffn_pairs"] = np.float32(0.05) * (np.arange(32)[:, None] // 2 == np.arange(16)).astype(np.float32)
    for k in ("Wq", "Wk", "Wv"):
        d["L2_attn_" + k] = a["L2_attn_" + k]
    wo = a["L2_attn_Wo"].reshape(8, 2, 32, P)
    both = np.zeros((2, 8, 2, 2, 32, P), np.float32)
    for b in range(2):
        both[b, :, :, b] = wo
    d["L2_attn_Wo"] = both.reshape(2, 8, P, P).transpose(2, 0, 1, 3)
    d["quarter"] = (np.arange(P)[:, None] // 32 == np.arange(4)).astype(np.float32)
    r, t = np.arange(SP)[:, None], np.arange(SP)[None, :]
    real = (r < S) & (t < S)
    decay = np.where((r <= t) & real, 0.99 ** np.maximum(t - r, 0), 0.0).astype(np.float32)
    d["la_left"] = np.concatenate([real.astype(np.float32), ((r > t) & real).astype(np.float32)])
    d["la_right"] = np.concatenate([decay, -((r <= t) & real).astype(np.float32)])
    d["la_decay"] = np.concatenate([decay, decay])
    d["L3_attn_norms"] = np.stack([a["L3_attn_norm1_w"], a["L3_attn_norm2_w"]], axis=1)
    for k in ("wq", "wo"):
        for g in "gl":
            d["L3_attn_%s_%s" % (g, k)] = a["L3_attn_%s_%s" % (g, k)]
    for k in ("g_kv_down", "g_k_up", "g_v_up", "l_wk", "l_wv"):
        d["L3_attn_" + k] = a["L3_attn_" + k]
    rotate = np.zeros((P, P), np.float32)
    even = np.arange(0, P, 2)
    rotate[even + 1, even], rotate[even, even + 1] = -1.0, 1.0
    d["rotate"] = rotate
    d["mean8"] = (head_of_feature[:, None] == head_of_feature[None, :]).astype(np.float32) / np.float32(DX)
    for g, base in (("g_", 1e6), ("l_", 1e4)):
        inv = (1.0 / np.float32(base) ** (np.arange(0, DX, 2, dtype=np.float32) / np.float32(DX))).astype(np.float32)
        angle = (np.arange(S, dtype=np.float32)[None, :] * inv[:, None]).astype(np.float32)
        angle = angle[(np.arange(P) % DX) // 2]
        d[g + "cos"], d[g + "sin"] = np.cos(angle).astype(np.float32), np.sin(angle).astype(np.float32)
        query, key = np.arange(P)[:, None] % SP, np.arange(S)[None, :]
        seen = (query >= key) & (query - key < (32 if g == "l_" else S))
        d[g + "mask"] = np.where(seen | (query >= S), 0.0, -1e30).astype(np.float32)


def decoder(nc, dram, out):
    with ExitStack() as ctx:
        chip = Chip(nc, ctx, dram)
        load_stage(chip, out)
        for stage in STAGES:
            normalise(chip, chip.x, chip.xn, True)
            stage(chip)
            chip.end_stage()
        store_stage(chip, chip.x, out)


def layouts(inputs):
    a = {k: np.asarray(v) for k, v in inputs.items()}
    d = {"x": a["x"].transpose(2, 0, 1)}
    D = P

    def by_feature(w):
        return w.reshape(-1, D).T

    def column(v):
        return v.reshape(-1, 1)

    d["L0_attn_W_Q"] = by_feature(a["L0_attn_W_Q"])
    d["L0_attn_W_K"] = by_feature(a["L0_attn_W_K"])
    v = a["L0_attn_W_V"]
    d["L0_attn_W_V"] = np.concatenate([by_feature(v[0::2]), by_feature(v[1::2])], axis=1)
    d["L0_attn_W_O"] = a["L0_attn_W_O"].transpose(0, 2, 1).reshape(8, D, D).transpose(1, 0, 2)
    for k in "QKV":
        d["L0_attn_b_" + k] = a["L0_attn_b_" + k].reshape(8, D).T
    d["L0_attn_b_O"] = column(a["L0_attn_b_O"])
    more_layouts(a, d)
    return {k: np.ascontiguousarray(v) for k, v in d.items()}


def kernel(**inputs):
    import concourse.bacc as _bacc
    from concourse.bass_utils import run_bass_kernel_spmd as _run

    nc = _bacc.Bacc("TRN2", target_bir_lowering=False, num_devices=1)
    arrays, dram = {}, {}
    for name, array in layouts(inputs).items():
        arrays["in_" + name] = array
        dram[name] = nc.dram_tensor("in_" + name, array.shape, F32, kind="ExternalInput").ap()
    out = nc.dram_tensor("out_x", (P, B, S), F32, kind="ExternalOutput").ap()
    decoder(nc, dram, out)
    result = _run(nc, [arrays], core_ids=[0])
    return result.results[0]["out_x"].transpose(1, 2, 0)
```

```python
from contextlib import ExitStack

import numpy as np
import concourse.bass as bass
from concourse import mybir

ALU = mybir.AluOpType
ACT = mybir.ActivationFunctionType
F32 = mybir.dt.float32
AX_X = mybir.AxisListType.X

P = 128
B = 32
S = 56
SP = 64
NP_ = B // 2
NK = 1500
KC = 125
NC_ = NK // KC
KB = 500
NB_ = NK // KB
CH = 4
CB = B // CH
CT = CB * S
CW = CB * SP
HX = 16
DX = P // HX
LN_EPS = 1e-5
RMS_EPS = 1e-6


class Step:

    def __init__(self, engine, semaphore, done=0):
        self.engine, self.semaphore, self.done, self.n = engine, semaphore, done, 0

    def __call__(self, instruction):
        self.n += 1
        instruction.then_inc(self.semaphore, 1)
        self.engine.wait_ge(self.semaphore, self.done + self.n)


class Chip:

    def __init__(self, nc, ctx, dram):
        self.nc, self.ctx, self.dram = nc, ctx, dram
        self.x = self.sbuf("x", [P, B, SP])
        self.xn_lead = self.sbuf("xn_lead", [P, SP + B * SP])
        self.xn = self.xn_lead[:, SP:].rearrange("p (b s) -> p b s", s=SP)
        self.ps = ctx.enter_context(nc.psum_tensor("ps", [P, 8, 512], F32))
        self.ones = self.sbuf("ones", [P, P])
        self.mean = self.sbuf("mean", [P, P])
        self.ident = self.sbuf("ident", [P, P])
        self.credit = self.sbuf("credit", [P, 4])
        self.eps = self.sbuf("eps", [P, 2])
        self.norm_calls = self.centre_calls = 0
        self.stage_sems = []
        self.norm_sems = {k: ctx.enter_context(nc.semaphore("norm_" + k)) for k in ("mean", "centred", "squared", "power", "log", "inverse", "out")}

    def sbuf(self, name, shape, dtype=F32):
        return self.ctx.enter_context(self.nc.sbuf_tensor(name, shape, dtype))

    def sem(self, name):
        semaphore = self.nc.alloc_semaphore(name=name)
        self.stage_sems.append(semaphore)
        return semaphore

    def end_stage(self):
        nc = self.nc
        with nc.Block(no_gpsimd_drain=True) as block:
            @block.gpsimd
            def _(pool):
                for semaphore in self.stage_sems:
                    pool.sem_clear(semaphore)
        for semaphore in self.stage_sems:
            nc.release_semaphore(semaphore)
        self.stage_sems = []


def spread(ap, axis, n):
    a = ap.unsqueeze(axis)
    shape = list(a.shape)
    shape[axis] = n
    return a.to_broadcast(shape)


def load_stage(chip, out):
    nc = chip.nc
    x_landed = chip.sem("x_landed")
    cleared = chip.sem("cleared")
    ident_cleared = chip.sem("ident_cleared")
    with nc.Block() as block:
        @block.sync
        def _(sp):
            sp.wait_ge(cleared, 1)
            for g in range(4):
                sp.dma_start(chip.x[32 * g:32 * g + 32, :, 0:S], chip.dram["x"][32 * g:32 * g + 32]).then_inc(x_landed, 16)
            sp.wait_ge(x_landed, 64)

        @block.vector
        def _(dve):
            nc.vector.memset(chip.x[:], 0.0).then_inc(cleared, 1)
            nc.vector.memset(chip.xn_lead[:], 0.0)
            nc.vector.memset(chip.ones[:], 1.0)
            nc.vector.memset(chip.mean[:], 1.0 / P)
            nc.vector.memset(chip.eps[:, 0:1], LN_EPS)
            nc.vector.memset(chip.eps[:, 1:2], RMS_EPS)

        @block.gpsimd
        def _(pool):
            nc.gpsimd.memset(chip.ident[:], 0.0).then_inc(ident_cleared, 1)
            pool.wait_ge(ident_cleared, 1)
            nc.gpsimd.affine_select(out=chip.ident[:], in_=chip.ident[:], compare_op=ALU.not_equal, fill=1.0,
                                    base=0, pattern=[[-1, P]], channel_multiplier=1).then_inc(ident_cleared, 1)


def store_stage(chip, src, out):
    nc = chip.nc
    stored = chip.sem("stored")
    with nc.Block() as block:
        @block.sync
        def _(sp):
            for g in range(4):
                sp.dma_start(out[32 * g:32 * g + 32], src[32 * g:32 * g + 32, :, 0:S]).then_inc(stored, 16)
            sp.wait_ge(stored, 64)


def normalise(chip, src, dst, centre, weight=None):
    nc, ps = chip.nc, chip.ps
    s = chip.norm_sems
    done = CH * chip.norm_calls
    done_centred = CH * chip.centre_calls
    tag = str(chip.norm_calls)
    which = 0 if centre else 1
    chip.norm_calls += 1
    chip.centre_calls += centre
    with ExitStack() as own, nc.Block(no_gpsimd_drain=True) as block:
        sq = own.enter_context(nc.sbuf_tensor("norm_sq" + tag, [P, CH, CW], F32))
        root = own.enter_context(nc.sbuf_tensor("norm_root" + tag, [P, CH, CW], F32))
        flat = src.rearrange("p (c b) s -> p c (b s)", c=CH)
        goal = dst.rearrange("p (c b) s -> p c (b s)", c=CH)
        centred = goal if centre else flat

        @block.tensor
        def _(pe):
            for c in range(CH):
                if centre:
                    nc.tensor.matmul(ps[:, c, :], chip.mean[:], flat[:, c, :], start=True, stop=True).then_inc(s["mean"], 1)
            for c in range(CH):
                pe.wait_ge(s["squared"], done + c + 1)
                nc.tensor.matmul(ps[:, 4 + c, :], chip.mean[:], sq[:, c, :], start=True, stop=True).then_inc(s["power"], 1)

        @block.scalar
        def _(act):
            for c in range(CH):
                if centre:
                    act.wait_ge(s["centred"], done_centred + c + 1)
                nc.scalar.activation(sq[:, c, :], centred[:, c, :], ACT.Square).then_inc(s["squared"], 1)
            for c in range(CH):
                act.wait_ge(s["power"], done + c + 1)
                nc.scalar.activation(root[:, c, :], ps[:, 4 + c, :], ACT.Ln, bias=chip.eps[:, which:which + 1]).then_inc(s["log"], 1)
            for c in range(CH):
                act.wait_ge(s["log"], done + c + 1)
                nc.scalar.activation(root[:, c, :], root[:, c, :], ACT.Exp, scale=-0.5).then_inc(s["inverse"], 1)

        @block.vector
        def _(dve):
            for c in range(CH):
                if centre:
                    dve.wait_ge(s["mean"], done_centred + c + 1)
                    nc.vector.tensor_tensor(goal[:, c, :], flat[:, c, :], ps[:, c, :], ALU.subtract).then_inc(s["centred"], 1)
            for c in range(CH):
                if centre:
                    dve.wait_ge(s["centred"], done_centred + c + 1)
                dve.wait_ge(s["inverse"], done + c + 1)
                if weight is None:
                    nc.vector.tensor_tensor(goal[:, c, :], centred[:, c, :], root[:, c, :], ALU.mult).then_inc(s["out"], 1)
                else:
                    nc.vector.scalar_tensor_tensor(goal[:, c, :], centred[:, c, :], weight, root[:, c, :], ALU.mult, ALU.mult).then_inc(s["out"], 1)


def self_attention_0(chip):
    nc, ps, xn, x = chip.nc, chip.ps, chip.xn, chip.x
    DH = 64
    HJ = HX // 2
    landed = chip.sem("a0_weights_landed")
    pads_clear = chip.sem("a0_pads_clear")
    tokens_ready = chip.sem("a0_tokens_ready")
    q_done, k_done, v_done = (chip.sem("a0_%s_done" % k) for k in "qkv")
    q_kept, k_kept, v_kept = (chip.sem("a0_%s_kept" % k) for k in "qkv")
    scores_done, shifted, exp_done = (chip.sem("a0_" + k) for k in ("scores_done", "shifted", "exp_done"))
    probs_ready, turned, probs_kept = (chip.sem("a0_" + k) for k in ("probs_ready", "turned", "probs_kept"))
    mixed, mixed_kept, projected, added = (chip.sem("a0_" + k) for k in ("mixed", "mixed_kept", "projected", "added"))
    dve_chain = chip.sem("a0_dve_chain")
    with ExitStack() as own:
        def sbuf(name, shape):
            return own.enter_context(nc.sbuf_tensor("a0_" + name, shape, F32))
        wq, wk, wv = (sbuf(n, [P, HX * DH]) for n in ("wq", "wk", "wv"))
        wo = sbuf("wo", [P, HJ, P])
        bq, bk, bv = (sbuf(n, [P, HJ]) for n in ("bq", "bk", "bv"))
        bo = sbuf("bo", [P, 1])
        tokens = sbuf("tokens", [P, P])
        q = sbuf("q", [P, HJ, P])
        k = sbuf("k", [P, HJ, 2, 2, SP])
        v = sbuf("v", [P, 2, HJ, 2, DH])
        probs = sbuf("probs", [P, HX, SP])
        probs_t = sbuf("probs_t", [P, HJ, P])
        mix = sbuf("mix", [P, HJ, 2, SP])
        top, total, inverse = (sbuf(n, [P, HX]) for n in ("top", "total", "inverse"))
        scores = ps[:, 6:8, :].rearrange("p k (h s) -> p (k h) s", s=SP)[:, :, 0:S]
        block = own.enter_context(nc.Block(no_gpsimd_drain=True))

        @block.sync
        def _(sp):
            for dst, name in ((wq, "L0_attn_W_Q"), (wk, "L0_attn_W_K"), (wv, "L0_attn_W_V"), (wo, "L0_attn_W_O"),
                              (bq, "L0_attn_b_Q"), (bk, "L0_attn_b_K"), (bv, "L0_attn_b_V"), (bo, "L0_attn_b_O")):
                sp.dma_start(dst[:], chip.dram[name]).then_inc(landed, 16)

        @block.tensor
        def _(pe):
            pe.wait_ge(landed, 8 * 16)
            with pe.Fori(0, NP_) as i:
                pe.wait_ge(tokens_ready, i + 1)
                for w, bank, done in ((wq, 0, q_done), (wk, 2, k_done)):
                    for j in range(HJ):
                        mm = nc.tensor.matmul(ps[:, bank + j // 4, P * (j % 4):P * (j % 4) + P], w[:, P * j:P * j + P],
                                              tokens[:], start=True, stop=True)
                    mm.then_inc(done, 1)
                pe.wait_ge(added, i + 1)
                for b in range(2):
                    for odd in range(2):
                        mm = nc.tensor.matmul(ps[64 * odd:64 * odd + 64, 4 + b, :], tokens[:, SP * b:SP * b + SP],
                                              wv[:, 512 * odd:512 * odd + 512], start=True, stop=True)
                mm.then_inc(v_done, 1)
                pe.wait_ge(q_kept, i + 1)
                pe.wait_ge(k_kept, 2 * i + 2)
                for j in range(HJ):
                    for b in range(2):
                        mm = nc.tensor.matmul(ps[64 * b:64 * b + 64, 6 + j // 4, P * (j % 4):P * (j % 4) + P],
                                              q[:, j, SP * b:SP * b + SP], k[:, j, b].rearrange("p h s -> p (h s)"),
                                              start=True, stop=True)
                mm.then_inc(scores_done, 1)
                pe.wait_ge(probs_ready, i + 1)
                for j in range(HJ):
                    mm = nc.tensor.transpose(ps[:, j // 4, P * (j % 4):P * (j % 4) + P],
                                             probs[:, 2 * j:2 * j + 2, :].rearrange("p h s -> p (h s)"), chip.ident[:])
                mm.then_inc(turned, 1)
                pe.wait_ge(probs_kept, i + 1)
                pe.wait_ge(v_kept, i + 1)
                for j in range(HJ):
                    for b in range(2):
                        mm = nc.tensor.matmul(ps[:, 2 + j // 4, P * (j % 4) + SP * b:P * (j % 4) + SP * b + S],
                                              v[:, b, j].rearrange("p h d -> p (h d)"), probs_t[:, j, SP * b:SP * b + S],
                                              start=True, stop=True)
                mm.then_inc(mixed, 1)
                pe.wait_ge(mixed_kept, i + 1)
                for j in range(HJ):
                    mm = nc.tensor.matmul(ps[:, 4, 0:P], wo[:, j, :], mix[:, j].rearrange("p b s -> p (b s)"),
                                          start=(j == 0), stop=(j == HJ - 1))
                mm.then_inc(projected, 1)

        @block.scalar
        def _(act):
            act.wait_ge(pads_clear, 1)
            with act.Fori(0, NP_) as i:
                act.wait_ge(v_done, i + 1)
                nc.scalar.copy(tokens[:], xn.rearrange("p b s -> p (b s)")[:, bass.ds(i * P, P)]).then_inc(tokens_ready, 1)
                act.wait_ge(v_done, i + 2)
                nc.scalar.copy(v[0:64, :, :, 0, :], ps[0:64, 4:6, :].rearrange("p b (j d) -> p b j d", d=DH))
                nc.scalar.copy(v[64:P, :, :, 1, :], ps[64:P, 4:6, :].rearrange("p b (j d) -> p b j d", d=DH)).then_inc(v_kept, 1)
                act.wait_ge(shifted, i + 1)
                nc.scalar.activation(probs[:, :, 0:S], probs[:, :, 0:S], ACT.Exp, scale=DH ** -0.5).then_inc(exp_done, 1)
                act.wait_ge(turned, i + 1)
                nc.scalar.copy(probs_t[:], ps[:, 0:2, :].rearrange("p k (j c) -> p (k j) c", c=P)).then_inc(probs_kept, 1)

        @block.vector
        def _(dve):
            nc.vector.memset(probs[:], 0.0).then_inc(v_done, 1)
            nc.vector.memset(k[:], 0.0).then_inc(added, 1)
            nc.vector.memset(mix[:], 0.0)
            nc.vector.memset(v[:], 0.0).then_inc(pads_clear, 1)
            dve.wait_ge(landed, 8 * 16)
            with dve.Fori(0, NP_) as i:
                dve.wait_ge(q_done, i + 1)
                nc.vector.tensor_tensor(q[:], ps[:, 0:2, :].rearrange("p k (j c) -> p (k j) c", c=P),
                                        spread(bq[:], 2, P), ALU.add).then_inc(q_kept, 1)
                dve.wait_ge(k_done, i + 1)
                for odd in range(2):
                    r = slice(64 * odd, 64 * odd + 64)
                    nc.vector.tensor_tensor(k[r, :, :, odd, :], ps[r, 2:4, :].rearrange("p k (j b s) -> p (k j) b s", j=4, b=2),
                                            spread(spread(bk[r], 2, 2), 3, SP), ALU.add).then_inc(k_kept, 1)
                dve.wait_ge(scores_done, i + 1)
                step = Step(dve, dve_chain, 3 * i)
                step(nc.vector.tensor_reduce(top[:], scores, AX_X, ALU.max))
                nc.vector.tensor_tensor(probs[:, :, 0:S], scores, spread(top[:], 2, S), ALU.subtract).then_inc(shifted, 1)
                dve.wait_ge(exp_done, i + 1)
                step(nc.vector.tensor_reduce(total[:], probs[:, :, 0:S], AX_X, ALU.add))
                step(nc.vector.reciprocal(inverse[:], total[:]))
                nc.vector.tensor_tensor(probs[:, :, 0:S], probs[:, :, 0:S], spread(inverse[:], 2, S),
                                        ALU.mult).then_inc(probs_ready, 1)
                dve.wait_ge(mixed, i + 1)
                nc.vector.tensor_tensor(
                    mix[:, :, :, 0:S], ps[:, 2:4, :].rearrange("p k (j b s) -> p (k j) b s", j=4, b=2)[:, :, :, 0:S],
                    spread(spread(bv[:], 2, 2), 3, S), ALU.add).then_inc(mixed_kept, 1)
                dve.wait_ge(projected, i + 1)
                pair = x[:, bass.ds(2 * i, 2), 0:S]
                nc.vector.scalar_tensor_tensor(pair, ps[:, 4, 0:P].rearrange("p (b s) -> p b s", s=SP)[:, :, 0:S],
                                               bo[:, 0:1], pair, ALU.add, ALU.add).then_inc(added, 1)


def context_mixing(chip):
    nc, ps, xn, x = chip.nc, chip.ps, chip.xn, chip.x
    landed = [chip.sem("cm_context_landed%d" % u) for u in range(2)]
    tokens_ready, top_ready, exp_done, probs_ready, turned, probs_kept = (
        chip.sem("cm_" + k) for k in ("tokens_ready", "top_ready", "exp_done", "probs_ready", "turned", "probs_kept"))
    scores_done, mixed, added = ([chip.sem("cm_%s%d" % (k, u)) for u in range(2)] for k in ("scores_done", "mixed", "added"))
    dve_chain = chip.sem("cm_dve_chain")
    with ExitStack() as own:
        def sbuf(name, shape):
            return own.enter_context(nc.sbuf_tensor("cm_" + name, shape, F32))
        ctx_t = [sbuf("ctx_t%d" % u, [P, 2, NK]) for u in range(2)]
        ctx_n = [sbuf("ctx_n%d" % u, [KC, 2, NC_, P]) for u in range(2)]
        tokens = [sbuf("tokens%d" % u, [P, P]) for u in range(2)]
        probs = [sbuf("probs%d" % u, [P, NB_, KB]) for u in range(2)]
        probs_t = [sbuf("probs_t%d" % u, [KC, NC_, P]) for u in range(2)]
        top = [sbuf("top%d" % u, [P, 1]) for u in range(2)]
        low = [sbuf("low%d" % u, [P, 1]) for u in range(2)]
        total = [sbuf("total%d" % u, [P, 1]) for u in range(2)]
        inverse = [sbuf("inverse%d" % u, [P, 1]) for u in range(2)]
        block = own.enter_context(nc.Block(no_gpsimd_drain=True))

        @block.sync
        def _(sp):
            with sp.Fori(0, NP_ // 2) as i:
                for u in range(2):
                    sp.wait_ge(mixed[u], i + 1)
                    for b in range(2):
                        seq = bass.ds(4 * i + 2 * u + b, 1)
                        sp.dma_start(ctx_t[u][:, b], chip.dram["ctx_t"][seq].rearrange("a p n -> (a p) n")).then_inc(landed[u], 16)
                        sp.dma_start(ctx_n[u][:, b], chip.dram["ctx_n"][seq].rearrange("a p c d -> (a p) c d")).then_inc(landed[u], 16)

        @block.tensor
        def _(pe):
            with pe.Fori(0, NP_ // 2) as i:
                for u in range(2):
                    pe.wait_ge(landed[u], 64 * i + 64)
                    pe.wait_ge(added[u], i + 1)
                    pe.wait_ge(tokens_ready, 2 * i + u + 1)
                    for n in range(NB_):
                        for b in range(2):
                            mm = nc.tensor.matmul(ps[SP * b:SP * b + SP, 3 * u + n, 0:KB], tokens[u][:, SP * b:SP * b + SP],
                                                  ctx_t[u][:, b, KB * n:KB * n + KB], start=True, stop=True)
                    mm.then_inc(scores_done[u], 1)
                for u in range(2):
                    pe.wait_ge(probs_ready, 2 * i + u + 1)
                    rows = probs[u].rearrange("p n k -> p (n k)")
                    for c in range(NC_):
                        mm = nc.tensor.transpose(ps[0:KC, 3 * u + c // 4, P * (c % 4):P * (c % 4) + P],
                                                 rows[:, KC * c:KC * c + KC], chip.ident[:])
                    mm.then_inc(turned, 1)
                    pe.wait_ge(probs_kept, 2 * i + u + 1)
                    for b in range(2):
                        for c in range(NC_):
                            mm = nc.tensor.matmul(ps[:, 6 + u, SP * b:SP * b + SP], ctx_n[u][:, b, c, :],
                                                  probs_t[u][:, c, SP * b:SP * b + SP], start=(c == 0), stop=(c == NC_ - 1))
                    mm.then_inc(mixed[u], 1)

        @block.scalar
        def _(act):
            with act.Fori(0, NP_ // 2) as i:
                for u in range(2):
                    act.wait_ge(scores_done[u], i + 1)
                    nc.scalar.copy(tokens[u][:], xn[:, bass.ds(4 * i + 2 * u, 2), :].rearrange("p b s -> p (b s)")).then_inc(tokens_ready, 1)
                for u in range(2):
                    act.wait_ge(top_ready, 2 * i + u + 1)
                    nc.scalar.activation(probs[u][:], ps[:, 3 * u:3 * u + 3, 0:KB], ACT.Exp, bias=low[u][:, 0:1],
                                         accum_out=total[u][:, 0:1]).then_inc(exp_done, 1)
                for u in range(2):
                    act.wait_ge(turned, 2 * i + u + 1)
                    nc.scalar.copy(probs_t[u][:], ps[0:KC, 3 * u:3 * u + 3, :].rearrange("p k (c s) -> p (k c) s", s=P)).then_inc(probs_kept, 1)

        @block.vector
        def _(dve):
            for u in range(2):
                nc.vector.memset(top[u][:], 0.0).then_inc(mixed[u], 1)
                nc.vector.memset(low[u][:], 0.0).then_inc(added[u], 1)
                nc.vector.memset(total[u][:], 0.0).then_inc(scores_done[u], 1)
            with dve.Fori(0, NP_ // 2) as i:
                for u in range(2):
                    dve.wait_ge(scores_done[u], i + 2)
                    Step(dve, dve_chain, 4 * i + u)(
                        nc.vector.tensor_reduce(top[u][:], ps[:, 3 * u:3 * u + 3, 0:KB], mybir.AxisListType.XY, ALU.max))
                    nc.vector.tensor_scalar(low[u][:], top[u][:], -1.0, None, ALU.mult).then_inc(top_ready, 1)
                for u in range(2):
                    dve.wait_ge(exp_done, 2 * i + u + 1)
                    step = Step(dve, dve_chain, 4 * i + 2 + u)
                    step(nc.vector.reciprocal(inverse[u][:], total[u][:]))
                    nc.vector.tensor_scalar(probs[u][:], probs[u][:], inverse[u][:, 0:1], None, ALU.mult).then_inc(probs_ready, 1)
                for u in range(2):
                    dve.wait_ge(mixed[u], i + 2)
                    pair = x[:, bass.ds(4 * i + 2 * u, 2), 0:S]
                    nc.vector.tensor_tensor(pair, pair, ps[:, 6 + u, 0:P].rearrange("p (b s) -> p b s", s=SP)[:, :, 0:S], ALU.add).then_inc(added[u], 1)


def coupled_twist(chip):
    nc, ps, xn, x = chip.nc, chip.ps, chip.xn, chip.x
    CYCLES = 3
    cleared, landed, ready = chip.sem("ct_cleared"), chip.sem("ct_landed"), chip.sem("ct_constants_ready")
    sums_ready = chip.sem("ct_sums_ready")
    global_done, global_kept = chip.sem("ct_global_done"), chip.sem("ct_global_kept")
    layer_done, layer_kept, twisted, coupled = (chip.sem("ct_" + k) for k in ("layer_done", "layer_kept", "twisted", "coupled"))
    stepped, dve_chain, added = chip.sem("ct_stepped"), chip.sem("ct_dve_chain"), chip.sem("ct_added")
    D2, D4 = P // 2, P // 4
    with ExitStack() as own:
        def sbuf(name, shape):
            return own.enter_context(nc.sbuf_tensor("ct_" + name, shape, F32))
        weights, biases = sbuf("weights", [P, 5, P]), sbuf("biases", [P, 5])
        cw2, cw3, gw1, gw2, cw1 = (weights[:, n] for n in range(5))
        cb2, cb3, gb1, gb2, cb1 = (biases[:, n:n + 1] for n in range(5))
        cw4, gw3 = sbuf("cw4", [P, 1]), sbuf("gw3", [P, 1])
        cb4, gb3 = sbuf("cb4", [P, 1]), sbuf("gb3", [P, 1])
        reach = sbuf("reach", [P, 1])
        twist = sbuf("twist", [P, P])
        cw4_all, gw3_all = sbuf("cw4_all", [P, P]), sbuf("gw3_all", [P, P])
        sums, g1, g2, gf, base = sbuf("sums", [P, B]), sbuf("g1", [P, B]), sbuf("g2", [P, B]), sbuf("gf", [P, B]), sbuf("base", [P, B])
        gain_g, gain_t, low = sbuf("gain_g", [P, 1]), sbuf("gain_t", [P, 1]), sbuf("low", [P, 1])
        hidden = [sbuf("hidden%d" % c, [P, CT]) for c in range(CH)]
        coupling = [sbuf("coupling%d" % c, [P, CT]) for c in range(CH)]
        y = [xn[:, CB * c:CB * c + CB, 0:S] for c in range(CH)]
        x_of = [x[:, CB * c:CB * c + CB, 0:S] for c in range(CH)]
        wide = [ps[:, 4 + c, 0:CT].rearrange("p (b s) -> p b s", s=S) for c in range(CH)]
        loads = [(cw1, "cn_w1"), (cw2[:, 0:D2], "cn_w2"), (cw3[0:D2, 0:D4], "cn_w3"), (cw4[0:D4], "cn_w4"),
                 (cb1, "cn_b1"), (cb2[0:D2], "cn_b2"), (cb3[0:D4], "cn_b3"), (gw1[:, 0:D2], "gc_w1"),
                 (gw2[0:D2, 0:D4], "gc_w2"), (gw3[0:D4], "gc_w3"), (gb1[0:D2], "gc_b1"), (gb2[0:D4], "gc_b2")]
        to_all = [(cb4, "cn_b4"), (gb3, "gc_b3"), (reach, "adaptive_range")]
        n_loads = len(loads) + len(to_all) + 1
        block = own.enter_context(nc.Block(no_gpsimd_drain=True))

        @block.sync
        def _(sp):
            sp.wait_ge(cleared, 4)
            for dst, name in loads:
                sp.dma_start(dst, chip.dram["L0_ffn_" + name]).then_inc(landed, 16)
            for dst, name in to_all:
                sp.dma_start(dst[:], chip.dram["L0_ffn_" + name].to_broadcast([P, 1])).then_inc(landed, 16)
            sp.dma_start(twist[:], chip.dram["twist"]).then_inc(landed, 16)

        @block.tensor
        def _(pe):
            pe.wait_ge(landed, 16 * n_loads)
            pe.wait_ge(ready, 2)
            pe.wait_ge(sums_ready, 1)
            nc.tensor.matmul(ps[:, 4, 0:B], gw1, sums[:], start=True, stop=True).then_inc(global_done, 1)
            pe.wait_ge(global_kept, 1)
            nc.tensor.matmul(ps[:, 5, 0:B], gw2, g1[:], start=True, stop=True).then_inc(global_done, 1)
            pe.wait_ge(global_kept, 2)
            nc.tensor.matmul(ps[:, 6, 0:B], gw3_all[:], g2[:], start=True, stop=True).then_inc(global_done, 1)
            pe.wait_ge(global_kept, 3)
            with pe.Fori(0, CYCLES) as i:
                for c in range(CH):
                    pe.wait_ge(stepped, CH * i + c + 1)
                    nc.tensor.matmul(ps[:, c, 0:CT], cw1, y[c], start=True, stop=True).then_inc(layer_done, 1)
                    nc.tensor.matmul(ps[:, 4 + c, 0:CT], twist[:], y[c], start=True, stop=True).then_inc(twisted, 1)
                for c in range(CH):
                    pe.wait_ge(layer_kept, 16 * i + c + 1)
                    nc.tensor.matmul(ps[:, c, 0:CT], cw2, hidden[c][:], start=True, stop=True).then_inc(layer_done, 1)
                for c in range(CH):
                    pe.wait_ge(layer_kept, 16 * i + 4 + c + 1)
                    nc.tensor.matmul(ps[:, c, 0:CT], cw3, hidden[c][:], start=True, stop=True).then_inc(layer_done, 1)
                for c in range(CH):
                    pe.wait_ge(layer_kept, 16 * i + 8 + c + 1)
                    nc.tensor.matmul(ps[:, c, 0:CT], cw4_all[:], hidden[c][:], start=True, stop=True).then_inc(layer_done, 1)

        @block.scalar
        def _(act):
            act.wait_ge(landed, 16 * n_loads)
            act.wait_ge(global_done, 1)
            nc.scalar.activation(g1[:], ps[:, 4, 0:B], ACT.Gelu, bias=gb1, scale=1.0 / S).then_inc(global_kept, 1)
            act.wait_ge(global_done, 2)
            nc.scalar.activation(g2[:], ps[:, 5, 0:B], ACT.Gelu, bias=gb2).then_inc(global_kept, 1)
            act.wait_ge(global_done, 3)
            nc.scalar.activation(gf[:], ps[:, 6, 0:B], ACT.Sigmoid, bias=gb3[:, 0:1]).then_inc(global_kept, 1)
            with act.Fori(0, CYCLES) as i:
                for n, bias in enumerate((cb1, cb2, cb3)):
                    for c in range(CH):
                        act.wait_ge(layer_done, 16 * i + 4 * n + c + 1)
                        nc.scalar.activation(hidden[c][:], ps[:, c, 0:CT], ACT.Gelu, bias=bias).then_inc(layer_kept, 1)
                for c in range(CH):
                    act.wait_ge(layer_done, 16 * i + 12 + c + 1)
                    nc.scalar.activation(coupling[c][:], ps[:, c, 0:CT], ACT.Sigmoid, bias=cb4[:, 0:1]).then_inc(layer_kept, 1)

        @block.vector
        def _(dve):
            for buffer in (weights, biases, cw4, gw3):
                nc.vector.memset(buffer[:], 0.0).then_inc(cleared, 1)
            nc.vector.tensor_reduce(sums[:], xn[:, :, 0:S], AX_X, ALU.add).then_inc(sums_ready, 1)
            dve.wait_ge(landed, 16 * n_loads)
            step = Step(dve, dve_chain)
            nc.vector.tensor_copy(cw4_all[:], cw4[:, 0:1].to_broadcast([P, P])).then_inc(ready, 1)
            nc.vector.tensor_copy(gw3_all[:], gw3[:, 0:1].to_broadcast([P, P])).then_inc(ready, 1)
            step(nc.vector.tensor_scalar(gain_g[:], reach[:], 1.4, None, ALU.mult))
            step(nc.vector.tensor_scalar(gain_t[:], reach[:], 0.6, None, ALU.mult))
            step(nc.vector.tensor_scalar(low[:], reach[:], -1.0, 0.1, ALU.mult, ALU.add))
            dve.wait_ge(global_kept, 3)
            step(nc.vector.tensor_scalar(base[:], gf[:], gain_g[:, 0:1], low[:, 0:1], ALU.mult, ALU.add))
            for c in range(CH):
                nc.vector.tensor_tensor(x_of[c], x_of[c], y[c], ALU.add).then_inc(stepped, 1)
            with dve.Fori(0, CYCLES) as i:
                for c in range(CH):
                    dve.wait_ge(layer_kept, 16 * i + 12 + c + 1)
                    dve.wait_ge(twisted, CH * i + c + 1)
                    cc = coupling[c].rearrange("p (b s) -> p b s", s=S)
                    step = Step(dve, coupled, 8 * i + 2 * c)
                    step(nc.vector.scalar_tensor_tensor(cc, cc, gain_t[:, 0:1], spread(base[:, CB * c:CB * c + CB], 2, S), ALU.mult, ALU.add))
                    step(nc.vector.tensor_tensor(cc, cc, wide[c], ALU.mult))
                    nc.vector.tensor_tensor(x_of[c], x_of[c], cc, ALU.add).then_inc(added, 1)
                    dve.wait_ge(added, CH * i + c + 1)
                    nc.vector.tensor_tensor(y[c], y[c], cc, ALU.add).then_inc(stepped, 1)


def gated_recurrence(chip):
    nc, ps, xn, x = chip.nc, chip.ps, chip.xn, chip.x
    W = B * SP
    TAPS = 4
    landed, conv_ready, gates_done, gates_kept = (chip.sem("gr_" + k) for k in ("landed", "conv_ready", "gates_done", "gates_kept"))
    dve_chain, act_chain = chip.sem("gr_dve_chain"), chip.sem("gr_act_chain")
    rate_ready, decay_ready, sums_ready = chip.sem("gr_rate_ready"), chip.sem("gr_decay_ready"), chip.sem("gr_sums_ready")
    root_needed, root_ready = chip.sem("gr_root_needed"), chip.sem("gr_root_ready")
    h_ready, out_done, squared, power_done, root_kept, added = (
        chip.sem("gr_" + k) for k in ("h_ready", "out_done", "squared", "power_done", "root_kept", "added"))
    with ExitStack() as own:
        def sbuf(name, shape):
            return own.enter_context(nc.sbuf_tensor("gr_" + name, shape, F32))
        wr, wi, wo = sbuf("wr", [P, P]), sbuf("wi", [P, P]), sbuf("wo", [P, P])
        taps, bc, br, bi, log_a, norm_w = sbuf("taps", [P, TAPS]), *(sbuf(n, [P, 1]) for n in ("bc", "br", "bi", "log_a", "norm_w"))
        rate = sbuf("rate", [P, 1])
        conv, r_gate, i_gate, alive, work = (sbuf(n, [P, W]) for n in ("conv", "r_gate", "i_gate", "alive", "work"))
        out_sb = sbuf("out", [P, CH, CW])
        flat = chip.xn_lead[:]
        loads = [(wr, "Wr_w"), (wi, "Wi_w"), (wo, "out_w"), (taps, "conv_weight"), (bc, "conv_bias"), (br, "Wr_b"), (bi, "Wi_b"),
                 (log_a, "log_a"), (norm_w, "norm_w")]
        block = own.enter_context(nc.Block(no_gpsimd_drain=True))

        @block.sync
        def _(sp):
            for dst, name in loads:
                sp.dma_start(dst[:], chip.dram["L1_attn_" + name]).then_inc(landed, 16)

        @block.tensor
        def _(pe):
            pe.wait_ge(conv_ready, 1)
            for c in range(CH):
                cols = conv[:, CW * c:CW * c + CW]
                nc.tensor.matmul(ps[:, c, :], wr[:], cols, start=True, stop=True).then_inc(gates_done, 1)
            for c in range(CH):
                cols = conv[:, CW * c:CW * c + CW]
                nc.tensor.matmul(ps[:, 4 + c, :], wi[:], cols, start=True, stop=True).then_inc(gates_done, 1)
            pe.wait_ge(h_ready, 1)
            for c in range(CH):
                nc.tensor.matmul(ps[:, c, :], wo[:], conv[:, CW * c:CW * c + CW], start=True, stop=True).then_inc(out_done, 1)
            for c in range(CH):
                pe.wait_ge(squared, c + 1)
                nc.tensor.matmul(ps[:, 4 + c, :], chip.mean[:], work[:, CW * c:CW * c + CW], start=True, stop=True).then_inc(power_done, 1)

        @block.scalar
        def _(act):
            act.wait_ge(landed, 16 * len(loads))
            for c in range(CH):
                act.wait_ge(gates_done, c + 1)
                nc.scalar.activation(r_gate[:, CW * c:CW * c + CW], ps[:, c, :], ACT.Sigmoid, bias=br[:, 0:1]).then_inc(gates_kept, 1)
            for c in range(CH):
                act.wait_ge(gates_done, 4 + c + 1)
                nc.scalar.activation(i_gate[:, CW * c:CW * c + CW], ps[:, 4 + c, :], ACT.Sigmoid, bias=bi[:, 0:1]).then_inc(gates_kept, 1)
            step = Step(act, act_chain)
            step(nc.scalar.activation(rate[:], log_a[:], ACT.Exp, scale=-1.0))
            nc.scalar.activation(rate[:], rate[:], ACT.Ln, bias=1.0).then_inc(rate_ready, 1)
            act.wait_ge(decay_ready, 1)
            nc.scalar.activation(r_gate[:], work[:], ACT.Exp).then_inc(rate_ready, 1)
            act.wait_ge(root_needed, 1)
            nc.scalar.activation(r_gate[:], r_gate[:], ACT.Sqrt).then_inc(root_ready, 1)
            act.wait_ge(sums_ready, 1)
            step(nc.scalar.activation(i_gate[:], work[:], ACT.Exp, scale=-1.0))
            nc.scalar.activation(work[:], work[:], ACT.Exp).then_inc(root_ready, 1)
            for c in range(CH):
                act.wait_ge(out_done, c + 1)
                nc.scalar.copy(out_sb[:, c, :], ps[:, c, :]).then_inc(act_chain, 1)
                act.wait_ge(act_chain, 3 + c)
                nc.scalar.activation(work[:, CW * c:CW * c + CW], out_sb[:, c, :], ACT.Square).then_inc(squared, 1)
            for c in range(CH):
                act.wait_ge(power_done, c + 1)
                nc.scalar.activation(r_gate[:, CW * c:CW * c + CW], ps[:, 4 + c, :], ACT.Sqrt, bias=chip.eps[:, 1:2]).then_inc(root_kept, 1)

        @block.vector
        def _(dve):
            step = Step(dve, dve_chain)
            nc.vector.memset(alive[:], 1.0)
            step(nc.vector.memset(work[:], 1.0))
            step(nc.vector.memset(alive.rearrange("p (b s) -> p b s", s=SP)[:, :, 0:1], 0.0))
            dve.wait_ge(landed, 16 * len(loads))
            step(nc.vector.tensor_scalar(conv[:], flat[:, SP:SP + W], taps[:, 3:4], bc[:, 0:1], ALU.mult, ALU.add))
            for t in range(TAPS - 1):
                shift = TAPS - 1 - t
                last = nc.vector.scalar_tensor_tensor(conv[:], flat[:, SP - shift:SP - shift + W], taps[:, t:t + 1], conv[:], ALU.mult, ALU.add)
                if t < TAPS - 2:
                    step(last)
            last.then_inc(conv_ready, 1)
            dve.wait_ge(rate_ready, 1)
            step(nc.vector.tensor_scalar(rate[:], rate[:], -8.0, None, ALU.mult))
            dve.wait_ge(gates_kept, 4)
            nc.vector.tensor_scalar(work[:], r_gate[:], rate[:, 0:1], None, ALU.mult).then_inc(decay_ready, 1)
            dve.wait_ge(decay_ready, 1)
            dve.wait_ge(rate_ready, 2)
            step(nc.vector.tensor_scalar(work[:], work[:], float(np.log(np.float32(1e-7))), None, ALU.max))
            step(nc.vector.tensor_tensor(r_gate[:], r_gate[:], r_gate[:], ALU.mult))
            step(nc.vector.tensor_scalar(r_gate[:], r_gate[:], -1.0, 1.0, ALU.mult, ALU.add))
            nc.vector.tensor_scalar(r_gate[:], r_gate[:], 1e-6, None, ALU.max).then_inc(root_needed, 1)
            step(nc.vector.tensor_tensor_scan(out_sb.rearrange("p c w -> p (c w)"), alive[:], work[:], 0.0, ALU.mult, ALU.add))
            dve.wait_ge(gates_kept, 8)
            step(nc.vector.tensor_tensor(conv[:], conv[:], i_gate[:], ALU.mult))
            nc.vector.tensor_scalar(work[:], out_sb.rearrange("p c w -> p (c w)"), -80.0, None, ALU.max).then_inc(sums_ready, 1)
            dve.wait_ge(root_ready, 1)
            step(nc.vector.tensor_tensor(conv[:], conv[:], r_gate[:], ALU.mult))
            dve.wait_ge(root_ready, 2)
            step(nc.vector.tensor_tensor(conv[:], conv[:], i_gate[:], ALU.mult))
            step(nc.vector.tensor_tensor_scan(out_sb.rearrange("p c w -> p (c w)"), alive[:], conv[:], 0.0, ALU.mult, ALU.add))
            nc.vector.tensor_tensor(conv[:], out_sb.rearrange("p c w -> p (c w)"), work[:], ALU.mult).then_inc(h_ready, 1)
            dve.wait_ge(h_ready, 1)
            for c in range(CH):
                cols = slice(CW * c, CW * c + CW)
                dve.wait_ge(root_kept, c + 1)
                step(nc.vector.reciprocal(r_gate[:, cols], r_gate[:, cols]))
                step(nc.vector.scalar_tensor_tensor(r_gate[:, cols], r_gate[:, cols], norm_w[:, 0:1], out_sb[:, c, :], ALU.mult, ALU.mult))
                goal = x[:, CB * c:CB * c + CB, 0:S]
                nc.vector.tensor_tensor(goal, goal, r_gate[:, cols].rearrange("p (b s) -> p b s", s=SP)[:, :, 0:S], ALU.add).then_inc(added, 1)


BF16 = mybir.dt.bfloat16
PR = HX // 2
RW = 2 * S
PF = 2 * DX
PARTS = 3
KEY_PART, QUERY_PART = (0, 0, 0, 1, 1, 2), (0, 1, 2, 0, 1, 0)
SLOTS = len(KEY_PART)
TALL = SLOTS * PF
KEPT = [0, 0, 1, 1, 2, 2, 2, 0]
VC = P // 32
VR = NC_ // VC
VW = PR * (PF + 1) + 32 - (PF + 1)


def cross_attention(chip, layer, scale):
    nc, ps, xn, x = chip.nc, chip.ps, chip.xn, chip.x
    tag = "x%d_" % layer
    (weights_landed, consts_ready, q_made, q_kept, q_high, q_rest, q_mid, q_low, q_cleared) = (chip.sem(tag + k) for k in (
        "weights_landed", "consts_ready", "q_made", "q_kept", "q_high", "q_rest", "q_mid", "q_low", "q_cleared"))
    pool_filled, act_filled, values_filled = (chip.sem(tag + k) for k in ("pool_filled", "act_filled", "values_filled"))
    ctx_landed, stacked = ([chip.sem(tag + k + str(u)) for u in range(2)] for k in ("ctx_landed", "stacked"))
    k_done, k_high, k_rest, k_mid, k_low, v_done, v_kept = (chip.sem(tag + k) for k in ("k_done", "k_high", "k_rest", "k_mid", "k_low", "v_done", "v_kept"))
    scores_done, topped, tops_made, tops_split, tops_turned, tops_placed = (
        chip.sem(tag + k) for k in ("scores_done", "topped", "tops_made", "tops_split", "tops_turned", "tops_placed"))
    turned_done, exp_done, mixed, mixed_kept, folded, mix_kept = (
        chip.sem(tag + k) for k in ("turned_done", "exp_done", "mixed", "mixed_kept", "folded", "mix_kept"))
    projected, added, tops_chain, mix_chain, first_placed, biased = (chip.sem(tag + k) for k in ("projected", "added", "tops_chain", "mix_chain", "first_placed", "biased"))
    TURNED, MIX, TURNS = 3, 6, 7
    BODY = range(1, B // 2 - 2)

    def wait(engine, semaphore, value):
        if not isinstance(value, int) or value > 0:
            engine.wait_ge(semaphore, value)

    def all_passes(engine, one_pass):
        for o in (-2, -1, 0, 1):
            one_pass(0, o)
        with engine.Fori(BODY.start, BODY.stop) as j:
            one_pass(j, 0)
            one_pass(j, 1)
        for o in range(5):
            one_pass(B // 2 - 2, o)

    def has(j, o, ahead):
        return not isinstance(j, int) or 0 <= 2 * j + o + ahead < B

    with ExitStack() as own:
        def sbuf(name, shape, dtype=F32):
            return own.enter_context(nc.sbuf_tensor(tag + name, shape, dtype))
        wq, wk, wv, wo = (sbuf(n, [P, P]) for n in ("wq", "wk", "wv", "wo"))
        bq, bk, bv, bo = (sbuf(n, [P, 1]) for n in ("bq", "bk", "bv", "bo"))
        place = sbuf("place", [P, 2, 2, 2, 32])
        pair_rows, ident_low = sbuf("pair_rows", [P, PR]), sbuf("ident_low", [P, P], BF16)
        ctx_t = [sbuf("ctx_t%d" % u, [P, NK]) for u in range(2)]
        key_parts = [[sbuf("key_part%d_%d" % (u, k), [P, NK], BF16) for k in range(PARTS)] for u in range(2)]
        query_parts = [sbuf("query_part%d" % k, [P, B, 2, S], BF16) for k in range(PARTS)]
        q, q_left = sbuf("q", [P, CH, CT]), [sbuf("q_left%d" % u, [P, CT]) for u in range(2)]
        key_left = [sbuf("key_left%d" % n, [P, KB]) for n in range(NB_)]
        nothing = sbuf("nothing", [P, KB])
        keys = [sbuf("keys%d" % u, [P, PR, NK], BF16) for u in range(2)]
        queries = [sbuf("queries%d" % u, [P, PR, RW], BF16) for u in range(2)]
        values = [sbuf("values%d" % u, [KC, NC_, VW]) for u in range(2)]
        probs_t = [sbuf("probs_t%d" % u, [KC, NC_, RW]) for u in range(2)]
        bank_top = sbuf("bank_top", [P, PR, NB_])
        top, top_left, top_parts = sbuf("top", [P, PR]), sbuf("top_left", [P, PR]), sbuf("top_parts", [P, 32], BF16)
        quarters = [sbuf("quarters%d" % u, [P, PR, 2, S]) for u in range(2)]
        inverse, mix = sbuf("inverse", [P, S]), sbuf("mix", [P, B, S])
        block = own.enter_context(nc.Block(no_gpsimd_drain=True))

        @block.sync
        def _(sp):
            for dst, name in ((wq, "Wq"), (wk, "Wk"), (wv, "Wv"), (wo, "Wo"), (bq, "bq"), (bk, "bk"), (bv, "bv"), (bo, "bo")):
                sp.dma_start(dst[:], chip.dram["L%d_xattn_%s" % (layer, name)]).then_inc(weights_landed, 16)
            for dst, name in ((place, "place"), (pair_rows, "pair_rows")):
                sp.dma_start(dst[:], chip.dram[name]).then_inc(weights_landed, 16)

            def context(j, o):
                wait(sp, v_done, VR * (2 * j + o - 1))
                source = chip.dram["ctx_t"].rearrange("(j u) p n -> u j p n", u=2)[o % 2, o // 2:][bass.ds(j, 1)].rearrange("a p n -> (a p) n")
                sp.dma_start(ctx_t[o % 2][:], source).then_inc(ctx_landed[o % 2], 16)

            def stack(j, o):
                u, i = o % 2, 2 * j + o
                wait(sp, turned_done, PR * (i - 1))
                if isinstance(j, int):
                    sp.wait_ge(k_low, NB_ * i + NB_)
                for s in range(SLOTS):
                    rows = slice(PF * s, PF * s + PF)
                    sp.dma_start(keys[u][rows].rearrange("r p n -> r (p n)"), key_parts[u][KEY_PART[s]][:]).then_inc(stacked[u], 16)
                    sp.dma_start(queries[u][rows].rearrange("r p n -> r (p n)"),
                                 query_parts[QUERY_PART[s]].rearrange("f (j u) c s -> f u j c s", u=2)[:, u, o // 2:][:, bass.ds(j, 1)].rearrange("f b c s -> f (b c s)")).then_inc(stacked[u], 16)

            context(0, 0)
            context(0, 1)

            def one_pass(j, o):
                if o == -1 and isinstance(j, int):
                    sp.wait_ge(q_low, 2 * CH)
                if has(j, o, 1):
                    stack(j, o + 1)
                if has(j, o, 3) and o + 3 > 1:
                    context(j, o + 3)
            all_passes(sp, one_pass)

        @block.tensor
        def _(pe):
            def make_keys(j, o, n):
                if n == 0:
                    wait(pe, ctx_landed[o % 2], 16 * (j + o // 2) + 16)
                    wait(pe, mix_kept, 2 * j + o - 3)
                    if isinstance(j, int) and 0 < 2 * j + o < 4:
                        pe.wait_ge(v_kept if 2 * j + o > 1 else k_rest, VR * (2 * j + o - 1) if 2 * j + o > 1 else NB_)
                else:
                    pe.wait_ge(k_rest, NB_ * (2 * j + o) + n)
                nc.tensor.matmul(ps[:, TURNS, 0:KB], wk[:], ctx_t[o % 2][:, KB * n:KB * n + KB], start=True, stop=True).then_inc(k_done, 1)

            def make_values(j, o, r):
                if r > 0:
                    pe.wait_ge(v_kept, VR * (2 * j + o) + r)
                elif has(j, o, 1):
                    pe.wait_ge(k_rest, NB_ * (2 * j + o + 1) + NB_)
                else:
                    pe.wait_ge(mix_kept, 2 * j + o - 2)
                for c in range(VC):
                    k0 = KC * (VC * r + c)
                    mm = nc.tensor.matmul(ps[0:KC, TURNS, P * c:P * c + P], ctx_t[o % 2][:, k0:k0 + KC], wv[:], start=True, stop=True)
                mm.then_inc(v_done, 1)

            def scores(j, o, p):
                if p == 0:
                    pe.wait_ge(stacked[o % 2], 2 * SLOTS * 16 * (j + o // 2 + 1))
                for n in range(NB_):
                    wait(pe, topped, NB_ * (PR * (2 * j + o) + p - 1) + n + 1)
                    nc.tensor.matmul(ps[0:RW, n, 0:KB], queries[o % 2][0:TALL, p, :], keys[o % 2][0:TALL, p, KB * n:KB * n + KB],
                                     start=True, stop=True).then_inc(scores_done, 1)

            def turn_tops(j, o):
                pe.wait_ge(tops_split, 2 * j + o + 1)
                nc.tensor.matmul(ps[TALL:P, 0, 0:RW], top_parts[:], ident_low[:, 0:RW], start=True, stop=True).then_inc(tops_turned, 1)

            def scores_by_key(j, o, p):
                if p == 0:
                    pe.wait_ge(first_placed, 2 * j + o + 1)
                    if isinstance(j, int) and j == 0:
                        pe.wait_ge(act_filled if o else pool_filled, 1)
                if p == 1:
                    pe.wait_ge(tops_placed, 2 * j + o + 1)
                if p == PR - 1 and has(j, o, 2):
                    pe.wait_ge(k_low, NB_ * (2 * j + o + 2) + NB_)
                wait(pe, exp_done, PR * (2 * j + o) + p)
                for c in range(NC_):
                    mm = nc.tensor.matmul(ps[0:KC, TURNED + c // VC, RW * (c % VC):RW * (c % VC) + RW],
                                          keys[o % 2][:, p, KC * c:KC * c + KC], queries[o % 2][:, p, :], start=True, stop=True)
                mm.then_inc(turned_done, 1)

            def mix_values(j, o, p):
                pe.wait_ge(exp_done, PR * (2 * j + o) + p + 1)
                if p % 4 == 0:
                    wait(pe, mixed_kept, 2 * (2 * j + o) + p // 4)
                if p == 0:
                    pe.wait_ge(v_kept, VR * (2 * j + o) + VR)
                for c in range(NC_):
                    g = c % 4
                    mm = nc.tensor.matmul(ps[32 * g:32 * g + 32, MIX, RW * (p % 4):RW * (p % 4) + RW], values[o % 2][:, c, (PF + 1) * p:(PF + 1) * p + 32],
                                          probs_t[p % 2][:, c, :], start=(c < 4), stop=(c >= NC_ - 4))
                if p % 4 == 3:
                    mm.then_inc(mixed, 1)

            def fold(j, o):
                pe.wait_ge(mixed_kept, 2 * (2 * j + o) + 2)
                if has(j, o, 2):
                    pe.wait_ge(v_kept, VR * (2 * j + o + 2) + VR)
                else:
                    pe.wait_ge(mix_kept, 2 * j + o)
                for what in range(2):
                    for step in range(4):
                        odd, parity = divmod(step, 2)
                        for g in range(4):
                            mm = nc.tensor.matmul(ps[32 * g:32 * g + 32, TURNS, S * what:S * what + S], place[:, parity, odd, what, :],
                                                  quarters[o % 2][:, 2 * g + odd, parity, :], start=(step == 0), stop=(step == 3))
                mm.then_inc(folded, 1)

            pe.wait_ge(weights_landed, 10 * 16)
            for c in range(CH):
                nc.tensor.matmul(ps[:, c, 0:CT], wq[:], xn[:, CB * c:CB * c + CB, 0:S], start=True, stop=True).then_inc(q_made, 1)
            pe.wait_ge(consts_ready, 1)
            pe.wait_ge(q_kept, CH)

            def one_pass(j, o):
                for step in range(PR):
                    if has(j, o, 0):
                        scores_by_key(j, o, step)
                    if step < NB_ and has(j, o, 2):
                        make_keys(j, o + 2, step)
                    if NB_ <= step < NB_ + VR and has(j, o, 1):
                        make_values(j, o + 1, step - NB_)
                    first = sum(KEPT[:step])
                    if has(j, o, 1) and KEPT[step] > 0:
                        scores(j, o + 1, first)
                    if step > 0 and has(j, o, 0):
                        mix_values(j, o, step - 1)
                    if has(j, o, 1) and KEPT[step] > 1:
                        scores(j, o + 1, first + 1)
                if has(j, o, 0):
                    mix_values(j, o, PR - 1)
                if has(j, o, -1):
                    fold(j, o - 1)
                if has(j, o, 1):
                    turn_tops(j, o + 1)
            all_passes(pe, one_pass)
            for c in range(CH):
                pe.wait_ge(biased, c + 1)
                nc.tensor.matmul(ps[:, c, 0:CT], wo[:], mix[:, CB * c:CB * c + CB, :].rearrange("p b s -> p (b s)"),
                                 start=True, stop=True).then_inc(projected, 1)

        @block.scalar
        def _(act):
            def keep_keys(j, o, n):
                act.wait_ge(k_done, NB_ * (2 * j + o) + n + 1)
                nc.scalar.activation(key_parts[o % 2][0][:, KB * n:KB * n + KB], ps[:, TURNS, 0:KB], ACT.Identity, bias=bk[:, 0:1]).then_inc(k_high, 1)

            def keep_values(j, o, r):
                act.wait_ge(v_done, VR * (2 * j + o) + r + 1)
                nc.scalar.copy(values[o % 2][:, VC * r:VC * r + VC, 0:PR * (PF + 1)].rearrange("p c (j f) -> p c j f", f=PF + 1)[:, :, :, 0:PF],
                               ps[0:KC, TURNS, :].rearrange("p (c j f) -> p c j f", c=VC, f=PF)).then_inc(v_kept, 1)

            def exponentials(j, o, p):
                act.wait_ge(turned_done, PR * (2 * j + o) + p + 1)
                nc.scalar.activation(probs_t[p % 2].rearrange("k (n c) r -> k n (c r)", c=VC), ps[0:KC, TURNED:TURNED + VR, 0:VC * RW],
                                     ACT.Exp, scale=scale).then_inc(exp_done, 1)

            def keep_mixed(j, o, half):
                act.wait_ge(mixed, 2 * (2 * j + o) + half + 1)
                nc.scalar.copy(quarters[o % 2][:, 4 * half:4 * half + 4].rearrange("p j c s -> p (j c s)"), ps[:, MIX, 0:4 * RW]).then_inc(mixed_kept, 1)

            act.wait_ge(q_cleared, 2 * PARTS)
            act.wait_ge(values_filled, 2)
            for c in range(CH):
                for half in range(2):
                    rows = slice(64 * half, 64 * half + 64)
                    if half == 0:
                        act.wait_ge(q_kept, c + 1)
                    nc.scalar.copy(query_parts[0][rows, CB * c:CB * c + CB, half, :], q[rows, c, :].rearrange("p (b s) -> p b s", s=S)).then_inc(q_high, 1)
                act.wait_ge(q_rest, 2 * c + 2)
                for half in range(2):
                    rows = slice(64 * half, 64 * half + 64)
                    nc.scalar.copy(query_parts[1][rows, CB * c:CB * c + CB, half, :],
                                   q_left[c % 2][rows, :].rearrange("p (b s) -> p b s", s=S)).then_inc(q_mid, 1)
            act.wait_ge(weights_landed, 10 * 16)
            nc.scalar.copy(keys[1][TALL:P], spread(pair_rows[TALL:P, :], 2, NK)).then_inc(act_filled, 1)

            def one_pass(j, o):
                for step in range(PR):
                    if has(j, o, 0):
                        exponentials(j, o, step)
                    if step < NB_ and has(j, o, 2):
                        keep_keys(j, o + 2, step)
                    if NB_ <= step < NB_ + VR and has(j, o, 1):
                        keep_values(j, o + 1, step - NB_)
                    if step == 4 and has(j, o, 0):
                        keep_mixed(j, o, 0)
                if has(j, o, 0):
                    keep_mixed(j, o, 1)
            all_passes(act, one_pass)

        @block.gpsimd
        def _(pool):
            pool.wait_ge(weights_landed, 10 * 16)
            nc.gpsimd.tensor_copy(keys[0][TALL:P], spread(pair_rows[TALL:P, :], 2, NK)).then_inc(pool_filled, 1)
            pool.wait_ge(pool_filled, 1)

            def one_pass(j, o):
                if not has(j, o, 2):
                    return
                for n in range(NB_):
                    part, cols = key_parts[o % 2], slice(KB * n, KB * n + KB)
                    pool.wait_ge(k_rest, NB_ * (2 * j + o + 2) + n + 1)
                    nc.gpsimd.tensor_tensor(part[1][:, cols], key_left[n][:], nothing[:], ALU.add).then_inc(k_mid, 1)
                    pool.wait_ge(k_mid, NB_ * (2 * j + o + 2) + n + 1)
                    nc.gpsimd.tensor_tensor(part[2][:, cols], key_left[n][:], part[1][:, cols], ALU.subtract).then_inc(k_low, 1)
            all_passes(pool, one_pass)

        @block.vector
        def _(dve):
            def rest_of_keys(j, o, n):
                dve.wait_ge(k_high, NB_ * (2 * j + o) + n + 1)
                wait(dve, k_low, NB_ * (2 * j + o - 1) + n + 1)
                nc.vector.scalar_tensor_tensor(key_left[n][:], ps[:, TURNS, 0:KB], bk[:, 0:1],
                                               key_parts[o % 2][0][:, KB * n:KB * n + KB], ALU.add, ALU.subtract).then_inc(k_rest, 1)

            def row_tops(j, o, p):
                for n in range(NB_):
                    dve.wait_ge(scores_done, NB_ * (PR * (2 * j + o) + p) + n + 1)
                    nc.vector.tensor_reduce(bank_top[0:RW, p, n:n + 1], ps[0:RW, n, 0:KB], AX_X, ALU.max).then_inc(topped, 1)

            def split_tops(j, o):
                n = 3 * (2 * j + o)
                dve.wait_ge(topped, NB_ * (PR * (2 * j + o) + PR))
                nc.vector.tensor_reduce(top[0:RW, :], bank_top[0:RW], AX_X, ALU.max).then_inc(tops_made, 1)
                dve.wait_ge(tops_made, 2 * j + o + 1)
                nc.vector.tensor_scalar(top_parts[0:RW, 0:PR], top[0:RW, :], -1.0, None, ALU.mult).then_inc(tops_chain, 1)
                dve.wait_ge(tops_chain, n + 1)
                nc.vector.scalar_tensor_tensor(top_left[0:RW, :], top[0:RW, :], -1.0, top_parts[0:RW, 0:PR], ALU.mult, ALU.subtract).then_inc(tops_chain, 1)
                dve.wait_ge(tops_chain, n + 2)
                nc.vector.tensor_copy(top_parts[0:RW, PR:2 * PR], top_left[0:RW, :]).then_inc(tops_chain, 1)
                dve.wait_ge(tops_chain, n + 3)
                nc.vector.tensor_tensor(top_parts[0:RW, 2 * PR:3 * PR], top_left[0:RW, :], top_parts[0:RW, PR:2 * PR], ALU.subtract).then_inc(tops_split, 1)
                dve.wait_ge(tops_turned, 2 * j + o + 1)
                turned = ps[TALL:P, 0, 0:RW]
                nc.vector.tensor_copy(queries[o % 2][TALL:P, 0, :], turned).then_inc(first_placed, 1)
                nc.vector.tensor_copy(queries[o % 2][TALL:P, 1:PR], spread(turned, 1, PR - 1)).then_inc(tops_placed, 1)

            def keep_mix(j, o):
                i = 2 * j + o
                dve.wait_ge(folded, i + 1)
                nc.vector.reciprocal(inverse[:], ps[:, TURNS, S:2 * S]).then_inc(mix_chain, 1)
                dve.wait_ge(mix_chain, i + 1)
                goal = mix[:, bass.ds(i, 1), :].rearrange("p b s -> p (b s)")
                nc.vector.tensor_tensor(goal, ps[:, TURNS, 0:S], inverse[:], ALU.mult).then_inc(mix_kept, 1)

            for k in range(PARTS):
                nc.vector.memset(query_parts[k][0:64, :, 1, :], 0.0).then_inc(q_cleared, 1)
                nc.vector.memset(query_parts[k][64:P, :, 0, :], 0.0).then_inc(q_cleared, 1)
            nc.vector.memset(nothing[:], 0.0)
            for u in range(2):
                nc.vector.memset(values[u][:], 1.0).then_inc(values_filled, 1)
            nc.vector.memset(top_parts[:], 0.0)
            nc.vector.tensor_copy(ident_low[:], chip.ident[:]).then_inc(consts_ready, 1)
            dve.wait_ge(weights_landed, 10 * 16)
            for c in range(CH):
                dve.wait_ge(q_made, c + 1)
                nc.vector.tensor_scalar(q[:, c, :], ps[:, c, 0:CT], bq[:, 0:1], None, ALU.add).then_inc(q_kept, 1)
            dve.wait_ge(q_kept, CH)
            for c in range(CH):
                left = q_left[c % 2]
                dve.wait_ge(q_high, 2 * c + 2)
                for half in range(2):
                    rows = slice(64 * half, 64 * half + 64)
                    nc.vector.tensor_tensor(left[rows, :].rearrange("p (b s) -> p b s", s=S), q[rows, c, :].rearrange("p (b s) -> p b s", s=S),
                                            query_parts[0][rows, CB * c:CB * c + CB, half, :], ALU.subtract).then_inc(q_rest, 1)
                dve.wait_ge(q_rest, 2 * c + 2)
                dve.wait_ge(q_mid, 2 * c + 2)
                for half in range(2):
                    rows = slice(64 * half, 64 * half + 64)
                    nc.vector.tensor_tensor(query_parts[2][rows, CB * c:CB * c + CB, half, :], left[rows, :].rearrange("p (b s) -> p b s", s=S),
                                            query_parts[1][rows, CB * c:CB * c + CB, half, :], ALU.subtract).then_inc(q_low, 1)

            def one_pass(j, o):
                for step in range(PR):
                    if step < NB_ and has(j, o, 2):
                        rest_of_keys(j, o + 2, step)
                    for p in range(sum(KEPT[:step]), sum(KEPT[:step + 1])):
                        if has(j, o, 1):
                            row_tops(j, o + 1, p)
                if has(j, o, 1):
                    split_tops(j, o + 1)
                if has(j, o, -1):
                    keep_mix(j, o - 1)
            all_passes(dve, one_pass)
            dve.wait_ge(mix_kept, B)
            for c in range(CH):
                chunk = mix[:, CB * c:CB * c + CB, :]
                nc.vector.tensor_scalar(chunk, chunk, bv[:, 0:1], None, ALU.add).then_inc(biased, 1)
            for c in range(CH):
                goal = x[:, CB * c:CB * c + CB, 0:S]
                dve.wait_ge(projected, c + 1)
                nc.vector.scalar_tensor_tensor(goal, ps[:, c, 0:CT].rearrange("p (b s) -> p b s", s=S), bo[:, 0:1], goal,
                                               ALU.add, ALU.add).then_inc(added, 1)


MARK = -2.0 ** 100


def spacer(n):
    return -2.0 ** (90 + n)


class Router:

    def __init__(self, chip, own, tag, experts, k, bias=None, scale=None):
        nc = chip.nc
        self.chip, self.tag, self.e, self.k, self.scale = chip, tag, experts, k, scale
        e = experts

        def sbuf(name, shape):
            return own.enter_context(nc.sbuf_tensor(tag + name, shape, F32))
        self.bias = bias
        self.top1, self.total = sbuf("top1", [P, NP_]), sbuf("total", [P, NP_])
        self.scores, self.weights = sbuf("scores", [P, NP_, e]), sbuf("weights", [P, NP_, e])
        self.found = sbuf("found", [P, NP_, e + 8 - k])
        self.marked = sbuf("marked", [P, NP_, e + 8 - k])
        self.top8 = sbuf("top8", [P, NP_, 8])
        self.logits_done, self.shifted, self.exp_done, self.chain, self.ready = (
            chip.sem(tag + n) for n in ("logits_done", "shifted", "exp_done", "route_chain", "weights_ready"))
        self.logits = chip.ps[:, 0:2, :].rearrange("p k (t e) -> p (k t) e", e=64)[:, :, 0:e]

    def make_logits(self, pe, source, weight):
        nc = self.chip.nc
        for t in range(NP_):
            mm = nc.tensor.matmul(self.chip.ps[:, t // 8, 64 * (t % 8):64 * (t % 8) + self.e], source[:, P * t:P * t + P], weight,
                                  start=True, stop=True)
        mm.then_inc(self.logits_done, 1)

    def exponentials(self, act):
        act.wait_ge(self.shifted, 1)
        self.chip.nc.scalar.activation(self.scores[:], self.scores[:], ACT.Exp).then_inc(self.exp_done, 1)

    def choose(self, dve):
        nc, e, k = self.chip.nc, self.e, self.k
        step = Step(dve, self.chain)
        for n in range(8 - k):
            nc.vector.memset(self.found[:, :, e + n:e + n + 1], spacer(n))
        dve.wait_ge(self.logits_done, 1)
        step(nc.vector.tensor_reduce(self.top1[:], self.logits, AX_X, ALU.max))
        nc.vector.tensor_tensor(self.scores[:], self.logits, spread(self.top1[:], 2, e), ALU.subtract).then_inc(self.shifted, 1)
        dve.wait_ge(self.exp_done, 1)
        step(nc.vector.tensor_reduce(self.total[:], self.scores[:], AX_X, ALU.add))
        step(nc.vector.reciprocal(self.total[:], self.total[:]))
        step(nc.vector.tensor_tensor(self.scores[:], self.scores[:], spread(self.total[:], 2, e), ALU.mult))
        if self.bias is None:
            step(nc.vector.tensor_copy(self.found[:, :, 0:e], self.scores[:]))
        else:
            step(nc.vector.tensor_tensor(self.found[:, :, 0:e], self.scores[:], spread(self.bias, 1, NP_), ALU.add))
        for t in range(NP_):
            last = nc.vector.max(self.top8[:, t, :], self.found[:, t, 0:e])
        step(last)
        for n in range(8 - k):
            last = nc.vector.memset(self.top8[:, :, k + n:k + n + 1], spacer(n))
        step(last)
        for t in range(NP_):
            last = nc.vector.match_replace(self.marked[:, t, :], self.top8[:, t, :], self.found[:, t, :], MARK)
        step(last)
        if self.scale is not None:
            step(nc.vector.tensor_scalar(self.weights[:], self.marked[:, :, 0:e], MARK, self.scale, ALU.is_equal, ALU.mult))
            nc.vector.tensor_tensor(self.weights[:], self.weights[:], self.scores[:], ALU.mult).then_inc(self.ready, 1)
        else:
            step(nc.vector.tensor_scalar(self.marked[:, :, 0:e], self.marked[:, :, 0:e], MARK, None, ALU.is_equal))
            step(nc.vector.tensor_tensor(self.weights[:], self.marked[:, :, 0:e], self.scores[:], ALU.mult))
            step(nc.vector.tensor_reduce(self.total[:], self.weights[:], AX_X, ALU.add))
            step(nc.vector.reciprocal(self.total[:], self.total[:]))
            nc.vector.tensor_tensor(self.weights[:], self.weights[:], spread(self.total[:], 2, e), ALU.mult).then_inc(self.ready, 1)
        return step


def experts(chip, tag, name, groups, subs, rows, gated, weight_rows):
    nc, ps, xn, x = chip.nc, chip.ps, chip.xn, chip.x
    landed = [chip.sem(tag + "landed%d" % u) for u in range(2)]
    used = [chip.sem(tag + "used%d" % u) for u in range(2)]
    zero_ready, up_done, gate_kept, hidden_ready, weighted, summed, added = (
        chip.sem(tag + k) for k in ("zero_ready", "up_done", "gate_kept", "hidden_ready", "weighted", "summed", "added"))
    M = 3 if gated else 2
    steps = [(u, s, c) for u in range(2) for s in range(subs) for c in range(CH)]
    N = len(steps)
    with ExitStack() as own:
        def sbuf(name, shape):
            return own.enter_context(nc.sbuf_tensor(tag + name, shape, F32))
        w = [sbuf("w%d" % u, [P, subs, M, P]) for u in range(2)]
        share = [sbuf("share%d" % u, [P, B * S]) for u in range(2)]
        silu = [sbuf("silu%d" % k, [P, CT]) for k in range(2)]
        hidden = [sbuf("hidden%d" % k, [P, CT]) for k in range(2)]
        zero = sbuf("zero", [P, P])
        tokens = [xn[:, CB * c:CB * c + CB, 0:S] for c in range(CH)]
        block = own.enter_context(nc.Block(no_gpsimd_drain=True))

        @block.sync
        def _(sp):
            with sp.Fori(0, groups // 2) as i:
                for u in range(2):
                    sp.wait_ge(used[u], i + 1)
                    sp.dma_start(w[u][:], chip.dram[name][bass.ds(2 * i + u, 1)].rearrange("g p s m d -> (g p) s m d")).then_inc(landed[u], 16)
                    for r in range(rows):
                        n = P // rows
                        sp.dma_start(share[u][n * r:n * r + n, :], weight_rows[bass.ds(rows * (2 * i + u) + r, 1), :].to_broadcast([n, B * S])).then_inc(landed[u], 16)

        @block.tensor
        def _(pe):
            def up(i, n):
                u, s, c = steps[n]
                if s == 0 and c == 0:
                    pe.wait_ge(landed[u], 16 * (rows + 1) * i + 16 * (rows + 1))
                for m in range(M - 1):
                    mm = nc.tensor.matmul(ps[:, 4 + 2 * (n % 2) + m, 0:CT], w[u][:, s, m, :], tokens[c], start=True, stop=True)
                mm.then_inc(up_done, 1)

            def down(i, n):
                u, s, c = steps[n]
                pe.wait_ge(hidden_ready, N * i + n + 1)
                mm = nc.tensor.matmul(ps[:, c, 0:CT], w[u][:, s, M - 1, :], hidden[n % 2][:], start=False, stop=False, skip_group_check=True)
                if s == subs - 1 and c == CH - 1:
                    mm.then_inc(used[u], 1)

            pe.wait_ge(zero_ready, 1)
            for c in range(CH):
                nc.tensor.matmul(ps[:, c, 0:CT], zero[:], tokens[c], start=True, stop=False, skip_group_check=True)
            with pe.Fori(0, groups // 2) as i:
                for n in range(N):
                    up(i, n)
                    if n:
                        down(i, n - 1)
                down(i, N - 1)
            for c in range(CH):
                nc.tensor.matmul(ps[:, c, 0:CT], zero[:], tokens[c], start=False, stop=True, skip_group_check=True).then_inc(summed, 1)

        @block.scalar
        def _(act):
            with act.Fori(0, groups // 2) as i:
                for n in range(N):
                    act.wait_ge(up_done, N * i + n + 1)
                    nc.scalar.activation(silu[n % 2][:], ps[:, 4 + 2 * (n % 2), 0:CT], ACT.Silu).then_inc(gate_kept, 1)

        @block.vector
        def _(dve):
            nc.vector.memset(zero[:], 0.0).then_inc(zero_ready, 1)
            for u in range(2):
                nc.vector.memset(chip.credit[:, u:u + 1], 0.0).then_inc(used[u], 1)
            with dve.Fori(0, groups // 2) as i:
                for n in range(N):
                    u, s, c = steps[n]
                    if s == 0 and c == 0:
                        dve.wait_ge(landed[u], 16 * (rows + 1) * i + 16 * (rows + 1))
                    if gated:
                        dve.wait_ge(up_done, N * i + n + 1)
                        nc.vector.tensor_tensor(hidden[n % 2][:], ps[:, 5 + 2 * (n % 2), 0:CT], share[u][:, CT * c:CT * c + CT], ALU.mult).then_inc(weighted, 1)
                        dve.wait_ge(weighted, N * i + n + 1)
                        dve.wait_ge(gate_kept, N * i + n + 1)
                        nc.vector.tensor_tensor(hidden[n % 2][:], hidden[n % 2][:], silu[n % 2][:], ALU.mult).then_inc(hidden_ready, 1)
                    else:
                        dve.wait_ge(gate_kept, N * i + n + 1)
                        nc.vector.tensor_tensor(hidden[n % 2][:], silu[n % 2][:], share[u][:, CT * c:CT * c + CT], ALU.mult).then_inc(hidden_ready, 1)
            for c in range(CH):
                goal = x[:, CB * c:CB * c + CB, 0:S]
                dve.wait_ge(summed, c + 1)
                nc.vector.tensor_tensor(goal, goal, ps[:, c, 0:CT].rearrange("p (b s) -> p b s", s=S), ALU.add).then_inc(added, 1)


def mixture_1(chip):
    nc, ps, xn, x = chip.nc, chip.ps, chip.xn, chip.x
    E_R, E_Z, K = 32, 8, 6
    E = E_R + E_Z
    scratch = nc.dram_tensor("m1_weight_rows", (E, B * S), F32, kind="Internal").ap()
    landed, turned, rows_kept, stored, passed, added, mask_ready, product_ready = (
        chip.sem("m1_" + k) for k in ("landed", "turned", "rows_kept", "stored", "passed", "added", "mask_ready", "product_ready"))
    with ExitStack() as own:
        def sbuf(name, shape):
            return own.enter_context(nc.sbuf_tensor("m1_" + name, shape, F32))
        classifier, bias = sbuf("classifier", [P, E]), sbuf("bias", [P, E])
        rows, passing, product = sbuf("rows", [E, NP_ * P]), sbuf("passing", [E, P]), sbuf("product", [P, CT])
        router = Router(chip, own, "m1_", E, K, bias[:], 2.5)
        flat = xn.rearrange("p b s -> p (b s)")
        block = own.enter_context(nc.Block())

        @block.sync
        def _(sp):
            sp.dma_start(classifier[:], chip.dram["L1_ffn_classifier_weight"]).then_inc(landed, 16)
            sp.dma_start(bias[:], chip.dram["L1_ffn_e_score_correction_bias"].to_broadcast([P, E])).then_inc(landed, 16)
            sp.wait_ge(rows_kept, 1)
            sp.dma_start(scratch.rearrange("e (b s) -> e b s", s=S), rows.rearrange("e (b s) -> e b s", s=SP)[:, :, 0:S]).then_inc(stored, 16)
            sp.wait_ge(stored, 16)

        @block.tensor
        def _(pe):
            pe.wait_ge(landed, 32)
            router.make_logits(pe, flat, classifier[:])
            pe.wait_ge(router.ready, 1)
            for t in range(NP_):
                mm = nc.tensor.transpose(ps[0:E, 4 + t // 4, P * (t % 4):P * (t % 4) + P], router.weights[:, t, :], chip.ident[:])
            mm.then_inc(turned, 1)
            pe.wait_ge(rows_kept, 1)
            pe.wait_ge(mask_ready, 2)
            for c in range(CH):
                nc.tensor.matmul(ps[:, c, 0:CT], passing[:], rows[:, CW * c:CW * c + CW].rearrange("e (b s) -> e b s", s=SP)[:, :, 0:S],
                                 start=True, stop=True).then_inc(passed, 1)

        @block.scalar
        def _(act):
            router.exponentials(act)
            act.wait_ge(turned, 1)
            nc.scalar.copy(rows[:], ps[0:E, 4:8, :].rearrange("e k n -> e (k n)")).then_inc(rows_kept, 1)

        @block.vector
        def _(dve):
            nc.vector.memset(passing[:], 0.0).then_inc(mask_ready, 1)
            dve.wait_ge(mask_ready, 1)
            nc.vector.memset(passing[E_R:E, :], 1.0).then_inc(mask_ready, 1)
            dve.wait_ge(landed, 32)
            router.choose(dve)
            for c in range(CH):
                goal, tokens = (v[:, CB * c:CB * c + CB, 0:S] for v in (x, xn))
                dve.wait_ge(passed, c + 1)
                if c:
                    dve.wait_ge(added, c)
                nc.vector.tensor_tensor(product.rearrange("p (b s) -> p b s", s=S), tokens,
                                        ps[:, c, 0:CT].rearrange("p (b s) -> p b s", s=S), ALU.mult).then_inc(product_ready, 1)
                dve.wait_ge(product_ready, c + 1)
                nc.vector.tensor_tensor(goal, goal, product.rearrange("p (b s) -> p b s", s=S), ALU.add).then_inc(added, 1)
    experts(chip, "e1_", "L1_ffn_experts", E_R // 2, 1, 2, True, scratch)


def mixture_2(chip):
    nc, ps, xn = chip.nc, chip.ps, chip.xn
    E, K, DFF = 8, 2, 512
    scratch = nc.dram_tensor("m2_weight_rows", (E, B * S), F32, kind="Internal").ap()
    landed, turned, rows_kept, stored = (chip.sem("m2_" + k) for k in ("landed", "turned", "rows_kept", "stored"))
    with ExitStack() as own:
        def sbuf(name, shape):
            return own.enter_context(nc.sbuf_tensor("m2_" + name, shape, F32))
        classifier = sbuf("classifier", [P, E])
        rows = sbuf("rows", [E, NP_ * P])
        router = Router(chip, own, "m2_", E, K)
        block = own.enter_context(nc.Block())

        @block.sync
        def _(sp):
            sp.dma_start(classifier[:], chip.dram["L2_ffn_Wr"]).then_inc(landed, 16)
            sp.wait_ge(rows_kept, 1)
            sp.dma_start(scratch.rearrange("e (b s) -> e b s", s=S), rows.rearrange("e (b s) -> e b s", s=SP)[:, :, 0:S]).then_inc(stored, 16)
            sp.wait_ge(stored, 16)

        @block.tensor
        def _(pe):
            pe.wait_ge(landed, 16)
            router.make_logits(pe, xn.rearrange("p b s -> p (b s)"), classifier[:])
            pe.wait_ge(router.ready, 1)
            for t in range(NP_):
                mm = nc.tensor.transpose(ps[0:E, 4 + t // 4, P * (t % 4):P * (t % 4) + P], router.weights[:, t, :], chip.ident[:])
            mm.then_inc(turned, 1)

        @block.scalar
        def _(act):
            router.exponentials(act)
            act.wait_ge(turned, 1)
            nc.scalar.copy(rows[:], ps[0:E, 4:8, :].rearrange("e k n -> e (k n)")).then_inc(rows_kept, 1)

        @block.vector
        def _(dve):
            router.choose(dve)
    experts(chip, "e2_", "L2_ffn_experts", E, DFF // P, 1, False, scratch)


def mixture_3(chip):
    nc, ps, xn = chip.nc, chip.ps, chip.xn
    E, A, K, INTER, HR, NS = 32, 16, 2, 256, P // 2, 6
    CAP = int(1.25 * B * S / E)
    ROUNDS = -(-CAP // 8)
    LAST = CAP - 8 * (ROUNDS - 1)
    T = B * S
    scratch = nc.dram_tensor("m3_weight_scratch", (E, T), F32, kind="Internal").ap()
    scratch_a = nc.dram_tensor("m3_adapter_scratch", (A, T), F32, kind="Internal").ap()
    sems = ("cleared landed tokens_turned tokens_kept stats_ready stats_turned stats_kept hidden_done hidden_kept squared rooted"
            " weights_turned weights_kept scores_ready scores_turned scores_kept chain rows_ready paired paired_kept stored")
    s = {k: chip.sem("m3_" + k) for k in sems.split()}
    with ExitStack() as own:
        def sbuf(name, shape):
            return own.enter_context(nc.sbuf_tensor("m3_" + name, shape, F32))
        r1, r1s, r2, rb = sbuf("r1", [P, P]), sbuf("r1s", [NS, P]), sbuf("r2", [P, E]), sbuf("rb", [P, 1])
        pairs = sbuf("pairs", [E, A])
        by_token, square = sbuf("by_token", [P, NP_, P]), sbuf("square", [P, NP_, P])
        stats = sbuf("stats", [P, NP_, NS])
        stats_t = sbuf("stats_t", [NS, NP_ * P])
        hidden = sbuf("hidden", [P, NP_ * P])
        routed = sbuf("routed", [P, NP_, E])
        weight_rows = sbuf("weight_rows", [E, NP_ * P])
        score_rows, top8 = sbuf("score_rows", [E, T + 8 - LAST]), sbuf("row_top8", [E, 8])
        final, adapters = sbuf("final", [E, T]), sbuf("adapters", [A, CH, CT])
        router = Router(chip, own, "m3_", E, K)
        flat = xn.rearrange("p b s -> p (b s)")
        block = own.enter_context(nc.Block())

        def real(rows):
            return rows.rearrange("e (b s) -> e b s", s=SP)[:, :, 0:S]

        @block.sync
        def _(sp):
            sp.wait_ge(s["cleared"], 4)
            for dst, name in ((r1[:, 0:HR], "r1"), (r1s[:, 0:HR], "r1_stats"), (r2[0:HR, :], "r2"), (rb[0:HR], "r1_b"), (pairs[:], "pairs")):
                sp.dma_start(dst, chip.dram["L3_ffn_" + name]).then_inc(s["landed"], 16)
            sp.wait_ge(s["rows_ready"], 1)
            sp.dma_start(scratch, final[:]).then_inc(s["stored"], 16)
            sp.wait_ge(s["paired_kept"], 4)
            sp.dma_start(scratch_a, adapters.rearrange("a c n -> a (c n)")).then_inc(s["stored"], 16)
            sp.wait_ge(s["stored"], 32)

        @block.tensor
        def _(pe):
            for t in range(NP_):
                mm = nc.tensor.transpose(ps[:, t // 4, P * (t % 4):P * (t % 4) + P], flat[:, P * t:P * t + P], chip.ident[:])
            mm.then_inc(s["tokens_turned"], 1)
            pe.wait_ge(s["stats_ready"], 1)
            for t in range(NP_):
                mm = nc.tensor.transpose(ps[0:NS, 4 + t // 4, P * (t % 4):P * (t % 4) + P], stats[:, t, :], chip.ident[:])
            mm.then_inc(s["stats_turned"], 1)
            pe.wait_ge(s["stats_kept"], 1)
            pe.wait_ge(s["landed"], 5 * 16)
            for c in range(CH):
                nc.tensor.matmul(ps[:, c, :], r1[:], flat[:, CW * c:CW * c + CW], start=True, stop=False)
                nc.tensor.matmul(ps[:, c, :], r1s[:], stats_t[:, CW * c:CW * c + CW], start=False, stop=True).then_inc(s["hidden_done"], 1)
            pe.wait_ge(s["hidden_kept"], CH)
            router.make_logits(pe, hidden, r2[:])
            pe.wait_ge(router.ready, 1)
            for t in range(NP_):
                mm = nc.tensor.transpose(ps[0:E, 4 + t // 4, P * (t % 4):P * (t % 4) + P], router.weights[:, t, :], chip.ident[:])
            mm.then_inc(s["weights_turned"], 1)
            pe.wait_ge(s["scores_ready"], 1)
            for t in range(NP_):
                mm = nc.tensor.transpose(ps[0:E, t // 4, P * (t % 4):P * (t % 4) + P], routed[:, t, :], chip.ident[:])
            mm.then_inc(s["scores_turned"], 1)
            pe.wait_ge(s["rows_ready"], 1)
            for c in range(CH):
                nc.tensor.matmul(ps[0:A, 4 + c, 0:CT], pairs[:], final[:, CT * c:CT * c + CT], start=True, stop=True).then_inc(s["paired"], 1)

        @block.scalar
        def _(act):
            act.wait_ge(s["tokens_turned"], 1)
            nc.scalar.copy(by_token[:], ps[:, 0:4, :].rearrange("p k (t d) -> p (k t) d", d=P)).then_inc(s["tokens_kept"], 1)
            act.wait_ge(s["squared"], 1)
            nc.scalar.activation(stats[:, :, 1], stats[:, :, 1], ACT.Sqrt, scale=1.0 / (P - 1)).then_inc(s["rooted"], 1)
            nc.scalar.activation(stats[:, :, 4], stats[:, :, 4], ACT.Sqrt).then_inc(s["rooted"], 1)
            act.wait_ge(s["stats_turned"], 1)
            nc.scalar.copy(stats_t[:], ps[0:NS, 4:8, :].rearrange("e k n -> e (k n)")).then_inc(s["stats_kept"], 1)
            act.wait_ge(s["landed"], 5 * 16)
            for c in range(CH):
                act.wait_ge(s["hidden_done"], c + 1)
                nc.scalar.activation(hidden[:, CW * c:CW * c + CW], ps[:, c, :], ACT.Gelu, bias=rb[:, 0:1]).then_inc(s["hidden_kept"], 1)
            router.exponentials(act)
            act.wait_ge(s["weights_turned"], 1)
            nc.scalar.copy(weight_rows[:], ps[0:E, 4:8, :].rearrange("e k n -> e (k n)")).then_inc(s["weights_kept"], 1)
            for c in range(CH):
                act.wait_ge(s["paired"], c + 1)
                nc.scalar.copy(adapters[:, c, :], ps[0:A, 4 + c, 0:CT]).then_inc(s["paired_kept"], 1)

        @block.vector
        def _(dve):
            step = Step(dve, s["chain"])
            for buffer in (r1, r1s, r2, rb):
                nc.vector.memset(buffer[:], 0.0).then_inc(s["cleared"], 1)
            dve.wait_ge(s["tokens_kept"], 1)
            nc.vector.tensor_reduce(stats[:, :, 2], by_token[:], AX_X, ALU.min)
            nc.vector.tensor_reduce(stats[:, :, 3], by_token[:], AX_X, ALU.max)
            step(nc.vector.tensor_reduce(stats[:, :, 0], by_token[:], AX_X, ALU.add))
            step(nc.vector.tensor_scalar(stats[:, :, 0], stats[:, :, 0], 1.0 / P, None, ALU.mult))
            step(nc.vector.tensor_tensor(square[:], by_token[:], by_token[:], ALU.mult))
            step(nc.vector.tensor_reduce(stats[:, :, 4], square[:], AX_X, ALU.add))
            step(nc.vector.scalar_tensor_tensor(square[:], by_token[:], -1.0, by_token[:], ALU.mult, ALU.max))
            step(nc.vector.tensor_scalar(square[:], square[:], 1e-6, None, ALU.is_lt))
            step(nc.vector.tensor_reduce(stats[:, :, 5], square[:], AX_X, ALU.add))
            step(nc.vector.tensor_scalar(stats[:, :, 5], stats[:, :, 5], 1.0 / P, None, ALU.mult))
            step(nc.vector.tensor_tensor(by_token[:], by_token[:], spread(stats[:, :, 0], 2, P), ALU.subtract))
            step(nc.vector.tensor_tensor(by_token[:], by_token[:], by_token[:], ALU.mult))
            nc.vector.tensor_reduce(stats[:, :, 1], by_token[:], AX_X, ALU.add).then_inc(s["squared"], 1)
            dve.wait_ge(s["rooted"], 2)
            nc.vector.memset(chip.credit[:, 2:3], 0.0).then_inc(s["stats_ready"], 1)
            router.choose(dve)
            step(nc.vector.tensor_scalar(routed[:], router.marked[:, :, 0:E], -1.0, None, ALU.add))
            step(nc.vector.tensor_tensor(router.scores[:], router.scores[:], router.marked[:, :, 0:E], ALU.mult))
            nc.vector.tensor_tensor(routed[:], routed[:], router.scores[:], ALU.add).then_inc(s["scores_ready"], 1)
            for n in range(8 - LAST):
                nc.vector.memset(score_rows[:, T + n:T + n + 1], spacer(n))
            dve.wait_ge(s["scores_turned"], 1)
            for c in range(CH):
                last = nc.vector.tensor_copy(score_rows[:, CT * c:CT * c + CT].rearrange("e (b s) -> e b s", s=S),
                                             ps[0:E, c, :].rearrange("e (b s) -> e b s", s=SP)[:, :, 0:S])
            step(last)
            for n in range(ROUNDS):
                step(nc.vector.max(top8[:], score_rows[:, 0:T]))
                if n == ROUNDS - 1:
                    for k in range(LAST, 8):
                        last = nc.vector.memset(top8[:, k:k + 1], spacer(k - LAST))
                    step(last)
                step(nc.vector.match_replace(score_rows[:], top8[:], score_rows[:], MARK))
            step(nc.vector.tensor_scalar(final[:], score_rows[:, 0:T], MARK, None, ALU.is_equal))
            dve.wait_ge(s["weights_kept"], 1)
            nc.vector.tensor_tensor(final.rearrange("e (b s) -> e b s", s=S), final.rearrange("e (b s) -> e b s", s=S),
                                    real(weight_rows), ALU.mult).then_inc(s["rows_ready"], 1)
    experts(chip, "e3_", "L3_ffn_experts", E, INTER // P, 1, True, scratch)
    experts(chip, "e4_", "L3_ffn_adapters", A, 1, 1, True, scratch_a)


def linear_attention_2(chip):
    nc, ps, xn, x = chip.nc, chip.ps, chip.xn, chip.x
    DH, HG, HJ = 32, 4, HX // 4
    HP = HX // 2
    sems = ("weights_landed cleared tokens_ready q_done k_done v_done q_kept k_kept v_kept products_done masked"
            " mixing_done mixing_kept mixed mixed_kept projected added")
    s = {k: chip.sem("la_" + k) for k in sems.split()}
    with ExitStack() as own:
        def sbuf(name, shape):
            return own.enter_context(nc.sbuf_tensor("la_" + name, shape, F32))
        wq, wk, wv = (sbuf(n, [P, HX * DH]) for n in ("wq", "wk", "wv"))
        wo = sbuf("wo", [P, 2, HP, P])
        quarter, left, right, decay = sbuf("quarter", [P, HG]), sbuf("left", [P, SP]), sbuf("right", [P, SP]), sbuf("decay", [P, SP])
        tokens = sbuf("tokens", [P, P])
        q_diag = sbuf("q_diag", [P, HJ, HG, P])
        k_twice = sbuf("k_twice", [P, HJ, 2, 2, SP])
        v_diag = sbuf("v_diag", [P, HX, 2, DH])
        lhs, rhs = sbuf("lhs", [P, 2, HX, SP]), sbuf("rhs", [P, 2, HX, SP])
        mixing = sbuf("mixing", [P, HX, SP])
        mixed = sbuf("mixed", [P, HP, NP_, SP])
        block = own.enter_context(nc.Block(no_gpsimd_drain=True))

        @block.sync
        def _(sp):
            for dst, name in ((wq, "Wq"), (wk, "Wk"), (wv, "Wv"), (wo, "Wo")):
                sp.dma_start(dst[:], chip.dram["L2_attn_" + name]).then_inc(s["weights_landed"], 16)
            for dst, name in ((quarter, "quarter"), (left, "la_left"), (right, "la_right"), (decay, "la_decay")):
                sp.dma_start(dst[:], chip.dram[name]).then_inc(s["weights_landed"], 16)

        @block.tensor
        def _(pe):
            pe.wait_ge(s["weights_landed"], 8 * 16)
            with pe.Fori(0, NP_) as i:
                pe.wait_ge(s["tokens_ready"], i + 1)
                pe.wait_ge(s["mixing_kept"], i + 1)
                for w, bank, done in ((wq, 0, "q_done"), (wk, 1, "k_done")):
                    for j in range(HJ):
                        mm = nc.tensor.matmul(ps[:, bank, P * j:P * j + P], w[:, P * j:P * j + P], tokens[:], start=True, stop=True)
                    mm.then_inc(s[done], 1)
                for b in range(2):
                    mm = nc.tensor.matmul(ps[SP * b:SP * b + SP, 2, :], tokens[:, SP * b:SP * b + SP], wv[:], start=True, stop=True)
                mm.then_inc(s["v_done"], 1)
                pe.wait_ge(s["q_kept"], i + 1)
                pe.wait_ge(s["k_kept"], i + 1)
                for b in range(2):
                    for j in range(HJ):
                        mm = nc.tensor.matmul(ps[:, 3 + 2 * b + j // 2, 256 * (j % 2):256 * (j % 2) + 256],
                                              k_twice[:, j, b].rearrange("p r s -> p (r s)"),
                                              q_diag[:, j, :, SP * b:SP * b + SP], start=True, stop=True)
                mm.then_inc(s["products_done"], 1)
                pe.wait_ge(s["masked"], i + 1)
                for h in range(HX):
                    for b in range(2):
                        mm = nc.tensor.matmul(ps[SP * b:SP * b + SP, h // 8, SP * (h % 8):SP * (h % 8) + SP], lhs[:, b, h, :],
                                              rhs[:, b, h, :], start=True, stop=True)
                mm.then_inc(s["mixing_done"], 1)
                pe.wait_ge(s["mixing_kept"], i + 2)
                pe.wait_ge(s["v_kept"], i + 1)
                pe.wait_ge(s["mixed_kept"], i + 1)
                for h in range(HX):
                    r = 64 * (h % 2)
                    mm = nc.tensor.matmul(ps[r:r + 64, 7, SP * (h // 2):SP * (h // 2) + SP], v_diag[:, h].rearrange("p b d -> p (b d)"),
                                          mixing[:, h, :], start=True, stop=True)
                mm.then_inc(s["mixed"], 1)
            pe.wait_ge(s["mixed_kept"], NP_ + 1)
            for n in range(4):
                b, half = n % 2, n // 2
                for j in range(HP):
                    mm = nc.tensor.matmul(ps[:, n, 0:CT], wo[:, b, j, :], mixed[:, j, 8 * half:8 * half + 8, 0:S],
                                          start=(j == 0), stop=(j == HP - 1))
                mm.then_inc(s["projected"], 1)

        @block.scalar
        def _(act):
            act.wait_ge(s["weights_landed"], 8 * 16)
            act.wait_ge(s["cleared"], 1)
            with act.Fori(0, NP_) as i:
                act.wait_ge(s["v_done"], i + 1)
                nc.scalar.copy(tokens[:], xn.rearrange("p b s -> p (b s)")[:, bass.ds(i * P, P)]).then_inc(s["tokens_ready"], 1)
                act.wait_ge(s["q_done"], i + 1)
                for g in range(HG):
                    last = nc.scalar.mul(q_diag[:, :, g, :], ps[:, 0, :].rearrange("p (j c) -> p j c", c=P), quarter[:, g:g + 1])
                last.then_inc(s["q_kept"], 1)
                act.wait_ge(s["v_done"], i + 2)
                for b in range(2):
                    r = slice(64 * b, 64 * b + 64)
                    last = nc.scalar.copy(v_diag[r, :, b, :], ps[r, 2, :].rearrange("p (h d) -> p h d", d=DH))
                last.then_inc(s["v_kept"], 1)
                act.wait_ge(s["mixed"], i + 1)
                nc.scalar.copy(mixed[:, :, bass.ds(i, 1), :].rearrange("p j n s -> p j (n s)"),
                               ps[:, 7, :].rearrange("p (j s) -> p j s", s=SP)).then_inc(s["mixed_kept"], 1)

        @block.vector
        def _(dve):
            nc.vector.memset(v_diag[:], 0.0).then_inc(s["cleared"], 1)
            for n, name in enumerate(("v_done", "mixing_kept", "mixed_kept")):
                nc.vector.memset(chip.credit[:, n:n + 1], 0.0).then_inc(s[name], 1)
            dve.wait_ge(s["weights_landed"], 8 * 16)
            with dve.Fori(0, NP_) as i:
                dve.wait_ge(s["k_done"], i + 1)
                for r in range(2):
                    last = nc.vector.tensor_copy(k_twice[:, :, :, r, :], ps[:, 1, :].rearrange("p (j b s) -> p j b s", j=HJ, b=2))
                last.then_inc(s["k_kept"], 1)
                dve.wait_ge(s["products_done"], i + 1)
                products = ps[:, 3:7, :].rearrange("p k (h s) -> p (k h) s", s=SP)
                nc.vector.tensor_tensor(lhs.rearrange("p b h s -> p (b h) s"), products, spread(left[:], 1, 2 * HX), ALU.mult)
                nc.vector.tensor_tensor(rhs.rearrange("p b h s -> p (b h) s"), products, spread(right[:], 1, 2 * HX), ALU.mult).then_inc(s["masked"], 1)
                dve.wait_ge(s["mixing_done"], i + 1)
                nc.vector.tensor_tensor(mixing[:], ps[:, 0:2, :].rearrange("p k (h s) -> p (k h) s", s=SP), spread(decay[:], 1, HX),
                                        ALU.mult).then_inc(s["mixing_kept"], 1)
            for n in range(4):
                b, half = n % 2, n // 2
                goal = x.rearrange("p (n b) s -> p n b s", b=2)[:, 8 * half:8 * half + 8, b, 0:S]
                dve.wait_ge(s["projected"], n + 1)
                nc.vector.tensor_tensor(goal, goal, ps[:, n, 0:CT].rearrange("p (n s) -> p n s", s=S), ALU.add).then_inc(s["added"], 1)


def rotary_attention(chip, tag, src, res, latent):
    nc, ps = chip.nc, chip.ps
    KV, REP = 4, HX // 4
    LAT = 32
    U = 2 * CH
    SCALE = DX ** -0.5
    sems = ("cleared landed spread latent_done latent_kept made kept rotated turned_cos roped squared power log root normed"
            " pair_ready diag_ready scores_done shifted exp_done turned turned_kept v_done v_kept mixed scaled flipped flipped_kept"
            " projected added chain")
    s = {k: chip.sem(tag + k) for k in sems.split()}
    with ExitStack() as own:
        def sbuf(name, shape):
            return own.enter_context(nc.sbuf_tensor(tag + name, shape, F32))
        wq, wo, rot, mean8 = (sbuf(n, [P, P]) for n in ("wq", "wo", "rot", "mean8"))
        wdown = sbuf("wdown", [P, P])
        wkv = sbuf("wkv", [P, 2, KV * DX])
        wk, wv = sbuf("wk", [P, P]), sbuf("wv", [P, 2, P])
        cos, sin, mask, own_head = sbuf("cos", [P, S]), sbuf("sin", [P, S]), sbuf("mask", [P, S]), sbuf("own_head", [P, HX])
        low = sbuf("low", [P, B, SP])
        qn, kn = sbuf("qn", [P, B, SP]), sbuf("kn", [P, B, SP])
        raw = [sbuf("raw%d" % n, [P, CT]) for n in range(4)]
        work = [sbuf("work%d" % n, [P, CT]) for n in range(4)]
        source = low if latent else src
        q_pair, v_pair = sbuf("q_pair", [P, P]), sbuf("v_pair", [P, P])
        k_diag = sbuf("k_diag", [P, 2, HX, S])
        probs, probs_t = sbuf("probs", [P, HX, SP]), sbuf("probs_t", [P, HX // 2, P])
        top, total, inverse = (sbuf(n, [P, HX]) for n in ("top", "total", "inverse"))
        values = sbuf("values", [P, 2, P])
        mix = sbuf("mix", [P, P])
        mix_t = sbuf("mix_t", [P, B, SP])
        first = chip.sem(tag + "weights_ready")
        loads = [(wq[:], "wq"), (wo[:], "wo")]
        if latent:
            loads += [(wdown[:, 0:LAT], "kv_down"), (wkv[0:LAT, 0], "k_up"), (wkv[0:LAT, 1], "v_up")]
        else:
            loads += [(wkv[:, 0], "wk"), (wkv[:, 1], "wv")]
        consts = ((rot, "rotate"), (mean8, "mean8"), (cos, tag + "cos"), (sin, tag + "sin"), (mask, tag + "mask"), (own_head, "own_head"))
        n_loads = len(loads) + len(consts)

        def unit(n):
            c = n % CH
            return c, n < CH

        with nc.Block(no_gpsimd_drain=True) as block:
            @block.sync
            def _(sp):
                sp.wait_ge(s["cleared"], 2)
                for dst, name in loads:
                    sp.dma_start(dst, chip.dram["L3_attn_" + tag + name]).then_inc(s["landed"], 16)
                for dst, name in consts:
                    sp.dma_start(dst[:], chip.dram[name]).then_inc(s["landed"], 16)

            @block.tensor
            def _(pe):
                pe.wait_ge(s["landed"], 16 * n_loads)
                if latent:
                    for c in range(CH):
                        nc.tensor.matmul(ps[:, 4 + c, 0:CT], wdown[:], src[:, CB * c:CB * c + CB, 0:S], start=True, stop=True).then_inc(s["latent_done"], 1)
                    pe.wait_ge(s["latent_kept"], CH)
                pe.wait_ge(first, 1)

                def make(n):
                    c, queries = unit(n)
                    t = (src if queries else source)[:, CB * c:CB * c + CB, 0:S]
                    if n >= 4:
                        pe.wait_ge(s["log"], n - 3)
                    nc.tensor.matmul(ps[:, n % 4, 0:CT], (wq if queries else wk)[:], t, start=True, stop=True).then_inc(s["made"], 1)

                def rotate(n):
                    pe.wait_ge(s["kept"], n + 1)
                    nc.tensor.matmul(ps[:, 4 + n % 4, 0:CT], rot[:], raw[n % 4][:], start=True, stop=True).then_inc(s["rotated"], 1)

                def power(n):
                    pe.wait_ge(s["squared"], n + 1)
                    nc.tensor.matmul(ps[:, n % 4, 0:CT], mean8[:], work[n % 4][:], start=True, stop=True).then_inc(s["power"], 1)

                for half in range(2):
                    for n in range(4 * half, 4 * half + 4):
                        make(n)
                    for n in range(4 * half, 4 * half + 4):
                        rotate(n)
                    for n in range(4 * half, 4 * half + 4):
                        power(n)

            @block.scalar
            def _(act):
                if latent:
                    for c in range(CH):
                        act.wait_ge(s["latent_done"], c + 1)
                        nc.scalar.copy(low[:, CB * c:CB * c + CB, 0:S], ps[:, 4 + c, 0:CT].rearrange("p (b s) -> p b s", s=S)).then_inc(s["latent_kept"], 1)
                for half in range(2):
                    units = range(4 * half, 4 * half + 4)
                    for n in units:
                        act.wait_ge(s["made"], n + 1)
                        if n >= 4:
                            act.wait_ge(s["normed"], n - 3)
                        nc.scalar.copy(raw[n % 4][:], ps[:, n % 4, 0:CT]).then_inc(s["kept"], 1)
                    for n in units:
                        act.wait_ge(s["roped"], n + 1)
                        nc.scalar.activation(work[n % 4][:], raw[n % 4][:], ACT.Square).then_inc(s["squared"], 1)
                    for n in units:
                        act.wait_ge(s["power"], n + 1)
                        nc.scalar.activation(work[n % 4][:], ps[:, n % 4, 0:CT], ACT.Ln, bias=chip.eps[:, 1:2]).then_inc(s["log"], 1)
                        act.wait_ge(s["log"], n + 1)
                        nc.scalar.activation(work[n % 4][:], work[n % 4][:], ACT.Exp, scale=-0.5).then_inc(s["root"], 1)

            @block.vector
            def _(dve):
                step = Step(dve, s["chain"])
                nc.vector.memset(low[:], 0.0)
                nc.vector.memset(qn[:], 0.0)
                nc.vector.memset(kn[:], 0.0)
                nc.vector.memset(probs[:], 0.0)
                nc.vector.memset(wdown[:], 0.0).then_inc(s["cleared"], 1)
                nc.vector.memset(wkv[:], 0.0).then_inc(s["cleared"], 1)
                step(nc.vector.memset(wv[:], 0.0))
                dve.wait_ge(s["landed"], 16 * n_loads)
                for kv in range(KV):
                    nc.vector.tensor_copy(wk[:, REP * DX * kv:REP * DX * (kv + 1)].rearrange("p (r d) -> p r d", d=DX),
                                          spread(wkv[:, 0, DX * kv:DX * kv + DX], 1, REP))
                    for odd in range(2):
                        v4 = wv[:, odd, REP * DX * kv:REP * DX * (kv + 1)].rearrange("p (r d) -> p r d", d=DX)
                        last = nc.vector.tensor_copy(v4[:, odd::2, :], spread(wkv[:, 1, DX * kv:DX * kv + DX], 1, REP // 2))
                last.then_inc(first, 1)
                for half in range(2):
                    units = range(4 * half, 4 * half + 4)
                    for n in units:
                        r3, w3 = (v[n % 4].rearrange("p (b s) -> p b s", s=S) for v in (raw, work))
                        dve.wait_ge(s["rotated"], n + 1)
                        step(nc.vector.tensor_tensor(w3, ps[:, 4 + n % 4, 0:CT].rearrange("p (b s) -> p b s", s=S), spread(sin[:], 1, CB), ALU.mult))
                        step(nc.vector.tensor_tensor(r3, r3, spread(cos[:], 1, CB), ALU.mult))
                        nc.vector.tensor_tensor(r3, r3, w3, ALU.add).then_inc(s["roped"], 1)
                    for n in units:
                        c, queries = unit(n)
                        r3, w3 = (v[n % 4].rearrange("p (b s) -> p b s", s=S) for v in (raw, work))
                        dve.wait_ge(s["root"], n + 1)
                        nc.vector.tensor_tensor((qn if queries else kn)[:, CB * c:CB * c + CB, 0:S], r3, w3, ALU.mult).then_inc(s["normed"], 1)

        with nc.Block(no_gpsimd_drain=True) as block:
            @block.tensor
            def _(pe):
                with pe.Fori(0, NP_) as i:
                    pe.wait_ge(s["flipped_kept"], i + 1)
                    pe.wait_ge(s["pair_ready"], 2 * i + 2)
                    for b in range(2):
                        for odd in range(2):
                            mm = nc.tensor.matmul(ps[64 * odd:64 * odd + 64, 4, P * b:P * b + P], v_pair[:, SP * b:SP * b + SP], wv[:, odd, :],
                                                  start=True, stop=True)
                    mm.then_inc(s["v_done"], 1)
                    pe.wait_ge(s["diag_ready"], i + 1)
                    for half in range(2):
                        for b in range(2):
                            mm = nc.tensor.matmul(ps[SP * b:SP * b + SP, half, :].rearrange("p (h s) -> p h s", s=SP)[:, :, 0:S],
                                                  q_pair[:, SP * b:SP * b + SP], k_diag[:, b, 8 * half:8 * half + 8, :], start=True, stop=True)
                    mm.then_inc(s["scores_done"], 1)
                    pe.wait_ge(s["exp_done"], i + 1)
                    for j in range(HX // 2):
                        mm = nc.tensor.transpose(ps[:, 2 + j // 4, P * (j % 4):P * (j % 4) + P],
                                                 probs[:, 2 * j:2 * j + 2, :].rearrange("p h s -> p (h s)"), chip.ident[:])
                    mm.then_inc(s["turned"], 1)
                    pe.wait_ge(s["turned_kept"], i + 1)
                    pe.wait_ge(s["v_kept"], i + 1)
                    for j in range(HX // 2):
                        for b in range(2):
                            mm = nc.tensor.matmul(ps[SP * b:SP * b + SP, 5, 16 * j:16 * j + 16], probs_t[:, j, SP * b:SP * b + SP],
                                                  values[:, b, 16 * j:16 * j + 16], start=True, stop=True)
                    mm.then_inc(s["mixed"], 1)
                    pe.wait_ge(s["scaled"], i + 1)
                    nc.tensor.transpose(ps[:, 4, 0:P], mix[:], chip.ident[:]).then_inc(s["flipped"], 1)
                pe.wait_ge(s["flipped_kept"], NP_ + 1)
                for c in range(CH):
                    nc.tensor.matmul(ps[:, c, 0:CT], wo[:], mix_t[:, CB * c:CB * c + CB, 0:S], start=True, stop=True).then_inc(s["projected"], 1)

            @block.scalar
            def _(act):
                with act.Fori(0, NP_) as i:
                    act.wait_ge(s["scores_done"], i + 1)
                    for dst, v in ((q_pair, qn), (v_pair, source)):
                        nc.scalar.copy(dst[:], v.rearrange("p b s -> p (b s)")[:, bass.ds(i * P, P)]).then_inc(s["pair_ready"], 1)
                    act.wait_ge(s["v_done"], i + 1)
                    nc.scalar.copy(values[:], ps[:, 4, 0:2 * P].rearrange("p (b d) -> p b d", d=P)).then_inc(s["v_kept"], 1)
                    act.wait_ge(s["shifted"], i + 1)
                    nc.scalar.activation(probs[:, :, 0:S], probs[:, :, 0:S], ACT.Exp).then_inc(s["exp_done"], 1)
                    act.wait_ge(s["turned"], i + 1)
                    nc.scalar.copy(probs_t[:], ps[:, 2:4, :].rearrange("p k (j c) -> p (k j) c", c=P)).then_inc(s["turned_kept"], 1)
                    act.wait_ge(s["flipped"], i + 1)
                    nc.scalar.copy(mix_t.rearrange("p b s -> p (b s)")[:, bass.ds(i * P, P)], ps[:, 4, 0:P]).then_inc(s["flipped_kept"], 1)

            @block.vector
            def _(dve):
                for n, name in enumerate(("scores_done", "flipped_kept")):
                    nc.vector.memset(chip.credit[:, n:n + 1], 0.0).then_inc(s[name], 1)
                done = s["chain"]
                base = 1 + 2 * U
                with dve.Fori(0, NP_) as i:
                    dve.wait_ge(s["scores_done"], i + 1)
                    for b in range(2):
                        last = nc.vector.tensor_tensor(k_diag[:, b], spread(kn[:, bass.ds(2 * i + b, 1), 0:S].rearrange("p b s -> p (b s)"), 1, HX),
                                                       spread(own_head[:], 2, S), ALU.mult)
                    last.then_inc(s["diag_ready"], 1)
                    dve.wait_ge(s["scores_done"], i + 2)
                    scores = ps[:, 0:2, :].rearrange("p k (h s) -> p (k h) s", s=SP)[:, :, 0:S]
                    step = Step(dve, done, 4 * i + base)
                    step(nc.vector.scalar_tensor_tensor(probs[:, :, 0:S], scores, SCALE, spread(mask[:], 1, HX), ALU.mult, ALU.add))
                    step(nc.vector.tensor_reduce(top[:], probs[:, :, 0:S], AX_X, ALU.max))
                    nc.vector.tensor_tensor(probs[:, :, 0:S], probs[:, :, 0:S], spread(top[:], 2, S), ALU.subtract).then_inc(s["shifted"], 1)
                    dve.wait_ge(s["exp_done"], i + 1)
                    step(nc.vector.tensor_reduce(total[:], probs[:, :, 0:S], AX_X, ALU.add))
                    step(nc.vector.reciprocal(inverse[:], total[:]))
                    dve.wait_ge(s["mixed"], i + 1)
                    nc.vector.tensor_tensor(mix.rearrange("p (h d) -> p h d", d=DX), ps[:, 5, 0:P].rearrange("p (h d) -> p h d", d=DX),
                                            spread(inverse[:], 2, DX), ALU.mult).then_inc(s["scaled"], 1)
                for c in range(CH):
                    goal = res[:, CB * c:CB * c + CB, 0:S]
                    dve.wait_ge(s["projected"], c + 1)
                    nc.vector.tensor_tensor(goal, goal, ps[:, c, 0:CT].rearrange("p (b s) -> p b s", s=S), ALU.add).then_inc(s["added"], 1)


def rotary_attention_3(chip):
    nc, x, xn = chip.nc, chip.x, chip.xn
    landed, added = chip.sem("ra_norms_landed"), chip.sem("ra_added")
    with ExitStack() as own:
        norms = own.enter_context(nc.sbuf_tensor("ra_norms", [P, 2], F32))
        normed = own.enter_context(nc.sbuf_tensor("ra_normed", [P, B, SP], F32))
        with nc.Block(no_gpsimd_drain=True) as block:
            @block.sync
            def _(sp):
                sp.dma_start(norms[:], chip.dram["L3_attn_norms"]).then_inc(landed, 16)
                sp.wait_ge(landed, 16)
        normalise(chip, xn, normed, False, norms[:, 0:1])
        rotary_attention(chip, "g_", normed, xn, True)
        normalise(chip, xn, normed, False, norms[:, 1:2])
        rotary_attention(chip, "l_", normed, xn, False)
        with nc.Block(no_gpsimd_drain=True) as block:
            @block.vector
            def _(dve):
                nc.vector.tensor_tensor(x[:, :, 0:S], x[:, :, 0:S], xn[:, :, 0:S], ALU.add).then_inc(added, 1)


STAGES = [self_attention_0, context_mixing, coupled_twist, gated_recurrence, lambda chip: cross_attention(chip, 1, DX ** -0.5),
          mixture_1, linear_attention_2, lambda chip: cross_attention(chip, 2, P ** -0.5), mixture_2,
          rotary_attention_3, lambda chip: cross_attention(chip, 3, DX ** -0.5), mixture_3]


def more_layouts(a, d):
    ctx = a["ctx_1024"]
    d["ctx_t"] = ctx.transpose(0, 2, 1)
    d["ctx_n"] = ctx.reshape(B, NC_, KC, P).transpose(0, 2, 1, 3)
    for k in ("w1", "w2", "w3", "w4"):
        d["L0_ffn_cn_" + k] = a["L0_ffn_cn_" + k]
    for k in ("w1", "w2", "w3"):
        d["L0_ffn_gc_" + k] = a["L0_ffn_gc_" + k]
    for k in ("cn_b1", "cn_b2", "cn_b3", "cn_b4", "gc_b1", "gc_b2", "gc_b3", "adaptive_range"):
        d["L0_ffn_" + k] = a["L0_ffn_" + k].reshape(-1, 1)
    twist = np.zeros((P, P), np.float32)
    for m in range(P):
        twist[(m + 64) % P, m] = (1.0, -1.0, -1.0, 1.0)[m // 32]
    d["twist"] = twist
    for k in ("Wr_w", "Wi_w", "out_w"):
        d["L1_attn_" + k] = a["L1_attn_" + k].T
    d["L1_attn_conv_weight"] = a["L1_attn_conv_weight"][:, 0, :]
    for k in ("conv_bias", "Wr_b", "Wi_b", "log_a", "norm_w"):
        d["L1_attn_" + k] = a["L1_attn_" + k].reshape(-1, 1)
    for n in (1, 2, 3):
        for k in ("Wq", "Wk", "Wv", "Wo"):
            w = a["L%d_xattn_%s" % (n, k)]
            d["L%d_xattn_%s" % (n, k)] = w if n == 1 or (n == 2 and k == "Wo") else w.transpose(1, 0, 2).reshape(P, P) if n == 2 else w.T
        for k in ("Wq", "Wk"):
            w = d["L%d_xattn_%s" % (n, k)]
            d["L%d_xattn_%s" % (n, k)] = w.reshape(P, PR, 2, DX).transpose(0, 2, 3, 1).reshape(P, P)
        for k in ("bq", "bk"):
            a["L%d_xattn_%s" % (n, k)] = a["L%d_xattn_%s" % (n, k)].reshape(PR, 2, DX).transpose(1, 2, 0)
        for k in ("bq", "bk", "bv", "bo"):
            d["L%d_xattn_%s" % (n, k)] = a["L%d_xattn_%s" % (n, k)].reshape(-1, 1)
    head_of_feature = np.arange(P) // DX
    d["own_head"] = (head_of_feature[:, None] == np.arange(HX)).astype(np.float32)
    row = np.arange(P)[:, None]
    d["place"] = np.zeros((P, 2, 2, 2, 32), np.float32)
    for parity in range(2):
        for odd in range(2):
            for f in range(DX * parity, DX * parity + DX):
                d["place"][f:P:32, parity, odd, 0, PF * odd + f] = 1.0
                d["place"][PF:P:32, parity, odd, 1, PF * odd + f] = 1.0
    d["pair_rows"] = (((row - TALL) % PR == np.arange(PR)) & (row >= TALL) & (row < TALL + PARTS * PR)).astype(np.float32)


    def blocks(*parts):
        return np.stack(parts, axis=3)

    w = a["L1_ffn_gate_up_proj"][:32].reshape(16, 2, 2, 64, P)
    gate, up = (w[:, :, k].reshape(16, 1, P, P).transpose(0, 3, 1, 2) for k in range(2))
    down = a["L1_ffn_down_proj"].reshape(16, 2, P, 64).transpose(0, 1, 3, 2).reshape(16, P, 1, P)
    d["L1_ffn_experts"] = blocks(gate, up, down)
    d["L1_ffn_classifier_weight"] = a["L1_ffn_classifier_weight"].T
    d["L1_ffn_e_score_correction_bias"] = a["L1_ffn_e_score_correction_bias"].reshape(1, -1)
    d["L2_ffn_Wr"] = a["L2_ffn_Wr"].T
    d["L2_ffn_experts"] = blocks(a["L2_ffn_W1"].reshape(8, 4, P, P).transpose(0, 3, 1, 2),
                                 a["L2_ffn_W2"].reshape(8, P, 4, P).transpose(0, 3, 2, 1))
    for n, groups, subs in (("", 32, 2), ("a", 16, 1)):
        w = a["L3_ffn_a_up" if n else "L3_ffn_w_up"].reshape(groups, 2, subs, P, P)
        gate, up = (w[:, k].transpose(0, 3, 1, 2) for k in range(2))
        down = a["L3_ffn_a_down" if n else "L3_ffn_w_down"].reshape(groups, P, subs, P).transpose(0, 3, 2, 1)
        d["L3_ffn_adapters" if n else "L3_ffn_experts"] = blocks(gate, up, down)
    d["L3_ffn_r1"] = a["L3_ffn_r1_w"][:, :P].T
    d["L3_ffn_r1_stats"] = a["L3_ffn_r1_w"][:, P:].T
    d["L3_ffn_r2"] = a["L3_ffn_r2_w"].T
    d["L3_ffn_r1_b"] = a["L3_ffn_r1_b"].reshape(-1, 1)
    d["L3_ffn_pairs"] = np.float32(0.05) * (np.arange(32)[:, None] // 2 == np.arange(16)).astype(np.float32)
    for k in ("Wq", "Wk", "Wv"):
        d["L2_attn_" + k] = a["L2_attn_" + k]
    wo = a["L2_attn_Wo"].reshape(8, 2, 32, P)
    both = np.zeros((2, 8, 2, 2, 32, P), np.float32)
    for b in range(2):
        both[b, :, :, b] = wo
    d["L2_attn_Wo"] = both.reshape(2, 8, P, P).transpose(2, 0, 1, 3)
    d["quarter"] = (np.arange(P)[:, None] // 32 == np.arange(4)).astype(np.float32)
    r, t = np.arange(SP)[:, None], np.arange(SP)[None, :]
    real = (r < S) & (t < S)
    decay = np.where((r <= t) & real, 0.99 ** np.maximum(t - r, 0), 0.0).astype(np.float32)
    d["la_left"] = np.concatenate([real.astype(np.float32), ((r > t) & real).astype(np.float32)])
    d["la_right"] = np.concatenate([decay, -((r <= t) & real).astype(np.float32)])
    d["la_decay"] = np.concatenate([decay, decay])
    d["L3_attn_norms"] = np.stack([a["L3_attn_norm1_w"], a["L3_attn_norm2_w"]], axis=1)
    for k in ("wq", "wo"):
        for g in "gl":
            d["L3_attn_%s_%s" % (g, k)] = a["L3_attn_%s_%s" % (g, k)]
    for k in ("g_kv_down", "g_k_up", "g_v_up", "l_wk", "l_wv"):
        d["L3_attn_" + k] = a["L3_attn_" + k]
    rotate = np.zeros((P, P), np.float32)
    even = np.arange(0, P, 2)
    rotate[even + 1, even], rotate[even, even + 1] = -1.0, 1.0
    d["rotate"] = rotate
    d["mean8"] = (head_of_feature[:, None] == head_of_feature[None, :]).astype(np.float32) / np.float32(DX)
    for g, base in (("g_", 1e6), ("l_", 1e4)):
        inv = (1.0 / np.float32(base) ** (np.arange(0, DX, 2, dtype=np.float32) / np.float32(DX))).astype(np.float32)
        angle = (np.arange(S, dtype=np.float32)[None, :] * inv[:, None]).astype(np.float32)
        angle = angle[(np.arange(P) % DX) // 2]
        d[g + "cos"], d[g + "sin"] = np.cos(angle).astype(np.float32), np.sin(angle).astype(np.float32)
        query, key = np.arange(P)[:, None] % SP, np.arange(S)[None, :]
        seen = (query >= key) & (query - key < (32 if g == "l_" else S))
        d[g + "mask"] = np.where(seen | (query >= S), 0.0, -1e30).astype(np.float32)


def decoder(nc, dram, out):
    with ExitStack() as ctx:
        chip = Chip(nc, ctx, dram)
        load_stage(chip, out)
        for stage in STAGES:
            normalise(chip, chip.x, chip.xn, True)
            stage(chip)
            chip.end_stage()
        store_stage(chip, chip.x, out)


def layouts(inputs):
    a = {k: np.asarray(v) for k, v in inputs.items()}
    d = {"x": a["x"].transpose(2, 0, 1)}
    D = P

    def by_feature(w):
        return w.reshape(-1, D).T

    def column(v):
        return v.reshape(-1, 1)

    d["L0_attn_W_Q"] = by_feature(a["L0_attn_W_Q"])
    d["L0_attn_W_K"] = by_feature(a["L0_attn_W_K"])
    v = a["L0_attn_W_V"]
    d["L0_attn_W_V"] = np.concatenate([by_feature(v[0::2]), by_feature(v[1::2])], axis=1)
    d["L0_attn_W_O"] = a["L0_attn_W_O"].transpose(0, 2, 1).reshape(8, D, D).transpose(1, 0, 2)
    for k in "QKV":
        d["L0_attn_b_" + k] = a["L0_attn_b_" + k].reshape(8, D).T
    d["L0_attn_b_O"] = column(a["L0_attn_b_O"])
    more_layouts(a, d)
    return {k: np.ascontiguousarray(v) for k, v in d.items()}


def kernel(**inputs):
    import concourse.bacc as _bacc
    from concourse.bass_utils import run_bass_kernel_spmd as _run

    nc = _bacc.Bacc("TRN2", target_bir_lowering=False, num_devices=1)
    arrays, dram = {}, {}
    for name, array in layouts(inputs).items():
        arrays["in_" + name] = array
        dram[name] = nc.dram_tensor("in_" + name, array.shape, F32, kind="ExternalInput").ap()
    out = nc.dram_tensor("out_x", (P, B, S), F32, kind="ExternalOutput").ap()
    decoder(nc, dram, out)
    result = _run(nc, [arrays], core_ids=[0])
    return result.results[0]["out_x"].transpose(1, 2, 0)
```

```python
from contextlib import ExitStack

import numpy as np
import concourse.bass as bass
from concourse import mybir

ALU = mybir.AluOpType
ACT = mybir.ActivationFunctionType
F32 = mybir.dt.float32
AX_X = mybir.AxisListType.X

P = 128
B = 32
S = 56
SP = 64
NP_ = B // 2
NK = 1500
KC = 125
NC_ = NK // KC
KB = 500
NB_ = NK // KB
CH = 4
CB = B // CH
CT = CB * S
CW = CB * SP
HX = 16
DX = P // HX
LN_EPS = 1e-5
RMS_EPS = 1e-6


class Step:

    def __init__(self, engine, semaphore, done=0):
        self.engine, self.semaphore, self.done, self.n = engine, semaphore, done, 0

    def __call__(self, instruction):
        self.n += 1
        instruction.then_inc(self.semaphore, 1)
        self.engine.wait_ge(self.semaphore, self.done + self.n)


class Chip:

    def __init__(self, nc, ctx, dram):
        self.nc, self.ctx, self.dram = nc, ctx, dram
        self.x = self.sbuf("x", [P, B, SP])
        self.xn_lead = self.sbuf("xn_lead", [P, SP + B * SP])
        self.xn = self.xn_lead[:, SP:].rearrange("p (b s) -> p b s", s=SP)
        self.ps = ctx.enter_context(nc.psum_tensor("ps", [P, 8, 512], F32))
        self.ones = self.sbuf("ones", [P, P])
        self.mean = self.sbuf("mean", [P, P])
        self.ident = self.sbuf("ident", [P, P])
        self.credit = self.sbuf("credit", [P, 4])
        self.eps = self.sbuf("eps", [P, 2])
        self.norm_calls = self.centre_calls = 0
        self.stage_sems = []
        self.norm_sems = {k: ctx.enter_context(nc.semaphore("norm_" + k)) for k in ("mean", "centred", "squared", "power", "log", "inverse", "out")}

    def sbuf(self, name, shape, dtype=F32):
        return self.ctx.enter_context(self.nc.sbuf_tensor(name, shape, dtype))

    def sem(self, name):
        semaphore = self.nc.alloc_semaphore(name=name)
        self.stage_sems.append(semaphore)
        return semaphore

    def end_stage(self):
        nc = self.nc
        with nc.Block(no_gpsimd_drain=True) as block:
            @block.gpsimd
            def _(pool):
                for semaphore in self.stage_sems:
                    pool.sem_clear(semaphore)
        for semaphore in self.stage_sems:
            nc.release_semaphore(semaphore)
        self.stage_sems = []


def spread(ap, axis, n):
    a = ap.unsqueeze(axis)
    shape = list(a.shape)
    shape[axis] = n
    return a.to_broadcast(shape)


def load_stage(chip, out):
    nc = chip.nc
    x_landed = chip.sem("x_landed")
    cleared = chip.sem("cleared")
    ident_cleared = chip.sem("ident_cleared")
    with nc.Block() as block:
        @block.sync
        def _(sp):
            sp.wait_ge(cleared, 1)
            for g in range(4):
                sp.dma_start(chip.x[32 * g:32 * g + 32, :, 0:S], chip.dram["x"][32 * g:32 * g + 32]).then_inc(x_landed, 16)
            sp.wait_ge(x_landed, 64)

        @block.vector
        def _(dve):
            nc.vector.memset(chip.x[:], 0.0).then_inc(cleared, 1)
            nc.vector.memset(chip.xn_lead[:], 0.0)
            nc.vector.memset(chip.ones[:], 1.0)
            nc.vector.memset(chip.mean[:], 1.0 / P)
            nc.vector.memset(chip.eps[:, 0:1], LN_EPS)
            nc.vector.memset(chip.eps[:, 1:2], RMS_EPS)

        @block.gpsimd
        def _(pool):
            nc.gpsimd.memset(chip.ident[:], 0.0).then_inc(ident_cleared, 1)
            pool.wait_ge(ident_cleared, 1)
            nc.gpsimd.affine_select(out=chip.ident[:], in_=chip.ident[:], compare_op=ALU.not_equal, fill=1.0,
                                    base=0, pattern=[[-1, P]], channel_multiplier=1).then_inc(ident_cleared, 1)


def store_stage(chip, src, out):
    nc = chip.nc
    stored = chip.sem("stored")
    with nc.Block() as block:
        @block.sync
        def _(sp):
            for g in range(4):
                sp.dma_start(out[32 * g:32 * g + 32], src[32 * g:32 * g + 32, :, 0:S]).then_inc(stored, 16)
            sp.wait_ge(stored, 64)


def normalise(chip, src, dst, centre, weight=None):
    nc, ps = chip.nc, chip.ps
    s = chip.norm_sems
    done = CH * chip.norm_calls
    done_centred = CH * chip.centre_calls
    tag = str(chip.norm_calls)
    which = 0 if centre else 1
    chip.norm_calls += 1
    chip.centre_calls += centre
    with ExitStack() as own, nc.Block(no_gpsimd_drain=True) as block:
        sq = own.enter_context(nc.sbuf_tensor("norm_sq" + tag, [P, CH, CW], F32))
        root = own.enter_context(nc.sbuf_tensor("norm_root" + tag, [P, CH, CW], F32))
        flat = src.rearrange("p (c b) s -> p c (b s)", c=CH)
        goal = dst.rearrange("p (c b) s -> p c (b s)", c=CH)
        centred = goal if centre else flat

        @block.tensor
        def _(pe):
            for c in range(CH):
                if centre:
                    nc.tensor.matmul(ps[:, c, :], chip.mean[:], flat[:, c, :], start=True, stop=True).then_inc(s["mean"], 1)
            for c in range(CH):
                pe.wait_ge(s["squared"], done + c + 1)
                nc.tensor.matmul(ps[:, 4 + c, :], chip.mean[:], sq[:, c, :], start=True, stop=True).then_inc(s["power"], 1)

        @block.scalar
        def _(act):
            for c in range(CH):
                if centre:
                    act.wait_ge(s["centred"], done_centred + c + 1)
                nc.scalar.activation(sq[:, c, :], centred[:, c, :], ACT.Square).then_inc(s["squared"], 1)
            for c in range(CH):
                act.wait_ge(s["power"], done + c + 1)
                nc.scalar.activation(root[:, c, :], ps[:, 4 + c, :], ACT.Ln, bias=chip.eps[:, which:which + 1]).then_inc(s["log"], 1)
            for c in range(CH):
                act.wait_ge(s["log"], done + c + 1)
                nc.scalar.activation(root[:, c, :], root[:, c, :], ACT.Exp, scale=-0.5).then_inc(s["inverse"], 1)

        @block.vector
        def _(dve):
            for c in range(CH):
                if centre:
                    dve.wait_ge(s["mean"], done_centred + c + 1)
                    nc.vector.tensor_tensor(goal[:, c, :], flat[:, c, :], ps[:, c, :], ALU.subtract).then_inc(s["centred"], 1)
            for c in range(CH):
                if centre:
                    dve.wait_ge(s["centred"], done_centred + c + 1)
                dve.wait_ge(s["inverse"], done + c + 1)
                if weight is None:
                    nc.vector.tensor_tensor(goal[:, c, :], centred[:, c, :], root[:, c, :], ALU.mult).then_inc(s["out"], 1)
                else:
                    nc.vector.scalar_tensor_tensor(goal[:, c, :], centred[:, c, :], weight, root[:, c, :], ALU.mult, ALU.mult).then_inc(s["out"], 1)


def self_attention_0(chip):
    nc, ps, xn, x = chip.nc, chip.ps, chip.xn, chip.x
    DH = 64
    HJ = HX // 2
    landed = chip.sem("a0_weights_landed")
    pads_clear = chip.sem("a0_pads_clear")
    tokens_ready = chip.sem("a0_tokens_ready")
    q_done, k_done, v_done = (chip.sem("a0_%s_done" % k) for k in "qkv")
    q_kept, k_kept, v_kept = (chip.sem("a0_%s_kept" % k) for k in "qkv")
    scores_done, shifted, exp_done = (chip.sem("a0_" + k) for k in ("scores_done", "shifted", "exp_done"))
    probs_ready, turned, probs_kept = (chip.sem("a0_" + k) for k in ("probs_ready", "turned", "probs_kept"))
    mixed, mixed_kept, projected, added = (chip.sem("a0_" + k) for k in ("mixed", "mixed_kept", "projected", "added"))
    dve_chain = chip.sem("a0_dve_chain")
    with ExitStack() as own:
        def sbuf(name, shape):
            return own.enter_context(nc.sbuf_tensor("a0_" + name, shape, F32))
        wq, wk, wv = (sbuf(n, [P, HX * DH]) for n in ("wq", "wk", "wv"))
        wo = sbuf("wo", [P, HJ, P])
        bq, bk, bv = (sbuf(n, [P, HJ]) for n in ("bq", "bk", "bv"))
        bo = sbuf("bo", [P, 1])
        def two(name, shape):
            return [sbuf("%s%d" % (name, u), shape) for u in range(2)]
        tokens, q = two("tokens", [P, P]), two("q", [P, HJ, P])
        k, v = two("k", [P, HJ, 2, 2, SP]), two("v", [P, 2, HJ, 2, DH])
        probs, probs_t, mix = two("probs", [P, HX, SP]), two("probs_t", [P, HJ, P]), two("mix", [P, HJ, 2, SP])
        top, total, inverse = (two(n, [P, HX]) for n in ("top", "total", "inverse"))
        scores = [ps[:, 4 * u + 2:4 * u + 4, :].rearrange("p k (h s) -> p (k h) s", s=SP)[:, :, 0:S] for u in range(2)]
        block = own.enter_context(nc.Block(no_gpsimd_drain=True))

        @block.sync
        def _(sp):
            for dst, name in ((wq, "L0_attn_W_Q"), (wk, "L0_attn_W_K"), (wv, "L0_attn_W_V"), (wo, "L0_attn_W_O"),
                              (bq, "L0_attn_b_Q"), (bk, "L0_attn_b_K"), (bv, "L0_attn_b_V"), (bo, "L0_attn_b_O")):
                sp.dma_start(dst[:], chip.dram[name]).then_inc(landed, 16)

        def all_pairs(engine, one_step):
            one_step(0, 0, True, False)
            with engine.Fori(0, NP_ // 2 - 1) as i:
                one_step(2 * i + 1, 1, True, True)
                one_step(2 * i + 2, 0, True, True)
            one_step(NP_ - 1, 1, True, True)
            one_step(NP_, 0, False, True)

        @block.tensor
        def _(pe):
            def project_qk(n, u):
                pe.wait_ge(tokens_ready, n + 1)
                pe.wait_ge(added, n + 1)
                for w, bank, done in ((wq, 4 * u, q_done), (wk, 4 * u + 2, k_done)):
                    for j in range(HJ):
                        mm = nc.tensor.matmul(ps[:, bank + j // 4, P * (j % 4):P * (j % 4) + P], w[:, P * j:P * j + P],
                                              tokens[u][:], start=True, stop=True)
                    mm.then_inc(done, 1)

            def project_values(n, u):
                pe.wait_ge(q_kept, n + 1)
                for b in range(2):
                    for odd in range(2):
                        mm = nc.tensor.matmul(ps[64 * odd:64 * odd + 64, 4 * u + b, :], tokens[u][:, SP * b:SP * b + SP],
                                              wv[:, 512 * odd:512 * odd + 512], start=True, stop=True)
                mm.then_inc(v_done, 1)

            def make_scores(n, u):
                pe.wait_ge(k_kept, 2 * n + 2)
                for j in range(HJ):
                    for b in range(2):
                        mm = nc.tensor.matmul(ps[64 * b:64 * b + 64, 4 * u + 2 + j // 4, P * (j % 4):P * (j % 4) + P],
                                              q[u][:, j, SP * b:SP * b + SP], k[u][:, j, b].rearrange("p h s -> p (h s)"),
                                              start=True, stop=True)
                mm.then_inc(scores_done, 1)

            def turn(n, u):
                pe.wait_ge(v_kept, n + 1)
                pe.wait_ge(probs_ready, n + 1)
                for j in range(HJ):
                    mm = nc.tensor.transpose(ps[:, 4 * u + j // 4, P * (j % 4):P * (j % 4) + P],
                                             probs[u][:, 2 * j:2 * j + 2, :].rearrange("p h s -> p (h s)"), chip.ident[:])
                mm.then_inc(turned, 1)

            def mix_values(n, u):
                pe.wait_ge(probs_kept, n + 1)
                for j in range(HJ):
                    for b in range(2):
                        mm = nc.tensor.matmul(ps[:, 4 * u + 2 + j // 4, P * (j % 4) + SP * b:P * (j % 4) + SP * b + S],
                                              v[u][:, b, j].rearrange("p h d -> p (h d)"), probs_t[u][:, j, SP * b:SP * b + S],
                                              start=True, stop=True)
                mm.then_inc(mixed, 1)

            def project_out(n, u):
                pe.wait_ge(mixed_kept, n + 1)
                for j in range(HJ):
                    mm = nc.tensor.matmul(ps[:, 4 * u, 0:P], wo[:, j, :], mix[u][:, j].rearrange("p b s -> p (b s)"),
                                          start=(j == 0), stop=(j == HJ - 1))
                mm.then_inc(projected, 1)

            def one_step(n, u, taking, finishing):
                if taking:
                    project_qk(n, u)
                if finishing:
                    turn(n - 1, 1 - u)
                if taking:
                    project_values(n, u)
                if finishing:
                    mix_values(n - 1, 1 - u)
                if taking:
                    make_scores(n, u)
                if finishing:
                    project_out(n - 1, 1 - u)

            pe.wait_ge(landed, 8 * 16)
            all_pairs(pe, one_step)

        @block.scalar
        def _(act):
            def take_tokens(n, u):
                act.wait_ge(v_done, n + 1)
                nc.scalar.copy(tokens[u][:], xn.rearrange("p b s -> p (b s)")[:, bass.ds(n * P, P)]).then_inc(tokens_ready, 1)

            def one_step(n, u, taking, finishing):
                if finishing:
                    act.wait_ge(turned, n)
                    nc.scalar.copy(probs_t[1 - u][:], ps[:, 4 * (1 - u):4 * (1 - u) + 2, :].rearrange("p k (j c) -> p (k j) c", c=P)).then_inc(probs_kept, 1)
                if taking:
                    act.wait_ge(v_done, n + 3)
                    banks = ps[:, 4 * u:4 * u + 2, :].rearrange("p b (j d) -> p b j d", d=DH)
                    nc.scalar.copy(v[u][0:64, :, :, 0, :], banks[0:64])
                    nc.scalar.copy(v[u][64:P, :, :, 1, :], banks[64:P]).then_inc(v_kept, 1)
                    if not isinstance(n, int) or n + 1 < NP_:
                        take_tokens(n + 1, 1 - u)
                    act.wait_ge(shifted, n + 1)
                    nc.scalar.activation(probs[u][:, :, 0:S], probs[u][:, :, 0:S], ACT.Exp, scale=DH ** -0.5).then_inc(exp_done, 1)

            act.wait_ge(pads_clear, 1)
            take_tokens(0, 0)
            all_pairs(act, one_step)

        @block.vector
        def _(dve):
            def keep_qk(n, u):
                dve.wait_ge(q_done, n + 1)
                nc.vector.tensor_tensor(q[u][:], ps[:, 4 * u:4 * u + 2, :].rearrange("p k (j c) -> p (k j) c", c=P),
                                        spread(bq[:], 2, P), ALU.add).then_inc(q_kept, 1)
                dve.wait_ge(k_done, n + 1)
                for odd in range(2):
                    r = slice(64 * odd, 64 * odd + 64)
                    nc.vector.tensor_tensor(k[u][r, :, :, odd, :], ps[r, 4 * u + 2:4 * u + 4, :].rearrange("p k (j b s) -> p (k j) b s", j=4, b=2),
                                            spread(spread(bk[r], 2, 2), 3, SP), ALU.add).then_inc(k_kept, 1)

            def shift(n, u):
                dve.wait_ge(scores_done, n + 1)
                Step(dve, dve_chain, 3 * n)(nc.vector.tensor_reduce(top[u][:], scores[u], AX_X, ALU.max))
                nc.vector.tensor_tensor(probs[u][:, :, 0:S], scores[u], spread(top[u][:], 2, S), ALU.subtract).then_inc(shifted, 1)

            def divide(n, u):
                dve.wait_ge(exp_done, n + 1)
                step = Step(dve, dve_chain, 3 * n + 1)
                step(nc.vector.tensor_reduce(total[u][:], probs[u][:, :, 0:S], AX_X, ALU.add))
                step(nc.vector.reciprocal(inverse[u][:], total[u][:]))
                nc.vector.tensor_tensor(probs[u][:, :, 0:S], probs[u][:, :, 0:S], spread(inverse[u][:], 2, S),
                                        ALU.mult).then_inc(probs_ready, 1)

            def keep_mix(n, u):
                dve.wait_ge(mixed, n + 1)
                nc.vector.tensor_tensor(
                    mix[u][:, :, :, 0:S], ps[:, 4 * u + 2:4 * u + 4, :].rearrange("p k (j b s) -> p (k j) b s", j=4, b=2)[:, :, :, 0:S],
                    spread(spread(bv[:], 2, 2), 3, S), ALU.add).then_inc(mixed_kept, 1)

            def add(n, u):
                dve.wait_ge(projected, n + 1)
                pair = x[:, bass.ds(2 * n, 2), 0:S]
                nc.vector.scalar_tensor_tensor(pair, ps[:, 4 * u, 0:P].rearrange("p (b s) -> p b s", s=SP)[:, :, 0:S],
                                               bo[:, 0:1], pair, ALU.add, ALU.add).then_inc(added, 1)

            def one_step(n, u, taking, finishing):
                if taking:
                    keep_qk(n, u)
                if finishing:
                    keep_mix(n - 1, 1 - u)
                if taking:
                    shift(n, u)
                if finishing:
                    add(n - 1, 1 - u)
                if taking:
                    divide(n, u)

            for u in range(2):
                nc.vector.memset(probs[u][:], 0.0).then_inc(v_done, 1)
                nc.vector.memset(k[u][:], 0.0).then_inc(added, 1)
                nc.vector.memset(mix[u][:], 0.0)
                last = nc.vector.memset(v[u][:], 0.0)
            last.then_inc(pads_clear, 1)
            dve.wait_ge(landed, 8 * 16)
            all_pairs(dve, one_step)


def context_mixing(chip):
    nc, ps, xn, x = chip.nc, chip.ps, chip.xn, chip.x
    t_landed, n_landed = ([chip.sem("cm_%s_landed%d" % (k, u)) for u in range(2)] for k in "tn")
    tokens_ready, top_ready, exp_done, turned, probs_kept, scaled, flipped = (
        chip.sem("cm_" + k) for k in ("tokens_ready", "top_ready", "exp_done", "turned", "probs_kept", "scaled", "flipped"))
    scores_done, mixed, added = ([chip.sem("cm_%s%d" % (k, u)) for u in range(2)] for k in ("scores_done", "mixed", "added"))
    dve_chain = chip.sem("cm_dve_chain")
    with ExitStack() as own:
        def sbuf(name, shape):
            return own.enter_context(nc.sbuf_tensor("cm_" + name, shape, F32))
        ctx_t = [sbuf("ctx_t%d" % u, [P, 2, NK]) for u in range(2)]
        ctx_n = [sbuf("ctx_n%d" % u, [KC, 2, NC_, P]) for u in range(2)]
        tokens = [sbuf("tokens%d" % u, [P, P]) for u in range(2)]
        probs = [sbuf("probs%d" % u, [P, NB_, KB]) for u in range(2)]
        probs_t = [sbuf("probs_t%d" % u, [KC, NC_, P]) for u in range(2)]
        top = [sbuf("top%d" % u, [P, 1]) for u in range(2)]
        low = [sbuf("low%d" % u, [P, 1]) for u in range(2)]
        total = [sbuf("total%d" % u, [P, 1]) for u in range(2)]
        inverse = [sbuf("inverse%d" % u, [P, 1]) for u in range(2)]
        mix = [sbuf("mix%d" % u, [P, P]) for u in range(2)]
        block = own.enter_context(nc.Block(no_gpsimd_drain=True))

        @block.sync
        def _(sp):
            with sp.Fori(0, NP_ // 2) as i:
                for free, buffer, name, done in ((scores_done, ctx_t, "ctx_t", t_landed), (mixed, ctx_n, "ctx_n", n_landed)):
                    for u in range(2):
                        sp.wait_ge(free[u], i + 1)
                        for b in range(2):
                            source = chip.dram[name][bass.ds(4 * i + 2 * u + b, 1)]
                            sp.dma_start(buffer[u][:, b], source.rearrange("a p n -> (a p) n") if name == "ctx_t" else
                                         source.rearrange("a p c d -> (a p) c d")).then_inc(done[u], 16)

        @block.tensor
        def _(pe):
            with pe.Fori(0, NP_ // 2) as i:
                for u in range(2):
                    pe.wait_ge(t_landed[u], 32 * i + 32)
                    pe.wait_ge(added[u], i + 1)
                    pe.wait_ge(tokens_ready, 2 * i + u + 1)
                    for n in range(NB_):
                        for b in range(2):
                            mm = nc.tensor.matmul(ps[SP * b:SP * b + SP, 3 * u + n, 0:KB], tokens[u][:, SP * b:SP * b + SP],
                                                  ctx_t[u][:, b, KB * n:KB * n + KB], start=True, stop=True)
                    mm.then_inc(scores_done[u], 1)
                for u in range(2):
                    pe.wait_ge(exp_done, 2 * i + u + 1)
                    rows = probs[u].rearrange("p n k -> p (n k)")
                    for c in range(NC_):
                        mm = nc.tensor.transpose(ps[0:KC, 3 * u + c // 4, P * (c % 4):P * (c % 4) + P],
                                                 rows[:, KC * c:KC * c + KC], chip.ident[:])
                    mm.then_inc(turned, 1)
                    pe.wait_ge(probs_kept, 2 * i + u + 1)
                    pe.wait_ge(n_landed[u], 32 * i + 32)
                    for c in range(NC_):
                        for b in range(2):
                            mm = nc.tensor.matmul(ps[SP * b:SP * b + SP, 6 + u, 0:P], probs_t[u][:, c, SP * b:SP * b + SP],
                                                  ctx_n[u][:, b, c, :], start=(c == 0), stop=(c == NC_ - 1))
                    mm.then_inc(mixed[u], 1)
                for u in range(2):
                    pe.wait_ge(scaled, 2 * i + u + 1)
                    nc.tensor.transpose(ps[:, 6 + u, P:2 * P], mix[u][:], chip.ident[:]).then_inc(flipped, 1)

        @block.scalar
        def _(act):
            with act.Fori(0, NP_ // 2) as i:
                for u in range(2):
                    act.wait_ge(scores_done[u], i + 1)
                    nc.scalar.copy(tokens[u][:], xn[:, bass.ds(4 * i + 2 * u, 2), :].rearrange("p b s -> p (b s)")).then_inc(tokens_ready, 1)
                for u in range(2):
                    act.wait_ge(top_ready, 2 * i + u + 1)
                    nc.scalar.activation(probs[u][:], ps[:, 3 * u:3 * u + 3, 0:KB], ACT.Exp, bias=low[u][:, 0:1],
                                         accum_out=total[u][:, 0:1]).then_inc(exp_done, 1)
                for u in range(2):
                    act.wait_ge(turned, 2 * i + u + 1)
                    nc.scalar.copy(probs_t[u][:], ps[0:KC, 3 * u:3 * u + 3, :].rearrange("p k (c s) -> p (k c) s", s=P)).then_inc(probs_kept, 1)

        @block.vector
        def _(dve):
            for u in range(2):
                nc.vector.memset(top[u][:], 0.0).then_inc(mixed[u], 1)
                nc.vector.memset(low[u][:], 0.0).then_inc(added[u], 1)
                nc.vector.memset(total[u][:], 0.0).then_inc(scores_done[u], 1)
            with dve.Fori(0, NP_ // 2) as i:
                for u in range(2):
                    dve.wait_ge(scores_done[u], i + 2)
                    Step(dve, dve_chain, 4 * i + u)(
                        nc.vector.tensor_reduce(top[u][:], ps[:, 3 * u:3 * u + 3, 0:KB], mybir.AxisListType.XY, ALU.max))
                    nc.vector.tensor_scalar(low[u][:], top[u][:], -1.0, None, ALU.mult).then_inc(top_ready, 1)
                for u in range(2):
                    dve.wait_ge(exp_done, 2 * i + u + 1)
                    step = Step(dve, dve_chain, 4 * i + 2 + u)
                    step(nc.vector.reciprocal(inverse[u][:], total[u][:]))
                    dve.wait_ge(mixed[u], i + 2)
                    nc.vector.tensor_scalar(mix[u][:], ps[:, 6 + u, 0:P], inverse[u][:, 0:1], None, ALU.mult).then_inc(scaled, 1)
                for u in range(2):
                    dve.wait_ge(flipped, 2 * i + u + 1)
                    pair = x[:, bass.ds(4 * i + 2 * u, 2), 0:S]
                    nc.vector.tensor_tensor(pair, pair, ps[:, 6 + u, P:2 * P].rearrange("p (b s) -> p b s", s=SP)[:, :, 0:S], ALU.add).then_inc(added[u], 1)


def coupled_twist(chip):
    nc, ps, xn, x = chip.nc, chip.ps, chip.xn, chip.x
    CYCLES = 3
    cleared, landed, ready = chip.sem("ct_cleared"), chip.sem("ct_landed"), chip.sem("ct_constants_ready")
    sums_ready = chip.sem("ct_sums_ready")
    global_done, global_kept = chip.sem("ct_global_done"), chip.sem("ct_global_kept")
    layer_done, layer_kept, twisted, coupled = (chip.sem("ct_" + k) for k in ("layer_done", "layer_kept", "twisted", "coupled"))
    stepped, dve_chain, added = chip.sem("ct_stepped"), chip.sem("ct_dve_chain"), chip.sem("ct_added")
    D2, D4 = P // 2, P // 4
    with ExitStack() as own:
        def sbuf(name, shape):
            return own.enter_context(nc.sbuf_tensor("ct_" + name, shape, F32))
        weights, biases = sbuf("weights", [P, 5, P]), sbuf("biases", [P, 5])
        cw2, cw3, gw1, gw2, cw1 = (weights[:, n] for n in range(5))
        cb2, cb3, gb1, gb2, cb1 = (biases[:, n:n + 1] for n in range(5))
        cw4, gw3 = sbuf("cw4", [P, 1]), sbuf("gw3", [P, 1])
        cb4, gb3 = sbuf("cb4", [P, 1]), sbuf("gb3", [P, 1])
        reach = sbuf("reach", [P, 1])
        twist = sbuf("twist", [P, P])
        cw4_all, gw3_all = sbuf("cw4_all", [P, P]), sbuf("gw3_all", [P, P])
        sums, g1, g2, gf, base = sbuf("sums", [P, B]), sbuf("g1", [P, B]), sbuf("g2", [P, B]), sbuf("gf", [P, B]), sbuf("base", [P, B])
        gain_g, gain_t, low = sbuf("gain_g", [P, 1]), sbuf("gain_t", [P, 1]), sbuf("low", [P, 1])
        hidden = [sbuf("hidden%d" % c, [P, CT]) for c in range(CH)]
        coupling = [sbuf("coupling%d" % c, [P, CT]) for c in range(CH)]
        y = [xn[:, CB * c:CB * c + CB, 0:S] for c in range(CH)]
        x_of = [x[:, CB * c:CB * c + CB, 0:S] for c in range(CH)]
        wide = [ps[:, 4 + c, 0:CT].rearrange("p (b s) -> p b s", s=S) for c in range(CH)]
        loads = [(cw1, "cn_w1"), (cw2[:, 0:D2], "cn_w2"), (cw3[0:D2, 0:D4], "cn_w3"), (cw4[0:D4], "cn_w4"),
                 (cb1, "cn_b1"), (cb2[0:D2], "cn_b2"), (cb3[0:D4], "cn_b3"), (gw1[:, 0:D2], "gc_w1"),
                 (gw2[0:D2, 0:D4], "gc_w2"), (gw3[0:D4], "gc_w3"), (gb1[0:D2], "gc_b1"), (gb2[0:D4], "gc_b2")]
        to_all = [(cb4, "cn_b4"), (gb3, "gc_b3"), (reach, "adaptive_range")]
        n_loads = len(loads) + len(to_all) + 1
        block = own.enter_context(nc.Block(no_gpsimd_drain=True))

        @block.sync
        def _(sp):
            sp.wait_ge(cleared, 4)
            for dst, name in loads:
                sp.dma_start(dst, chip.dram["L0_ffn_" + name]).then_inc(landed, 16)
            for dst, name in to_all:
                sp.dma_start(dst[:], chip.dram["L0_ffn_" + name].to_broadcast([P, 1])).then_inc(landed, 16)
            sp.dma_start(twist[:], chip.dram["twist"]).then_inc(landed, 16)

        @block.tensor
        def _(pe):
            pe.wait_ge(landed, 16 * n_loads)
            pe.wait_ge(ready, 2)
            pe.wait_ge(sums_ready, 1)
            nc.tensor.matmul(ps[:, 4, 0:B], gw1, sums[:], start=True, stop=True).then_inc(global_done, 1)
            pe.wait_ge(global_kept, 1)
            nc.tensor.matmul(ps[:, 5, 0:B], gw2, g1[:], start=True, stop=True).then_inc(global_done, 1)
            pe.wait_ge(global_kept, 2)
            nc.tensor.matmul(ps[:, 6, 0:B], gw3_all[:], g2[:], start=True, stop=True).then_inc(global_done, 1)
            pe.wait_ge(global_kept, 3)
            with pe.Fori(0, CYCLES) as i:
                for c in range(CH):
                    pe.wait_ge(stepped, CH * i + c + 1)
                    nc.tensor.matmul(ps[:, c, 0:CT], cw1, y[c], start=True, stop=True).then_inc(layer_done, 1)
                    nc.tensor.matmul(ps[:, 4 + c, 0:CT], twist[:], y[c], start=True, stop=True).then_inc(twisted, 1)
                for c in range(CH):
                    pe.wait_ge(layer_kept, 16 * i + c + 1)
                    nc.tensor.matmul(ps[:, c, 0:CT], cw2, hidden[c][:], start=True, stop=True).then_inc(layer_done, 1)
                for c in range(CH):
                    pe.wait_ge(layer_kept, 16 * i + 4 + c + 1)
                    nc.tensor.matmul(ps[:, c, 0:CT], cw3, hidden[c][:], start=True, stop=True).then_inc(layer_done, 1)
                for c in range(CH):
                    pe.wait_ge(layer_kept, 16 * i + 8 + c + 1)
                    nc.tensor.matmul(ps[:, c, 0:CT], cw4_all[:], hidden[c][:], start=True, stop=True).then_inc(layer_done, 1)

        @block.scalar
        def _(act):
            act.wait_ge(landed, 16 * n_loads)
            act.wait_ge(global_done, 1)
            nc.scalar.activation(g1[:], ps[:, 4, 0:B], ACT.Gelu, bias=gb1, scale=1.0 / S).then_inc(global_kept, 1)
            act.wait_ge(global_done, 2)
            nc.scalar.activation(g2[:], ps[:, 5, 0:B], ACT.Gelu, bias=gb2).then_inc(global_kept, 1)
            act.wait_ge(global_done, 3)
            nc.scalar.activation(gf[:], ps[:, 6, 0:B], ACT.Sigmoid, bias=gb3[:, 0:1]).then_inc(global_kept, 1)
            with act.Fori(0, CYCLES) as i:
                for n, bias in enumerate((cb1, cb2, cb3)):
                    for c in range(CH):
                        act.wait_ge(layer_done, 16 * i + 4 * n + c + 1)
                        nc.scalar.activation(hidden[c][:], ps[:, c, 0:CT], ACT.Gelu, bias=bias).then_inc(layer_kept, 1)
                for c in range(CH):
                    act.wait_ge(layer_done, 16 * i + 12 + c + 1)
                    nc.scalar.activation(coupling[c][:], ps[:, c, 0:CT], ACT.Sigmoid, bias=cb4[:, 0:1]).then_inc(layer_kept, 1)

        @block.vector
        def _(dve):
            for buffer in (weights, biases, cw4, gw3):
                nc.vector.memset(buffer[:], 0.0).then_inc(cleared, 1)
            nc.vector.tensor_reduce(sums[:], xn[:, :, 0:S], AX_X, ALU.add).then_inc(sums_ready, 1)
            dve.wait_ge(landed, 16 * n_loads)
            step = Step(dve, dve_chain)
            nc.vector.tensor_copy(cw4_all[:], cw4[:, 0:1].to_broadcast([P, P])).then_inc(ready, 1)
            nc.vector.tensor_copy(gw3_all[:], gw3[:, 0:1].to_broadcast([P, P])).then_inc(ready, 1)
            step(nc.vector.tensor_scalar(gain_g[:], reach[:], 1.4, None, ALU.mult))
            step(nc.vector.tensor_scalar(gain_t[:], reach[:], 0.6, None, ALU.mult))
            step(nc.vector.tensor_scalar(low[:], reach[:], -1.0, 0.1, ALU.mult, ALU.add))
            dve.wait_ge(global_kept, 3)
            step(nc.vector.tensor_scalar(base[:], gf[:], gain_g[:, 0:1], low[:, 0:1], ALU.mult, ALU.add))
            for c in range(CH):
                nc.vector.tensor_tensor(x_of[c], x_of[c], y[c], ALU.add).then_inc(stepped, 1)
            with dve.Fori(0, CYCLES) as i:
                for c in range(CH):
                    dve.wait_ge(layer_kept, 16 * i + 12 + c + 1)
                    dve.wait_ge(twisted, CH * i + c + 1)
                    cc = coupling[c].rearrange("p (b s) -> p b s", s=S)
                    step = Step(dve, coupled, 8 * i + 2 * c)
                    step(nc.vector.scalar_tensor_tensor(cc, cc, gain_t[:, 0:1], spread(base[:, CB * c:CB * c + CB], 2, S), ALU.mult, ALU.add))
                    step(nc.vector.tensor_tensor(cc, cc, wide[c], ALU.mult))
                    nc.vector.tensor_tensor(x_of[c], x_of[c], cc, ALU.add).then_inc(added, 1)
                    dve.wait_ge(added, CH * i + c + 1)
                    nc.vector.tensor_tensor(y[c], y[c], cc, ALU.add).then_inc(stepped, 1)


def gated_recurrence(chip):
    nc, ps, xn, x = chip.nc, chip.ps, chip.xn, chip.x
    W = B * SP
    TAPS = 4
    landed, conv_ready, gates_done, gates_kept = (chip.sem("gr_" + k) for k in ("landed", "conv_ready", "gates_done", "gates_kept"))
    dve_chain, act_chain = chip.sem("gr_dve_chain"), chip.sem("gr_act_chain")
    rate_ready, decay_ready, sums_ready = chip.sem("gr_rate_ready"), chip.sem("gr_decay_ready"), chip.sem("gr_sums_ready")
    root_needed, root_ready = chip.sem("gr_root_needed"), chip.sem("gr_root_ready")
    h_ready, out_done, squared, power_done, root_kept, added = (
        chip.sem("gr_" + k) for k in ("h_ready", "out_done", "squared", "power_done", "root_kept", "added"))
    with ExitStack() as own:
        def sbuf(name, shape):
            return own.enter_context(nc.sbuf_tensor("gr_" + name, shape, F32))
        wr, wi, wo = sbuf("wr", [P, P]), sbuf("wi", [P, P]), sbuf("wo", [P, P])
        taps, bc, br, bi, log_a, norm_w = sbuf("taps", [P, TAPS]), *(sbuf(n, [P, 1]) for n in ("bc", "br", "bi", "log_a", "norm_w"))
        rate = sbuf("rate", [P, 1])
        conv, r_gate, i_gate, alive, work = (sbuf(n, [P, W]) for n in ("conv", "r_gate", "i_gate", "alive", "work"))
        out_sb = sbuf("out", [P, CH, CW])
        flat = chip.xn_lead[:]
        loads = [(wr, "Wr_w"), (wi, "Wi_w"), (wo, "out_w"), (taps, "conv_weight"), (bc, "conv_bias"), (br, "Wr_b"), (bi, "Wi_b"),
                 (log_a, "log_a"), (norm_w, "norm_w")]
        block = own.enter_context(nc.Block(no_gpsimd_drain=True))

        @block.sync
        def _(sp):
            for dst, name in loads:
                sp.dma_start(dst[:], chip.dram["L1_attn_" + name]).then_inc(landed, 16)

        @block.tensor
        def _(pe):
            pe.wait_ge(conv_ready, 1)
            for c in range(CH):
                cols = conv[:, CW * c:CW * c + CW]
                nc.tensor.matmul(ps[:, c, :], wr[:], cols, start=True, stop=True).then_inc(gates_done, 1)
            for c in range(CH):
                cols = conv[:, CW * c:CW * c + CW]
                nc.tensor.matmul(ps[:, 4 + c, :], wi[:], cols, start=True, stop=True).then_inc(gates_done, 1)
            pe.wait_ge(h_ready, 1)
            for c in range(CH):
                nc.tensor.matmul(ps[:, c, :], wo[:], conv[:, CW * c:CW * c + CW], start=True, stop=True).then_inc(out_done, 1)
            for c in range(CH):
                pe.wait_ge(squared, c + 1)
                nc.tensor.matmul(ps[:, 4 + c, :], chip.mean[:], work[:, CW * c:CW * c + CW], start=True, stop=True).then_inc(power_done, 1)

        @block.scalar
        def _(act):
            act.wait_ge(landed, 16 * len(loads))
            for c in range(CH):
                act.wait_ge(gates_done, c + 1)
                nc.scalar.activation(r_gate[:, CW * c:CW * c + CW], ps[:, c, :], ACT.Sigmoid, bias=br[:, 0:1]).then_inc(gates_kept, 1)
            for c in range(CH):
                act.wait_ge(gates_done, 4 + c + 1)
                nc.scalar.activation(i_gate[:, CW * c:CW * c + CW], ps[:, 4 + c, :], ACT.Sigmoid, bias=bi[:, 0:1]).then_inc(gates_kept, 1)
            step = Step(act, act_chain)
            step(nc.scalar.activation(rate[:], log_a[:], ACT.Exp, scale=-1.0))
            nc.scalar.activation(rate[:], rate[:], ACT.Ln, bias=1.0).then_inc(rate_ready, 1)
            act.wait_ge(decay_ready, 1)
            nc.scalar.activation(r_gate[:], work[:], ACT.Exp).then_inc(rate_ready, 1)
            act.wait_ge(root_needed, 1)
            nc.scalar.activation(r_gate[:], r_gate[:], ACT.Sqrt).then_inc(root_ready, 1)
            act.wait_ge(sums_ready, 1)
            step(nc.scalar.activation(i_gate[:], work[:], ACT.Exp, scale=-1.0))
            nc.scalar.activation(work[:], work[:], ACT.Exp).then_inc(root_ready, 1)
            for c in range(CH):
                act.wait_ge(out_done, c + 1)
                nc.scalar.copy(out_sb[:, c, :], ps[:, c, :]).then_inc(act_chain, 1)
                act.wait_ge(act_chain, 3 + c)
                nc.scalar.activation(work[:, CW * c:CW * c + CW], out_sb[:, c, :], ACT.Square).then_inc(squared, 1)
            for c in range(CH):
                act.wait_ge(power_done, c + 1)
                nc.scalar.activation(r_gate[:, CW * c:CW * c + CW], ps[:, 4 + c, :], ACT.Sqrt, bias=chip.eps[:, 1:2]).then_inc(root_kept, 1)

        @block.vector
        def _(dve):
            step = Step(dve, dve_chain)
            nc.vector.memset(alive[:], 1.0)
            step(nc.vector.memset(work[:], 1.0))
            step(nc.vector.memset(alive.rearrange("p (b s) -> p b s", s=SP)[:, :, 0:1], 0.0))
            dve.wait_ge(landed, 16 * len(loads))
            step(nc.vector.tensor_scalar(conv[:], flat[:, SP:SP + W], taps[:, 3:4], bc[:, 0:1], ALU.mult, ALU.add))
            for t in range(TAPS - 1):
                shift = TAPS - 1 - t
                last = nc.vector.scalar_tensor_tensor(conv[:], flat[:, SP - shift:SP - shift + W], taps[:, t:t + 1], conv[:], ALU.mult, ALU.add)
                if t < TAPS - 2:
                    step(last)
            last.then_inc(conv_ready, 1)
            dve.wait_ge(rate_ready, 1)
            step(nc.vector.tensor_scalar(rate[:], rate[:], -8.0, None, ALU.mult))
            dve.wait_ge(gates_kept, 4)
            nc.vector.tensor_scalar(work[:], r_gate[:], rate[:, 0:1], None, ALU.mult).then_inc(decay_ready, 1)
            dve.wait_ge(decay_ready, 1)
            dve.wait_ge(rate_ready, 2)
            step(nc.vector.tensor_scalar(work[:], work[:], float(np.log(np.float32(1e-7))), None, ALU.max))
            step(nc.vector.tensor_tensor(r_gate[:], r_gate[:], r_gate[:], ALU.mult))
            step(nc.vector.tensor_scalar(r_gate[:], r_gate[:], -1.0, 1.0, ALU.mult, ALU.add))
            nc.vector.tensor_scalar(r_gate[:], r_gate[:], 1e-6, None, ALU.max).then_inc(root_needed, 1)
            step(nc.vector.tensor_tensor_scan(out_sb.rearrange("p c w -> p (c w)"), alive[:], work[:], 0.0, ALU.mult, ALU.add))
            dve.wait_ge(gates_kept, 8)
            step(nc.vector.tensor_tensor(conv[:], conv[:], i_gate[:], ALU.mult))
            nc.vector.tensor_scalar(work[:], out_sb.rearrange("p c w -> p (c w)"), -80.0, None, ALU.max).then_inc(sums_ready, 1)
            dve.wait_ge(root_ready, 1)
            step(nc.vector.tensor_tensor(conv[:], conv[:], r_gate[:], ALU.mult))
            dve.wait_ge(root_ready, 2)
            step(nc.vector.tensor_tensor(conv[:], conv[:], i_gate[:], ALU.mult))
            step(nc.vector.tensor_tensor_scan(out_sb.rearrange("p c w -> p (c w)"), alive[:], conv[:], 0.0, ALU.mult, ALU.add))
            nc.vector.tensor_tensor(conv[:], out_sb.rearrange("p c w -> p (c w)"), work[:], ALU.mult).then_inc(h_ready, 1)
            dve.wait_ge(h_ready, 1)
            for c in range(CH):
                cols = slice(CW * c, CW * c + CW)
                dve.wait_ge(root_kept, c + 1)
                step(nc.vector.reciprocal(r_gate[:, cols], r_gate[:, cols]))
                step(nc.vector.scalar_tensor_tensor(r_gate[:, cols], r_gate[:, cols], norm_w[:, 0:1], out_sb[:, c, :], ALU.mult, ALU.mult))
                goal = x[:, CB * c:CB * c + CB, 0:S]
                nc.vector.tensor_tensor(goal, goal, r_gate[:, cols].rearrange("p (b s) -> p b s", s=SP)[:, :, 0:S], ALU.add).then_inc(added, 1)


BF16 = mybir.dt.bfloat16
PR = HX // 2
RW = 2 * S
PF = 2 * DX
PARTS = 3
KEY_PART, QUERY_PART = (0, 0, 0, 1, 1, 2), (0, 1, 2, 0, 1, 0)
SLOTS = len(KEY_PART)
TALL = SLOTS * PF
KEPT = [1, 1, 1, 1, 1, 1, 2, 0]
VC = P // 32
VR = NC_ // VC
VW = PR * (PF + 1) + 32 - (PF + 1)


def cross_attention(chip, layer, scale):
    nc, ps, xn, x = chip.nc, chip.ps, chip.xn, chip.x
    tag = "x%d_" % layer
    (weights_landed, consts_ready, q_made, q_kept, q_high, q_rest, q_mid, q_low) = (chip.sem(tag + k) for k in (
        "weights_landed", "consts_ready", "q_made", "q_kept", "q_high", "q_rest", "q_mid", "q_low"))
    filled, both_filled, values_filled = (chip.sem(tag + k) for k in ("filled", "both_filled", "values_filled"))
    ctx_landed = [chip.sem(tag + "ctx_landed%d" % u) for u in range(2)]
    stacked = [[chip.sem(tag + "stacked%d_%d" % (u, h)) for h in range(2)] for u in range(2)]
    k_done, k_high, k_rest, k_mid, k_low, v_done, v_kept = (chip.sem(tag + k) for k in ("k_done", "k_high", "k_rest", "k_mid", "k_low", "v_done", "v_kept"))
    scores_done, topped, tops_made, tops_split, tops_turned, tops_placed = (
        chip.sem(tag + k) for k in ("scores_done", "topped", "tops_made", "tops_split", "tops_turned", "tops_placed"))
    turned_done, exp_done, mixed, mixed_kept, folded, mix_kept = (
        chip.sem(tag + k) for k in ("turned_done", "exp_done", "mixed", "mixed_kept", "folded", "mix_kept"))
    projected, added, tops_chain, mix_chain, first_placed, biased = (chip.sem(tag + k) for k in ("projected", "added", "tops_chain", "mix_chain", "first_placed", "biased"))
    TURNED, MIX, TURNS = 3, 6, 7
    BODY = range(1, B // 2 - 2)

    def wait(engine, semaphore, value):
        if not isinstance(value, int) or value > 0:
            engine.wait_ge(semaphore, value)

    def all_passes(engine, one_pass):
        for o in (-2, -1, 0, 1):
            one_pass(0, o)
        with engine.Fori(BODY.start, BODY.stop) as j:
            one_pass(j, 0)
            one_pass(j, 1)
        for o in range(5):
            one_pass(B // 2 - 2, o)

    def has(j, o, ahead):
        return not isinstance(j, int) or 0 <= 2 * j + o + ahead < B

    with ExitStack() as own:
        def sbuf(name, shape, dtype=F32):
            return own.enter_context(nc.sbuf_tensor(tag + name, shape, dtype))
        wq, wk, wv, wo = (sbuf(n, [P, P]) for n in ("wq", "wk", "wv", "wo"))
        bq, bk, bv, bo = (sbuf(n, [P, 1]) for n in ("bq", "bk", "bv", "bo"))
        place = sbuf("place", [P, 2, 2, 2, 32])
        parity = sbuf("parity", [P, 2])
        pair_rows, ident_low = sbuf("pair_rows", [P, PR]), sbuf("ident_low", [P, P], BF16)
        ctx_t = [sbuf("ctx_t%d" % u, [P, NK]) for u in range(2)]
        key_parts = [[sbuf("key_part%d_%d" % (u, k), [P, NK], BF16) for k in range(PARTS)] for u in range(2)]
        query_parts = [sbuf("query_part%d" % k, [P, B, 2, S], BF16) for k in range(PARTS)]
        q, q_left = sbuf("q", [P, CH, CT]), [sbuf("q_left%d" % k, [P, CT]) for k in range(2)]
        key_left = [sbuf("key_left%d" % n, [P, KB]) for n in range(NB_)]
        nothing = sbuf("nothing", [P, KB])
        keys = [sbuf("keys%d" % u, [P, PR, NK], BF16) for u in range(2)]
        queries = [sbuf("queries%d" % u, [P, PR, RW], BF16) for u in range(2)]
        values = [sbuf("values%d" % u, [KC, NC_, VW]) for u in range(2)]
        probs_t = [sbuf("probs_t%d" % u, [KC, NC_, RW]) for u in range(2)]
        bank_top = sbuf("bank_top", [P, PR, NB_])
        top, top_left, top_parts = sbuf("top", [P, PR]), sbuf("top_left", [P, PR]), sbuf("top_parts", [P, 32], BF16)
        quarters = [sbuf("quarters%d" % u, [P, PR, 2, S]) for u in range(2)]
        inverse, mix = sbuf("inverse", [P, S]), sbuf("mix", [P, B, S])
        block = own.enter_context(nc.Block(no_gpsimd_drain=True))

        @block.sync
        def _(sp):
            for dst, name in ((wq, "Wq"), (wk, "Wk"), (wv, "Wv"), (wo, "Wo"), (bq, "bq"), (bk, "bk"), (bv, "bv"), (bo, "bo")):
                sp.dma_start(dst[:], chip.dram["L%d_xattn_%s" % (layer, name)]).then_inc(weights_landed, 16)
            for dst, name in ((place, "place"), (parity, "parity"), (pair_rows, "pair_rows")):
                sp.dma_start(dst[:], chip.dram[name]).then_inc(weights_landed, 16)

            def context(j, o):
                wait(sp, v_done, VR * (2 * j + o - 1))
                source = chip.dram["ctx_t"].rearrange("(j u) p n -> u j p n", u=2)[o % 2, o // 2:][bass.ds(j, 1)].rearrange("a p n -> (a p) n")
                sp.dma_start(ctx_t[o % 2][:], source).then_inc(ctx_landed[o % 2], 16)

            def stack(j, o, h):
                u = o % 2
                wait(sp, turned_done, PR * (2 * j + o - 2) + (5 if h == 0 else PR))
                if isinstance(j, int):
                    sp.wait_ge(k_low, NB_ * (2 * j + o) + NB_)
                source = slice(64 * h, 64 * h + 64)
                for s in range(SLOTS):
                    rows = slice(PF * s, PF * s + PF)
                    sp.dma_start(keys[u][rows, 4 * h:4 * h + 4].rearrange("r p n -> r (p n)"),
                                 key_parts[u][KEY_PART[s]][source]).then_inc(stacked[u][h], 16)
                    queries_of = query_parts[QUERY_PART[s]].rearrange("f (j u) c s -> f u j c s", u=2)[source, u, o // 2:]
                    sp.dma_start(queries[u][rows, 4 * h:4 * h + 4].rearrange("r p n -> r (p n)"),
                                 queries_of[:, bass.ds(j, 1)].rearrange("f b c s -> f (b c s)")).then_inc(stacked[u][h], 16)

            context(0, 0)
            context(0, 1)

            def one_pass(j, o):
                if o == -2:
                    sp.wait_ge(q_low, 2 * CH)
                if has(j, o, 1):
                    stack(j, o + 1, 1)
                if has(j, o, 2):
                    stack(j, o + 2, 0)
                if has(j, o, 3) and o + 3 > 1:
                    context(j, o + 3)
                if o == -2:
                    sp.wait_ge(filled, 1)
                    sp.dma_start(keys[0][TALL:P].rearrange("r p n -> r (p n)"), keys[1][TALL:P].rearrange("r p n -> r (p n)")).then_inc(both_filled, 16)
            all_passes(sp, one_pass)

        @block.tensor
        def _(pe):
            def make_keys(j, o, n):
                if n == 0:
                    wait(pe, ctx_landed[o % 2], 16 * (j + o // 2) + 16)
                    wait(pe, mix_kept, 2 * j + o - 3)
                    if isinstance(j, int) and 0 < 2 * j + o < 4:
                        pe.wait_ge(v_kept if 2 * j + o > 1 else k_rest, VR * (2 * j + o - 1) if 2 * j + o > 1 else NB_)
                else:
                    pe.wait_ge(k_rest, NB_ * (2 * j + o) + n)
                nc.tensor.matmul(ps[:, TURNS, 0:KB], wk[:], ctx_t[o % 2][:, KB * n:KB * n + KB], start=True, stop=True).then_inc(k_done, 1)

            def make_values(j, o, r):
                if r > 0:
                    pe.wait_ge(v_kept, VR * (2 * j + o) + r)
                elif has(j, o, 1):
                    pe.wait_ge(k_rest, NB_ * (2 * j + o + 1) + NB_)
                else:
                    pe.wait_ge(mix_kept, 2 * j + o - 2)
                for c in range(VC):
                    k0 = KC * (VC * r + c)
                    mm = nc.tensor.matmul(ps[0:KC, TURNS, P * c:P * c + P], ctx_t[o % 2][:, k0:k0 + KC], wv[:], start=True, stop=True)
                mm.then_inc(v_done, 1)

            def scores(j, o, p):
                if p % 4 == 0:
                    pe.wait_ge(stacked[o % 2][p // 4], 2 * SLOTS * 16 * (j + o // 2 + 1))
                if p == 0:
                    wait(pe, tops_placed, 2 * j + o)
                for n in range(NB_):
                    wait(pe, topped, NB_ * (PR * (2 * j + o) + p - 1) + n + 1)
                    nc.tensor.matmul(ps[0:RW, n, 0:KB], queries[o % 2][0:TALL, p, :], keys[o % 2][0:TALL, p, KB * n:KB * n + KB],
                                     start=True, stop=True).then_inc(scores_done, 1)

            def turn_tops(j, o):
                pe.wait_ge(tops_split, 2 * j + o + 1)
                nc.tensor.matmul(ps[TALL:P, 0, 0:RW], top_parts[:], ident_low[:, 0:RW], start=True, stop=True).then_inc(tops_turned, 1)

            def scores_by_key(j, o, p):
                if p == 0:
                    pe.wait_ge(first_placed, 2 * j + o + 1)
                    if isinstance(j, int) and j == 0:
                        pe.wait_ge(both_filled, 16)
                if p == 1:
                    pe.wait_ge(tops_placed, 2 * j + o + 1)
                if p == 4 and has(j, o, 2):
                    pe.wait_ge(k_low, NB_ * (2 * j + o + 2) + NB_)
                wait(pe, exp_done, PR * (2 * j + o) + p)
                for c in range(NC_):
                    mm = nc.tensor.matmul(ps[0:KC, TURNED + c // VC, RW * (c % VC):RW * (c % VC) + RW],
                                          keys[o % 2][:, p, KC * c:KC * c + KC], queries[o % 2][:, p, :], start=True, stop=True)
                mm.then_inc(turned_done, 1)

            def mix_values(j, o, p):
                pe.wait_ge(exp_done, PR * (2 * j + o) + p + 1)
                if p % 4 == 0:
                    wait(pe, mixed_kept, 2 * (2 * j + o) + p // 4)
                if p == 0:
                    pe.wait_ge(v_kept, VR * (2 * j + o) + VR)
                for c in range(NC_):
                    g = c % 4
                    mm = nc.tensor.matmul(ps[32 * g:32 * g + 32, MIX, RW * (p % 4):RW * (p % 4) + RW], values[o % 2][:, c, (PF + 1) * p:(PF + 1) * p + 32],
                                          probs_t[p % 2][:, c, :], start=(c < 4), stop=(c >= NC_ - 4))
                if p % 4 == 3:
                    mm.then_inc(mixed, 1)

            def fold(j, o):
                pe.wait_ge(mixed_kept, 2 * (2 * j + o) + 2)
                if has(j, o, 2):
                    pe.wait_ge(v_kept, VR * (2 * j + o + 2) + VR)
                else:
                    pe.wait_ge(mix_kept, 2 * j + o)
                for what in range(2):
                    for step in range(4):
                        odd, parity = divmod(step, 2)
                        for g in range(4):
                            mm = nc.tensor.matmul(ps[32 * g:32 * g + 32, TURNS, S * what:S * what + S], place[:, parity, odd, what, :],
                                                  quarters[o % 2][:, 2 * g + odd, parity, :], start=(step == 0), stop=(step == 3))
                mm.then_inc(folded, 1)

            pe.wait_ge(weights_landed, 11 * 16)
            for c in range(CH):
                nc.tensor.matmul(ps[:, c, 0:CT], wq[:], xn[:, CB * c:CB * c + CB, 0:S], start=True, stop=True).then_inc(q_made, 1)
            pe.wait_ge(consts_ready, 1)
            pe.wait_ge(q_kept, CH)

            def one_pass(j, o):
                for step in range(PR):
                    if has(j, o, 0):
                        scores_by_key(j, o, step)
                    if step < NB_ and has(j, o, 2):
                        make_keys(j, o + 2, step)
                    if NB_ <= step < NB_ + VR and has(j, o, 1):
                        make_values(j, o + 1, step - NB_)
                    first = sum(KEPT[:step])
                    if has(j, o, 1) and KEPT[step] > 0:
                        scores(j, o + 1, first)
                    if step > 0 and has(j, o, 0):
                        mix_values(j, o, step - 1)
                    if has(j, o, 1) and KEPT[step] > 1:
                        scores(j, o + 1, first + 1)
                if has(j, o, 0):
                    mix_values(j, o, PR - 1)
                if has(j, o, 1):
                    turn_tops(j, o + 1)
                if has(j, o, -1):
                    fold(j, o - 1)
            all_passes(pe, one_pass)
            for c in range(CH):
                pe.wait_ge(biased, c + 1)
                nc.tensor.matmul(ps[:, c, 0:CT], wo[:], mix[:, CB * c:CB * c + CB, :].rearrange("p b s -> p (b s)"),
                                 start=True, stop=True).then_inc(projected, 1)

        @block.scalar
        def _(act):
            def keep_keys(j, o, n):
                act.wait_ge(k_done, NB_ * (2 * j + o) + n + 1)
                nc.scalar.activation(key_parts[o % 2][0][:, KB * n:KB * n + KB], ps[:, TURNS, 0:KB], ACT.Identity, bias=bk[:, 0:1]).then_inc(k_high, 1)

            def keep_values(j, o, r):
                act.wait_ge(v_done, VR * (2 * j + o) + r + 1)
                nc.scalar.copy(values[o % 2][:, VC * r:VC * r + VC, 0:PR * (PF + 1)].rearrange("p c (j f) -> p c j f", f=PF + 1)[:, :, :, 0:PF],
                               ps[0:KC, TURNS, :].rearrange("p (c j f) -> p c j f", c=VC, f=PF)).then_inc(v_kept, 1)

            def exponentials(j, o, p):
                act.wait_ge(turned_done, PR * (2 * j + o) + p + 1)
                nc.scalar.activation(probs_t[p % 2].rearrange("k (n c) r -> k n (c r)", c=VC), ps[0:KC, TURNED:TURNED + VR, 0:VC * RW],
                                     ACT.Exp, scale=scale).then_inc(exp_done, 1)

            def keep_mixed(j, o, half):
                act.wait_ge(mixed, 2 * (2 * j + o) + half + 1)
                nc.scalar.copy(quarters[o % 2][:, 4 * half:4 * half + 4].rearrange("p j c s -> p (j c s)"), ps[:, MIX, 0:4 * RW]).then_inc(mixed_kept, 1)

            act.wait_ge(values_filled, 2)
            act.wait_ge(weights_landed, 11 * 16)
            for c in range(CH):
                act.wait_ge(q_kept, c + 1)
                for k in range(2):
                    nc.scalar.activation(query_parts[0][:, CB * c:CB * c + CB, k, :], q[:, c, :].rearrange("p (b s) -> p b s", s=S),
                                         ACT.Copy, scale=parity[:, k:k + 1]).then_inc(q_high, 1)
                for k in range(2):
                    act.wait_ge(q_rest, 2 * c + k + 1)
                    nc.scalar.copy(query_parts[1][:, CB * c:CB * c + CB, k, :], q_left[k].rearrange("p (b s) -> p b s", s=S)).then_inc(q_mid, 1)

            def one_pass(j, o):
                for step in range(PR):
                    if has(j, o, 0):
                        exponentials(j, o, step)
                    if step < NB_ and has(j, o, 2):
                        keep_keys(j, o + 2, step)
                    if NB_ <= step < NB_ + VR and has(j, o, 1):
                        keep_values(j, o + 1, step - NB_)
                    if step == 4 and has(j, o, 0):
                        keep_mixed(j, o, 0)
                if has(j, o, 0):
                    keep_mixed(j, o, 1)
                if o == -2:
                    nc.scalar.copy(keys[1][TALL:P], spread(pair_rows[TALL:P, :], 2, NK)).then_inc(filled, 1)
            all_passes(act, one_pass)

        @block.gpsimd
        def _(pool):

            def one_pass(j, o):
                if not has(j, o, 2):
                    return
                for n in range(NB_):
                    part, cols = key_parts[o % 2], slice(KB * n, KB * n + KB)
                    pool.wait_ge(k_rest, NB_ * (2 * j + o + 2) + n + 1)
                    nc.gpsimd.tensor_tensor(part[1][:, cols], key_left[n][:], nothing[:], ALU.add).then_inc(k_mid, 1)
                    pool.wait_ge(k_mid, NB_ * (2 * j + o + 2) + n + 1)
                    nc.gpsimd.tensor_tensor(part[2][:, cols], key_left[n][:], part[1][:, cols], ALU.subtract).then_inc(k_low, 1)
            all_passes(pool, one_pass)

        @block.vector
        def _(dve):
            def rest_of_keys(j, o, n):
                dve.wait_ge(k_high, NB_ * (2 * j + o) + n + 1)
                wait(dve, k_low, NB_ * (2 * j + o - 1) + n + 1)
                nc.vector.scalar_tensor_tensor(key_left[n][:], ps[:, TURNS, 0:KB], bk[:, 0:1],
                                               key_parts[o % 2][0][:, KB * n:KB * n + KB], ALU.add, ALU.subtract).then_inc(k_rest, 1)

            def row_tops(j, o, p):
                for n in range(NB_):
                    dve.wait_ge(scores_done, NB_ * (PR * (2 * j + o) + p) + n + 1)
                    nc.vector.tensor_reduce(bank_top[0:RW, p, n:n + 1], ps[0:RW, n, 0:KB], AX_X, ALU.max).then_inc(topped, 1)

            def split_tops(j, o):
                n = 3 * (2 * j + o)
                dve.wait_ge(topped, NB_ * (PR * (2 * j + o) + PR))
                nc.vector.tensor_reduce(top[0:RW, :], bank_top[0:RW], AX_X, ALU.max).then_inc(tops_made, 1)
                dve.wait_ge(tops_made, 2 * j + o + 1)
                nc.vector.tensor_scalar(top_parts[0:RW, 0:PR], top[0:RW, :], -1.0, None, ALU.mult).then_inc(tops_chain, 1)
                dve.wait_ge(tops_chain, n + 1)
                nc.vector.scalar_tensor_tensor(top_left[0:RW, :], top[0:RW, :], -1.0, top_parts[0:RW, 0:PR], ALU.mult, ALU.subtract).then_inc(tops_chain, 1)
                dve.wait_ge(tops_chain, n + 2)
                nc.vector.tensor_copy(top_parts[0:RW, PR:2 * PR], top_left[0:RW, :]).then_inc(tops_chain, 1)
                dve.wait_ge(tops_chain, n + 3)
                nc.vector.tensor_tensor(top_parts[0:RW, 2 * PR:3 * PR], top_left[0:RW, :], top_parts[0:RW, PR:2 * PR], ALU.subtract).then_inc(tops_split, 1)
                dve.wait_ge(tops_turned, 2 * j + o + 1)
                turned = ps[TALL:P, 0, 0:RW]
                nc.vector.tensor_copy(queries[o % 2][TALL:P, 0, :], turned).then_inc(first_placed, 1)
                nc.vector.tensor_copy(queries[o % 2][TALL:P, 1:PR], spread(turned, 1, PR - 1)).then_inc(tops_placed, 1)

            def keep_mix(j, o):
                i = 2 * j + o
                dve.wait_ge(folded, i + 1)
                nc.vector.reciprocal(inverse[:], ps[:, TURNS, S:2 * S]).then_inc(mix_chain, 1)
                dve.wait_ge(mix_chain, i + 1)
                goal = mix[:, bass.ds(i, 1), :].rearrange("p b s -> p (b s)")
                nc.vector.tensor_tensor(goal, ps[:, TURNS, 0:S], inverse[:], ALU.mult).then_inc(mix_kept, 1)

            nc.vector.memset(nothing[:], 0.0)
            for u in range(2):
                nc.vector.memset(values[u][:], 1.0).then_inc(values_filled, 1)
            nc.vector.memset(top_parts[:], 0.0)
            nc.vector.tensor_copy(ident_low[:], chip.ident[:]).then_inc(consts_ready, 1)
            dve.wait_ge(weights_landed, 11 * 16)
            for c in range(CH):
                dve.wait_ge(q_made, c + 1)
                nc.vector.tensor_scalar(q[:, c, :], ps[:, c, 0:CT], bq[:, 0:1], None, ALU.add).then_inc(q_kept, 1)
            dve.wait_ge(q_kept, CH)
            for c in range(CH):
                for k in range(2):
                    dve.wait_ge(q_high, 2 * c + k + 1)
                    if c > 0:
                        dve.wait_ge(q_low, 2 * c - 1 + k)
                    nc.vector.scalar_tensor_tensor(q_left[k].rearrange("p (b s) -> p b s", s=S), q[:, c, :].rearrange("p (b s) -> p b s", s=S),
                                                   parity[:, k:k + 1], query_parts[0][:, CB * c:CB * c + CB, k, :],
                                                   ALU.mult, ALU.subtract).then_inc(q_rest, 1)
                for k in range(2):
                    dve.wait_ge(q_rest, 2 * c + k + 1)
                    dve.wait_ge(q_mid, 2 * c + k + 1)
                    nc.vector.tensor_tensor(query_parts[2][:, CB * c:CB * c + CB, k, :], q_left[k].rearrange("p (b s) -> p b s", s=S),
                                            query_parts[1][:, CB * c:CB * c + CB, k, :], ALU.subtract).then_inc(q_low, 1)

            def one_pass(j, o):
                for step in range(PR):
                    if step < NB_ and has(j, o, 2):
                        rest_of_keys(j, o + 2, step)
                    for p in range(sum(KEPT[:step]), sum(KEPT[:step + 1])):
                        if has(j, o, 1):
                            row_tops(j, o + 1, p)
                if has(j, o, 1):
                    split_tops(j, o + 1)
                if has(j, o, -1):
                    keep_mix(j, o - 1)
            all_passes(dve, one_pass)
            dve.wait_ge(mix_kept, B)
            for c in range(CH):
                chunk = mix[:, CB * c:CB * c + CB, :]
                nc.vector.tensor_scalar(chunk, chunk, bv[:, 0:1], None, ALU.add).then_inc(biased, 1)
            for c in range(CH):
                goal = x[:, CB * c:CB * c + CB, 0:S]
                dve.wait_ge(projected, c + 1)
                nc.vector.scalar_tensor_tensor(goal, ps[:, c, 0:CT].rearrange("p (b s) -> p b s", s=S), bo[:, 0:1], goal,
                                               ALU.add, ALU.add).then_inc(added, 1)


MARK = -2.0 ** 100


def spacer(n):
    return -2.0 ** (90 + n)


class Router:

    def __init__(self, chip, own, tag, experts, k, bias=None, scale=None):
        nc = chip.nc
        self.chip, self.tag, self.e, self.k, self.scale = chip, tag, experts, k, scale
        e = experts

        def sbuf(name, shape):
            return own.enter_context(nc.sbuf_tensor(tag + name, shape, F32))
        self.bias = bias
        self.top1, self.total = sbuf("top1", [P, NP_]), sbuf("total", [P, NP_])
        self.scores, self.weights = sbuf("scores", [P, NP_, e]), sbuf("weights", [P, NP_, e])
        self.found = sbuf("found", [P, NP_, e + 8 - k])
        self.marked = sbuf("marked", [P, NP_, e + 8 - k])
        self.top8 = sbuf("top8", [P, NP_, 8])
        self.logits_done, self.shifted, self.exp_done, self.chain, self.ready = (
            chip.sem(tag + n) for n in ("logits_done", "shifted", "exp_done", "route_chain", "weights_ready"))
        self.logits = chip.ps[:, 0:2, :].rearrange("p k (t e) -> p (k t) e", e=64)[:, :, 0:e]

    def make_logits(self, pe, source, weight):
        nc = self.chip.nc
        for t in range(NP_):
            mm = nc.tensor.matmul(self.chip.ps[:, t // 8, 64 * (t % 8):64 * (t % 8) + self.e], source[:, P * t:P * t + P], weight,
                                  start=True, stop=True)
        mm.then_inc(self.logits_done, 1)

    def exponentials(self, act):
        act.wait_ge(self.shifted, 1)
        self.chip.nc.scalar.activation(self.scores[:], self.scores[:], ACT.Exp).then_inc(self.exp_done, 1)

    def choose(self, dve):
        nc, e, k = self.chip.nc, self.e, self.k
        step = Step(dve, self.chain)
        for n in range(8 - k):
            nc.vector.memset(self.found[:, :, e + n:e + n + 1], spacer(n))
        dve.wait_ge(self.logits_done, 1)
        step(nc.vector.tensor_reduce(self.top1[:], self.logits, AX_X, ALU.max))
        nc.vector.tensor_tensor(self.scores[:], self.logits, spread(self.top1[:], 2, e), ALU.subtract).then_inc(self.shifted, 1)
        dve.wait_ge(self.exp_done, 1)
        step(nc.vector.tensor_reduce(self.total[:], self.scores[:], AX_X, ALU.add))
        step(nc.vector.reciprocal(self.total[:], self.total[:]))
        step(nc.vector.tensor_tensor(self.scores[:], self.scores[:], spread(self.total[:], 2, e), ALU.mult))
        if self.bias is None:
            step(nc.vector.tensor_copy(self.found[:, :, 0:e], self.scores[:]))
        else:
            step(nc.vector.tensor_tensor(self.found[:, :, 0:e], self.scores[:], spread(self.bias, 1, NP_), ALU.add))
        for t in range(NP_):
            last = nc.vector.max(self.top8[:, t, :], self.found[:, t, 0:e])
        step(last)
        for n in range(8 - k):
            last = nc.vector.memset(self.top8[:, :, k + n:k + n + 1], spacer(n))
        step(last)
        for t in range(NP_):
            last = nc.vector.match_replace(self.marked[:, t, :], self.top8[:, t, :], self.found[:, t, :], MARK)
        step(last)
        if self.scale is not None:
            step(nc.vector.tensor_scalar(self.weights[:], self.marked[:, :, 0:e], MARK, self.scale, ALU.is_equal, ALU.mult))
            nc.vector.tensor_tensor(self.weights[:], self.weights[:], self.scores[:], ALU.mult).then_inc(self.ready, 1)
        else:
            step(nc.vector.tensor_scalar(self.marked[:, :, 0:e], self.marked[:, :, 0:e], MARK, None, ALU.is_equal))
            step(nc.vector.tensor_tensor(self.weights[:], self.marked[:, :, 0:e], self.scores[:], ALU.mult))
            step(nc.vector.tensor_reduce(self.total[:], self.weights[:], AX_X, ALU.add))
            step(nc.vector.reciprocal(self.total[:], self.total[:]))
            nc.vector.tensor_tensor(self.weights[:], self.weights[:], spread(self.total[:], 2, e), ALU.mult).then_inc(self.ready, 1)
        return step


def experts(chip, tag, name, groups, subs, rows, gated, weight_rows):
    nc, ps, xn, x = chip.nc, chip.ps, chip.xn, chip.x
    landed = [chip.sem(tag + "landed%d" % u) for u in range(2)]
    used = [chip.sem(tag + "used%d" % u) for u in range(2)]
    zero_ready, up_done, gate_kept, hidden_ready, weighted, summed, added = (
        chip.sem(tag + k) for k in ("zero_ready", "up_done", "gate_kept", "hidden_ready", "weighted", "summed", "added"))
    M = 3 if gated else 2
    steps = [(u, s, c) for u in range(2) for s in range(subs) for c in range(CH)]
    N = len(steps)
    with ExitStack() as own:
        def sbuf(name, shape):
            return own.enter_context(nc.sbuf_tensor(tag + name, shape, F32))
        w = [sbuf("w%d" % u, [P, subs, M, P]) for u in range(2)]
        share = [sbuf("share%d" % u, [P, B * S]) for u in range(2)]
        silu = [sbuf("silu%d" % k, [P, CT]) for k in range(2)]
        hidden = [sbuf("hidden%d" % k, [P, CT]) for k in range(2)]
        zero = sbuf("zero", [P, P])
        tokens = [xn[:, CB * c:CB * c + CB, 0:S] for c in range(CH)]
        block = own.enter_context(nc.Block(no_gpsimd_drain=True))

        @block.sync
        def _(sp):
            with sp.Fori(0, groups // 2) as i:
                for u in range(2):
                    sp.wait_ge(used[u], i + 1)
                    sp.dma_start(w[u][:], chip.dram[name][bass.ds(2 * i + u, 1)].rearrange("g p s m d -> (g p) s m d")).then_inc(landed[u], 16)
                    for r in range(rows):
                        n = P // rows
                        sp.dma_start(share[u][n * r:n * r + n, :], weight_rows[bass.ds(rows * (2 * i + u) + r, 1), :].to_broadcast([n, B * S])).then_inc(landed[u], 16)

        @block.tensor
        def _(pe):
            def up(i, n):
                u, s, c = steps[n]
                if s == 0 and c == 0:
                    pe.wait_ge(landed[u], 16 * (rows + 1) * i + 16 * (rows + 1))
                for m in range(M - 1):
                    mm = nc.tensor.matmul(ps[:, 4 + 2 * (n % 2) + m, 0:CT], w[u][:, s, m, :], tokens[c], start=True, stop=True)
                mm.then_inc(up_done, 1)

            def down(i, n):
                u, s, c = steps[n]
                pe.wait_ge(hidden_ready, N * i + n + 1)
                mm = nc.tensor.matmul(ps[:, c, 0:CT], w[u][:, s, M - 1, :], hidden[n % 2][:], start=False, stop=False, skip_group_check=True)
                if s == subs - 1 and c == CH - 1:
                    mm.then_inc(used[u], 1)

            pe.wait_ge(zero_ready, 1)
            for c in range(CH):
                nc.tensor.matmul(ps[:, c, 0:CT], zero[:], tokens[c], start=True, stop=False, skip_group_check=True)
            with pe.Fori(0, groups // 2) as i:
                for n in range(N):
                    up(i, n)
                    if n:
                        down(i, n - 1)
                down(i, N - 1)
            for c in range(CH):
                nc.tensor.matmul(ps[:, c, 0:CT], zero[:], tokens[c], start=False, stop=True, skip_group_check=True).then_inc(summed, 1)

        @block.scalar
        def _(act):
            with act.Fori(0, groups // 2) as i:
                for n in range(N):
                    act.wait_ge(up_done, N * i + n + 1)
                    nc.scalar.activation(silu[n % 2][:], ps[:, 4 + 2 * (n % 2), 0:CT], ACT.Silu).then_inc(gate_kept, 1)

        @block.vector
        def _(dve):
            nc.vector.memset(zero[:], 0.0).then_inc(zero_ready, 1)
            for u in range(2):
                nc.vector.memset(chip.credit[:, u:u + 1], 0.0).then_inc(used[u], 1)
            with dve.Fori(0, groups // 2) as i:
                for n in range(N):
                    u, s, c = steps[n]
                    if s == 0 and c == 0:
                        dve.wait_ge(landed[u], 16 * (rows + 1) * i + 16 * (rows + 1))
                    if gated:
                        dve.wait_ge(up_done, N * i + n + 1)
                        nc.vector.tensor_tensor(hidden[n % 2][:], ps[:, 5 + 2 * (n % 2), 0:CT], share[u][:, CT * c:CT * c + CT], ALU.mult).then_inc(weighted, 1)
                        dve.wait_ge(weighted, N * i + n + 1)
                        dve.wait_ge(gate_kept, N * i + n + 1)
                        nc.vector.tensor_tensor(hidden[n % 2][:], hidden[n % 2][:], silu[n % 2][:], ALU.mult).then_inc(hidden_ready, 1)
                    else:
                        dve.wait_ge(gate_kept, N * i + n + 1)
                        nc.vector.tensor_tensor(hidden[n % 2][:], silu[n % 2][:], share[u][:, CT * c:CT * c + CT], ALU.mult).then_inc(hidden_ready, 1)
            for c in range(CH):
                goal = x[:, CB * c:CB * c + CB, 0:S]
                dve.wait_ge(summed, c + 1)
                nc.vector.tensor_tensor(goal, goal, ps[:, c, 0:CT].rearrange("p (b s) -> p b s", s=S), ALU.add).then_inc(added, 1)


def mixture_1(chip):
    nc, ps, xn, x = chip.nc, chip.ps, chip.xn, chip.x
    E_R, E_Z, K = 32, 8, 6
    E = E_R + E_Z
    scratch = nc.dram_tensor("m1_weight_rows", (E, B * S), F32, kind="Internal").ap()
    landed, turned, rows_kept, stored, passed, added, mask_ready, product_ready = (
        chip.sem("m1_" + k) for k in ("landed", "turned", "rows_kept", "stored", "passed", "added", "mask_ready", "product_ready"))
    with ExitStack() as own:
        def sbuf(name, shape):
            return own.enter_context(nc.sbuf_tensor("m1_" + name, shape, F32))
        classifier, bias = sbuf("classifier", [P, E]), sbuf("bias", [P, E])
        rows, passing, product = sbuf("rows", [E, NP_ * P]), sbuf("passing", [E, P]), sbuf("product", [P, CT])
        router = Router(chip, own, "m1_", E, K, bias[:], 2.5)
        flat = xn.rearrange("p b s -> p (b s)")
        block = own.enter_context(nc.Block())

        @block.sync
        def _(sp):
            sp.dma_start(classifier[:], chip.dram["L1_ffn_classifier_weight"]).then_inc(landed, 16)
            sp.dma_start(bias[:], chip.dram["L1_ffn_e_score_correction_bias"].to_broadcast([P, E])).then_inc(landed, 16)
            sp.wait_ge(rows_kept, 1)
            sp.dma_start(scratch.rearrange("e (b s) -> e b s", s=S), rows.rearrange("e (b s) -> e b s", s=SP)[:, :, 0:S]).then_inc(stored, 16)
            sp.wait_ge(stored, 16)

        @block.tensor
        def _(pe):
            pe.wait_ge(landed, 32)
            router.make_logits(pe, flat, classifier[:])
            pe.wait_ge(router.ready, 1)
            for t in range(NP_):
                mm = nc.tensor.transpose(ps[0:E, 4 + t // 4, P * (t % 4):P * (t % 4) + P], router.weights[:, t, :], chip.ident[:])
            mm.then_inc(turned, 1)
            pe.wait_ge(rows_kept, 1)
            pe.wait_ge(mask_ready, 2)
            for c in range(CH):
                nc.tensor.matmul(ps[:, c, 0:CT], passing[:], rows[:, CW * c:CW * c + CW].rearrange("e (b s) -> e b s", s=SP)[:, :, 0:S],
                                 start=True, stop=True).then_inc(passed, 1)

        @block.scalar
        def _(act):
            router.exponentials(act)
            act.wait_ge(turned, 1)
            nc.scalar.copy(rows[:], ps[0:E, 4:8, :].rearrange("e k n -> e (k n)")).then_inc(rows_kept, 1)

        @block.vector
        def _(dve):
            nc.vector.memset(passing[:], 0.0).then_inc(mask_ready, 1)
            dve.wait_ge(mask_ready, 1)
            nc.vector.memset(passing[E_R:E, :], 1.0).then_inc(mask_ready, 1)
            dve.wait_ge(landed, 32)
            router.choose(dve)
            for c in range(CH):
                goal, tokens = (v[:, CB * c:CB * c + CB, 0:S] for v in (x, xn))
                dve.wait_ge(passed, c + 1)
                if c:
                    dve.wait_ge(added, c)
                nc.vector.tensor_tensor(product.rearrange("p (b s) -> p b s", s=S), tokens,
                                        ps[:, c, 0:CT].rearrange("p (b s) -> p b s", s=S), ALU.mult).then_inc(product_ready, 1)
                dve.wait_ge(product_ready, c + 1)
                nc.vector.tensor_tensor(goal, goal, product.rearrange("p (b s) -> p b s", s=S), ALU.add).then_inc(added, 1)
    experts(chip, "e1_", "L1_ffn_experts", E_R // 2, 1, 2, True, scratch)


def mixture_2(chip):
    nc, ps, xn = chip.nc, chip.ps, chip.xn
    E, K, DFF = 8, 2, 512
    scratch = nc.dram_tensor("m2_weight_rows", (E, B * S), F32, kind="Internal").ap()
    landed, turned, rows_kept, stored = (chip.sem("m2_" + k) for k in ("landed", "turned", "rows_kept", "stored"))
    with ExitStack() as own:
        def sbuf(name, shape):
            return own.enter_context(nc.sbuf_tensor("m2_" + name, shape, F32))
        classifier = sbuf("classifier", [P, E])
        rows = sbuf("rows", [E, NP_ * P])
        router = Router(chip, own, "m2_", E, K)
        block = own.enter_context(nc.Block())

        @block.sync
        def _(sp):
            sp.dma_start(classifier[:], chip.dram["L2_ffn_Wr"]).then_inc(landed, 16)
            sp.wait_ge(rows_kept, 1)
            sp.dma_start(scratch.rearrange("e (b s) -> e b s", s=S), rows.rearrange("e (b s) -> e b s", s=SP)[:, :, 0:S]).then_inc(stored, 16)
            sp.wait_ge(stored, 16)

        @block.tensor
        def _(pe):
            pe.wait_ge(landed, 16)
            router.make_logits(pe, xn.rearrange("p b s -> p (b s)"), classifier[:])
            pe.wait_ge(router.ready, 1)
            for t in range(NP_):
                mm = nc.tensor.transpose(ps[0:E, 4 + t // 4, P * (t % 4):P * (t % 4) + P], router.weights[:, t, :], chip.ident[:])
            mm.then_inc(turned, 1)

        @block.scalar
        def _(act):
            router.exponentials(act)
            act.wait_ge(turned, 1)
            nc.scalar.copy(rows[:], ps[0:E, 4:8, :].rearrange("e k n -> e (k n)")).then_inc(rows_kept, 1)

        @block.vector
        def _(dve):
            router.choose(dve)
    experts(chip, "e2_", "L2_ffn_experts", E, DFF // P, 1, False, scratch)


def experts_by_slot(chip, weight_rows, slot_rows, slot_of, by_token, CAP):
    nc, ps, xn, x = chip.nc, chip.ps, chip.xn, chip.x
    PAIRS, SUBS, LOADS = 16, 2, 6
    BLOCKS = 2 * SUBS + 2
    landed, used = ([chip.sem("e3_%s%d" % (k, u)) for u in range(2)] for k in ("landed", "used"))
    (zero_ready, consts_landed, marks_ready, gathered, gathered_kept, up_done, gate_kept, hidden_ready, down_done, down_kept,
     spread_ready, summed, added) = (chip.sem("e3_" + k) for k in (
         "zero_ready", "consts_landed", "marks_ready", "gathered", "gathered_kept", "up_done", "gate_kept", "hidden_ready", "down_done",
         "down_kept", "spread_ready", "summed", "added"))
    with ExitStack() as own:
        def two(name, shape):
            return [own.enter_context(nc.sbuf_tensor("e3_%s%d" % (name, u), shape, F32)) for u in range(2)]

        def sbuf(name, shape):
            return own.enter_context(nc.sbuf_tensor("e3_" + name, shape, F32))
        w, adapter = two("w", [P, 2, SUBS, 3, P]), two("adapter", [P, 3, P])
        share, spread_out = two("share", [CAP, 2, B * S]), two("spread_out", [CAP, 2, B * S])
        marks = two("marks", [P, NP_, 2, CAP])
        zero, slot, slot_names = sbuf("zero", [P, P]), sbuf("slot", [P, 1]), sbuf("slot_names", [P, CAP])
        tokens_of, silu, hidden = sbuf("tokens_of", [P, 2, CAP]), sbuf("silu", [P, BLOCKS, CAP]), sbuf("hidden", [P, BLOCKS, CAP])
        result = sbuf("result", [CAP, 2, P])
        chunk = [xn[:, CB * c:CB * c + CB, 0:S] for c in range(CH)]
        GATE, UP = 5, 6

        def gather_bank(u):
            return (4, 7)[u]

        def all_steps(engine, one_step):
            with engine.Fori(0, PAIRS // 2 - 1) as i:
                for u in range(2):
                    one_step(i, u, 2)
            for u in range(2):
                one_step(PAIRS // 2 - 1, u, 1 - u)
        block = own.enter_context(nc.Block(no_gpsimd_drain=True))

        @block.sync
        def _(sp):
            for dst, name in ((slot, "slot"), (slot_names, "slot_names")):
                sp.dma_start(dst[:], chip.dram[name]).then_inc(consts_landed, 16)
            with sp.Fori(0, PAIRS // 2) as i:
                for u in range(2):
                    n = 2 * i + u
                    sp.wait_ge(used[u], i + 1)
                    sp.dma_start(w[u][:], chip.dram["L3_ffn_experts"][bass.ds(2 * n, 2)].rearrange("e p s m d -> p e s m d")).then_inc(landed[u], 16)
                    sp.dma_start(adapter[u][:], chip.dram["L3_ffn_adapters"][bass.ds(n, 1)].rearrange("g p s m d -> (g p s) m d")).then_inc(landed[u], 16)
                    for e in range(2):
                        for dst, rows in ((share, weight_rows), (spread_out, slot_rows)):
                            sp.dma_start(dst[u][:, e, :], rows[bass.ds(2 * n + e, 1), :].to_broadcast([CAP, B * S])).then_inc(landed[u], 16)

        @block.tensor
        def _(pe):
            def gather(i, u):
                pe.wait_ge(marks_ready, 2 * i + u + 1)
                for t in range(NP_):
                    mm = nc.tensor.matmul(ps[:, gather_bank(u), 0:2 * CAP], by_token[:, t, :], marks[u][:, t].rearrange("p e k -> p (e k)"),
                                          start=(t == 0), stop=(t == NP_ - 1))
                mm.then_inc(gathered, 1)

            def one_step(i, u, more):
                n = 2 * i + u
                pe.wait_ge(landed[u], 16 * LOADS * i + 16 * LOADS)
                pe.wait_ge(gathered_kept, n + 1)
                for m, bank in ((0, GATE), (1, UP)):
                    for e in range(2):
                        for k in range(SUBS):
                            c0 = CAP * (SUBS * e + k)
                            nc.tensor.matmul(ps[:, bank, c0:c0 + CAP], w[u][:, e, k, m, :], tokens_of[:, e, :], start=True, stop=True)
                    mm = nc.tensor.matmul(ps[:, bank, 2 * SUBS * CAP:BLOCKS * CAP], adapter[u][:, m, :], tokens_of.rearrange("p e k -> p (e k)"),
                                          start=True, stop=True)
                mm.then_inc(up_done, 1)
                if more:
                    gather(i + (u + 1) // 2, (u + 1) % 2)
                pe.wait_ge(hidden_ready, n + 1)
                for e in range(2):
                    for k in range(SUBS + 1):
                        block_of, down = (SUBS * e + k, w[u][:, e, k, 2, :]) if k < SUBS else (2 * SUBS + e, adapter[u][:, 2, :])
                        mm = nc.tensor.matmul(ps[0:CAP, gather_bank(u), 2 * P + P * e:2 * P + P * e + P], hidden[:, block_of, :], down,
                                              start=(k == 0), stop=(k == SUBS))
                mm.then_inc(down_done, 1)
                pe.wait_ge(spread_ready, 2 * n + 2)
                pe.wait_ge(down_kept, n + 1)
                for e in range(2):
                    for c in range(CH):
                        mm = nc.tensor.matmul(ps[:, c, 0:CT], result[:, e, :], spread_out[u][:, e, CT * c:CT * c + CT],
                                              start=False, stop=False, skip_group_check=True)
                mm.then_inc(used[u], 1)

            pe.wait_ge(zero_ready, 1)
            for c in range(CH):
                nc.tensor.matmul(ps[:, c, 0:CT], zero[:], chunk[c], start=True, stop=False, skip_group_check=True)
            gather(0, 0)
            all_steps(pe, one_step)
            for c in range(CH):
                nc.tensor.matmul(ps[:, c, 0:CT], zero[:], chunk[c], start=False, stop=True, skip_group_check=True).then_inc(summed, 1)

        @block.scalar
        def _(act):
            def keep_gathered(i, u):
                act.wait_ge(gathered, 2 * i + u + 1)
                nc.scalar.copy(tokens_of.rearrange("p e k -> p (e k)"), ps[:, gather_bank(u), 0:2 * CAP]).then_inc(gathered_kept, 1)

            def one_step(i, u, more):
                n = 2 * i + u
                act.wait_ge(up_done, n + 1)
                nc.scalar.activation(silu.rearrange("p a k -> p (a k)"), ps[:, GATE, 0:BLOCKS * CAP], ACT.Silu).then_inc(gate_kept, 1)
                if more:
                    keep_gathered(i + (u + 1) // 2, (u + 1) % 2)
                act.wait_ge(down_done, n + 1)
                nc.scalar.copy(result.rearrange("k e d -> k (e d)"), ps[0:CAP, gather_bank(u), 2 * P:4 * P]).then_inc(down_kept, 1)

            keep_gathered(0, 0)
            all_steps(act, one_step)

        @block.vector
        def _(dve):
            def mark(i, u):
                for e in range(2):
                    last = nc.vector.tensor_tensor(marks[u][:, :, e, :], slot_of[:, :, bass.ds(2 * (2 * i + u) + e, 1)].to_broadcast([P, NP_, CAP]),
                                                   spread(slot_names[:], 1, NP_), ALU.is_equal)
                last.then_inc(marks_ready, 1)

            def one_step(i, u, more):
                n = 2 * i + u
                dve.wait_ge(landed[u], 16 * LOADS * i + 16 * LOADS)
                for e in range(2):
                    nc.vector.scalar_tensor_tensor(spread_out[u][:, e, :], spread_out[u][:, e, :], slot[0:CAP, 0:1], share[u][:, e, :],
                                                   ALU.is_equal, ALU.mult).then_inc(spread_ready, 1)
                dve.wait_ge(up_done, n + 1)
                dve.wait_ge(gate_kept, n + 1)
                ups = ps[:, UP, 0:BLOCKS * CAP].rearrange("p (a k) -> p a k", k=CAP)
                own_blocks, shared_blocks = slice(0, 2 * SUBS), slice(2 * SUBS, BLOCKS)
                nc.vector.tensor_tensor(hidden[:, own_blocks, :], silu[:, own_blocks, :], ups[:, own_blocks, :], ALU.mult)
                nc.vector.scalar_tensor_tensor(hidden[:, shared_blocks, :], silu[:, shared_blocks, :], 0.05, ups[:, shared_blocks, :],
                                               ALU.mult, ALU.mult).then_inc(hidden_ready, 1)
                if more == 2:
                    mark(i + 1, u)

            nc.vector.memset(zero[:], 0.0).then_inc(zero_ready, 1)
            for u in range(2):
                nc.vector.memset(chip.credit[:, u:u + 1], 0.0).then_inc(used[u], 1)
            dve.wait_ge(consts_landed, 32)
            mark(0, 0)
            mark(0, 1)
            all_steps(dve, one_step)
            for c in range(CH):
                goal = x[:, CB * c:CB * c + CB, 0:S]
                dve.wait_ge(summed, c + 1)
                nc.vector.tensor_tensor(goal, goal, ps[:, c, 0:CT].rearrange("p (b s) -> p b s", s=S), ALU.add).then_inc(added, 1)


def mixture_3(chip):
    nc, ps, xn = chip.nc, chip.ps, chip.xn
    E, K, HR, NS = 32, 2, P // 2, 6
    CAP = int(1.25 * B * S / E)
    ROUNDS = -(-CAP // 8)
    LAST = CAP - 8 * (ROUNDS - 1)
    T = B * S
    scratch = nc.dram_tensor("m3_weight_scratch", (E, T), F32, kind="Internal").ap()
    scratch_s = nc.dram_tensor("m3_slot_scratch", (E, T), F32, kind="Internal").ap()
    sems = ("cleared landed tokens_turned tokens_kept stats_ready stats_turned stats_kept hidden_done hidden_kept squared rooted"
            " weights_turned weights_kept scores_ready scores_turned scores_kept chain rows_ready slots_ready slots_turned slots_kept stored")
    s = {k: chip.sem("m3_" + k) for k in sems.split()}
    with ExitStack() as kept, ExitStack() as own:
        tokens = kept.enter_context(nc.sbuf_tensor("m3_tokens", [P, NP_, P], F32))
        slot_of = kept.enter_context(nc.sbuf_tensor("m3_slot_of", [P, NP_, E], F32))
        def sbuf(name, shape):
            return own.enter_context(nc.sbuf_tensor("m3_" + name, shape, F32))
        r1, r1s, r2, rb = sbuf("r1", [P, P]), sbuf("r1s", [NS, P]), sbuf("r2", [P, E]), sbuf("rb", [P, 1])
        by_token, square = sbuf("by_token", [P, NP_, P]), sbuf("square", [P, NP_, P])
        stats = sbuf("stats", [P, NP_, NS])
        stats_t = sbuf("stats_t", [NS, NP_ * P])
        hidden = sbuf("hidden", [P, NP_ * P])
        routed = sbuf("routed", [P, NP_, E])
        weight_rows = sbuf("weight_rows", [E, NP_ * P])
        score_rows, top8 = sbuf("score_rows", [E, T + 8 - LAST]), sbuf("row_top8", [E, 8])
        final, ones_row, slots = sbuf("final", [E, T]), sbuf("ones_row", [E, T]), sbuf("slots", [E, NP_ * P])
        order = sbuf("order", [E, T])
        router = Router(chip, own, "m3_", E, K)
        flat = xn.rearrange("p b s -> p (b s)")
        block = own.enter_context(nc.Block())

        def real(rows):
            return rows.rearrange("e (b s) -> e b s", s=SP)[:, :, 0:S]

        @block.sync
        def _(sp):
            sp.wait_ge(s["cleared"], 4)
            for dst, name in ((r1[:, 0:HR], "r1"), (r1s[:, 0:HR], "r1_stats"), (r2[0:HR, :], "r2"), (rb[0:HR], "r1_b")):
                sp.dma_start(dst, chip.dram["L3_ffn_" + name]).then_inc(s["landed"], 16)
            sp.wait_ge(s["rows_ready"], 1)
            sp.dma_start(scratch, final[:]).then_inc(s["stored"], 16)
            sp.wait_ge(s["slots_ready"], 1)
            sp.dma_start(scratch_s.rearrange("e (b s) -> e b s", s=S), real(slots)).then_inc(s["stored"], 16)
            sp.wait_ge(s["stored"], 32)

        @block.tensor
        def _(pe):
            for t in range(NP_):
                mm = nc.tensor.transpose(ps[:, t // 4, P * (t % 4):P * (t % 4) + P], flat[:, P * t:P * t + P], chip.ident[:])
            mm.then_inc(s["tokens_turned"], 1)
            pe.wait_ge(s["stats_ready"], 1)
            for t in range(NP_):
                mm = nc.tensor.transpose(ps[0:NS, 4 + t // 4, P * (t % 4):P * (t % 4) + P], stats[:, t, :], chip.ident[:])
            mm.then_inc(s["stats_turned"], 1)
            pe.wait_ge(s["stats_kept"], 1)
            pe.wait_ge(s["tokens_kept"], 2)
            pe.wait_ge(s["landed"], 4 * 16)
            for c in range(CH):
                nc.tensor.matmul(ps[:, c, :], r1[:], flat[:, CW * c:CW * c + CW], start=True, stop=False)
                nc.tensor.matmul(ps[:, c, :], r1s[:], stats_t[:, CW * c:CW * c + CW], start=False, stop=True).then_inc(s["hidden_done"], 1)
            pe.wait_ge(s["hidden_kept"], CH)
            router.make_logits(pe, hidden, r2[:])
            pe.wait_ge(router.ready, 1)
            for t in range(NP_):
                mm = nc.tensor.transpose(ps[0:E, 4 + t // 4, P * (t % 4):P * (t % 4) + P], router.weights[:, t, :], chip.ident[:])
            mm.then_inc(s["weights_turned"], 1)
            pe.wait_ge(s["scores_ready"], 1)
            for t in range(NP_):
                mm = nc.tensor.transpose(ps[0:E, t // 4, P * (t % 4):P * (t % 4) + P], routed[:, t, :], chip.ident[:])
            mm.then_inc(s["scores_turned"], 1)
            pe.wait_ge(s["slots_ready"], 1)
            for t in range(NP_):
                mm = nc.tensor.transpose(ps[:, 0, E * t:E * t + E], slots[:, P * t:P * t + P], chip.ident[0:E, 0:E])
            mm.then_inc(s["slots_turned"], 1)

        @block.scalar
        def _(act):
            act.wait_ge(s["tokens_turned"], 1)
            nc.scalar.copy(by_token[:], ps[:, 0:4, :].rearrange("p k (t d) -> p (k t) d", d=P)).then_inc(s["tokens_kept"], 1)
            nc.scalar.copy(tokens[:], ps[:, 0:4, :].rearrange("p k (t d) -> p (k t) d", d=P)).then_inc(s["tokens_kept"], 1)
            act.wait_ge(s["squared"], 1)
            nc.scalar.activation(stats[:, :, 1], stats[:, :, 1], ACT.Sqrt, scale=1.0 / (P - 1)).then_inc(s["rooted"], 1)
            nc.scalar.activation(stats[:, :, 4], stats[:, :, 4], ACT.Sqrt).then_inc(s["rooted"], 1)
            act.wait_ge(s["stats_turned"], 1)
            nc.scalar.copy(stats_t[:], ps[0:NS, 4:8, :].rearrange("e k n -> e (k n)")).then_inc(s["stats_kept"], 1)
            act.wait_ge(s["landed"], 4 * 16)
            for c in range(CH):
                act.wait_ge(s["hidden_done"], c + 1)
                nc.scalar.activation(hidden[:, CW * c:CW * c + CW], ps[:, c, :], ACT.Gelu, bias=rb[:, 0:1]).then_inc(s["hidden_kept"], 1)
            router.exponentials(act)
            act.wait_ge(s["weights_turned"], 1)
            nc.scalar.copy(weight_rows[:], ps[0:E, 4:8, :].rearrange("e k n -> e (k n)")).then_inc(s["weights_kept"], 1)
            act.wait_ge(s["slots_turned"], 1)
            nc.scalar.copy(slot_of[:], ps[:, 0, :].rearrange("p (t e) -> p t e", e=E)).then_inc(s["slots_kept"], 1)

        @block.vector
        def _(dve):
            step = Step(dve, s["chain"])
            for buffer in (r1, r1s, r2, rb):
                nc.vector.memset(buffer[:], 0.0).then_inc(s["cleared"], 1)
            dve.wait_ge(s["tokens_kept"], 1)
            nc.vector.tensor_reduce(stats[:, :, 2], by_token[:], AX_X, ALU.min)
            nc.vector.tensor_reduce(stats[:, :, 3], by_token[:], AX_X, ALU.max)
            step(nc.vector.tensor_reduce(stats[:, :, 0], by_token[:], AX_X, ALU.add))
            step(nc.vector.tensor_scalar(stats[:, :, 0], stats[:, :, 0], 1.0 / P, None, ALU.mult))
            step(nc.vector.tensor_tensor(square[:], by_token[:], by_token[:], ALU.mult))
            step(nc.vector.tensor_reduce(stats[:, :, 4], square[:], AX_X, ALU.add))
            step(nc.vector.scalar_tensor_tensor(square[:], by_token[:], -1.0, by_token[:], ALU.mult, ALU.max))
            step(nc.vector.tensor_scalar(square[:], square[:], 1e-6, None, ALU.is_lt))
            step(nc.vector.tensor_reduce(stats[:, :, 5], square[:], AX_X, ALU.add))
            step(nc.vector.tensor_scalar(stats[:, :, 5], stats[:, :, 5], 1.0 / P, None, ALU.mult))
            step(nc.vector.tensor_tensor(by_token[:], by_token[:], spread(stats[:, :, 0], 2, P), ALU.subtract))
            step(nc.vector.tensor_tensor(by_token[:], by_token[:], by_token[:], ALU.mult))
            nc.vector.tensor_reduce(stats[:, :, 1], by_token[:], AX_X, ALU.add).then_inc(s["squared"], 1)
            dve.wait_ge(s["rooted"], 2)
            nc.vector.memset(chip.credit[:, 2:3], 0.0).then_inc(s["stats_ready"], 1)
            router.choose(dve)
            step(nc.vector.tensor_scalar(routed[:], router.marked[:, :, 0:E], -1.0, None, ALU.add))
            step(nc.vector.tensor_tensor(router.scores[:], router.scores[:], router.marked[:, :, 0:E], ALU.mult))
            nc.vector.tensor_tensor(routed[:], routed[:], router.scores[:], ALU.add).then_inc(s["scores_ready"], 1)
            for n in range(8 - LAST):
                nc.vector.memset(score_rows[:, T + n:T + n + 1], spacer(n))
            dve.wait_ge(s["scores_turned"], 1)
            for c in range(CH):
                last = nc.vector.tensor_copy(score_rows[:, CT * c:CT * c + CT].rearrange("e (b s) -> e b s", s=S),
                                             ps[0:E, c, :].rearrange("e (b s) -> e b s", s=SP)[:, :, 0:S])
            step(last)
            for n in range(ROUNDS):
                step(nc.vector.max(top8[:], score_rows[:, 0:T]))
                if n == ROUNDS - 1:
                    for k in range(LAST, 8):
                        last = nc.vector.memset(top8[:, k:k + 1], spacer(k - LAST))
                    step(last)
                step(nc.vector.match_replace(score_rows[:], top8[:], score_rows[:], MARK))
            step(nc.vector.tensor_scalar(final[:], score_rows[:, 0:T], MARK, None, ALU.is_equal))
            step(nc.vector.memset(ones_row[:], 1.0))
            step(nc.vector.memset(slots[:], 0.0))
            step(nc.vector.tensor_tensor_scan(order[:], ones_row[:], final[:], 0.0, ALU.mult, ALU.add))
            nc.vector.tensor_tensor(real(slots), order.rearrange("e (b s) -> e b s", s=S), final.rearrange("e (b s) -> e b s", s=S),
                                    ALU.mult).then_inc(s["slots_ready"], 1)
            dve.wait_ge(s["slots_ready"], 1)
            dve.wait_ge(s["weights_kept"], 1)
            nc.vector.tensor_tensor(final.rearrange("e (b s) -> e b s", s=S), final.rearrange("e (b s) -> e b s", s=S),
                                    real(weight_rows), ALU.mult).then_inc(s["rows_ready"], 1)
        own.close()
        experts_by_slot(chip, scratch, scratch_s, slot_of, tokens, CAP)


def linear_attention_2(chip):
    nc, ps, xn, x = chip.nc, chip.ps, chip.xn, chip.x
    DH, HG, HJ = 32, 4, HX // 4
    HP = HX // 2
    sems = ("weights_landed cleared tokens_ready q_done k_done v_done q_kept k_kept v_kept products_done masked"
            " mixing_done mixing_kept mixed mixed_kept projected added")
    s = {k: chip.sem("la_" + k) for k in sems.split()}
    with ExitStack() as own:
        def sbuf(name, shape):
            return own.enter_context(nc.sbuf_tensor("la_" + name, shape, F32))
        wq, wk, wv = (sbuf(n, [P, HX * DH]) for n in ("wq", "wk", "wv"))
        wo = sbuf("wo", [P, 2, HP, P])
        quarter, left, right, decay = sbuf("quarter", [P, HG]), sbuf("left", [P, SP]), sbuf("right", [P, SP]), sbuf("decay", [P, SP])
        tokens = sbuf("tokens", [P, P])
        q_diag = sbuf("q_diag", [P, HJ, HG, P])
        k_twice = sbuf("k_twice", [P, HJ, 2, 2, SP])
        v_diag = sbuf("v_diag", [P, HX, 2, DH])
        lhs, rhs = sbuf("lhs", [P, 2, HX, SP]), sbuf("rhs", [P, 2, HX, SP])
        mixing = sbuf("mixing", [P, HX, SP])
        mixed = sbuf("mixed", [P, HP, NP_, SP])
        block = own.enter_context(nc.Block(no_gpsimd_drain=True))

        @block.sync
        def _(sp):
            for dst, name in ((wq, "Wq"), (wk, "Wk"), (wv, "Wv"), (wo, "Wo")):
                sp.dma_start(dst[:], chip.dram["L2_attn_" + name]).then_inc(s["weights_landed"], 16)
            for dst, name in ((quarter, "quarter"), (left, "la_left"), (right, "la_right"), (decay, "la_decay")):
                sp.dma_start(dst[:], chip.dram[name]).then_inc(s["weights_landed"], 16)

        def all_passes(engine, one_pass):
            with engine.Fori(0, NP_ - 1) as i:
                one_pass(i, True)
            one_pass(NP_ - 1, False)

        @block.tensor
        def _(pe):
            def project(i):
                pe.wait_ge(s["tokens_ready"], i + 1)
                for w, bank, done in ((wq, 0, "q_done"), (wk, 1, "k_done")):
                    for j in range(HJ):
                        mm = nc.tensor.matmul(ps[:, bank, P * j:P * j + P], w[:, P * j:P * j + P], tokens[:], start=True, stop=True)
                    mm.then_inc(s[done], 1)
                for b in range(2):
                    mm = nc.tensor.matmul(ps[SP * b:SP * b + SP, 2, :], tokens[:, SP * b:SP * b + SP], wv[:], start=True, stop=True)
                mm.then_inc(s["v_done"], 1)

            def one_pass(i, more):
                pe.wait_ge(s["mixing_kept"], i + 1)
                pe.wait_ge(s["q_kept"], i + 1)
                pe.wait_ge(s["k_kept"], i + 1)
                for b in range(2):
                    for j in range(HJ):
                        mm = nc.tensor.matmul(ps[:, 3 + 2 * b + j // 2, 256 * (j % 2):256 * (j % 2) + 256],
                                              k_twice[:, j, b].rearrange("p r s -> p (r s)"),
                                              q_diag[:, j, :, SP * b:SP * b + SP], start=True, stop=True)
                mm.then_inc(s["products_done"], 1)
                pe.wait_ge(s["v_kept"], i + 1)
                if more:
                    project(i + 1)
                pe.wait_ge(s["masked"], i + 1)
                for h in range(HX):
                    for b in range(2):
                        mm = nc.tensor.matmul(ps[SP * b:SP * b + SP, 3 + h // 8, SP * (h % 8):SP * (h % 8) + SP], lhs[:, b, h, :],
                                              rhs[:, b, h, :], start=True, stop=True)
                mm.then_inc(s["mixing_done"], 1)
                pe.wait_ge(s["mixing_kept"], i + 2)
                pe.wait_ge(s["mixed_kept"], i + 1)
                for h in range(HX):
                    r = 64 * (h % 2)
                    mm = nc.tensor.matmul(ps[r:r + 64, 7, SP * (h // 2):SP * (h // 2) + SP], v_diag[:, h].rearrange("p b d -> p (b d)"),
                                          mixing[:, h, :], start=True, stop=True)
                mm.then_inc(s["mixed"], 1)

            pe.wait_ge(s["weights_landed"], 8 * 16)
            project(0)
            all_passes(pe, one_pass)
            pe.wait_ge(s["mixed_kept"], NP_ + 1)
            for n in range(4):
                b, half = n % 2, n // 2
                for j in range(HP):
                    mm = nc.tensor.matmul(ps[:, n, 0:CT], wo[:, b, j, :], mixed[:, j, 8 * half:8 * half + 8, 0:S],
                                          start=(j == 0), stop=(j == HP - 1))
                mm.then_inc(s["projected"], 1)

        @block.scalar
        def _(act):
            def take_tokens(i):
                nc.scalar.copy(tokens[:], xn.rearrange("p b s -> p (b s)")[:, bass.ds(i * P, P)]).then_inc(s["tokens_ready"], 1)

            def keep_queries(i):
                act.wait_ge(s["q_done"], i + 1)
                for g in range(HG):
                    last = nc.scalar.mul(q_diag[:, :, g, :], ps[:, 0, :].rearrange("p (j c) -> p j c", c=P), quarter[:, g:g + 1])
                last.then_inc(s["q_kept"], 1)

            def keep_values(i):
                act.wait_ge(s["v_done"], i + 1)
                for b in range(2):
                    r = slice(64 * b, 64 * b + 64)
                    last = nc.scalar.copy(v_diag[r, :, b, :], ps[r, 2, :].rearrange("p (h d) -> p h d", d=DH))
                last.then_inc(s["v_kept"], 1)

            def one_pass(i, more):
                if more:
                    act.wait_ge(s["v_done"], i + 1)
                    take_tokens(i + 1)
                    keep_queries(i + 1)
                act.wait_ge(s["mixed"], i + 1)
                nc.scalar.copy(mixed[:, :, bass.ds(i, 1), :].rearrange("p j n s -> p j (n s)"),
                               ps[:, 7, :].rearrange("p (j s) -> p j s", s=SP)).then_inc(s["mixed_kept"], 1)
                if more:
                    keep_values(i + 1)

            act.wait_ge(s["weights_landed"], 8 * 16)
            act.wait_ge(s["cleared"], 1)
            take_tokens(0)
            keep_queries(0)
            keep_values(0)
            all_passes(act, one_pass)

        @block.vector
        def _(dve):
            nc.vector.memset(v_diag[:], 0.0).then_inc(s["cleared"], 1)
            for n, name in enumerate(("mixing_kept", "mixed_kept")):
                nc.vector.memset(chip.credit[:, n:n + 1], 0.0).then_inc(s[name], 1)
            dve.wait_ge(s["weights_landed"], 8 * 16)
            def keep_keys(i):
                dve.wait_ge(s["k_done"], i + 1)
                for r in range(2):
                    last = nc.vector.tensor_copy(k_twice[:, :, :, r, :], ps[:, 1, :].rearrange("p (j b s) -> p j b s", j=HJ, b=2))
                last.then_inc(s["k_kept"], 1)

            def one_pass(i, more):
                dve.wait_ge(s["products_done"], i + 1)
                products = ps[:, 3:7, :].rearrange("p k (h s) -> p (k h) s", s=SP)
                nc.vector.tensor_tensor(lhs.rearrange("p b h s -> p (b h) s"), products, spread(left[:], 1, 2 * HX), ALU.mult)
                nc.vector.tensor_tensor(rhs.rearrange("p b h s -> p (b h) s"), products, spread(right[:], 1, 2 * HX), ALU.mult).then_inc(s["masked"], 1)
                if more:
                    keep_keys(i + 1)
                dve.wait_ge(s["mixing_done"], i + 1)
                nc.vector.tensor_tensor(mixing[:], ps[:, 3:5, :].rearrange("p k (h s) -> p (k h) s", s=SP), spread(decay[:], 1, HX),
                                        ALU.mult).then_inc(s["mixing_kept"], 1)

            keep_keys(0)
            all_passes(dve, one_pass)
            for n in range(4):
                b, half = n % 2, n // 2
                goal = x.rearrange("p (n b) s -> p n b s", b=2)[:, 8 * half:8 * half + 8, b, 0:S]
                dve.wait_ge(s["projected"], n + 1)
                nc.vector.tensor_tensor(goal, goal, ps[:, n, 0:CT].rearrange("p (n s) -> p n s", s=S), ALU.add).then_inc(s["added"], 1)


def rotary_attention(chip, tag, src, res, latent):
    nc, ps = chip.nc, chip.ps
    KV, REP = 4, HX // 4
    LAT = 32
    U = 2 * CH
    SCALE = DX ** -0.5
    sems = ("cleared landed spread latent_done latent_kept made kept rotated turned_cos roped squared power log root normed"
            " pair_ready diag_ready scores_done shifted exp_done turned turned_kept v_done v_kept mixed scaled flipped flipped_kept"
            " projected added chain")
    s = {k: chip.sem(tag + k) for k in sems.split()}
    with ExitStack() as own:
        def sbuf(name, shape):
            return own.enter_context(nc.sbuf_tensor(tag + name, shape, F32))
        wq, wo, rot, mean8 = (sbuf(n, [P, P]) for n in ("wq", "wo", "rot", "mean8"))
        wdown = sbuf("wdown", [P, P])
        wkv = sbuf("wkv", [P, 2, KV * DX])
        wk, wv = sbuf("wk", [P, P]), sbuf("wv", [P, 2, P])
        cos, sin, mask, own_head = sbuf("cos", [P, S]), sbuf("sin", [P, S]), sbuf("mask", [P, S]), sbuf("own_head", [P, HX])
        low = sbuf("low", [P, B, SP])
        qn, kn = sbuf("qn", [P, B, SP]), sbuf("kn", [P, B, SP])
        raw = [sbuf("raw%d" % n, [P, CT]) for n in range(4)]
        work = [sbuf("work%d" % n, [P, CT]) for n in range(4)]
        source = low if latent else src
        def two(name, shape):
            return [sbuf("%s%d" % (name, u), shape) for u in range(2)]
        q_pair, v_pair, k_diag = two("q_pair", [P, P]), two("v_pair", [P, P]), two("k_diag", [P, 2, HX, S])
        probs, probs_t = two("probs", [P, HX, SP]), two("probs_t", [P, HX // 2, P])
        top, total, inverse = (two(n, [P, HX]) for n in ("top", "total", "inverse"))
        values, mix = two("values", [P, 2, P]), two("mix", [P, P])
        mix_t = sbuf("mix_t", [P, B, SP])
        first = chip.sem(tag + "weights_ready")
        loads = [(wq[:], "wq"), (wo[:], "wo")]
        if latent:
            loads += [(wdown[:, 0:LAT], "kv_down"), (wkv[0:LAT, 0], "k_up"), (wkv[0:LAT, 1], "v_up")]
        else:
            loads += [(wkv[:, 0], "wk"), (wkv[:, 1], "wv")]
        consts = ((rot, "rotate"), (mean8, "mean8"), (cos, tag + "cos"), (sin, tag + "sin"), (mask, tag + "mask"), (own_head, "own_head"))
        n_loads = len(loads) + len(consts)

        def unit(n):
            c = n % CH
            return c, n < CH

        with nc.Block(no_gpsimd_drain=True) as block:
            @block.sync
            def _(sp):
                sp.wait_ge(s["cleared"], 2)
                for dst, name in loads:
                    sp.dma_start(dst, chip.dram["L3_attn_" + tag + name]).then_inc(s["landed"], 16)
                for dst, name in consts:
                    sp.dma_start(dst[:], chip.dram[name]).then_inc(s["landed"], 16)

            @block.tensor
            def _(pe):
                pe.wait_ge(s["landed"], 16 * n_loads)
                if latent:
                    for c in range(CH):
                        nc.tensor.matmul(ps[:, 4 + c, 0:CT], wdown[:], src[:, CB * c:CB * c + CB, 0:S], start=True, stop=True).then_inc(s["latent_done"], 1)
                    pe.wait_ge(s["latent_kept"], CH)
                pe.wait_ge(first, 1)

                def make(n):
                    c, queries = unit(n)
                    t = (src if queries else source)[:, CB * c:CB * c + CB, 0:S]
                    if n >= 4:
                        pe.wait_ge(s["log"], n - 3)
                    nc.tensor.matmul(ps[:, n % 4, 0:CT], (wq if queries else wk)[:], t, start=True, stop=True).then_inc(s["made"], 1)

                def rotate(n):
                    pe.wait_ge(s["kept"], n + 1)
                    nc.tensor.matmul(ps[:, 4 + n % 4, 0:CT], rot[:], raw[n % 4][:], start=True, stop=True).then_inc(s["rotated"], 1)

                def power(n):
                    pe.wait_ge(s["squared"], n + 1)
                    nc.tensor.matmul(ps[:, n % 4, 0:CT], mean8[:], work[n % 4][:], start=True, stop=True).then_inc(s["power"], 1)

                for half in range(2):
                    for n in range(4 * half, 4 * half + 4):
                        make(n)
                    for n in range(4 * half, 4 * half + 4):
                        rotate(n)
                    for n in range(4 * half, 4 * half + 4):
                        power(n)

            @block.scalar
            def _(act):
                if latent:
                    for c in range(CH):
                        act.wait_ge(s["latent_done"], c + 1)
                        nc.scalar.copy(low[:, CB * c:CB * c + CB, 0:S], ps[:, 4 + c, 0:CT].rearrange("p (b s) -> p b s", s=S)).then_inc(s["latent_kept"], 1)
                for half in range(2):
                    units = range(4 * half, 4 * half + 4)
                    for n in units:
                        act.wait_ge(s["made"], n + 1)
                        if n >= 4:
                            act.wait_ge(s["normed"], n - 3)
                        nc.scalar.copy(raw[n % 4][:], ps[:, n % 4, 0:CT]).then_inc(s["kept"], 1)
                    for n in units:
                        act.wait_ge(s["roped"], n + 1)
                        nc.scalar.activation(work[n % 4][:], raw[n % 4][:], ACT.Square).then_inc(s["squared"], 1)
                    for n in units:
                        act.wait_ge(s["power"], n + 1)
                        nc.scalar.activation(work[n % 4][:], ps[:, n % 4, 0:CT], ACT.Ln, bias=chip.eps[:, 1:2]).then_inc(s["log"], 1)
                    for n in units:
                        act.wait_ge(s["log"], n + 1)
                        nc.scalar.activation(work[n % 4][:], work[n % 4][:], ACT.Exp, scale=-0.5).then_inc(s["root"], 1)

            @block.vector
            def _(dve):
                step = Step(dve, s["chain"])
                nc.vector.memset(low[:], 0.0)
                nc.vector.memset(qn[:], 0.0)
                nc.vector.memset(kn[:], 0.0)
                for u in range(2):
                    nc.vector.memset(probs[u][:], 0.0)
                nc.vector.memset(wdown[:], 0.0).then_inc(s["cleared"], 1)
                nc.vector.memset(wkv[:], 0.0).then_inc(s["cleared"], 1)
                step(nc.vector.memset(wv[:], 0.0))
                dve.wait_ge(s["landed"], 16 * n_loads)
                for kv in range(KV):
                    nc.vector.tensor_copy(wk[:, REP * DX * kv:REP * DX * (kv + 1)].rearrange("p (r d) -> p r d", d=DX),
                                          spread(wkv[:, 0, DX * kv:DX * kv + DX], 1, REP))
                    for odd in range(2):
                        v4 = wv[:, odd, REP * DX * kv:REP * DX * (kv + 1)].rearrange("p (r d) -> p r d", d=DX)
                        last = nc.vector.tensor_copy(v4[:, odd::2, :], spread(wkv[:, 1, DX * kv:DX * kv + DX], 1, REP // 2))
                last.then_inc(first, 1)
                for half in range(2):
                    units = range(4 * half, 4 * half + 4)
                    for n in units:
                        r3, w3 = (v[n % 4].rearrange("p (b s) -> p b s", s=S) for v in (raw, work))
                        dve.wait_ge(s["rotated"], n + 1)
                        step(nc.vector.tensor_tensor(w3, ps[:, 4 + n % 4, 0:CT].rearrange("p (b s) -> p b s", s=S), spread(sin[:], 1, CB), ALU.mult))
                        step(nc.vector.tensor_tensor(r3, r3, spread(cos[:], 1, CB), ALU.mult))
                        nc.vector.tensor_tensor(r3, r3, w3, ALU.add).then_inc(s["roped"], 1)
                    for n in units:
                        c, queries = unit(n)
                        r3, w3 = (v[n % 4].rearrange("p (b s) -> p b s", s=S) for v in (raw, work))
                        dve.wait_ge(s["root"], n + 1)
                        nc.vector.tensor_tensor((qn if queries else kn)[:, CB * c:CB * c + CB, 0:S], r3, w3, ALU.mult).then_inc(s["normed"], 1)

        with nc.Block(no_gpsimd_drain=True) as block:
            def bank(u):
                return 3 * u

            def last_bank(u, first, columns):
                return ps[:, 3 * u + 2, first:first + columns]

            def all_pairs(engine, one_step):
                one_step(0, 0, True, False)
                with engine.Fori(0, NP_ // 2 - 1) as i:
                    one_step(2 * i + 1, 1, True, True)
                    one_step(2 * i + 2, 0, True, True)
                one_step(NP_ - 1, 1, True, True)
                one_step(NP_, 0, False, True)

            @block.tensor
            def _(pe):
                def make_scores(n, u):
                    pe.wait_ge(s["pair_ready"], 2 * n + 2)
                    pe.wait_ge(s["diag_ready"], n + 1)
                    for half in range(2):
                        for b in range(2):
                            mm = nc.tensor.matmul(ps[SP * b:SP * b + SP, bank(u) + half, :].rearrange("p (h s) -> p h s", s=SP)[:, :, 0:S],
                                                  q_pair[u][:, SP * b:SP * b + SP], k_diag[u][:, b, 8 * half:8 * half + 8, :], start=True, stop=True)
                    mm.then_inc(s["scores_done"], 1)

                def turn(n, u):
                    pe.wait_ge(s["exp_done"], n + 1)
                    for j in range(HX // 2):
                        mm = nc.tensor.transpose(ps[:, bank(u) + j // 4, P * (j % 4):P * (j % 4) + P],
                                                 probs[u][:, 2 * j:2 * j + 2, :].rearrange("p h s -> p (h s)"), chip.ident[:])
                    mm.then_inc(s["turned"], 1)

                def make_values(n, u):
                    pe.wait_ge(s["flipped_kept"], n + 1)
                    for b in range(2):
                        for odd in range(2):
                            mm = nc.tensor.matmul(last_bank(u, P * b, P)[64 * odd:64 * odd + 64], v_pair[u][:, SP * b:SP * b + SP], wv[:, odd, :],
                                                  start=True, stop=True)
                    mm.then_inc(s["v_done"], 1)

                def mix_values(n, u):
                    pe.wait_ge(s["turned_kept"], n + 1)
                    pe.wait_ge(s["v_kept"], n + 1)
                    for j in range(HX // 2):
                        for b in range(2):
                            mm = nc.tensor.matmul(last_bank(u, 2 * P + 16 * j, 16)[SP * b:SP * b + SP], probs_t[u][:, j, SP * b:SP * b + SP],
                                                  values[u][:, b, 16 * j:16 * j + 16], start=True, stop=True)
                    mm.then_inc(s["mixed"], 1)

                def flip(n, u):
                    pe.wait_ge(s["scaled"], n + 1)
                    nc.tensor.transpose(last_bank(u, 3 * P, P), mix[u][:], chip.ident[:]).then_inc(s["flipped"], 1)

                def one_step(n, u, taking, finishing):
                    if taking:
                        make_scores(n, u)
                    if finishing:
                        turn(n - 1, 1 - u)
                    if taking:
                        make_values(n, u)
                    if finishing:
                        mix_values(n - 1, 1 - u)
                        flip(n - 1, 1 - u)

                all_pairs(pe, one_step)
                pe.wait_ge(s["flipped_kept"], NP_ + 2)
                for c in range(CH):
                    nc.tensor.matmul(ps[:, c, 0:CT], wo[:], mix_t[:, CB * c:CB * c + CB, 0:S], start=True, stop=True).then_inc(s["projected"], 1)

            @block.scalar
            def _(act):
                def take_pair(n, u):
                    if not isinstance(n, int) or n > 1:
                        act.wait_ge(s["scores_done"], n - 1)
                    for dst, v in ((q_pair[u], qn), (v_pair[u], source)):
                        nc.scalar.copy(dst[:], v.rearrange("p b s -> p (b s)")[:, bass.ds(n * P, P)]).then_inc(s["pair_ready"], 1)

                def one_step(n, u, taking, finishing):
                    if finishing:
                        act.wait_ge(s["turned"], n)
                        nc.scalar.copy(probs_t[1 - u][:], ps[:, bank(1 - u):bank(1 - u) + 2, :].rearrange("p k (j c) -> p (k j) c", c=P)).then_inc(s["turned_kept"], 1)
                    if taking:
                        act.wait_ge(s["v_done"], n + 1)
                        nc.scalar.copy(values[u][:], last_bank(u, 0, 2 * P).rearrange("p (b d) -> p b d", d=P)).then_inc(s["v_kept"], 1)
                        if not isinstance(n, int) or n + 1 < NP_:
                            take_pair(n + 1, 1 - u)
                        act.wait_ge(s["shifted"], n + 1)
                        nc.scalar.activation(probs[u][:, :, 0:S], probs[u][:, :, 0:S], ACT.Exp).then_inc(s["exp_done"], 1)
                    if finishing:
                        act.wait_ge(s["flipped"], n)
                        nc.scalar.copy(mix_t.rearrange("p b s -> p (b s)")[:, bass.ds((n - 1) * P, P)], last_bank(1 - u, 3 * P, P)).then_inc(s["flipped_kept"], 1)

                take_pair(0, 0)
                all_pairs(act, one_step)

            @block.gpsimd
            def _(pool):
                def spread_keys(n, u):
                    for b in range(2):
                        last = nc.gpsimd.tensor_tensor(k_diag[u][:, b], spread(kn[:, bass.ds(2 * n + b, 1), 0:S].rearrange("p b s -> p (b s)"), 1, HX),
                                                       spread(own_head[:], 2, S), ALU.mult)
                    last.then_inc(s["diag_ready"], 1)

                for u in range(2):
                    spread_keys(u, u)
                with pool.Fori(1, NP_ // 2) as i:
                    for u in range(2):
                        pool.wait_ge(s["scores_done"], 2 * i + u - 1)
                        spread_keys(2 * i + u, u)

            @block.vector
            def _(dve):
                for credit in range(2):
                    nc.vector.memset(chip.credit[:, credit:credit + 1], 0.0).then_inc(s["flipped_kept"], 1)
                done = s["chain"]
                base = 1 + 2 * U

                def one_step(n, u, taking, finishing):
                    if taking:
                        probs_u = probs[u][:, :, 0:S]
                        dve.wait_ge(s["scores_done"], n + 1)
                        scores = ps[:, bank(u):bank(u) + 2, :].rearrange("p k (h s) -> p (k h) s", s=SP)[:, :, 0:S]
                        step = Step(dve, done, 4 * n + base)
                        step(nc.vector.scalar_tensor_tensor(probs_u, scores, SCALE, spread(mask[:], 1, HX), ALU.mult, ALU.add))
                        step(nc.vector.tensor_reduce(top[u][:], probs_u, AX_X, ALU.max))
                        nc.vector.tensor_tensor(probs_u, probs_u, spread(top[u][:], 2, S), ALU.subtract).then_inc(s["shifted"], 1)
                    if finishing:
                        dve.wait_ge(s["mixed"], n)
                        nc.vector.tensor_tensor(mix[1 - u].rearrange("p (h d) -> p h d", d=DX), last_bank(1 - u, 2 * P, P).rearrange("p (h d) -> p h d", d=DX),
                                                spread(inverse[1 - u][:], 2, DX), ALU.mult).then_inc(s["scaled"], 1)
                    if taking:
                        dve.wait_ge(s["exp_done"], n + 1)
                        step = Step(dve, done, 4 * n + 2 + base)
                        step(nc.vector.tensor_reduce(total[u][:], probs[u][:, :, 0:S], AX_X, ALU.add))
                        step(nc.vector.reciprocal(inverse[u][:], total[u][:]))

                all_pairs(dve, one_step)
                for c in range(CH):
                    goal = res[:, CB * c:CB * c + CB, 0:S]
                    dve.wait_ge(s["projected"], c + 1)
                    nc.vector.tensor_tensor(goal, goal, ps[:, c, 0:CT].rearrange("p (b s) -> p b s", s=S), ALU.add).then_inc(s["added"], 1)


def rotary_attention_3(chip):
    nc, x, xn = chip.nc, chip.x, chip.xn
    landed, added = chip.sem("ra_norms_landed"), chip.sem("ra_added")
    with ExitStack() as own:
        norms = own.enter_context(nc.sbuf_tensor("ra_norms", [P, 2], F32))
        normed = own.enter_context(nc.sbuf_tensor("ra_normed", [P, B, SP], F32))
        with nc.Block(no_gpsimd_drain=True) as block:
            @block.sync
            def _(sp):
                sp.dma_start(norms[:], chip.dram["L3_attn_norms"]).then_inc(landed, 16)
                sp.wait_ge(landed, 16)
        normalise(chip, xn, normed, False, norms[:, 0:1])
        rotary_attention(chip, "g_", normed, xn, True)
        normalise(chip, xn, normed, False, norms[:, 1:2])
        rotary_attention(chip, "l_", normed, xn, False)
        with nc.Block(no_gpsimd_drain=True) as block:
            @block.vector
            def _(dve):
                nc.vector.tensor_tensor(x[:, :, 0:S], x[:, :, 0:S], xn[:, :, 0:S], ALU.add).then_inc(added, 1)


STAGES = [self_attention_0, context_mixing, coupled_twist, gated_recurrence, lambda chip: cross_attention(chip, 1, DX ** -0.5),
          mixture_1, linear_attention_2, lambda chip: cross_attention(chip, 2, P ** -0.5), mixture_2,
          rotary_attention_3, lambda chip: cross_attention(chip, 3, DX ** -0.5), mixture_3]


def more_layouts(a, d):
    ctx = a["ctx_1024"]
    d["ctx_t"] = ctx.transpose(0, 2, 1)
    d["ctx_n"] = ctx.reshape(B, NC_, KC, P).transpose(0, 2, 1, 3)
    for k in ("w1", "w2", "w3", "w4"):
        d["L0_ffn_cn_" + k] = a["L0_ffn_cn_" + k]
    for k in ("w1", "w2", "w3"):
        d["L0_ffn_gc_" + k] = a["L0_ffn_gc_" + k]
    for k in ("cn_b1", "cn_b2", "cn_b3", "cn_b4", "gc_b1", "gc_b2", "gc_b3", "adaptive_range"):
        d["L0_ffn_" + k] = a["L0_ffn_" + k].reshape(-1, 1)
    twist = np.zeros((P, P), np.float32)
    for m in range(P):
        twist[(m + 64) % P, m] = (1.0, -1.0, -1.0, 1.0)[m // 32]
    d["twist"] = twist
    for k in ("Wr_w", "Wi_w", "out_w"):
        d["L1_attn_" + k] = a["L1_attn_" + k].T
    d["L1_attn_conv_weight"] = a["L1_attn_conv_weight"][:, 0, :]
    for k in ("conv_bias", "Wr_b", "Wi_b", "log_a", "norm_w"):
        d["L1_attn_" + k] = a["L1_attn_" + k].reshape(-1, 1)
    for n in (1, 2, 3):
        for k in ("Wq", "Wk", "Wv", "Wo"):
            w = a["L%d_xattn_%s" % (n, k)]
            d["L%d_xattn_%s" % (n, k)] = w if n == 1 or (n == 2 and k == "Wo") else w.transpose(1, 0, 2).reshape(P, P) if n == 2 else w.T
        for k in ("Wq", "Wk"):
            w = d["L%d_xattn_%s" % (n, k)]
            d["L%d_xattn_%s" % (n, k)] = w.reshape(P, 2, 4, 2, DX).transpose(0, 1, 3, 4, 2).reshape(P, P)
        for k in ("bq", "bk"):
            a["L%d_xattn_%s" % (n, k)] = a["L%d_xattn_%s" % (n, k)].reshape(2, 4, 2, DX).transpose(0, 2, 3, 1)
        for k in ("bq", "bk", "bv", "bo"):
            d["L%d_xattn_%s" % (n, k)] = a["L%d_xattn_%s" % (n, k)].reshape(-1, 1)
    head_of_feature = np.arange(P) // DX
    d["own_head"] = (head_of_feature[:, None] == np.arange(HX)).astype(np.float32)
    row = np.arange(P)[:, None]
    d["parity"] = (row // 32 % 2 == np.arange(2)).astype(np.float32)
    d["place"] = np.zeros((P, 2, 2, 2, 32), np.float32)
    for parity in range(2):
        for odd in range(2):
            for f in range(DX * parity, DX * parity + DX):
                d["place"][f:P:32, parity, odd, 0, PF * odd + f] = 1.0
                d["place"][PF:P:32, parity, odd, 1, PF * odd + f] = 1.0
    d["pair_rows"] = (((row - TALL) % PR == np.arange(PR)) & (row >= TALL) & (row < TALL + PARTS * PR)).astype(np.float32)


    def blocks(*parts):
        return np.stack(parts, axis=3)

    w = a["L1_ffn_gate_up_proj"][:32].reshape(16, 2, 2, 64, P)
    gate, up = (w[:, :, k].reshape(16, 1, P, P).transpose(0, 3, 1, 2) for k in range(2))
    down = a["L1_ffn_down_proj"].reshape(16, 2, P, 64).transpose(0, 1, 3, 2).reshape(16, P, 1, P)
    d["L1_ffn_experts"] = blocks(gate, up, down)
    d["L1_ffn_classifier_weight"] = a["L1_ffn_classifier_weight"].T
    d["L1_ffn_e_score_correction_bias"] = a["L1_ffn_e_score_correction_bias"].reshape(1, -1)
    d["L2_ffn_Wr"] = a["L2_ffn_Wr"].T
    d["L2_ffn_experts"] = blocks(a["L2_ffn_W1"].reshape(8, 4, P, P).transpose(0, 3, 1, 2),
                                 a["L2_ffn_W2"].reshape(8, P, 4, P).transpose(0, 3, 2, 1))
    for n, groups, subs in (("", 32, 2), ("a", 16, 1)):
        w = a["L3_ffn_a_up" if n else "L3_ffn_w_up"].reshape(groups, 2, subs, P, P)
        gate, up = (w[:, k].transpose(0, 3, 1, 2) for k in range(2))
        down = a["L3_ffn_a_down" if n else "L3_ffn_w_down"].reshape(groups, P, subs, P).transpose(0, 3, 2, 1)
        d["L3_ffn_adapters" if n else "L3_ffn_experts"] = blocks(gate, up, down)
    d["L3_ffn_r1"] = a["L3_ffn_r1_w"][:, :P].T
    d["L3_ffn_r1_stats"] = a["L3_ffn_r1_w"][:, P:].T
    d["L3_ffn_r2"] = a["L3_ffn_r2_w"].T
    d["L3_ffn_r1_b"] = a["L3_ffn_r1_b"].reshape(-1, 1)
    cap = int(1.25 * B * S / 32)
    d["slot"] = np.arange(1, P + 1, dtype=np.float32).reshape(P, 1)
    d["slot_names"] = np.broadcast_to(np.arange(1, cap + 1, dtype=np.float32), (P, cap))
    for k in ("Wq", "Wk", "Wv"):
        d["L2_attn_" + k] = a["L2_attn_" + k]
    wo = a["L2_attn_Wo"].reshape(8, 2, 32, P)
    both = np.zeros((2, 8, 2, 2, 32, P), np.float32)
    for b in range(2):
        both[b, :, :, b] = wo
    d["L2_attn_Wo"] = both.reshape(2, 8, P, P).transpose(2, 0, 1, 3)
    d["quarter"] = (np.arange(P)[:, None] // 32 == np.arange(4)).astype(np.float32)
    r, t = np.arange(SP)[:, None], np.arange(SP)[None, :]
    real = (r < S) & (t < S)
    decay = np.where((r <= t) & real, 0.99 ** np.maximum(t - r, 0), 0.0).astype(np.float32)
    d["la_left"] = np.concatenate([real.astype(np.float32), ((r > t) & real).astype(np.float32)])
    d["la_right"] = np.concatenate([decay, -((r <= t) & real).astype(np.float32)])
    d["la_decay"] = np.concatenate([decay, decay])
    d["L3_attn_norms"] = np.stack([a["L3_attn_norm1_w"], a["L3_attn_norm2_w"]], axis=1)
    for k in ("wq", "wo"):
        for g in "gl":
            d["L3_attn_%s_%s" % (g, k)] = a["L3_attn_%s_%s" % (g, k)]
    for k in ("g_kv_down", "g_k_up", "g_v_up", "l_wk", "l_wv"):
        d["L3_attn_" + k] = a["L3_attn_" + k]
    rotate = np.zeros((P, P), np.float32)
    even = np.arange(0, P, 2)
    rotate[even + 1, even], rotate[even, even + 1] = -1.0, 1.0
    d["rotate"] = rotate
    d["mean8"] = (head_of_feature[:, None] == head_of_feature[None, :]).astype(np.float32) / np.float32(DX)
    for g, base in (("g_", 1e6), ("l_", 1e4)):
        inv = (1.0 / np.float32(base) ** (np.arange(0, DX, 2, dtype=np.float32) / np.float32(DX))).astype(np.float32)
        angle = (np.arange(S, dtype=np.float32)[None, :] * inv[:, None]).astype(np.float32)
        angle = angle[(np.arange(P) % DX) // 2]
        d[g + "cos"], d[g + "sin"] = np.cos(angle).astype(np.float32), np.sin(angle).astype(np.float32)
        query, key = np.arange(P)[:, None] % SP, np.arange(S)[None, :]
        seen = (query >= key) & (query - key < (32 if g == "l_" else S))
        d[g + "mask"] = np.where(seen | (query >= S), 0.0, -1e30).astype(np.float32)


def decoder(nc, dram, out):
    with ExitStack() as ctx:
        chip = Chip(nc, ctx, dram)
        load_stage(chip, out)
        for stage in STAGES:
            normalise(chip, chip.x, chip.xn, True)
            stage(chip)
            chip.end_stage()
        store_stage(chip, chip.x, out)


def layouts(inputs):
    a = {k: np.asarray(v) for k, v in inputs.items()}
    d = {"x": a["x"].transpose(2, 0, 1)}
    D = P

    def by_feature(w):
        return w.reshape(-1, D).T

    def column(v):
        return v.reshape(-1, 1)

    d["L0_attn_W_Q"] = by_feature(a["L0_attn_W_Q"])
    d["L0_attn_W_K"] = by_feature(a["L0_attn_W_K"])
    v = a["L0_attn_W_V"]
    d["L0_attn_W_V"] = np.concatenate([by_feature(v[0::2]), by_feature(v[1::2])], axis=1)
    d["L0_attn_W_O"] = a["L0_attn_W_O"].transpose(0, 2, 1).reshape(8, D, D).transpose(1, 0, 2)
    for k in "QKV":
        d["L0_attn_b_" + k] = a["L0_attn_b_" + k].reshape(8, D).T
    d["L0_attn_b_O"] = column(a["L0_attn_b_O"])
    more_layouts(a, d)
    return {k: np.ascontiguousarray(v) for k, v in d.items()}


def kernel(**inputs):
    import concourse.bacc as _bacc
    from concourse.bass_utils import run_bass_kernel_spmd as _run

    nc = _bacc.Bacc("TRN2", target_bir_lowering=False, num_devices=1)
    arrays, dram = {}, {}
    for name, array in layouts(inputs).items():
        arrays["in_" + name] = array
        dram[name] = nc.dram_tensor("in_" + name, array.shape, F32, kind="ExternalInput").ap()
    out = nc.dram_tensor("out_x", (P, B, S), F32, kind="ExternalOutput").ap()
    decoder(nc, dram, out)
    result = _run(nc, [arrays], core_ids=[0])
    return result.results[0]["out_x"].transpose(1, 2, 0)
```
